# Optimizing a Trainium2 kernel written in Bass

```python
import numpy as np
import jax
import jax.numpy as jnp

def _softmax(x, axis=-1):
    return jax.nn.softmax(x, axis=axis)

def _gelu(x):
    return jax.nn.gelu(x, approximate=True)

def _silu(x):
    return jax.nn.silu(x)

def _sigmoid(x):
    return jax.nn.sigmoid(x)

def _layernorm(x, axis=-1, eps=1e-05):
    m = jnp.mean(x, axis=axis, keepdims=True)
    v = jnp.var(x, axis=axis, keepdims=True)
    return (x - m) / jnp.sqrt(v + eps)

def _scatter_add(tgt, idx, src, axis=0):
    return tgt.at[idx].add(src)

def _segment_sum(src, seg, n):
    return jax.ops.segment_sum(src, seg, n)
kernel_name = 'mk_perceiver_d4_seqx_r4_2107cb'

def setup_inputs(seed: int=0):
    np.random.seed(seed)
    _w = jnp.asarray

    def _rec_inputs():
        import jax
        import jax.numpy as jnp
        _rk = jax.random.key(seed)
        x = 0.002226 + 0.9996 * jax.random.normal(jax.random.fold_in(_rk, 1), (1, 128, 256), jnp.float32)
        _lenS = 128 - jax.random.randint(jax.random.fold_in(_rk, 7), (1,), 0, max(1, 128 // 4) + 1, jnp.int32)
        _lenS2 = 12544 - jax.random.randint(jax.random.fold_in(_rk, 8), (1,), 0, max(1, 12544 // 4) + 1, jnp.int32)
        _ctx_1024P = jax.random.normal(jax.random.fold_in(_rk, 11), (1, 16, 256), jnp.float32)
        _ctx_1024c = jax.random.dirichlet(jax.random.fold_in(_rk, 511), 0.3 * jnp.ones((16,), jnp.float32), (1, 12544))
        _ctx_1024t = jnp.einsum('bsk,bkd->bsd', _ctx_1024c, _ctx_1024P)
        _ctx_1024t = _ctx_1024t * jax.lax.rsqrt(jnp.mean(jnp.square(_ctx_1024t)) + 1e-12) * 0.953939
        ctx_1024 = -7.10856e-05 + 0.999911 * (_ctx_1024t + 0.3 * jax.random.normal(jax.random.fold_in(_rk, 611), (1, 12544, 256), jnp.float32))
        _validS = jnp.arange(128)[None, :] < _lenS[:, None]
        _validS2 = jnp.arange(12544)[None, :] < _lenS2[:, None]
        _causal = jnp.tril(jnp.ones((128, 128), dtype=bool))
        mask_BxS2_ff1 = jnp.where(jnp.ones((1, 12544), dtype=bool), 1.0, 0.0).astype(jnp.float32)
        mask_BxSxS2_bk0 = jnp.logical_not(jnp.broadcast_to(_validS2[:, None, :], (1, 128, 12544)))
        return (x, ctx_1024, mask_BxS2_ff1, mask_BxSxS2_bk0)
    x, ctx_1024, mask_BxS2_ff1, mask_BxSxS2_bk0 = _rec_inputs()

    def _L0_xattn_setup():
        import jax, jax.numpy as jnp
        import numpy as np
        DIM = 256
        HEAD_DIM = 64
        NUM_HEADS = 8
        INNER = HEAD_DIM * NUM_HEADS
        ROT_DIM = HEAD_DIM
        ROPE_BASE = 10000.0
        EPS = 1e-05

        def layer_norm(x, g, b):
            mu = jnp.mean(x, axis=-1, keepdims=True)
            var = jnp.var(x, axis=-1, keepdims=True)
            return (x - mu) * jax.lax.rsqrt(var + EPS) * g + b

        def rope_rotate_k(k):
            n = k.shape[1]
            half = ROT_DIM // 2
            inv_freq = 1.0 / ROPE_BASE ** (jnp.arange(0, ROT_DIM, 2, dtype=jnp.float32) / ROT_DIM)
            theta = jnp.arange(n, dtype=jnp.float32)[:, None] * inv_freq[None, :]
            angles = jnp.concatenate([theta, theta], axis=-1)
            cos = jnp.cos(angles)[None, :, None, :].astype(k.dtype)
            sin = jnp.sin(angles)[None, :, None, :].astype(k.dtype)
            k_rope, k_pass = (k[..., :ROT_DIM], k[..., ROT_DIM:])
            neg_half = jnp.concatenate([-k_rope[..., half:], k_rope[..., :half]], axis=-1)
            k_rope = k_rope * cos + neg_half * sin
            return jnp.concatenate([k_rope, k_pass], axis=-1)
        key = jax.random.key(seed)
        ks = jax.random.split(key, 5)
        b, n, m = (8, 2048, 64)
        s = 1.0 / np.sqrt(DIM)
        return {'x': jax.random.normal(ks[0], (b, n, DIM), jnp.float32), 'latents': jax.random.normal(ks[1], (b, m, DIM), jnp.float32), 'gamma_x': jnp.ones((DIM,), jnp.float32), 'beta_x': jnp.zeros((DIM,), jnp.float32), 'gamma_l': jnp.ones((DIM,), jnp.float32), 'beta_l': jnp.zeros((DIM,), jnp.float32), 'Wq': jax.random.normal(ks[2], (DIM, INNER), jnp.float32) * s, 'Wkv': jax.random.normal(ks[3], (DIM, 2 * INNER), jnp.float32) * s, 'Wo': jax.random.normal(ks[4], (INNER, DIM), jnp.float32) * (1.0 / np.sqrt(INNER))}
    _L0_xattn_all = _L0_xattn_setup()
    _L0_xattn_in = {k: v for k, v in _L0_xattn_all.items() if k in ('gamma_x', 'beta_x', 'gamma_l', 'beta_l', 'Wq', 'Wkv', 'Wo')}
    del _L0_xattn_all

    def _L0_attn_setup():
        import jax, jax.numpy as jnp
        from jax import lax
        import numpy as np
        INPUT_DIM, STATE_DIM, CONV_K, EXPAND = (256, 16, 4, 2)
        INNER = INPUT_DIM * EXPAND
        BATCH, SEQ = (2, 512)
        key = jax.random.key(seed)
        ks = jax.random.split(key, 6)
        x = jax.random.normal(ks[0], (BATCH, SEQ, INPUT_DIM), jnp.float32)
        W_in = jax.random.normal(ks[1], (2 * INNER, INPUT_DIM), jnp.float32) * 0.02
        conv_w = jax.random.normal(ks[2], (INNER, 1, CONV_K), jnp.float32) * 0.1
        conv_b = jnp.zeros((INNER,), jnp.float32)
        A_log = jax.random.normal(ks[3], (INNER, STATE_DIM), jnp.float32)
        D = jnp.ones((INNER,), jnp.float32)
        W_out = jax.random.normal(ks[4], (INPUT_DIM, INNER), jnp.float32) * 0.02
        return {'x': x, 'W_in': W_in, 'conv_w': conv_w, 'conv_b': conv_b, 'A_log': A_log, 'D': D, 'W_out': W_out}
    _L0_attn_all = _L0_attn_setup()
    _L0_attn_in = {k: v for k, v in _L0_attn_all.items() if k in ('W_in', 'conv_w', 'conv_b', 'A_log', 'D', 'W_out')}
    del _L0_attn_all

    def _L0_ffn_setup():
        import jax, jax.numpy as jnp
        import numpy as np
        D_MODEL = 256
        D_FF = 1024
        N_EXP = 8
        TOP_K = 2

        def _gelu(x):
            return jax.nn.gelu(x, approximate=False)
        key = jax.random.key(seed)
        ks = jax.random.split(key, 12)
        s = 0.02
        return {'x': jax.random.normal(ks[0], (4, 512, D_MODEL), dtype=jnp.float32), 'shared_w1': jax.random.normal(ks[1], (D_MODEL, D_FF), dtype=jnp.float32) * s, 'shared_b1': jnp.zeros((D_FF,), jnp.float32), 'shared_w2': jax.random.normal(ks[2], (D_FF, D_MODEL), dtype=jnp.float32) * s, 'shared_b2': jnp.zeros((D_MODEL,), jnp.float32), 'router_w': jax.random.normal(ks[3], (D_MODEL, N_EXP), dtype=jnp.float32) * s, 'router_b': jnp.zeros((N_EXP,), jnp.float32), 'exp_w1': jax.random.normal(ks[4], (N_EXP, D_MODEL, D_FF), dtype=jnp.float32) * s, 'exp_b1': jnp.zeros((N_EXP, D_FF), jnp.float32), 'exp_w2': jax.random.normal(ks[5], (N_EXP, D_FF, D_MODEL), dtype=jnp.float32) * s, 'exp_b2': jnp.zeros((N_EXP, D_MODEL), jnp.float32)}
    _L0_ffn_all = _L0_ffn_setup()
    _L0_ffn_in = {k: v for k, v in _L0_ffn_all.items() if k in ('shared_w1', 'shared_b1', 'shared_w2', 'shared_b2', 'router_w', 'router_b', 'exp_w1', 'exp_b1', 'exp_w2', 'exp_b2')}
    del _L0_ffn_all

    def _L1_xattn_setup():
        import jax, jax.numpy as jnp
        import numpy as np
        DIM = 256
        N_HEADS = 16
        key = jax.random.key(seed)
        ks = jax.random.split(key, 9)
        B, S, D = (4, 512, DIM)
        inp = {'q': jax.random.normal(ks[0], (B, S, D), dtype=jnp.float32), 'k': jax.random.normal(ks[1], (B, S, D), dtype=jnp.float32), 'v': jax.random.normal(ks[2], (B, S, D), dtype=jnp.float32), 'mask': jnp.ones((B, S), dtype=jnp.float32), 'wq': jax.random.normal(ks[3], (D, D), dtype=jnp.float32) / np.sqrt(D), 'bq': jnp.zeros((D,), dtype=jnp.float32), 'wk': jax.random.normal(ks[4], (D, D), dtype=jnp.float32) / np.sqrt(D), 'bk': jnp.zeros((D,), dtype=jnp.float32), 'wv': jax.random.normal(ks[5], (D, D), dtype=jnp.float32) / np.sqrt(D), 'bv': jnp.zeros((D,), dtype=jnp.float32)}
        return inp
    _L1_xattn_all = _L1_xattn_setup()
    _L1_xattn_in = {k: v for k, v in _L1_xattn_all.items() if k in ('wq', 'bq', 'wk', 'bk', 'wv', 'bv')}
    del _L1_xattn_all

    def _L1_attn_setup():
        import jax, jax.numpy as jnp
        import numpy as np
        B, TT, C, H, T = (4, 1024, 256, 16, 128)
        K = C // H
        HEAD_DIV = 8.0
        EPS = 1e-05
        LAYER_ID, N_LAYER = (12, 24)
        key = jax.random.key(seed)
        ks = jax.random.split(key, 8)
        r01 = LAYER_ID / (N_LAYER - 1)
        r1a0 = 1.0 - LAYER_ID / N_LAYER
        ddd = (jnp.arange(C, dtype=jnp.float32) / C).reshape(1, 1, C)
        h = jnp.arange(H, dtype=jnp.float32)
        scale = 0.02
        return {'xq': jax.random.normal(ks[0], (B, TT, C), jnp.float32), 'time_mix_k': ddd ** r1a0, 'time_mix_v': ddd ** r1a0 + 0.3 * r01, 'time_mix_r': ddd ** (0.5 * r1a0), 'time_mix_g': ddd ** (0.5 * r1a0), 'time_decay': -8.0 + 7.0 * (h / (H - 1)) ** (0.7 + 1.3 * r01), 'time_faaaa': r01 * (1.0 - h / (H - 1)), 'W_r': jax.random.normal(ks[1], (C, C), jnp.float32) * scale, 'W_k': jax.random.normal(ks[2], (C, C), jnp.float32) * scale, 'W_v': jax.random.normal(ks[3], (C, C), jnp.float32) * scale, 'W_g': jax.random.normal(ks[4], (C, C), jnp.float32) * scale, 'W_o': jax.random.normal(ks[5], (C, C), jnp.float32) * scale, 'ln_w': jnp.ones((C,), jnp.float32), 'ln_b': jnp.zeros((C,), jnp.float32)}
    _L1_attn_all = _L1_attn_setup()
    _L1_attn_in = {k: v for k, v in _L1_attn_all.items() if k in ('time_mix_k', 'time_mix_v', 'time_mix_r', 'time_mix_g', 'time_decay', 'time_faaaa', 'W_r', 'W_k', 'W_v', 'W_g', 'W_o', 'ln_w', 'ln_b')}
    del _L1_attn_all

    def _L1_ffn_setup():
        import jax, jax.numpy as jnp
        import numpy as np
        E, D, H = (8, 256, 1024)
        B, S = (4, 1024)
        TEMPERATURE = 1.0
        key = jax.random.key(seed)
        ks = jax.random.split(key, 7)
        sc = 0.02
        return {'x': jax.random.normal(ks[0], (B, S, D), dtype=jnp.float32), 'W1': jax.random.normal(ks[1], (E, D, H), dtype=jnp.float32) * sc, 'b1': jax.random.normal(ks[2], (E, H), dtype=jnp.float32) * sc, 'W2': jax.random.normal(ks[3], (E, H, D), dtype=jnp.float32) * sc, 'b2': jax.random.normal(ks[4], (E, D), dtype=jnp.float32) * sc, 'Wr': jax.random.normal(ks[5], (D, E), dtype=jnp.float32) * sc, 'br': jax.random.normal(ks[6], (E,), dtype=jnp.float32) * sc}
    _L1_ffn_all = _L1_ffn_setup()
    _L1_ffn_in = {k: v for k, v in _L1_ffn_all.items() if k in ('W1', 'b1', 'W2', 'b2', 'Wr', 'br')}
    del _L1_ffn_all

    def _L2_xattn_setup():
        import jax, jax.numpy as jnp
        import numpy as np
        H, D, DIM = (8, 128, 256)
        QB, N = (16, 128)

        def layer_norm(x, g, b, eps=1e-05):
            mu = x.mean(-1, keepdims=True)
            var = ((x - mu) ** 2).mean(-1, keepdims=True)
            return (x - mu) / jnp.sqrt(var + eps) * g + b
        key = jax.random.key(seed)
        ks = jax.random.split(key, 8)
        rn = lambda k, shape, s=1.0: jax.random.normal(k, shape, jnp.float32) * s
        return {'q': rn(ks[0], (QB, N, DIM)), 'k': rn(ks[1], (QB, N, DIM)), 'v': rn(ks[2], (QB, N, DIM)), 'ln_g': jnp.ones(DIM, jnp.float32), 'ln_b': jnp.zeros(DIM, jnp.float32), 'w_in': rn(ks[3], (H * D, DIM), 0.02), 'wp_w1': rn(ks[4], (D, 2 * D), 0.05), 'wp_b1': jnp.zeros(D, jnp.float32), 'wp_ln_g': jnp.ones(D, jnp.float32), 'wp_ln_b': jnp.zeros(D, jnp.float32), 'wp_w2': rn(ks[5], (3, D), 0.05), 'wp_b2': jnp.zeros(3, jnp.float32), 'w_out': rn(ks[6], (DIM, H * D), 0.02), 'b_out': jnp.zeros(DIM, jnp.float32)}
    _L2_xattn_all = _L2_xattn_setup()
    _L2_xattn_in = {k: v for k, v in _L2_xattn_all.items() if k in ('ln_g', 'ln_b', 'w_in', 'wp_w1', 'wp_b1', 'wp_ln_g', 'wp_ln_b', 'wp_w2', 'wp_b2', 'w_out', 'b_out')}
    del _L2_xattn_all

    def _L2_attn_setup():
        import jax, jax.numpy as jnp
        import numpy as np
        import math
        D_MODEL = 256
        D_STATE = 16
        D_CONV = 4
        EXPAND = 2
        D_INNER = EXPAND * D_MODEL
        DT_RANK = math.ceil(D_MODEL / 16)
        BATCH, SEQ = (4, 256)
        DT_MIN, DT_MAX = (0.001, 0.1)

        def _forward(x, W_in, W_conv, b_conv, W_xproj, W_dt, b_dt, A_log, D, W_out):
            b, l, _ = x.shape
            d_inner = W_in.shape[1] // 2
            d_conv = W_conv.shape[-1]
            n = A_log.shape[1]
            r = W_dt.shape[0]
            xz = x @ W_in
            xi, z = jnp.split(xz, 2, axis=-1)
            xi_t = jnp.moveaxis(xi, 1, 2)
            xi_pad = jnp.pad(xi_t, ((0, 0), (0, 0), (d_conv - 1, 0)))
            conv = jax.lax.conv_general_dilated(xi_pad, W_conv, window_strides=(1,), padding='VALID', feature_group_count=d_inner)
            xc = jax.nn.silu(jnp.moveaxis(conv + b_conv[None, :, None], 2, 1))
            dbc = xc @ W_xproj
            delta_lr, B, C = jnp.split(dbc, [r, r + n], axis=-1)
            delta = jax.nn.softplus(delta_lr @ W_dt + b_dt)
            A = -jnp.exp(A_log)
            dA = jnp.exp(delta[..., None] * A)
            dBx = delta[..., None] * B[:, :, None, :] * xc[..., None]

            def step(h, inp):
                dA_t, dBx_t, C_t, x_t = inp
                h = dA_t * h + dBx_t
                y = jnp.einsum('bdn,bn->bd', h, C_t) + D * x_t
                return (h, y)
            h0 = jnp.zeros((b, d_inner, n), x.dtype)
            _, ys = jax.lax.scan(step, h0, (jnp.moveaxis(dA, 1, 0), jnp.moveaxis(dBx, 1, 0), jnp.moveaxis(C, 1, 0), jnp.moveaxis(xc, 1, 0)))
            y = jnp.moveaxis(ys, 0, 1)
            return y * jax.nn.silu(z) @ W_out
        key = jax.random.key(seed)
        ks = jax.random.split(key, 8)
        x = jax.random.normal(ks[0], (BATCH, SEQ, D_MODEL), dtype=jnp.float32)
        W_in = jax.random.normal(ks[1], (D_MODEL, 2 * D_INNER), jnp.float32) * 0.02
        W_conv = jax.random.normal(ks[2], (D_INNER, 1, D_CONV), jnp.float32) * 0.2
        b_conv = jnp.zeros((D_INNER,), jnp.float32)
        W_xproj = jax.random.normal(ks[3], (D_INNER, DT_RANK + 2 * D_STATE), jnp.float32) * 0.02
        dt_init_std = DT_RANK ** (-0.5)
        W_dt = jax.random.uniform(ks[4], (DT_RANK, D_INNER), jnp.float32, -dt_init_std, dt_init_std)
        u = jax.random.uniform(ks[5], (D_INNER,), jnp.float32)
        dt = jnp.clip(jnp.exp(u * (math.log(DT_MAX) - math.log(DT_MIN)) + math.log(DT_MIN)), DT_MIN, None)
        b_dt = dt + jnp.log(-jnp.expm1(-dt))
        A_log = jnp.log(jnp.tile(jnp.arange(1, D_STATE + 1, dtype=jnp.float32)[None, :], (D_INNER, 1)))
        D = jnp.ones((D_INNER,), jnp.float32)
        W_out = jax.random.normal(ks[6], (D_INNER, D_MODEL), jnp.float32) * 0.02
        return {'x': x, 'W_in': W_in, 'W_conv': W_conv, 'b_conv': b_conv, 'W_xproj': W_xproj, 'W_dt': W_dt, 'b_dt': b_dt, 'A_log': A_log, 'D': D, 'W_out': W_out}
    _L2_attn_all = _L2_attn_setup()
    _L2_attn_in = {k: v for k, v in _L2_attn_all.items() if k in ('W_in', 'W_conv', 'b_conv', 'W_xproj', 'W_dt', 'b_dt', 'A_log', 'D', 'W_out')}
    del _L2_attn_all

    def _L2_ffn_setup():
        import jax, jax.numpy as jnp
        import numpy as np
        TEMPERATURE = 1.0
        NUM_EXPERTS = 8
        key = jax.random.key(seed)
        ks = jax.random.split(key, 7)
        B, S, H, E = (4, 1024, 256, NUM_EXPERTS)
        scale = 1.0 / np.sqrt(H)
        return {'hidden_states': jax.random.normal(ks[0], (B, S, H), dtype=jnp.float32), 'w1': jax.random.normal(ks[1], (H, H // 2), dtype=jnp.float32) * scale, 'b1': jax.random.normal(ks[2], (H // 2,), dtype=jnp.float32) * 0.01, 'w2': jax.random.normal(ks[3], (H // 2, E), dtype=jnp.float32) * (1.0 / np.sqrt(H // 2)), 'b2': jax.random.normal(ks[4], (E,), dtype=jnp.float32) * 0.01, 'expert_W': jax.random.normal(ks[5], (E, H, H), dtype=jnp.float32) * scale, 'expert_b': jax.random.normal(ks[6], (E, H), dtype=jnp.float32) * 0.01}
    _L2_ffn_all = _L2_ffn_setup()
    _L2_ffn_in = {k: v for k, v in _L2_ffn_all.items() if k in ('w1', 'b1', 'w2', 'b2', 'expert_W', 'expert_b')}
    del _L2_ffn_all

    def _L3_xattn_setup():
        import jax, jax.numpy as jnp
        import numpy as np
        N_HEADS = 16
        NEG_BIAS = -1000000000.0
        key = jax.random.key(seed)
        kq, kk, kv = jax.random.split(key, 3)
        B, S, D = (2, 512, 256)
        queries = jax.random.normal(kq, (B, S, D), dtype=jnp.float32)
        keys = jax.random.normal(kk, (B, S, D), dtype=jnp.float32)
        values = jax.random.normal(kv, (B, S, D), dtype=jnp.float32)
        mask = jnp.broadcast_to(jnp.tril(jnp.ones((S, S), dtype=bool)), (B, S, S))
        return {'queries': queries, 'keys': keys, 'values': values, 'mask': mask}
    _L3_xattn_all = _L3_xattn_setup()
    _L3_xattn_in = {k: v for k, v in _L3_xattn_all.items() if k in ()}
    del _L3_xattn_all

    def _L3_attn_setup():
        import jax, jax.numpy as jnp
        import numpy as np
        HEADS = 16
        D_MODEL = 256
        D_K = D_MODEL // HEADS
        SEQ = 512
        BSZ = 2
        BASE = 10000.0

        def _rope(x):
            s = x.shape[0]
            d = x.shape[-1]
            ar = jnp.arange(0, d, 2, dtype=jnp.float32)
            theta = 1.0 / (jnp.power(BASE, ar) / d)
            pos = jnp.arange(s, dtype=jnp.float32)
            idx_theta = pos[:, None] * theta[None, :]
            idx2 = jnp.concatenate([idx_theta, idx_theta], -1)
            cos = jnp.cos(idx2)[:, None, None, :]
            sin = jnp.sin(idx2)[:, None, None, :]
            neg_x = jnp.concatenate([-x[..., d // 2:], x[..., :d // 2]], axis=-1)
            return x * cos + neg_x * sin

        def _softmax_one(x, axis):
            x = x - jnp.max(x, axis=axis, keepdims=True)
            e = jnp.exp(x)
            return e / (1.0 + jnp.sum(e, axis=axis, keepdims=True))
        key = jax.random.key(seed)
        ks = jax.random.split(key, 7)
        sc = 1.0 / np.sqrt(D_MODEL)
        return {'x': jax.random.normal(ks[0], (SEQ, BSZ, D_MODEL), jnp.float32), 'Wq': jax.random.normal(ks[1], (D_MODEL, D_MODEL), jnp.float32) * sc, 'bq': jnp.zeros((D_MODEL,), jnp.float32), 'Wk': jax.random.normal(ks[2], (D_MODEL, D_MODEL), jnp.float32) * sc, 'bk': jnp.zeros((D_MODEL,), jnp.float32), 'Wv': jax.random.normal(ks[3], (D_MODEL, D_MODEL), jnp.float32) * sc, 'bv': jnp.zeros((D_MODEL,), jnp.float32)}
    _L3_attn_all = _L3_attn_setup()
    _L3_attn_in = {k: v for k, v in _L3_attn_all.items() if k in ('Wq', 'bq', 'Wk', 'bk', 'Wv', 'bv')}
    del _L3_attn_all

    def _L3_ffn_setup():
        import jax, jax.numpy as jnp
        import numpy as np
        HIDDEN = 256
        NUM_EXPERTS = 8
        TOP_K = 2
        B, S = (2, 512)
        key = jax.random.key(seed)
        k1, k2, k3, k4, k5 = jax.random.split(key, 5)
        d, dff, E = (HIDDEN, 4 * HIDDEN, NUM_EXPERTS)
        x = jax.random.normal(k1, (B, S, d), dtype=jnp.float32)
        W1 = jax.random.normal(k2, (E, d, dff), dtype=jnp.float32) * (1.0 / np.sqrt(d))
        b1 = jax.random.normal(k3, (E, dff), dtype=jnp.float32) * 0.01
        W2 = jax.random.normal(k4, (E, dff, d), dtype=jnp.float32) * (1.0 / np.sqrt(dff))
        b2 = jax.random.normal(k5, (E, d), dtype=jnp.float32) * 0.01
        return {'x': x, 'W1': W1, 'b1': b1, 'W2': W2, 'b2': b2}
    _L3_ffn_all = _L3_ffn_setup()
    _L3_ffn_in = {k: v for k, v in _L3_ffn_all.items() if k in ('W1', 'b1', 'W2', 'b2')}
    del _L3_ffn_all
    return {'x': x, 'ctx_1024': ctx_1024, 'mask_BxS2_ff1': mask_BxS2_ff1, 'mask_BxSxS2_bk0': mask_BxSxS2_bk0, 'L0_xattn_gamma_x': _L0_xattn_in['gamma_x'], 'L0_xattn_beta_x': _L0_xattn_in['beta_x'], 'L0_xattn_gamma_l': _L0_xattn_in['gamma_l'], 'L0_xattn_beta_l': _L0_xattn_in['beta_l'], 'L0_xattn_Wq': _L0_xattn_in['Wq'], 'L0_xattn_Wkv': _L0_xattn_in['Wkv'], 'L0_xattn_Wo': _L0_xattn_in['Wo'], 'L0_attn_W_in': _L0_attn_in['W_in'], 'L0_attn_conv_w': _L0_attn_in['conv_w'], 'L0_attn_conv_b': _L0_attn_in['conv_b'], 'L0_attn_A_log': _L0_attn_in['A_log'], 'L0_attn_D': _L0_attn_in['D'], 'L0_attn_W_out': _L0_attn_in['W_out'], 'L0_ffn_shared_w1': _L0_ffn_in['shared_w1'], 'L0_ffn_shared_b1': _L0_ffn_in['shared_b1'], 'L0_ffn_shared_w2': _L0_ffn_in['shared_w2'], 'L0_ffn_shared_b2': _L0_ffn_in['shared_b2'], 'L0_ffn_router_w': _L0_ffn_in['router_w'], 'L0_ffn_router_b': _L0_ffn_in['router_b'], 'L0_ffn_exp_w1': _L0_ffn_in['exp_w1'], 'L0_ffn_exp_b1': _L0_ffn_in['exp_b1'], 'L0_ffn_exp_w2': _L0_ffn_in['exp_w2'], 'L0_ffn_exp_b2': _L0_ffn_in['exp_b2'], 'L1_xattn_wq': _L1_xattn_in['wq'], 'L1_xattn_bq': _L1_xattn_in['bq'], 'L1_xattn_wk': _L1_xattn_in['wk'], 'L1_xattn_bk': _L1_xattn_in['bk'], 'L1_xattn_wv': _L1_xattn_in['wv'], 'L1_xattn_bv': _L1_xattn_in['bv'], 'L1_attn_time_mix_k': _L1_attn_in['time_mix_k'], 'L1_attn_time_mix_v': _L1_attn_in['time_mix_v'], 'L1_attn_time_mix_r': _L1_attn_in['time_mix_r'], 'L1_attn_time_mix_g': _L1_attn_in['time_mix_g'], 'L1_attn_time_decay': _L1_attn_in['time_decay'], 'L1_attn_time_faaaa': _L1_attn_in['time_faaaa'], 'L1_attn_W_r': _L1_attn_in['W_r'], 'L1_attn_W_k': _L1_attn_in['W_k'], 'L1_attn_W_v': _L1_attn_in['W_v'], 'L1_attn_W_g': _L1_attn_in['W_g'], 'L1_attn_W_o': _L1_attn_in['W_o'], 'L1_attn_ln_w': _L1_attn_in['ln_w'], 'L1_attn_ln_b': _L1_attn_in['ln_b'], 'L1_ffn_W1': _L1_ffn_in['W1'], 'L1_ffn_b1': _L1_ffn_in['b1'], 'L1_ffn_W2': _L1_ffn_in['W2'], 'L1_ffn_b2': _L1_ffn_in['b2'], 'L1_ffn_Wr': _L1_ffn_in['Wr'], 'L1_ffn_br': _L1_ffn_in['br'], 'L2_xattn_ln_g': _L2_xattn_in['ln_g'], 'L2_xattn_ln_b': _L2_xattn_in['ln_b'], 'L2_xattn_w_in': _L2_xattn_in['w_in'], 'L2_xattn_wp_w1': _L2_xattn_in['wp_w1'], 'L2_xattn_wp_b1': _L2_xattn_in['wp_b1'], 'L2_xattn_wp_ln_g': _L2_xattn_in['wp_ln_g'], 'L2_xattn_wp_ln_b': _L2_xattn_in['wp_ln_b'], 'L2_xattn_wp_w2': _L2_xattn_in['wp_w2'], 'L2_xattn_wp_b2': _L2_xattn_in['wp_b2'], 'L2_xattn_w_out': _L2_xattn_in['w_out'], 'L2_xattn_b_out': _L2_xattn_in['b_out'], 'L2_attn_W_in': _L2_attn_in['W_in'], 'L2_attn_W_conv': _L2_attn_in['W_conv'], 'L2_attn_b_conv': _L2_attn_in['b_conv'], 'L2_attn_W_xproj': _L2_attn_in['W_xproj'], 'L2_attn_W_dt': _L2_attn_in['W_dt'], 'L2_attn_b_dt': _L2_attn_in['b_dt'], 'L2_attn_A_log': _L2_attn_in['A_log'], 'L2_attn_D': _L2_attn_in['D'], 'L2_attn_W_out': _L2_attn_in['W_out'], 'L2_ffn_w1': _L2_ffn_in['w1'], 'L2_ffn_b1': _L2_ffn_in['b1'], 'L2_ffn_w2': _L2_ffn_in['w2'], 'L2_ffn_b2': _L2_ffn_in['b2'], 'L2_ffn_expert_W': _L2_ffn_in['expert_W'], 'L2_ffn_expert_b': _L2_ffn_in['expert_b'], 'L3_attn_Wq': _L3_attn_in['Wq'], 'L3_attn_bq': _L3_attn_in['bq'], 'L3_attn_Wk': _L3_attn_in['Wk'], 'L3_attn_bk': _L3_attn_in['bk'], 'L3_attn_Wv': _L3_attn_in['Wv'], 'L3_attn_bv': _L3_attn_in['bv'], 'L3_ffn_W1': _L3_ffn_in['W1'], 'L3_ffn_b1': _L3_ffn_in['b1'], 'L3_ffn_W2': _L3_ffn_in['W2'], 'L3_ffn_b2': _L3_ffn_in['b2']}

def reference(x, ctx_1024, mask_BxS2_ff1, mask_BxSxS2_bk0, L0_xattn_gamma_x, L0_xattn_beta_x, L0_xattn_gamma_l, L0_xattn_beta_l, L0_xattn_Wq, L0_xattn_Wkv, L0_xattn_Wo, L0_attn_W_in, L0_attn_conv_w, L0_attn_conv_b, L0_attn_A_log, L0_attn_D, L0_attn_W_out, L0_ffn_shared_w1, L0_ffn_shared_b1, L0_ffn_shared_w2, L0_ffn_shared_b2, L0_ffn_router_w, L0_ffn_router_b, L0_ffn_exp_w1, L0_ffn_exp_b1, L0_ffn_exp_w2, L0_ffn_exp_b2, L1_xattn_wq, L1_xattn_bq, L1_xattn_wk, L1_xattn_bk, L1_xattn_wv, L1_xattn_bv, L1_attn_time_mix_k, L1_attn_time_mix_v, L1_attn_time_mix_r, L1_attn_time_mix_g, L1_attn_time_decay, L1_attn_time_faaaa, L1_attn_W_r, L1_attn_W_k, L1_attn_W_v, L1_attn_W_g, L1_attn_W_o, L1_attn_ln_w, L1_attn_ln_b, L1_ffn_W1, L1_ffn_b1, L1_ffn_W2, L1_ffn_b2, L1_ffn_Wr, L1_ffn_br, L2_xattn_ln_g, L2_xattn_ln_b, L2_xattn_w_in, L2_xattn_wp_w1, L2_xattn_wp_b1, L2_xattn_wp_ln_g, L2_xattn_wp_ln_b, L2_xattn_wp_w2, L2_xattn_wp_b2, L2_xattn_w_out, L2_xattn_b_out, L2_attn_W_in, L2_attn_W_conv, L2_attn_b_conv, L2_attn_W_xproj, L2_attn_W_dt, L2_attn_b_dt, L2_attn_A_log, L2_attn_D, L2_attn_W_out, L2_ffn_w1, L2_ffn_b1, L2_ffn_w2, L2_ffn_b2, L2_ffn_expert_W, L2_ffn_expert_b, L3_attn_Wq, L3_attn_bq, L3_attn_Wk, L3_attn_bk, L3_attn_Wv, L3_attn_bv, L3_ffn_W1, L3_ffn_b1, L3_ffn_W2, L3_ffn_b2):
    import jax
    import jax.numpy as jnp

    def _L0_xattn_ref(x, latents, gamma_x, beta_x, gamma_l, beta_l, Wq, Wkv, Wo):
        import jax, jax.numpy as jnp
        import numpy as np
        DIM = 256
        HEAD_DIM = 64
        NUM_HEADS = 8
        INNER = HEAD_DIM * NUM_HEADS
        ROT_DIM = HEAD_DIM
        ROPE_BASE = 10000.0
        EPS = 1e-05

        def layer_norm(x, g, b):
            mu = jnp.mean(x, axis=-1, keepdims=True)
            var = jnp.var(x, axis=-1, keepdims=True)
            return (x - mu) * jax.lax.rsqrt(var + EPS) * g + b

        def rope_rotate_k(k):
            n = k.shape[1]
            half = ROT_DIM // 2
            inv_freq = 1.0 / ROPE_BASE ** (jnp.arange(0, ROT_DIM, 2, dtype=jnp.float32) / ROT_DIM)
            theta = jnp.arange(n, dtype=jnp.float32)[:, None] * inv_freq[None, :]
            angles = jnp.concatenate([theta, theta], axis=-1)
            cos = jnp.cos(angles)[None, :, None, :].astype(k.dtype)
            sin = jnp.sin(angles)[None, :, None, :].astype(k.dtype)
            k_rope, k_pass = (k[..., :ROT_DIM], k[..., ROT_DIM:])
            neg_half = jnp.concatenate([-k_rope[..., half:], k_rope[..., :half]], axis=-1)
            k_rope = k_rope * cos + neg_half * sin
            return jnp.concatenate([k_rope, k_pass], axis=-1)
        b, n, _ = x.shape
        m = latents.shape[1]
        h, d = (NUM_HEADS, HEAD_DIM)
        scale = d ** (-0.5)
        xn = layer_norm(x, gamma_x, beta_x)
        ln = layer_norm(latents, gamma_l, beta_l)
        q = (ln @ Wq).reshape(b, m, h, d)
        kv_x = xn @ Wkv
        k_x, v_x = (kv_x[..., :INNER], kv_x[..., INNER:])
        kv_l = ln @ Wkv
        k_l, v_l = (kv_l[..., :INNER], kv_l[..., INNER:])
        k_x = k_x.reshape(b, n, h, d)
        v_x = v_x.reshape(b, n, h, d)
        k_x = rope_rotate_k(k_x)
        q = jnp.transpose(q, (0, 2, 1, 3)) * scale
        k_x = jnp.transpose(k_x, (0, 2, 1, 3))
        v_x = jnp.transpose(v_x, (0, 2, 1, 3))
        k_l = jnp.transpose(k_l.reshape(b, m, h, d), (0, 2, 1, 3))
        v_l = jnp.transpose(v_l.reshape(b, m, h, d), (0, 2, 1, 3))
        k = jnp.concatenate([k_x, k_l], axis=2)
        v = jnp.concatenate([v_x, v_l], axis=2)
        sim = jnp.einsum('bhid,bhjd->bhij', q, k)
        attn = jax.nn.softmax(sim, axis=-1)
        out = jnp.einsum('bhij,bhjd->bhid', attn, v)
        out = jnp.transpose(out, (0, 2, 1, 3)).reshape(b, m, INNER)
        return out @ Wo

    def _L0_attn_ref(x, W_in, conv_w, conv_b, A_log, D, W_out):
        import jax, jax.numpy as jnp
        from jax import lax
        import numpy as np
        INPUT_DIM, STATE_DIM, CONV_K, EXPAND = (256, 16, 4, 2)
        INNER = INPUT_DIM * EXPAND
        BATCH, SEQ = (2, 512)
        b, s, _ = x.shape
        inner = W_in.shape[0] // 2
        K = conv_w.shape[-1]
        state = A_log.shape[1]
        xr = x @ W_in.T
        x_ssm, res = (xr[..., :inner], xr[..., inner:])
        xc = jnp.transpose(x_ssm, (0, 2, 1))
        xc = jnp.pad(xc, ((0, 0), (0, 0), (K - 1, 0)))
        xc = lax.conv_general_dilated(xc, conv_w, (1,), 'VALID', feature_group_count=inner, dimension_numbers=('NCH', 'OIH', 'NCH'))
        x_conv = jax.nn.silu(jnp.transpose(xc, (0, 2, 1)) + conv_b)
        delta = jax.nn.softplus(x_conv)
        A = -jnp.exp(A_log)
        A_d = jnp.exp(delta[..., None] * A)
        Bx = x_conv * x_conv

        def step(h, inp):
            a_t, bx_t, c_t = inp
            h = a_t * h + bx_t[..., None]
            y = c_t * jnp.sum(h, axis=-1)
            return (h, y)
        h0 = jnp.zeros((b, inner, state), x.dtype)
        _, ys = lax.scan(step, h0, (jnp.moveaxis(A_d, 1, 0), jnp.moveaxis(Bx, 1, 0), jnp.moveaxis(x_conv, 1, 0)))
        y_ssm = jnp.moveaxis(ys, 0, 1)
        y = y_ssm * jax.nn.silu(res) + D * x_conv
        return y @ W_out.T

    def _L0_ffn_ref(x, shared_w1, shared_b1, shared_w2, shared_b2, router_w, router_b, exp_w1, exp_b1, exp_w2, exp_b2):
        import jax, jax.numpy as jnp
        import numpy as np
        D_MODEL = 256
        D_FF = 1024
        N_EXP = 8
        TOP_K = 2

        def _gelu(x):
            return jax.nn.gelu(x, approximate=False)
        leading = x.shape[:-1]
        d = x.shape[-1]
        xf = x.reshape(-1, d)
        T = xf.shape[0]
        h_shared = _gelu(xf @ shared_w1 + shared_b1) @ shared_w2 + shared_b2
        logits = xf @ router_w + router_b
        routing = jax.nn.softmax(logits, axis=-1)
        sel_w, sel_idx = jax.lax.top_k(routing, TOP_K)
        sel_w = sel_w / (jnp.sum(sel_w, axis=-1, keepdims=True) + 1e-09)
        combine = jnp.zeros((T, N_EXP), routing.dtype)
        combine = combine.at[jnp.arange(T)[:, None], sel_idx].add(sel_w)
        residual = jnp.zeros_like(xf)
        for e in range(N_EXP):
            h = _gelu(xf @ exp_w1[e] + exp_b1[e])
            y = h @ exp_w2[e] + exp_b2[e]
            residual = residual + combine[:, e:e + 1] * y
        out = h_shared + residual
        return out.reshape(*leading, d)

    def _L1_xattn_ref(q, k, v, mask, wq, bq, wk, bk, wv, bv):
        import jax, jax.numpy as jnp
        import numpy as np
        DIM = 256
        N_HEADS = 16
        B, Sq, D = q.shape
        Skv = k.shape[1]
        H = N_HEADS
        Dh = D // H
        qp = q @ wq.T + bq
        kp = k @ wk.T + bk
        vp = v @ wv.T + bv
        qh = qp.reshape(B, Sq, H, Dh).transpose(0, 2, 1, 3)
        kh = kp.reshape(B, Skv, H, Dh).transpose(0, 2, 1, 3)
        vh = vp.reshape(B, Skv, H, Dh).transpose(0, 2, 1, 3)
        scores = jnp.einsum('bhqd,bhkd->bhqk', qh, kh) / np.sqrt(Dh).astype(np.float32)
        scores = scores - 10000.0 * (1.0 - mask[:, None, None, :])
        attn = jax.nn.softmax(scores, axis=-1)
        out = jnp.einsum('bhqk,bhkd->bhqd', attn, vh)
        out = out.transpose(0, 2, 1, 3).reshape(B, Sq, D)
        return out

    def _L1_attn_ref(xq, time_mix_k, time_mix_v, time_mix_r, time_mix_g, time_decay, time_faaaa, W_r, W_k, W_v, W_g, W_o, ln_w, ln_b):
        import jax, jax.numpy as jnp
        import numpy as np
        B, TT, C, H, T = (4, 1024, 256, 16, 128)
        K = C // H
        HEAD_DIV = 8.0
        EPS = 1e-05
        LAYER_ID, N_LAYER = (12, 24)
        x = xq
        B_, TT_, C_ = x.shape
        N = TT_ // T
        xx = jnp.pad(x, ((0, 0), (1, 0), (0, 0)))[:, :-1]
        xr = x * time_mix_r + xx * (1 - time_mix_r)
        xk = x * time_mix_k + xx * (1 - time_mix_k)
        xv = x * time_mix_v + xx * (1 - time_mix_v)
        xg = x * time_mix_g + xx * (1 - time_mix_g)
        r = (xr @ W_r.T).reshape(B_, TT_, H, K).transpose(0, 2, 1, 3)
        k = (xk @ W_k.T).reshape(B_, TT_, H, K).transpose(0, 2, 1, 3)
        v = (xv @ W_v.T).reshape(B_, TT_, H, K).transpose(0, 2, 1, 3)
        g = jax.nn.silu(xg @ W_g.T)
        decay = jnp.exp(-jnp.exp(time_decay))
        u = time_faaaa
        ws = decay ** T
        i_idx = jnp.arange(T)
        wb = decay[:, None] ** i_idx
        wk = decay[:, None] ** (T - 1 - i_idx)
        diff = i_idx[:, None] - i_idx[None, :]
        pw = decay[:, None, None] ** jnp.maximum(diff - 1, 0)
        w_mat = jnp.where(diff > 0, pw, 0.0) + jnp.eye(T, dtype=x.dtype) * u[:, None, None]
        rc = r.reshape(B_, H, N, T, K).transpose(2, 0, 1, 3, 4)
        kc = k.reshape(B_, H, N, T, K).transpose(2, 0, 1, 3, 4)
        vc = v.reshape(B_, H, N, T, K).transpose(2, 0, 1, 3, 4)
        s0 = jnp.zeros((B_, H, K, K), x.dtype)

        def step(s, chunk):
            rr, kk, vv = chunk
            att = jnp.einsum('bhik,bhjk->bhij', rr, kk) * w_mat
            out = att @ vv + jnp.einsum('bhik,bhkv->bhiv', rr, s) * wb[None, :, :, None]
            s_new = ws[None, :, None, None] * s + jnp.einsum('bhjk,bhjv->bhkv', kk * wk[None, :, :, None], vv)
            return (s_new, out)
        _, xo = jax.lax.scan(step, s0, (rc, kc, vc))
        xo = xo.transpose(1, 0, 3, 2, 4).reshape(B_, TT_, H, K)
        y = xo / HEAD_DIV
        mu = y.mean(-1, keepdims=True)
        var = y.var(-1, keepdims=True)
        y = (y - mu) / jnp.sqrt(var + EPS)
        y = y * ln_w.reshape(H, K) + ln_b.reshape(H, K)
        y = y.reshape(B_, TT_, C_)
        return y * g @ W_o.T

    def _L1_ffn_ref(x, W1, b1, W2, b2, Wr, br):
        import jax, jax.numpy as jnp
        import numpy as np
        E, D, H = (8, 256, 1024)
        B, S = (4, 1024)
        TEMPERATURE = 1.0
        routing_logits = (x @ Wr + br) / TEMPERATURE
        routing_probs = jax.nn.softmax(routing_logits, axis=-1)
        indices = jnp.argmax(routing_probs, axis=-1)
        out = jnp.zeros_like(x)
        num_experts = W1.shape[0]
        for i in range(num_experts):
            mask = (indices == i).astype(x.dtype)[..., None]
            xi = x * mask
            h = jax.nn.relu(xi @ W1[i] + b1[i])
            out = out + (h @ W2[i] + b2[i])
        return out

    def _L2_xattn_ref(q, k, v, ln_g, ln_b, w_in, wp_w1, wp_b1, wp_ln_g, wp_ln_b, wp_w2, wp_b2, w_out, b_out):
        import jax, jax.numpy as jnp
        import numpy as np
        H, D, DIM = (8, 128, 256)
        QB, N = (16, 128)

        def layer_norm(x, g, b, eps=1e-05):
            mu = x.mean(-1, keepdims=True)
            var = ((x - mu) ** 2).mean(-1, keepdims=True)
            return (x - mu) / jnp.sqrt(var + eps) * g + b

        def proj(t):
            x = layer_norm(t, ln_g, ln_b) @ w_in.T
            Qd, Nd = (t.shape[0], t.shape[1])
            return x.reshape(Qd, Nd, H, D).transpose(2, 0, 1, 3)
        f_q, f_k, f_v = (proj(q), proj(k), proj(v))
        dots = jnp.einsum('hqnd,hqmd->hqnm', f_q, f_k)
        qn = jnp.linalg.norm(f_q, axis=-1)
        kn = jnp.linalg.norm(f_k, axis=-1)
        cosine_sim = dots / (qn[..., :, None] * kn[..., None, :])
        q_centered = f_q - f_q.mean(-1, keepdims=True)
        q_var = jnp.var(f_q, axis=-1, ddof=1)
        k_var = jnp.var(f_k, axis=-1, ddof=1)
        q_ratio = 2.0 * jnp.minimum(q_var, 1.0) / (q_var + 1.0)
        k_ratio = 2.0 * jnp.minimum(k_var, 1.0) / (k_var + 1.0)
        var_component = jnp.einsum('hqn,hqm->hqnm', q_ratio, k_ratio)
        q_flat = q_centered.reshape(H, -1, D)
        feat_corr = jnp.einsum('hnd,hne->hde', q_flat, q_flat) / q_flat.shape[1]
        feat_corr = feat_corr * (1.0 - jnp.eye(D, dtype=feat_corr.dtype))
        decorr_score = jnp.linalg.norm(feat_corr, axis=(-2, -1)) / (D * D)
        decorr_scale = jnp.exp(-5.0 * decorr_score)[:, None, None, None]
        cov_component = cosine_sim * decorr_scale
        q_global = f_q.mean(axis=(1, 2))
        k_global = f_k.mean(axis=(1, 2))
        feats = jnp.concatenate([q_global, k_global], axis=-1)
        h1 = jnp.maximum(layer_norm(feats @ wp_w1.T + wp_b1, wp_ln_g, wp_ln_b), 0.0)
        weights = jax.nn.softmax(h1 @ wp_w2.T + wp_b2, axis=-1)
        cw = weights[:, 0][:, None, None, None]
        vw = weights[:, 1][:, None, None, None]
        ww = weights[:, 2][:, None, None, None]
        mixed = cw * cosine_sim + vw * cov_component + ww * var_component
        out = jnp.einsum('hqnm,hqmd->hqnd', mixed, f_v)
        out = out.transpose(1, 2, 0, 3).reshape(q.shape[0], q.shape[1], H * D)
        return out @ w_out.T + b_out

    def _L2_attn_ref(x, W_in, W_conv, b_conv, W_xproj, W_dt, b_dt, A_log, D, W_out):
        import jax, jax.numpy as jnp
        import numpy as np
        import math
        D_MODEL = 256
        D_STATE = 16
        D_CONV = 4
        EXPAND = 2
        D_INNER = EXPAND * D_MODEL
        DT_RANK = math.ceil(D_MODEL / 16)
        BATCH, SEQ = (4, 256)
        DT_MIN, DT_MAX = (0.001, 0.1)

        def _forward(x, W_in, W_conv, b_conv, W_xproj, W_dt, b_dt, A_log, D, W_out):
            b, l, _ = x.shape
            d_inner = W_in.shape[1] // 2
            d_conv = W_conv.shape[-1]
            n = A_log.shape[1]
            r = W_dt.shape[0]
            xz = x @ W_in
            xi, z = jnp.split(xz, 2, axis=-1)
            xi_t = jnp.moveaxis(xi, 1, 2)
            xi_pad = jnp.pad(xi_t, ((0, 0), (0, 0), (d_conv - 1, 0)))
            conv = jax.lax.conv_general_dilated(xi_pad, W_conv, window_strides=(1,), padding='VALID', feature_group_count=d_inner)
            xc = jax.nn.silu(jnp.moveaxis(conv + b_conv[None, :, None], 2, 1))
            dbc = xc @ W_xproj
            delta_lr, B, C = jnp.split(dbc, [r, r + n], axis=-1)
            delta = jax.nn.softplus(delta_lr @ W_dt + b_dt)
            A = -jnp.exp(A_log)
            dA = jnp.exp(delta[..., None] * A)
            dBx = delta[..., None] * B[:, :, None, :] * xc[..., None]

            def step(h, inp):
                dA_t, dBx_t, C_t, x_t = inp
                h = dA_t * h + dBx_t
                y = jnp.einsum('bdn,bn->bd', h, C_t) + D * x_t
                return (h, y)
            h0 = jnp.zeros((b, d_inner, n), x.dtype)
            _, ys = jax.lax.scan(step, h0, (jnp.moveaxis(dA, 1, 0), jnp.moveaxis(dBx, 1, 0), jnp.moveaxis(C, 1, 0), jnp.moveaxis(xc, 1, 0)))
            y = jnp.moveaxis(ys, 0, 1)
            return y * jax.nn.silu(z) @ W_out
        return _forward(x, W_in, W_conv, b_conv, W_xproj, W_dt, b_dt, A_log, D, W_out)

    def _L2_ffn_ref(hidden_states, w1, b1, w2, b2, expert_W, expert_b):
        import jax, jax.numpy as jnp
        import numpy as np
        TEMPERATURE = 1.0
        NUM_EXPERTS = 8
        h = jax.nn.relu(jnp.einsum('bsh,hm->bsm', hidden_states, w1) + b1)
        routing_scores = (jnp.einsum('bsm,me->bse', h, w2) + b2) / TEMPERATURE
        expert_probs = jax.nn.softmax(routing_scores, axis=-1)
        top_idx = jnp.argmax(expert_probs, axis=-1)
        onehot = jax.nn.one_hot(top_idx, NUM_EXPERTS, dtype=hidden_states.dtype)
        routed = jnp.zeros_like(hidden_states)
        for e in range(NUM_EXPERTS):
            mask = onehot[..., e:e + 1]
            expert_out = jnp.einsum('bsh,hd->bsd', hidden_states * mask, expert_W[e]) + expert_b[e]
            routed = routed + expert_out * mask
        return routed

    def _L3_xattn_ref(queries, keys, values, mask):
        import jax, jax.numpy as jnp
        import numpy as np
        N_HEADS = 16
        NEG_BIAS = -1000000000.0
        B, S, D = queries.shape
        H = N_HEADS
        dh = D // H

        def split_heads(t):
            return t.reshape(B, -1, H, dh).transpose(0, 2, 1, 3)
        q = split_heads(queries)
        k = split_heads(keys)
        v = split_heads(values)
        sim = jnp.einsum('bhqd,bhkd->bhqk', q, k) / jnp.sqrt(jnp.asarray(dh, q.dtype))
        bias = NEG_BIAS * (~mask).astype(sim.dtype)
        masked = sim + bias[:, None, :, :]
        weights = jax.nn.softmax(masked, axis=-1)
        out = jnp.einsum('bhqk,bhkd->bhqd', weights, v)
        out = out.transpose(0, 2, 1, 3).reshape(B, S, D)
        return out

    def _L3_attn_ref(x, Wq, bq, Wk, bk, Wv, bv):
        import jax, jax.numpy as jnp
        import numpy as np
        HEADS = 16
        D_MODEL = 256
        D_K = D_MODEL // HEADS
        SEQ = 512
        BSZ = 2
        BASE = 10000.0

        def _rope(x):
            s = x.shape[0]
            d = x.shape[-1]
            ar = jnp.arange(0, d, 2, dtype=jnp.float32)
            theta = 1.0 / (jnp.power(BASE, ar) / d)
            pos = jnp.arange(s, dtype=jnp.float32)
            idx_theta = pos[:, None] * theta[None, :]
            idx2 = jnp.concatenate([idx_theta, idx_theta], -1)
            cos = jnp.cos(idx2)[:, None, None, :]
            sin = jnp.sin(idx2)[:, None, None, :]
            neg_x = jnp.concatenate([-x[..., d // 2:], x[..., :d // 2]], axis=-1)
            return x * cos + neg_x * sin

        def _softmax_one(x, axis):
            x = x - jnp.max(x, axis=axis, keepdims=True)
            e = jnp.exp(x)
            return e / (1.0 + jnp.sum(e, axis=axis, keepdims=True))
        s, b, dm = x.shape
        q = (x @ Wq.T + bq).reshape(s, b, HEADS, D_K)
        k = (x @ Wk.T + bk).reshape(s, b, HEADS, D_K)
        v = (x @ Wv.T + bv).reshape(s, b, HEADS, D_K)
        q = _rope(q)
        k = _rope(k)
        scores = jnp.einsum('ibhd,jbhd->ijbh', q, k) / np.sqrt(D_K)
        mask = jnp.tril(jnp.ones((s, s), dtype=bool))[:, :, None, None]
        scores = jnp.where(mask, scores, -jnp.inf)
        attn = _softmax_one(scores, axis=1)
        out = jnp.einsum('ijbh,jbhd->ibhd', attn, v)
        return out.reshape(s, b, dm)

    def _L3_ffn_ref(x, W1, b1, W2, b2):
        import jax, jax.numpy as jnp
        import numpy as np
        HIDDEN = 256
        NUM_EXPERTS = 8
        TOP_K = 2
        B, S = (2, 512)
        Bm, Sm, d = x.shape
        E = W1.shape[0]
        x_flat = x.reshape(-1, d)
        h = jnp.mod(x_flat[:, :TOP_K].sum(axis=1).astype(jnp.int32), E)
        sel = jnp.stack([h, jnp.mod(h + 1, E)], axis=1)

        def step(acc, params):
            e, W1e, b1e, W2e, b2e = params
            w = jnp.any(sel == e, axis=1).astype(x.dtype) / TOP_K
            y = jnp.maximum(x_flat @ W1e + b1e, 0.0) @ W2e + b2e
            return (acc + w[:, None] * y, None)
        init = jnp.zeros_like(x_flat)
        out_flat, _ = jax.lax.scan(step, init, (jnp.arange(E), W1, b1, W2, b2))
        return out_flat.reshape(Bm, Sm, d)
    x = x + _L0_xattn_ref(ctx_1024, _layernorm(x, axis=-1), L0_xattn_gamma_x, L0_xattn_beta_x, L0_xattn_gamma_l, L0_xattn_beta_l, L0_xattn_Wq, L0_xattn_Wkv, L0_xattn_Wo)
    x = x + _L0_attn_ref(_layernorm(x, axis=-1), L0_attn_W_in, L0_attn_conv_w, L0_attn_conv_b, L0_attn_A_log, L0_attn_D, L0_attn_W_out)
    x = x + _L0_ffn_ref(_layernorm(x, axis=-1), L0_ffn_shared_w1, L0_ffn_shared_b1, L0_ffn_shared_w2, L0_ffn_shared_b2, L0_ffn_router_w, L0_ffn_router_b, L0_ffn_exp_w1, L0_ffn_exp_b1, L0_ffn_exp_w2, L0_ffn_exp_b2)
    x = x + _L1_xattn_ref(_layernorm(x, axis=-1), ctx_1024, ctx_1024, mask_BxS2_ff1, L1_xattn_wq, L1_xattn_bq, L1_xattn_wk, L1_xattn_bk, L1_xattn_wv, L1_xattn_bv)
    x = x + _L1_attn_ref(_layernorm(x, axis=-1), L1_attn_time_mix_k, L1_attn_time_mix_v, L1_attn_time_mix_r, L1_attn_time_mix_g, L1_attn_time_decay, L1_attn_time_faaaa, L1_attn_W_r, L1_attn_W_k, L1_attn_W_v, L1_attn_W_g, L1_attn_W_o, L1_attn_ln_w, L1_attn_ln_b)
    x = x + _L1_ffn_ref(_layernorm(x, axis=-1), L1_ffn_W1, L1_ffn_b1, L1_ffn_W2, L1_ffn_b2, L1_ffn_Wr, L1_ffn_br)
    x = x + _L2_xattn_ref(_layernorm(x, axis=-1), ctx_1024, ctx_1024, L2_xattn_ln_g, L2_xattn_ln_b, L2_xattn_w_in, L2_xattn_wp_w1, L2_xattn_wp_b1, L2_xattn_wp_ln_g, L2_xattn_wp_ln_b, L2_xattn_wp_w2, L2_xattn_wp_b2, L2_xattn_w_out, L2_xattn_b_out)
    x = x + _L2_attn_ref(_layernorm(x, axis=-1), L2_attn_W_in, L2_attn_W_conv, L2_attn_b_conv, L2_attn_W_xproj, L2_attn_W_dt, L2_attn_b_dt, L2_attn_A_log, L2_attn_D, L2_attn_W_out)
    x = x + _L2_ffn_ref(_layernorm(x, axis=-1), L2_ffn_w1, L2_ffn_b1, L2_ffn_w2, L2_ffn_b2, L2_ffn_expert_W, L2_ffn_expert_b)
    x = x + _L3_xattn_ref(_layernorm(x, axis=-1), ctx_1024, ctx_1024, mask_BxSxS2_bk0)
    x = x + _L3_attn_ref(_layernorm(x, axis=-1), L3_attn_Wq, L3_attn_bq, L3_attn_Wk, L3_attn_bk, L3_attn_Wv, L3_attn_bv)
    x = x + _L3_ffn_ref(_layernorm(x, axis=-1), L3_ffn_W1, L3_ffn_b1, L3_ffn_W2, L3_ffn_b2)
    return x

_drawn_inputs = setup_inputs


def setup_inputs(seed=0):
    import zlib

    import numpy as np

    out = dict(_drawn_inputs(seed))
    spreads = {'L0_xattn_gamma_x': (1.0, 0.2),
     'L0_xattn_beta_x': (0.0, 0.1),
     'L0_xattn_gamma_l': (1.0, 0.2),
     'L0_xattn_beta_l': (0.0, 0.1),
     'L0_attn_conv_b': (0.0, 0.1),
     'L0_attn_D': (1.0, 0.2),
     'L0_ffn_shared_b1': (0.0, 0.1),
     'L0_ffn_shared_b2': (0.0, 0.1),
     'L0_ffn_router_b': (0.0, 0.1),
     'L0_ffn_exp_b1': (0.0, 0.1),
     'L0_ffn_exp_b2': (0.0, 0.1),
     'L1_xattn_bq': (0.0, 0.1),
     'L1_xattn_bk': (0.0, 0.1),
     'L1_xattn_bv': (0.0, 0.1),
     'L1_attn_ln_w': (1.0, 0.2),
     'L1_attn_ln_b': (0.0, 0.1),
     'L2_xattn_ln_g': (1.0, 0.2),
     'L2_xattn_ln_b': (0.0, 0.1),
     'L2_xattn_wp_b1': (0.0, 0.1),
     'L2_xattn_wp_ln_g': (1.0, 0.2),
     'L2_xattn_wp_ln_b': (0.0, 0.1),
     'L2_xattn_wp_b2': (0.0, 0.1),
     'L2_xattn_b_out': (0.0, 0.1),
     'L2_attn_b_conv': (0.0, 0.1),
     'L2_attn_D': (1.0, 0.2),
     'L3_attn_bq': (0.0, 0.1),
     'L3_attn_bk': (0.0, 0.1),
     'L3_attn_bv': (0.0, 0.1)}
    factors = {}
    for name, (base, spread) in spreads.items():
        noise = np.random.default_rng([zlib.crc32(name.encode()), seed]).standard_normal(out[name].shape)
        drawn = base * np.exp(spread * noise) if base else spread * noise
        out[name] = jnp.asarray(drawn.astype(out[name].dtype))
    for name, factor in factors.items():
        out[name] = (out[name] * factor).astype(out[name].dtype)
    return out
```

```python
from contextlib import ExitStack

import numpy as np

import concourse.bass as bass
from concourse import mybir

P = 128
DIM = 256
DC = DIM // P
BANK = 512
EPS = 1e-5

ALU = mybir.AluOpType
ACT = mybir.ActivationFunctionType
AX = mybir.AxisListType
F32 = mybir.dt.float32
BF16 = mybir.dt.bfloat16
U8 = mybir.dt.uint8

MAX_CHUNK = 448
TILES = 7
CHUNK = TILES * P
MASK_BIG = 952.0 * 2 ** 20


class Stage:

    def __init__(self, nc, name):
        self.nc, self.name = nc, name
        self.memory, self.sems = ExitStack(), {}

    def __enter__(self):
        self.memory.__enter__()
        return self

    def sb(self, name, shape, dt=F32):
        return self.memory.enter_context(self.nc.sbuf_tensor(f"{self.name}_{name}", shape, dt))

    def psum(self, name, banks=1):
        shape = [P, BANK] if banks == 1 else [P, banks, BANK]
        return self.memory.enter_context(self.nc.psum_tensor(f"{self.name}_{name}", shape, F32))

    def sem(self, name):
        if name not in self.sems:
            self.sems[name] = self.memory.enter_context(self.nc.semaphore(f"{self.name}_{name}"))
        return self.sems[name]

    def __exit__(self, *e):
        if e[0] is None:
            for s in self.sems.values():
                self.nc.gpsimd.sem_clear(s)
            self.nc.all_engine_barrier()
        return self.memory.__exit__(*e)


class Link:

    def __init__(self, eng, sem):
        self.eng, self.sem, self.n = eng, sem, 0

    def __call__(self, ins):
        self.n += 1
        ins.then_inc(self.sem, 1)
        self.eng.wait_ge(self.sem, self.n)


class Loads:

    def __init__(self, sem):
        self.sem, self.total = sem, 0

    def __call__(self, ins):
        ins.then_inc(self.sem, 16)
        self.total += 16



def norm_vector(dve, link, S, tag, x, xn, w, rows=P):
    link(dve.bn_stats(w[:rows, 0:6], x))
    link(dve.bn_aggr(w[:rows, 6:8], w[:rows, 0:6]))
    dve.tensor_scalar(w[:rows, 8:9], w[:rows, 7:8], EPS, None, ALU.add).then_inc(S.sem(tag + "_var"), 1)
    dve.wait_ge(S.sem(tag + "_std"), 1)
    link(dve.reciprocal(w[:rows, 10:11], w[:rows, 9:10]))
    dve.tensor_scalar(xn, x, w[:rows, 6:7], w[:rows, 10:11], ALU.subtract, ALU.mult).then_inc(
        S.sem(tag + "_xn"), 1)
    dve.wait_ge(S.sem(tag + "_xn"), 1)


def norm_scalar(act, S, tag, w, rows=P):
    act.wait_ge(S.sem(tag + "_var"), 1)
    act.activation(w[:rows, 9:10], w[:rows, 8:9], ACT.Sqrt).then_inc(S.sem(tag + "_std"), 1)


def turn_tensor(pe, S, tag, xn, ps, ident, ready=None):
    pe.wait_ge(S.sem(ready or tag + "_xn"), 1)
    for c in range(DC):
        last = pe.transpose(ps[:, c * P:(c + 1) * P], xn[:, c * P:(c + 1) * P], ident[:, :])
    last.then_inc(S.sem(tag + "_turned"), 1)


def turn_vector(dve, S, tag, xT, ps):
    dve.wait_ge(S.sem(tag + "_turned"), 1)
    dve.tensor_copy(xT[:, :, :], ps[:, 0:DIM].rearrange("p (c t) -> p c t", c=DC)).then_inc(
        S.sem(tag + "_xT"), 1)
    dve.wait_ge(S.sem(tag + "_xT"), 1)


def by_rows(w):
    return w.rearrange("(c p) n -> p c n", p=P)


def column(v):
    return v.rearrange("(c p) -> p c", p=P)


def first_of_max(dve, link, onehot, vals, top, tmp, idx_down):
    link(dve.tensor_reduce(top, vals, AX.X, ALU.max))
    link(dve.tensor_scalar(tmp, vals, top, None, ALU.is_equal))
    link(dve.tensor_tensor(tmp, tmp, idx_down, ALU.mult))
    link(dve.tensor_reduce(onehot[:, 0:1], tmp, AX.X, ALU.max))
    link(dve.tensor_scalar(onehot[:, 8:9], onehot[:, 0:1], 0.0, None, ALU.add))
    link(dve.tensor_scalar(onehot[:, 0:8], tmp, onehot[:, 8:9], None, ALU.is_equal))


def softmax8_vector(dve, link, S, tag, logits, probs, w):
    link(dve.tensor_reduce(w[:, 0:1], logits, AX.X, ALU.max))
    dve.tensor_scalar(probs, logits, w[:, 0:1], None, ALU.subtract).then_inc(S.sem(tag + "_shifted"), 1)
    dve.wait_ge(S.sem(tag + "_exp"), 1)
    link(dve.reciprocal(w[:, 2:3], w[:, 1:2]))
    link(dve.tensor_scalar(probs, probs, w[:, 2:3], None, ALU.mult))


def softmax8_scalar(act, S, tag, probs, w):
    act.wait_ge(S.sem(tag + "_shifted"), 1)
    act.activation(probs, probs, ACT.Exp, accum_out=w[:, 1:2]).then_inc(S.sem(tag + "_exp"), 1)


def l3_attn(nc, A, R):
    H, HD = 16, 16
    with Stage(nc, "l3a") as S:
        w = S.sb("w", [P, DC, 3 * DIM])
        bias = S.sb("bias", [P, 3 * DIM])
        xn, xT, nw = S.sb("xn", [P, DIM]), S.sb("xT", [P, DC, P]), S.sb("nw", [P, 16])
        qkv = S.sb("qkv", [P, 3 * DIM])
        qk, s, e, top = S.sb("qk", [P, DIM]), S.sb("s", [P, H]), S.sb("e", [P, H]), S.sb("top", [P, H])
        pt, pqk, pv = S.psum("pt"), S.psum("pqk"), S.psum("pv")
        loads = Loads(S.sem("weights"))
        block = S.nc.Block()
        with block as block:
            @block.sync
            def _(sp):
                for n, name in enumerate(("Wq", "Wk", "Wv")):
                    loads(sp.dma_start(w[:, :, n * DIM:(n + 1) * DIM], by_rows(A[f"L3_attn_{name}"])))
                for n, name in enumerate(("bq", "bk", "bv")):
                    loads(sp.dma_start(bias[:, n * DIM:(n + 1) * DIM],
                                       A[f"L3_attn_{name}"].partition_broadcast(P)))

            @block.vector
            def _(dve):
                link = Link(dve, S.sem("dve_link"))
                norm_vector(dve, link, S, "n", R.x[:, :], xn[:, :], nw)
                turn_vector(dve, S, "n", xT, pt)
                dve.wait_ge(S.sem("weights"), loads.total)
                dve.wait_ge(S.sem("projected"), 1)
                link(dve.tensor_tensor(qkv[:, 0:2 * DIM], pqk[:, :], bias[:, 0:2 * DIM], ALU.add))
                link(dve.tensor_tensor(qkv[:, 2 * DIM:], pv[:, 0:DIM], bias[:, 2 * DIM:], ALU.add))
                link(dve.tensor_tensor(qk[:, :], qkv[:, 0:DIM], qkv[:, DIM:2 * DIM], ALU.mult))
                link(dve.tensor_reduce(s[:, :], qk[:, :].rearrange("p (h d) -> p h d", h=H), AX.X, ALU.add))
                link(dve.tensor_scalar(s[:, :], s[:, :], HD ** -0.5, None, ALU.mult))
                link(dve.tensor_reduce(top[:, :], s[:, :].unsqueeze(2), AX.X, ALU.max))
                dve.tensor_tensor(e[:, :], s[:, :], top[:, :], ALU.subtract).then_inc(S.sem("shifted"), 1)
                dve.wait_ge(S.sem("exp"), 1)
                link(dve.tensor_scalar(s[:, :], e[:, :], 1.0, None, ALU.add))
                link(dve.reciprocal(s[:, :], s[:, :]))
                link(dve.tensor_tensor(e[:, :], e[:, :], s[:, :], ALU.mult))
                link(dve.tensor_tensor(qk[:, :].rearrange("p (h d) -> p h d", h=H),
                                       qkv[:, 2 * DIM:].rearrange("p (h d) -> p h d", h=H),
                                       e[:, :].unsqueeze(2).broadcast_to([P, H, HD]), ALU.mult))
                link(dve.tensor_tensor(R.x[:, :], R.x[:, :], qk[:, :], ALU.add))

            @block.scalar
            def _(act):
                norm_scalar(act, S, "n", nw)
                act.wait_ge(S.sem("shifted"), 1)
                act.activation(e[:, :], e[:, :], ACT.Exp).then_inc(S.sem("exp"), 1)

            @block.tensor
            def _(pe):
                turn_tensor(pe, S, "n", xn, pt, R.ident)
                pe.wait_ge(S.sem("weights"), loads.total)
                pe.wait_ge(S.sem("n_xT"), 1)
                for c in range(DC):
                    pe.matmul(pqk[:, :], xT[:, c, :], w[:, c, 0:2 * DIM], start=(c == 0), stop=(c == DC - 1))
                for c in range(DC):
                    last = pe.matmul(pv[:, 0:DIM], xT[:, c, :], w[:, c, 2 * DIM:], start=(c == 0),
                                     stop=(c == DC - 1))
                last.then_inc(S.sem("projected"), 1)


def l3_ffn(nc, A, R):
    E, FF = 8, 1024
    FC = FF // P
    LIM = 24
    with Stage(nc, "l3f") as S:
        w1 = [S.sb(f"w1_{b}", [P, DC, FF]) for b in range(2)]
        w2 = [S.sb(f"w2_{b}", [P, FC, DIM]) for b in range(2)]
        b1 = S.sb("b1", [P, E, FC])
        b1r = S.sb("b1r", [E * FC, P])
        b2 = S.sb("b2", [E, DIM])
        xn, xT, nw = S.sb("xn", [P, DIM]), S.sb("xT", [P, DC, P]), S.sb("nw", [P, 16])
        steps = S.sb("steps", [P, 2, LIM])
        r = S.sb("r", [P, 8])
        we, wt = S.sb("we", [P, E]), S.sb("wt", [P, E])
        weT = S.sb("weT", [E, P])
        hT = [S.sb(f"hT{b}", [P, FC, P]) for b in range(2)]
        acc = S.sb("acc", [P, DIM])
        pt, pm = S.psum("pt"), S.psum("pm")
        ph = [S.psum(f"ph{b}", 2) for b in range(2)]
        py = [S.psum(f"py{b}") for b in range(2)]
        loads = Loads(S.sem("small"))
        with S.nc.Block() as block:
            @block.sync
            def _(sp):
                loads(sp.dma_start(b1r[:, :], A["L3_ffn_b1"].rearrange("e (f p) -> (e f) p", p=P)))
                loads(sp.dma_start(b2[:, :], A["L3_ffn_b2"]))
                with sp.Fori(0, E // 2) as i:
                    for b in range(2):
                        e = 2 * i + b
                        sp.wait_ge(S.sem(f"used{b}"), i)
                        sp.dma_start(w1[b][:, :, :], A["L3_ffn_W1"][bass.ds(e, 1)].rearrange(
                            "e (c p) n -> p (e c) n", p=P)).then_inc(S.sem(f"w1_{b}"), 16)
                        sp.dma_start(w2[b][:, :, :], A["L3_ffn_W2"][bass.ds(e, 1)].rearrange(
                            "e (c p) n -> p (e c) n", p=P)).then_inc(S.sem(f"w2_{b}"), 16)

            @block.vector
            def _(dve):
                link = Link(dve, S.sem("dve_link"))
                norm_vector(dve, link, S, "n", R.x[:, :], xn[:, :], nw)
                turn_vector(dve, S, "n", xT, pt)
                link(dve.tensor_tensor(r[:, 0:1], xn[:, 0:1], xn[:, 1:2], ALU.add))
                link(dve.tensor_scalar(r[:, 1:2], r[:, 0:1], -1.0, None, ALU.mult))
                for side in range(2):
                    link(dve.tensor_scalar(steps[:, side, :], R.count[:, 1:LIM + 1],
                                           r[:, side:side + 1], None, ALU.is_le))
                    link(dve.tensor_reduce(r[:, 2 + side:3 + side], steps[:, side, :], AX.X, ALU.add))
                link(dve.tensor_tensor(r[:, 4:5], r[:, 2:3], r[:, 3:4], ALU.subtract))
                link(dve.tensor_scalar(r[:, 4:5], r[:, 4:5], float(LIM), None, ALU.add))
                link(dve.tensor_scalar(steps[:, 0, 0:2 * LIM // 8], R.count8[:, 1:2 * LIM // 8 + 1],
                                       r[:, 4:5], None, ALU.is_le))
                link(dve.tensor_reduce(r[:, 5:6], steps[:, 0, 0:2 * LIM // 8], AX.X, ALU.add))
                link(dve.tensor_scalar(r[:, 5:6], r[:, 5:6], -8.0, r[:, 4:5], ALU.mult, ALU.add))
                link(dve.tensor_scalar(we[:, :], R.count[:, 0:E], r[:, 5:6], None, ALU.subtract))
                link(dve.tensor_scalar(wt[:, :], we[:, :], 0.0, 0.5, ALU.is_equal, ALU.mult))
                for off in (1.0, -7.0):
                    link(dve.tensor_scalar(acc[:, 0:E], we[:, :], off, 0.5, ALU.is_equal, ALU.mult))
                    link(dve.tensor_tensor(wt[:, :], wt[:, :], acc[:, 0:E], ALU.add))
                dve.sem_inc(S.sem("weights_of_experts"), 1)
                dve.wait_ge(S.sem("b1_turned"), 1)
                dve.tensor_copy(b1[:, :, :], pm[:, 0:E * FC].rearrange("p (e f) -> p e f", e=E)).then_inc(
                    S.sem("b1_ready"), 1)
                dve.wait_ge(S.sem("we_turned"), 1)
                dve.tensor_copy(weT[:, :], pm[0:E, P:2 * P]).then_inc(S.sem("weT_ready"), 1)
                dve.wait_ge(S.sem("b2_mixed"), 1)
                link(dve.tensor_tensor(acc[:, :], pm[:, DIM:2 * DIM], R.x[:, :], ALU.add))
                dve.sem_inc(S.sem("acc_link"), 1)
                with dve.Fori(0, E // 2) as i:
                    for b in range(2):
                        dve.wait_ge(S.sem(f"y{b}"), i + 1)
                        dve.wait_ge(S.sem("acc_link"), i * 2 + b + 1)
                        dve.scalar_tensor_tensor(acc[:, :], py[b][:, 0:DIM], wt[:, bass.ds(i * 2 + b, 1)],
                                                 acc[:, :], ALU.mult, ALU.add).then_inc(
                            S.sem("acc_link"), 1)
                dve.wait_ge(S.sem("acc_link"), E + 1)
                dve.tensor_copy(R.x[:, :], acc[:, :])

            @block.scalar
            def _(act):
                norm_scalar(act, S, "n", nw)
                act.wait_ge(S.sem("b1_ready"), 1)
                with act.Fori(0, E // 2) as i:
                    for b in range(2):
                        act.wait_ge(S.sem("b1_ready"), 1)
                        act.wait_ge(S.sem(f"h{b}"), i + 1)
                        act.wait_ge(S.sem(f"y{b}"), i)
                        for f in range(FC):
                            last = act.activation(hT[b][:, f, :], ph[b][:, f // 4, (f % 4) * P:(f % 4 + 1) * P],
                                                  ACT.Relu, bias=b1[:, bass.ds(i * 2 + b, 1), f])
                        last.then_inc(S.sem(f"hT{b}"), 1)

            @block.tensor
            def _(pe):
                turn_tensor(pe, S, "n", xn, pt, R.ident)
                pe.wait_ge(S.sem("small"), loads.total)
                pe.transpose(pm[:, 0:E * FC], b1r[:, :], R.ident[0:E * FC, 0:E * FC]).then_inc(
                    S.sem("b1_turned"), 1)
                pe.wait_ge(S.sem("weights_of_experts"), 1)
                pe.wait_ge(S.sem("b1_ready"), 1)
                pe.transpose(pm[0:E, P:2 * P], wt[:, :], R.ident[:, :]).then_inc(S.sem("we_turned"), 1)
                pe.wait_ge(S.sem("weT_ready"), 1)
                pe.matmul(pm[:, DIM:2 * DIM], weT[:, :], b2[:, :], start=True, stop=True).then_inc(
                    S.sem("b2_mixed"), 1)
                pe.wait_ge(S.sem("n_xT"), 1)
                with pe.Fori(0, E // 2) as i:
                    for b in range(2):
                        pe.wait_ge(S.sem(f"w1_{b}"), (i + 1) * 16)
                        pe.wait_ge(S.sem(f"hT{b}"), i)
                        for f in range(FC):
                            for c in range(DC):
                                last = pe.matmul(ph[b][:, f // 4, (f % 4) * P:(f % 4 + 1) * P],
                                                 w1[b][:, c, f * P:(f + 1) * P], xT[:, c, :],
                                                 start=(c == 0), stop=(c == DC - 1))
                        last.then_inc(S.sem(f"h{b}"), 1)
                    for b in range(2):
                        pe.wait_ge(S.sem(f"w2_{b}"), (i + 1) * 16)
                        pe.wait_ge(S.sem(f"hT{b}"), i + 1)
                        pe.wait_ge(S.sem("acc_link"), i * 2 + b)
                        for f in range(FC):
                            last = pe.matmul(py[b][:, 0:DIM], hT[b][:, f, :], w2[b][:, f, :],
                                             start=(f == 0), stop=(f == FC - 1))
                        last.then_inc(S.sem(f"y{b}"), 1)
                        pe.wait_ge(S.sem(f"y{b}"), i + 1)
                        pe.sem_inc(S.sem(f"used{b}"), 1)



def ctx_norm(nc, A, R):
    steps = R.keys // CHUNK // 2
    rows = A["ctx"].rearrange("(n t p) d -> n p t d", t=TILES, p=P)
    turned = R.nT.rearrange("c p (n k) -> n p c k", k=CHUNK)
    with Stage(nc, "norm") as S:
        raw = [S.sb(f"raw{b}", [P, TILES, DIM]) for b in range(2)]
        out = [S.sb(f"out{b}", [P, DC, CHUNK]) for b in range(2)]
        st = [S.sb(f"st{b}", [P, TILES, 6]) for b in range(2)]
        mv = [S.sb(f"mv{b}", [P, TILES, 2]) for b in range(2)]
        ve = [S.sb(f"ve{b}", [P, TILES]) for b in range(2)]
        sd = [S.sb(f"sd{b}", [P, TILES]) for b in range(2)]
        pt = [S.psum(f"pt{b}", 4) for b in range(2)]
        with S.nc.Block() as block:
            @block.sync
            def _(sp):
                with sp.Fori(0, steps) as i:
                    for b in range(2):
                        sp.wait_ge(S.sem(f"turned{b}"), i)
                        sp.dma_start(raw[b][:, :, :], rows[bass.ds(i * 2 + b, 1)].squeeze(0)).then_inc(
                            S.sem(f"raw{b}"), 16)
                    for b in range(2):
                        sp.wait_ge(S.sem(f"out{b}"), i + 1)
                        sp.dma_start(turned[bass.ds(i * 2 + b, 1)].squeeze(0), out[b][:, :, :]).then_inc(
                            S.sem(f"stored{b}"), 16)
                for b in range(2):
                    sp.wait_ge(S.sem(f"stored{b}"), steps * 16)

            @block.vector
            def _(dve):
                def stats(b, i):
                    dve.wait_ge(S.sem(f"raw{b}"), (i + 1) * 16)
                    for t in range(TILES):
                        last = dve.bn_stats(st[b][:, t, :], raw[b][:, t, :])
                    last.then_inc(S.sem(f"st{b}"), 1)
                    dve.wait_ge(S.sem(f"raw{b}"), 16)
                    dve.wait_ge(S.sem(f"st{b}"), i + 1)
                    for t in range(TILES):
                        last = dve.bn_aggr(mv[b][:, t, :], st[b][:, t, :])
                    last.then_inc(S.sem(f"mv{b}"), 1)
                    dve.wait_ge(S.sem(f"mv{b}"), i + 1)
                    dve.tensor_scalar(ve[b][:, :], mv[b][:, :, 1], EPS, None, ALU.add).then_inc(
                        S.sem(f"ve{b}"), 1)

                def scale(b, i):
                    dve.wait_ge(S.sem(f"sd{b}"), i + 1)
                    dve.reciprocal(sd[b][:, :], sd[b][:, :]).then_inc(S.sem(f"rs{b}"), 1)
                    dve.wait_ge(S.sem(f"rs{b}"), i + 1)
                    for t in range(TILES):
                        last = dve.tensor_scalar(raw[b][:, t, :], raw[b][:, t, :], mv[b][:, t, 0:1],
                                                 sd[b][:, t:t + 1], ALU.subtract, ALU.mult)
                    last.then_inc(S.sem(f"normed{b}"), 1)

                with dve.Fori(0, steps) as i:
                    stats(0, i)
                    stats(1, i)
                    scale(0, i)
                    scale(1, i)

            @block.scalar
            def _(act):
                with act.Fori(0, steps) as i:
                    for b in range(2):
                        act.wait_ge(S.sem(f"ve{b}"), i + 1)
                        act.activation(sd[b][:, :], ve[b][:, :], ACT.Sqrt).then_inc(S.sem(f"sd{b}"), 1)
                    for b in range(2):
                        act.wait_ge(S.sem(f"turned{b}"), i + 1)
                        act.wait_ge(S.sem(f"stored{b}"), i * 16)
                        for c in range(DC):
                            act.activation(out[b][:, c, 0:BANK], pt[b][:, 2 * c, :], ACT.Copy)
                            last = act.activation(out[b][:, c, BANK:CHUNK], pt[b][:, 2 * c + 1, 0:CHUNK - BANK],
                                                  ACT.Copy)
                        last.then_inc(S.sem(f"out{b}"), 1)

            @block.tensor
            def _(pe):
                with pe.Fori(0, steps) as i:
                    for b in range(2):
                        pe.wait_ge(S.sem(f"normed{b}"), i + 1)
                        pe.wait_ge(S.sem(f"out{b}"), i)
                        for t in range(TILES):
                            for c in range(DC):
                                last = pe.transpose(pt[b][:, 2 * c + t // 4, (t % 4) * P:(t % 4 + 1) * P],
                                                    raw[b][:, t, c * P:(c + 1) * P], R.ident[:, :])
                        last.then_inc(S.sem(f"turned{b}"), 1)


def find_maximum(nc, S, A, R, heads, kc, per_chunk, qb, source, project, w_k, bias_k, top, masks):
    nc = S.nc
    n_chunks = R.keys // MAX_CHUNK
    steps = n_chunks // 2
    src = source.rearrange("c p (n k) -> n p c k", k=MAX_CHUNK)
    mem = ExitStack()
    with mem:
        def sb(name, shape, dt=F32):
            return mem.enter_context(nc.sbuf_tensor(f"{S.name}_max_{name}", shape, dt))
        xin = [sb(f"xin{b}", [P, DC, MAX_CHUNK]) for b in range(2)]
        kf = [sb(f"kf{b}", [P, kc, MAX_CHUNK]) for b in range(2)] if project else xin
        kb = [sb(f"kb{b}", [P, kc, MAX_CHUNK], BF16) for b in range(2)]
        red = [sb(f"red{b}", [P, heads]) for b in range(2)]
        if project == "rope":
            cs = [sb(f"cs{b}", [P, 2, MAX_CHUNK]) for b in range(2)]
            ks = [sb(f"ks{b}", [P, kc, MAX_CHUNK]) for b in range(2)]
            kt = [sb(f"kt{b}", [P, kc, MAX_CHUNK]) for b in range(2)]
            cos = A["c_cos"].rearrange("p (n k) -> n p k", k=MAX_CHUNK)
            sin = A["c_sin"].rearrange("p (n k) -> n p k", k=MAX_CHUNK)
        if project:
            kt_dram = R.KT[0:kc].rearrange("c p (n k) -> n p c k", k=MAX_CHUNK)
        if masks == "query_key":
            mq = [sb(f"mq{b}", [P, MAX_CHUNK], U8) for b in range(2)]
            mb = [sb(f"mb{b}", [P, MAX_CHUNK], BF16) for b in range(2)]
            mask_src = A["mask_qk"].rearrange("q (n k) -> n q k", k=MAX_CHUNK)
        psc = [mem.enter_context(nc.psum_tensor(f"{S.name}_max_ps{b}", [P, 2, BANK], F32)) for b in range(2)]
        pk = [mem.enter_context(nc.psum_tensor(f"{S.name}_max_pk{b}", [P, BANK], F32)) for b in range(kc if project else 0)]
        sem = lambda n: S.sem("max_" + n)
        pairs = heads // 2
        with nc.Block() as block:
            @block.sync
            def _(sp):
                with sp.Fori(0, steps) as i:
                    for b in range(2):
                        n = i * 2 + b
                        if project:
                            sp.wait_ge(sem(f"xin_used{b}"), i)
                        else:
                            sp.wait_ge(sem(f"kb{b}"), i)
                        sp.dma_start(xin[b][:, :, :], src[bass.ds(n, 1)].squeeze(0)).then_inc(sem(f"xin{b}"), 16)
                        if project == "rope":
                            sp.wait_ge(sem(f"turned{b}"), i)
                            sp.dma_start(cs[b][:, 0, :], cos[bass.ds(n, 1)].squeeze(0)).then_inc(sem(f"cs{b}"), 16)
                            sp.dma_start(cs[b][:, 1, :], sin[bass.ds(n, 1)].squeeze(0)).then_inc(sem(f"cs{b}"), 16)
                        if masks == "query_key":
                            sp.wait_ge(sem(f"mb{b}"), i)
                            sp.dma_start(mq[b][:, :], mask_src[bass.ds(n, 1)].squeeze(0)).then_inc(
                                sem(f"mq{b}"), 16)

            if project == "rope":
                @block.gpsimd
                def _(pool):
                    with pool.Fori(0, steps) as i:
                        for b in range(2):
                            pool.wait_ge(sem(f"turned{b}"), i + 1)
                            pool.wait_ge(sem(f"kb{b}"), i)
                            pool.wait_ge(sem(f"spilled{b}"), i * 16)
                            pool.tensor_tensor(kf[b][:, :, :], kt[b][:, :, :], ks[b][:, :, :],
                                               ALU.add).then_inc(sem(f"kf{b}"), 1)

            @block.vector
            def _(dve):
                dve.memset(top[:, :], -3.0e38).then_inc(sem("top"), 1)

                def turn(b, i):
                    dve.wait_ge(sem(f"cs{b}"), (i + 1) * 32)
                    dve.wait_ge(sem(f"kf{b}"), i)
                    for c in range(kc):
                        dve.wait_ge(sem(f"k_proj{c}"), i * 2 + b + 1)
                        last = dve.scalar_tensor_tensor(kt[b][:, c, :], pk[c][:, 0:MAX_CHUNK], bias_k[:, c:c + 1],
                                                        cs[b][:, 0, :], ALU.add, ALU.mult)
                        last.then_inc(sem(f"k_read{c}"), 1)
                    dve.wait_ge(sem(f"swapped{b}"), i + 1)
                    dve.tensor_tensor(ks[b][:, :, :], ks[b][:, :, :],
                                      cs[b][:, 1, :].unsqueeze(1).broadcast_to([P, kc, MAX_CHUNK]),
                                      ALU.mult).then_inc(sem(f"turned{b}"), 1)

                with dve.Fori(0, steps) as i:
                    for b in range(2):
                        if project == "rope":
                            turn(b, i)
                        if masks == "query_key":
                            dve.wait_ge(sem(f"mq{b}"), (i + 1) * 16)
                            dve.wait_ge(sem(f"scored{b}"), i)
                            dve.tensor_scalar(mb[b][:, :], mq[b][:, :], -1.0, 1.0, ALU.mult,
                                              ALU.add).then_inc(sem(f"mb{b}"), 1)
                        dve.wait_ge(sem(f"top{b}"), i)
                        for pr in range(pairs):
                            u = pr % 2
                            per = pairs // 2
                            dve.wait_ge(sem(f"scores{u}"), i * (2 * per) + b * per + pr // 2 + 1)
                            last = dve.tensor_reduce(red[b][:, 2 * pr:2 * pr + 2], psc[u][:, :, 0:MAX_CHUNK], AX.X,
                                                     ALU.max)
                            last.then_inc(sem(f"scores_read{u}"), 1)
                        for u in range(2):
                            dve.wait_ge(sem(f"scores_read{u}"), i * (2 * per) + (b + 1) * per)
                        dve.wait_ge(sem("top"), i * 2 + b + 1)
                        dve.tensor_tensor(top[:, :], top[:, :], red[b][:, :], ALU.max).then_inc(sem("top"), 1)
                        dve.wait_ge(sem("top"), i * 2 + b + 2)
                        dve.sem_inc(sem(f"top{b}"), 1)

            @block.scalar
            def _(act):
                with act.Fori(0, steps) as i:
                    for b in range(2):
                        if project == "rope":
                            act.wait_ge(sem(f"turned{b}"), i)
                            act.wait_ge(sem(f"kf{b}"), i)
                            for c in range(kc):
                                act.wait_ge(sem(f"k_read{c}"), i * 2 + b + 1)
                                act.activation(ks[b][0:64, c, :], pk[c][64:P, 0:MAX_CHUNK], ACT.Identity,
                                               scale=-1.0, bias=R.nbias_k[0:64, c:c + 1])
                                last = act.activation(ks[b][64:P, c, :], pk[c][0:64, 0:MAX_CHUNK], ACT.Identity,
                                                      bias=R.nbias_k[64:P, c:c + 1])
                                last.then_inc(sem(f"k_swapped{c}"), 1)
                            act.wait_ge(sem(f"k_swapped{kc - 1}"), i * 2 + b + 1)
                            act.sem_inc(sem(f"swapped{b}"), 1)
                            act.wait_ge(sem(f"kf{b}"), i + 1)
                        elif project:
                            act.wait_ge(sem(f"kb{b}"), i)
                            act.wait_ge(sem(f"spilled{b}"), i * 16)
                            for c in range(kc):
                                act.wait_ge(sem(f"k_proj{c}"), i * 2 + b + 1)
                                act.activation(kf[b][:, c, :], pk[c][:, 0:MAX_CHUNK], ACT.Identity,
                                               bias=bias_k[:, c:c + 1]).then_inc(sem(f"k_swapped{c}"), 1)
                            act.wait_ge(sem(f"k_swapped{kc - 1}"), i * 2 + b + 1)
                            act.sem_inc(sem(f"kf{b}"), 1)
                        else:
                            act.wait_ge(sem(f"xin{b}"), (i + 1) * 16)
                        act.wait_ge(sem(f"scored{b}"), i)
                        act.activation(kb[b][:, :, :], kf[b][:, :, :], ACT.Copy).then_inc(sem(f"kb{b}"), 1)
                        if project:
                            act.dma_start(kt_dram[bass.ds(i * 2 + b, 1)].squeeze(0), kf[b][:, :, :]).then_inc(
                                sem(f"spilled{b}"), 16)
                if project:
                    for b in range(2):
                        act.wait_ge(sem(f"spilled{b}"), steps * 16)

            @block.tensor
            def _(pe):
                def proj(b, i):
                    pe.wait_ge(sem(f"xin{b}"), (i + 1) * 16)
                    for c in range(kc):
                        pe.wait_ge(sem(f"k_swapped{c}"), i * 2 + b)
                        for d in range(DC):
                            last = pe.matmul(pk[c][:, 0:MAX_CHUNK], w_k[:, d, c * P:(c + 1) * P], xin[b][:, d, :],
                                             start=(d == 0), stop=(d == DC - 1))
                        last.then_inc(sem(f"k_proj{c}"), 1)
                    pe.wait_ge(sem(f"k_proj{kc - 1}"), i * 2 + b + 1)
                    pe.sem_inc(sem(f"xin_used{b}"), 1)

                def scores(b, i):
                    pe.wait_ge(sem(f"kb{b}"), i + 1)
                    if masks == "query_key":
                        pe.wait_ge(sem(f"mb{b}"), i + 1)
                    for pr in range(pairs):
                        u = pr % 2
                        per = pairs // 2
                        pe.wait_ge(sem(f"scores_read{u}"), i * (2 * per) + b * per + pr // 2)
                        for j in range(2):
                            h = 2 * pr + j
                            c = h // per_chunk
                            out = psc[u][:, j, 0:MAX_CHUNK]
                            last = pe.matmul(out, qb[c][:, h % per_chunk, :], kb[b][:, c, :], start=True,
                                             stop=(masks is None))
                            if masks == "query_key":
                                last = pe.matmul(out, R.neg_big[:, :], mb[b][:, :], start=False, stop=True)
                            if masks == "key":
                                last = pe.matmul(out, R.ones3[:, :],
                                                 R.mask3[:, bass.ds(i * (2 * MAX_CHUNK) + b * MAX_CHUNK, MAX_CHUNK)],
                                                 start=False, stop=True)
                        last.then_inc(sem(f"scores{u}"), 1)
                    pe.wait_ge(sem(f"scores{(pairs - 1) % 2}"), i * (2 * per) + (b + 1) * per)
                    pe.sem_inc(sem(f"scored{b}"), 1)

                with pe.Fori(0, steps) as i:
                    if project:
                        proj(0, i)
                        proj(1, i)
                    scores(0, i)
                    scores(1, i)


def split_rows(nc, S, R, name, top, heads, extra_top=None):
    m3 = S.sb(name, [3, heads * P], BF16)
    scratch = nc.dram_tensor(f"{S.name}_{name}_rows", (3, heads, P), BF16, kind="Internal").ap()
    mem = ExitStack()
    with mem:
        tT = mem.enter_context(nc.sbuf_tensor(f"{S.name}_topT", [heads, P], F32))
        parts = [mem.enter_context(nc.sbuf_tensor(f"{S.name}_part{n}", [heads, P], BF16)) for n in range(3)]
        ps = mem.enter_context(nc.psum_tensor(f"{S.name}_topps", [P, BANK], F32))
        with nc.Block() as block:
            @block.tensor
            def _(pe):
                pe.transpose(ps[0:heads, 0:P], top[:, :], R.ident[:, :]).then_inc(S.sem("top_turned"), 1)

            @block.vector
            def _(dve):
                link = Link(dve, S.sem("split_link"))
                dve.wait_ge(S.sem("top_turned"), 1)
                link(dve.tensor_scalar(tT[:, :], ps[0:heads, 0:P], -1.0, None, ALU.mult))
                for n in range(3):
                    link(dve.tensor_copy(parts[n][:, :], tT[:, :]))
                    link(dve.tensor_tensor(tT[:, :], tT[:, :], parts[n][:, :], ALU.subtract))
                dve.sem_inc(S.sem("split"), 1)

            @block.sync
            def _(sp):
                sp.wait_ge(S.sem("split"), 1)
                for n in range(3):
                    sp.dma_start(scratch[n], parts[n][:, :]).then_inc(S.sem("rows_out"), 16)
                sp.wait_ge(S.sem("rows_out"), 48)
                sp.dma_start(m3[:, :], scratch.rearrange("n h q -> n (h q)")).then_inc(S.sem("rows_in"), 16)
                sp.wait_ge(S.sem("rows_in"), 16)
    return m3


def attend(nc, S, A, R, heads, kc, per_chunk, q, kt_src, v_src, w_v, bias_v, m3, masks, O, sums, last_tile=None):
    nc = S.nc
    wide = heads == 8
    vd = DIM // heads * (2 if wide else 1)
    steps = R.keys // CHUNK // 2
    octets = heads // 8
    mem = ExitStack()
    kt_src = kt_src.rearrange("c p (n k) -> n p c k", k=CHUNK)
    project = w_v is not None
    if project:
        v_src = v_src.rearrange("c p (n k) -> n p c k", k=CHUNK)
    else:
        v_src = v_src.rearrange("(n t p) d -> n p t d", t=TILES, p=P)
    with mem:
        def sb(name, shape, dt=F32):
            return mem.enter_context(nc.sbuf_tensor(f"{S.name}_att_{name}", shape, dt))
        kt = [sb(f"kt{b}", [P, kc, CHUNK]) for b in range(2)]
        vin = [sb(f"vin{b}", [P, DC, CHUNK] if project else [P, TILES, DIM]) for b in range(2)]
        if wide:
            v = [sb(f"v{b}", [P, heads, vd]) for b in range(2)]
        else:
            v = [sb(f"v{b}", [P, heads, vd + 1]) for b in range(2)]
        pt = [sb(f"pt{b}", [P, 8, P]) for b in range(2)]
        ones3 = sb("ones3", [3, P], BF16)
        zl, zr = sb("zl", [P, P]), sb("zr", [P, BANK])
        if masks == "query_key":
            mq = [sb(f"mq{b}", [P, CHUNK], U8) for b in range(2)]
            mb = [sb(f"mb{b}", [P, CHUNK], BF16) for b in range(2)]
            mask_src = A["mask_qk"].rearrange("q (n k) -> n q k", k=CHUNK)
        psc = [mem.enter_context(nc.psum_tensor(f"{S.name}_att_ps{b}", [P, 2, BANK], F32)) for b in range(2)]
        pv = [mem.enter_context(nc.psum_tensor(f"{S.name}_att_pv{b}", [P, BANK], F32)) for b in range(2)]
        sem = lambda n: S.sem("att_" + n)
        per_body = 2 * TILES
        uses = per_body * octets // 2
        vuses = per_body // 2

        def octet_counts(i, t, o):
            k = t * octets + o
            return k % 2, i * uses + k // 2

        def tile_counts(i, t):
            return t % 2, i * vuses + t // 2

        with nc.Block() as block:
            @block.sync
            def _(sp):
                with sp.Fori(0, steps) as i:
                    for b in range(2):
                        n = i * 2 + b
                        sp.wait_ge(sem(f"chunk_used{b}"), i)
                        sp.dma_start(kt[b][:, :, :], kt_src[bass.ds(n, 1)].squeeze(0)).then_inc(sem(f"kt{b}"), 16)
                        if not project:
                            sp.wait_ge(sem(f"v_copied{b}"), i)
                        sp.dma_start(vin[b][:, :, :], v_src[bass.ds(n, 1)].squeeze(0)).then_inc(
                            sem(f"vin{b}"), 16)
                        if masks == "query_key":
                            sp.wait_ge(sem(f"mb{b}"), i)
                            sp.dma_start(mq[b][:, :], mask_src[bass.ds(n, 1)].squeeze(0)).then_inc(
                                sem(f"mq{b}"), 16)

            @block.vector
            def _(dve):
                dve.memset(zl[:, :], 0.0)
                dve.memset(zr[:, :], 0.0)
                if wide:
                    dve.memset(sums[:, :, :], 0.0)
                else:
                    for b in range(2):
                        dve.memset(v[b][:, :, vd:vd + 1], 1.0)
                dve.memset(ones3[:, :], 1.0).then_inc(sem("constants"), 1)
                dve.wait_ge(sem("constants"), 1)

                def weights_sum(i, t):
                    u, j = octet_counts(i, t, 0)
                    dve.wait_ge(sem(f"probs{u}"), j + 1)
                    dve.wait_ge(sem(f"summed{1 - u}"), j + (1 if u else 0))
                    dve.tensor_tensor(sums[:, :, :], sums[:, :, :], pt[u][:, :, :], ALU.add).then_inc(
                        sem(f"summed{u}"), 1)

                def tile(i, t):
                    b, s = t // TILES, t % TILES
                    vb, j = tile_counts(i, t)
                    if masks == "query_key" and s == 0:
                        dve.wait_ge(sem(f"mq{b}"), (i + 1) * 16)
                        dve.wait_ge(sem(f"chunk_used{b}"), i)
                        dve.tensor_scalar(mb[b][:, :], mq[b][:, :], -1.0, 1.0, ALU.mult, ALU.add).then_inc(
                            sem(f"mb{b}"), 1)
                    dve.wait_ge(sem(f"v_used{vb}"), j)
                    if project:
                        dve.wait_ge(sem(f"v_proj{vb}"), j + 1)
                        dve.tensor_tensor(v[vb][:, :, 0:vd],
                                          pv[vb][:, 0:heads * vd].rearrange("p (h d) -> p h d", h=heads),
                                          bias_v[:, :].rearrange("p (h d) -> p h d", h=heads),
                                          ALU.add).then_inc(sem(f"v{vb}"), 1)
                    else:
                        dve.wait_ge(sem(f"vin{b}"), (i + 1) * 16)
                        dve.tensor_copy(v[vb][:, :, 0:vd],
                                        vin[b][:, s, :].rearrange("p (h d) -> p h d", h=heads)).then_inc(
                            sem(f"v{vb}"), 1)
                        if s == TILES - 1:
                            dve.wait_ge(sem(f"v{vb}"), j + 1)
                            dve.sem_inc(sem(f"v_copied{b}"), 1)

                with dve.Fori(0, steps) as i:
                    for t in range(per_body):
                        tile(i, t)
                        if wide and t:
                            weights_sum(i, t - 1)
                    if wide:
                        weights_sum(i, per_body - 1)
                if last_tile:
                    weights_sum(steps, 0)

            @block.scalar
            def _(act):
                def exps(i, t, o):
                    u, j = octet_counts(i, t, o)
                    if masks == "key":
                        act.wait_ge(S.sem("mask_split"), 1)
                    act.wait_ge(sem(f"scores{u}"), j + 1)
                    act.wait_ge(sem(f"pv{u}"), j)
                    if wide:
                        act.wait_ge(sem(f"summed{u}"), j)
                    if masks == "key":
                        tile_ap = R.mask_col[:, bass.ds(i * per_body + t, 1)]
                        ins = act.activation(pt[u][:, :, :], psc[u][:, :, :].rearrange("p a (b q) -> p (a b) q", q=P),
                                             ACT.Exp, bias=tile_ap)
                    else:
                        ins = act.activation(pt[u][:, :, :], psc[u][:, :, :].rearrange("p a (b q) -> p (a b) q", q=P),
                                             ACT.Exp)
                    ins.then_inc(sem(f"probs{u}"), 1)

                with act.Fori(0, steps) as i:
                    for t in range(per_body):
                        for o in range(octets):
                            exps(i, t, o)
                if last_tile:
                    exps(steps, 0, 0)

            @block.tensor
            def _(pe):
                pe.wait_ge(sem("constants"), 1)
                pe.matmul(O[:, :], zl[:, :], zr[:, :], start=True, stop=True)

                def values(i, t):
                    b, s = t // TILES, t % TILES
                    vb, j = tile_counts(i, t)
                    pe.wait_ge(sem(f"vin{b}"), (i + 1) * 16)
                    pe.wait_ge(sem(f"v{vb}"), j)
                    for d in range(DC):
                        last = pe.matmul(pv[vb][:, 0:heads * vd], vin[b][:, d, s * P:(s + 1) * P], w_v[:, d, :],
                                         start=(d == 0), stop=(d == DC - 1))
                    last.then_inc(sem(f"v_proj{vb}"), 1)

                def scores(i, t, o, keys=None):
                    b, s = t // TILES, t % TILES
                    u, j = octet_counts(i, t, o)
                    if o == 0 and s == 0 and keys is None:
                        pe.wait_ge(sem(f"kt{b}"), (i + 1) * 16)
                        if masks == "query_key":
                            pe.wait_ge(sem(f"mb{b}"), i + 1)
                    pe.wait_ge(sem(f"probs{u}"), j)
                    for half in range(2):
                        for k in range(4):
                            h = 8 * o + 4 * half + k
                            c = h // per_chunk
                            lhs = kt[b][:, c, s * P:(s + 1) * P] if keys is None else keys[:, c, :]
                            pe.matmul(psc[u][:, half, k * P:(k + 1) * P], lhs, q[c][:, h % per_chunk, :],
                                      start=(k == 0), stop=False, skip_group_check=True)
                        if masks == "query_key":
                            pe.matmul(psc[u][:, half, :].rearrange("p (k q) -> p k q", k=4),
                                      mb[b][:, s * P:(s + 1) * P],
                                      R.neg_big[:, :].unsqueeze(1).broadcast_to([P, 4, P]),
                                      start=False, stop=False, skip_group_check=True)
                        h0 = 8 * o + 4 * half
                        last = pe.matmul(psc[u][:, half, :], ones3[:, :], m3[:, h0 * P:(h0 + 4) * P],
                                         start=False, stop=True, skip_group_check=True)
                    last.then_inc(sem(f"scores{u}"), 1)

                def weigh(i, t, o, vals=None):
                    u, j = octet_counts(i, t, o)
                    vb, jv = tile_counts(i, t)
                    pe.wait_ge(sem(f"probs{u}"), j + 1)
                    if vals is None:
                        pe.wait_ge(sem(f"v{vb}"), jv + 1)
                    vv = v[vb] if vals is None else vals
                    for k in range(8):
                        h = 8 * o + k
                        if wide:
                            out = O[64 * (h % 2):64 * (h % 2) + vd, (h // 2) * P:(h // 2 + 1) * P]
                            lhs = vv[:, h, :]
                        else:
                            out = O[32 * (h % 4):32 * (h % 4) + vd + 1, (h // 4) * P:(h // 4 + 1) * P]
                            lhs = vv[:, h, :]
                        last = pe.matmul(out, lhs, pt[u][:, k, :], start=False, stop=False, skip_group_check=True)
                    last.then_inc(sem(f"pv{u}"), 1)
                    if o == octets - 1:
                        pe.wait_ge(sem(f"pv{u}"), j + 1)
                        if vals is None:
                            pe.sem_inc(sem(f"v_used{vb}"), 1)
                        if t % TILES == TILES - 1 and vals is None:
                            pe.sem_inc(sem(f"chunk_used{t // TILES}"), 1)

                with pe.Fori(0, steps) as i:
                    order = [(t, o) for t in range(per_body) for o in range(octets)]
                    if project:
                        values(i, 0)
                    for n, (t, o) in enumerate(order):
                        scores(i, t, o)
                        if project and o == 0 and t + 1 < per_body:
                            values(i, t + 1)
                        if n:
                            weigh(i, *order[n - 1])
                    weigh(i, *order[-1])
                if last_tile:
                    scores(steps, 0, 0, keys=last_tile[0])
                    weigh(steps, 0, 0, vals=last_tile[1])


def finish_heads16(nc, S, A, R, O, bias=None):
    with ExitStack() as mem:
        o_sb = mem.enter_context(nc.sbuf_tensor(f"{S.name}_o", [P, 4, P], F32))
        rec = mem.enter_context(nc.sbuf_tensor(f"{S.name}_rec", [P, 16], F32))
        out = mem.enter_context(nc.sbuf_tensor(f"{S.name}_out", [P, 16, 16], F32))
        ps = mem.enter_context(nc.psum_tensor(f"{S.name}_ops", [P, BANK], F32))
        with nc.Block() as block:
            @block.tensor
            def _(pe):
                pe.wait_ge(S.sem("o_copied"), 1)
                for s in range(4):
                    last = pe.transpose(ps[:, s * P:(s + 1) * P], o_sb[:, s, :], R.ident[:, :])
                last.then_inc(S.sem("o_turned"), 1)

            @block.vector
            def _(dve):
                link = Link(dve, S.sem("finish_link"))
                dve.tensor_copy(o_sb[:, :, :], O[:, :].rearrange("p (s q) -> p s q", s=4)).then_inc(
                    S.sem("o_copied"), 1)
                dve.wait_ge(S.sem("o_turned"), 1)
                rows = ps[:, :].rearrange("p (h f) -> p h f", f=32)
                link(dve.reciprocal(rec[:, :], rows[:, :, 16]))
                link(dve.tensor_tensor(out[:, :, :], rows[:, :, 0:16],
                                       rec[:, :].unsqueeze(2).broadcast_to([P, 16, 16]), ALU.mult))
                link(dve.tensor_tensor(R.x[:, :], R.x[:, :], out[:, :, :].rearrange("p h d -> p (h d)"), ALU.add))


def l3_xattn(nc, A, R):
    H = 16
    with Stage(nc, "l3x") as S:
        xn, nw = S.sb("xn", [P, DIM]), S.sb("nw", [P, 16])
        q = [S.sb(f"q{c}", [P, 8, P]) for c in range(DC)]
        qb = [S.sb(f"qb{c}", [P, 8, P], BF16) for c in range(DC)]
        hm = S.sb("hm", [P, 8])
        R.neg_big = S.sb("neg_big", [P, P], BF16)
        top = S.sb("top", [P, H])
        with ExitStack() as mem:
            pt = mem.enter_context(nc.psum_tensor("l3x_pt", [P, BANK], F32))
            with nc.Block() as block:
                @block.sync
                def _(sp):
                    sp.dma_start(hm[:, :], A["c_head16"]).then_inc(S.sem("hm"), 16)

                @block.scalar
                def _(act):
                    norm_scalar(act, S, "n", nw)

                @block.vector
                def _(dve):
                    link = Link(dve, S.sem("dve_link"))
                    norm_vector(dve, link, S, "n", R.x[:, :], xn[:, :], nw)
                    link(dve.tensor_scalar(R.neg_big[:, :], R.ident[:, :], -MASK_BIG, None, ALU.mult))
                    dve.wait_ge(S.sem("n_turned"), 1)
                    dve.wait_ge(S.sem("hm"), 16)
                    spread_queries(dve, link, pt, q, qb, hm, 8, 0.25)

                @block.tensor
                def _(pe):
                    turn_tensor(pe, S, "n", xn, pt, R.ident)
        ctxT = A["ctxT"].rearrange("(c p) n -> c p n", p=P)
        find_maximum(nc, S, A, R, H, DC, 8, qb, ctxT, None, None, None, top, "query_key")
        m3 = split_rows(nc, S, R, "m3", top, H)
        O = S.psum("O")
        attend(nc, S, A, R, H, DC, 8, q, ctxT, A["ctx"], None, None, m3, "query_key", O, None)
        finish_heads16(nc, S, A, R, O)


def spread_queries(dve, link, pt, q, qb, head_mask, per_chunk, scale):
    for c in range(len(q)):
        link(dve.scalar_tensor_tensor(
            q[c][:, :, :], pt[:, c * P:(c + 1) * P].unsqueeze(1).broadcast_to([P, per_chunk, P]), scale,
            head_mask[:, :].unsqueeze(2).broadcast_to([P, per_chunk, P]), ALU.mult, ALU.mult))
        link(dve.tensor_copy(qb[c][:, :, :], q[c][:, :, :]))


def l1_xattn(nc, A, R):
    H = 16
    n_tiles = R.keys // P
    with Stage(nc, "l1x") as S:
        xn, xT, nw = S.sb("xn", [P, DIM]), S.sb("xT", [P, DC, P]), S.sb("nw", [P, 16])
        q = [S.sb(f"q{c}", [P, 8, P]) for c in range(DC)]
        qb = [S.sb(f"qb{c}", [P, 8, P], BF16) for c in range(DC)]
        hm = S.sb("hm", [P, 8])
        top = S.sb("top", [P, H])
        w = S.sb("w", [P, 3, DC, DIM])
        bq, bk, bv = S.sb("bq", [P, DC]), S.sb("bk", [P, DC]), S.sb("bv", [P, DIM])
        qT = S.sb("qT", [P, DC * P])
        R.mask_col = S.sb("mask_col", [P, n_tiles])
        R.ones3 = S.sb("ones3", [3, P], BF16)
        with ExitStack() as mem:
            mask = mem.enter_context(nc.sbuf_tensor("l1x_mask", [n_tiles, P], F32))
            parts = [mem.enter_context(nc.sbuf_tensor(f"l1x_mpart{n}", [n_tiles, P], BF16)) for n in range(3)]
            pt, pq, pm = [mem.enter_context(nc.psum_tensor(f"l1x_p{n}", [P, BANK], F32)) for n in range(3)]
            scratch = nc.dram_tensor("l1x_mask_rows", (3, n_tiles, P), BF16, kind="Internal").ap()
            loads = Loads(S.sem("loads"))
            with nc.Block() as block:
                @block.sync
                def _(sp):
                    loads(sp.dma_start(mask[:, :], A["mask_row"]))
                    loads(sp.dma_start(hm[:, :], A["c_head16"]))
                    for n, name in enumerate(("wq", "wk", "wv")):
                        loads(sp.dma_start(w[:, n, :, :], by_rows(A[f"L1_xattn_{name}"])))
                    loads(sp.dma_start(bv[:, :], A["L1_xattn_bv"].partition_broadcast(P)))
                    loads(sp.dma_start(bq[:, :], column(A["L1_xattn_bq"]), allow_slow_non_contiguous=True))
                    loads(sp.dma_start(bk[:, :], column(A["L1_xattn_bk"]), allow_slow_non_contiguous=True))
                    sp.wait_ge(S.sem("mask_split"), 1)
                    for n in range(3):
                        sp.dma_start(scratch[n], parts[n][:, :]).then_inc(S.sem("mask_out"), 16)
                    sp.wait_ge(S.sem("mask_out"), 48)

                @block.scalar
                def _(act):
                    norm_scalar(act, S, "n", nw)

                @block.vector
                def _(dve):
                    link = Link(dve, S.sem("dve_link"))
                    dve.memset(R.ones3[:, :], 1.0)
                    norm_vector(dve, link, S, "n", R.x[:, :], xn[:, :], nw)
                    turn_vector(dve, S, "n", xT, pt)
                    dve.wait_ge(S.sem("loads"), loads.total)
                    link(dve.tensor_scalar(mask[:, :], mask[:, :], -1.0, 1.0, ALU.mult, ALU.add))
                    dve.tensor_scalar(mask[:, :], mask[:, :], -10000.0, None, ALU.mult).then_inc(
                        S.sem("mask_bias"), 1)
                    dve.wait_ge(S.sem("mask_turned"), 1)
                    link(dve.tensor_copy(R.mask_col[:, :], pm[:, 0:n_tiles]))
                    for n in range(3):
                        link(dve.tensor_copy(parts[n][:, :], mask[:, :]))
                        link(dve.tensor_tensor(mask[:, :], mask[:, :], parts[n][:, :], ALU.subtract))
                    dve.sem_inc(S.sem("mask_split"), 1)
                    dve.wait_ge(S.sem("q_proj"), 1)
                    for c in range(DC):
                        link(dve.tensor_scalar(qT[:, c * P:(c + 1) * P], pq[:, c * P:(c + 1) * P], bq[:, c:c + 1],
                                               None, ALU.add))
                    spread_queries(dve, link, qT, q, qb, hm, 8, 0.25)

                @block.tensor
                def _(pe):
                    turn_tensor(pe, S, "n", xn, pt, R.ident)
                    pe.wait_ge(S.sem("mask_bias"), 1)
                    pe.transpose(pm[:, 0:n_tiles], mask[:, :], R.ident[0:n_tiles, 0:n_tiles]).then_inc(
                        S.sem("mask_turned"), 1)
                    pe.wait_ge(S.sem("n_xT"), 1)
                    pe.wait_ge(S.sem("loads"), loads.total)
                    for o in range(DC):
                        for c in range(DC):
                            last = pe.matmul(pq[:, o * P:(o + 1) * P], w[:, 0, c, o * P:(o + 1) * P], xT[:, c, :],
                                             start=(c == 0), stop=(c == DC - 1))
                    last.then_inc(S.sem("q_proj"), 1)
        ctxT = A["ctxT"].rearrange("(c p) n -> c p n", p=P)
        with ExitStack() as mem:
            R.mask3 = mem.enter_context(nc.sbuf_tensor("l1x_mask3", [3, R.keys], BF16))
            with nc.Block() as block:
                @block.sync
                def _(sp):
                    sp.dma_start(R.mask3[:, :], scratch.rearrange("n t p -> n (t p)")).then_inc(S.sem("mask_in"), 16)
                    sp.wait_ge(S.sem("mask_in"), 16)
            find_maximum(nc, S, A, R, H, DC, 8, qb, ctxT, "plain", w[:, 1, :, :], bk, top, "key")
        m3 = split_rows(nc, S, R, "m3", top, H)
        O = S.psum("O")
        attend(nc, S, A, R, H, DC, 8, q, R.KT[0:DC], ctxT, w[:, 2, :, :], bv, m3, "key", O, None)
        finish_heads16(nc, S, A, R, O)


def l0_xattn(nc, A, R):
    H, HD, KC = 8, 64, 4
    INNER = H * HD
    with Stage(nc, "l0x") as S:
        q = [S.sb(f"q{c}", [P, 2, P]) for c in range(KC)]
        qb = [S.sb(f"qb{c}", [P, 2, P], BF16) for c in range(KC)]
        hm = S.sb("hm", [P, 2])
        top = S.sb("top", [P, H])
        wk, wv = S.sb("wk", [P, DC, INNER]), S.sb("wv", [P, DC, INNER])
        bias_k, bias_v = S.sb("bias_k", [P, KC]), S.sb("bias_v", [P, INNER])
        R.nbias_k = S.sb("nbias_k", [P, KC])
        kl, vl = S.sb("kl", [P, KC, P]), S.sb("vl", [P, H, HD])
        klb = S.sb("klb", [P, KC, P], BF16)
        ltop = S.sb("ltop", [P, H])
        with ExitStack() as mem:
            def sb(name, shape, dt=F32):
                return mem.enter_context(nc.sbuf_tensor(f"l0x_{name}", shape, dt))
            xn, nw, nw2 = sb("xn", [P, DIM]), sb("nw", [P, 16]), sb("nw2", [P, 16])
            ln, lT = sb("ln", [P, DIM]), sb("lT", [P, DC, P])
            wq = sb("wq", [P, DC, INNER])
            gl, bl = sb("gl", [P, DIM]), sb("bl", [P, DIM])
            gx, bx = sb("gx", [P, DC]), sb("bx", [P, DC])
            bxb = sb("bxb", [P, DC, P])
            pq, pk, pv, pbk, pbv, ps0, ps1, pt = [
                mem.enter_context(nc.psum_tensor(f"l0x_p{n}", [P, BANK], F32)) for n in range(8)]
            loads = Loads(S.sem("loads"))
            with nc.Block() as block:
                @block.sync
                def _(sp):
                    loads(sp.dma_start(hm[:, :], A["c_head64"]))
                    loads(sp.dma_start(gl[:, :], A["L0_xattn_gamma_l"].partition_broadcast(P)))
                    loads(sp.dma_start(bl[:, :], A["L0_xattn_beta_l"].partition_broadcast(P)))
                    loads(sp.dma_start(gx[:, :], column(A["L0_xattn_gamma_x"]), allow_slow_non_contiguous=True))
                    loads(sp.dma_start(bx[:, :], column(A["L0_xattn_beta_x"]), allow_slow_non_contiguous=True))
                    loads(sp.dma_start(wq[:, :, :], by_rows(A["L0_xattn_Wq"])))
                    loads(sp.dma_start(wk[:, :, :], by_rows(A["L0_xattn_Wk"])))
                    loads(sp.dma_start(wv[:, :, :], by_rows(A["L0_xattn_Wv"])))

                @block.scalar
                def _(act):
                    norm_scalar(act, S, "n", nw)
                    norm_scalar(act, S, "m", nw2)

                @block.vector
                def _(dve):
                    link = Link(dve, S.sem("dve_link"))
                    norm_vector(dve, link, S, "n", R.x[:, :], xn[:, :], nw)
                    norm_vector(dve, link, S, "m", xn[:, :], ln[:, :], nw2)
                    dve.wait_ge(S.sem("loads"), loads.total)
                    link(dve.tensor_tensor(ln[:, :], ln[:, :], gl[:, :], ALU.mult))
                    dve.tensor_tensor(ln[:, :], ln[:, :], bl[:, :], ALU.add).then_inc(S.sem("ln"), 1)
                    turn_vector(dve, S, "l", lT, pt)
                    link(dve.tensor_copy(bxb[:, :, :], bx[:, :].unsqueeze(2).broadcast_to([P, DC, P])))
                    dve.sem_inc(S.sem("bxb"), 1)
                    dve.wait_ge(S.sem("q_proj"), 1)
                    spread_queries(dve, link, pq, q, qb, hm, 2, HD ** -0.5)
                    dve.sem_inc(S.sem("q"), 1)
                    dve.wait_ge(S.sem("latents_proj"), 1)
                    link(dve.tensor_copy(kl[:, :, :], pk[:, :].rearrange("p (c t) -> p c t", c=KC)))
                    dve.tensor_copy(klb[:, :, :], kl[:, :, :]).then_inc(S.sem("klb"), 1)
                    dve.tensor_copy(vl[:, :, :], pv[:, :].rearrange("p (h d) -> p h d", h=H))
                    dve.wait_ge(S.sem("bias_proj"), 1)
                    link(dve.tensor_copy(bias_k[:, :], pbk[:, 0:KC]))
                    dve.tensor_copy(R.nbias_k[64:P, :], pbk[0:64, 0:KC])
                    dve.tensor_scalar(R.nbias_k[0:64, :], pbk[64:P, 0:KC], -1.0, None, ALU.mult)
                    dve.tensor_copy(bias_v[:, :], pbv[:, :])
                    for c in range(DC):
                        dve.tensor_scalar(wk[:, c, :], wk[:, c, :], gx[:, c:c + 1], None, ALU.mult)
                        dve.tensor_scalar(wv[:, c, :], wv[:, c, :], gx[:, c:c + 1], None, ALU.mult)
                    dve.wait_ge(S.sem("latent_scores"), 1)
                    dve.tensor_reduce(ltop[:, 0:4], ps0[:, :].rearrange("p (h k) -> p h k", h=4), AX.X, ALU.max)
                    dve.tensor_reduce(ltop[:, 4:8], ps1[:, :].rearrange("p (h k) -> p h k", h=4), AX.X, ALU.max)

                @block.tensor
                def _(pe):
                    turn_tensor(pe, S, "l", ln, pt, R.ident, ready="ln")
                    pe.wait_ge(S.sem("l_xT"), 1)
                    pe.wait_ge(S.sem("loads"), loads.total)
                    for o in range(KC):
                        for c in range(DC):
                            last = pe.matmul(pq[:, o * P:(o + 1) * P], wq[:, c, o * P:(o + 1) * P], lT[:, c, :],
                                             start=(c == 0), stop=(c == DC - 1))
                    last.then_inc(S.sem("q_proj"), 1)
                    for o in range(KC):
                        for c in range(DC):
                            pe.matmul(pk[:, o * P:(o + 1) * P], wk[:, c, o * P:(o + 1) * P], lT[:, c, :],
                                      start=(c == 0), stop=(c == DC - 1))
                    for c in range(DC):
                        last = pe.matmul(pv[:, :], lT[:, c, :], wv[:, c, :], start=(c == 0), stop=(c == DC - 1))
                    last.then_inc(S.sem("latents_proj"), 1)
                    pe.wait_ge(S.sem("bxb"), 1)
                    for o in range(KC):
                        for c in range(DC):
                            pe.matmul(pbk[:, o:o + 1], wk[:, c, o * P:(o + 1) * P], bx[:, c:c + 1],
                                      start=(c == 0), stop=(c == DC - 1))
                    for c in range(DC):
                        last = pe.matmul(pbv[:, :], bxb[:, c, :], wv[:, c, :], start=(c == 0), stop=(c == DC - 1))
                    last.then_inc(S.sem("bias_proj"), 1)
                    pe.wait_ge(S.sem("q"), 1)
                    pe.wait_ge(S.sem("klb"), 1)
                    for h in range(H):
                        last = pe.matmul((ps0 if h < 4 else ps1)[:, (h % 4) * P:(h % 4 + 1) * P],
                                         qb[h // 2][:, h % 2, :], klb[:, h // 2, :], start=True, stop=True)
                    last.then_inc(S.sem("latent_scores"), 1)
        find_maximum(nc, S, A, R, H, KC, 2, qb, R.nT, "rope", wk, bias_k, top, None)
        with nc.Block() as block:
            @block.vector
            def _(dve):
                dve.tensor_tensor(top[:, :], top[:, :], ltop[:, :], ALU.max)
        m3 = split_rows(nc, S, R, "m3", top, H)
        O = S.psum("O")
        sums = S.sb("sums", [P, H, P])
        attend(nc, S, A, R, H, KC, 2, q, R.KT, R.nT, wv, bias_v, m3, None, O, sums, last_tile=(kl, vl))
        with ExitStack() as mem:
            def sb(name, shape, dt=F32):
                return mem.enter_context(nc.sbuf_tensor(f"l0x_{name}", shape, dt))
            ones = sb("ones", [P, P])
            rec = sb("rec", [P, H, P])
            oT = sb("oT", [P, KC, P])
            wo = sb("wo", [P, KC, DIM])
            pr = [mem.enter_context(nc.psum_tensor(f"l0x_pr{n}", [P, BANK], F32)) for n in range(2)]
            py = mem.enter_context(nc.psum_tensor("l0x_py", [P, BANK], F32))
            with nc.Block() as block:
                @block.sync
                def _(sp):
                    sp.dma_start(wo[:, :, :], by_rows(A["L0_xattn_Wo"])).then_inc(S.sem("wo"), 16)

                @block.vector
                def _(dve):
                    link = Link(dve, S.sem("finish_link"))
                    dve.memset(ones[:, :], 1.0).then_inc(S.sem("ones"), 1)
                    dve.wait_ge(S.sem("totals"), 1)
                    for n in range(2):
                        link(dve.reciprocal(rec[:, 4 * n:4 * n + 4, :], pr[n][:, :].rearrange("p (h q) -> p h q", h=4)))
                    for g in range(2):
                        rows = slice(64 * g, 64 * g + 64)
                        last = dve.tensor_tensor(oT[rows, :, :], O[rows, :].rearrange("p (s q) -> p s q", s=KC),
                                                 rec[rows, g:H:2, :], ALU.mult)
                        link(last)
                    dve.sem_inc(S.sem("oT"), 1)
                    dve.wait_ge(S.sem("y"), 1)
                    dve.tensor_tensor(R.x[:, :], R.x[:, :], py[:, 0:DIM], ALU.add)

                @block.tensor
                def _(pe):
                    pe.wait_ge(S.sem("ones"), 1)
                    for n in range(2):
                        last = pe.matmul(pr[n][:, :], ones[:, :],
                                         sums[:, 4 * n:4 * n + 4, :].rearrange("p h q -> p (h q)"), start=True, stop=True)
                    last.then_inc(S.sem("totals"), 1)
                    pe.wait_ge(S.sem("oT"), 1)
                    pe.wait_ge(S.sem("wo"), 16)
                    for c in range(KC):
                        last = pe.matmul(py[:, 0:DIM], oT[:, c, :], wo[:, c, :], start=(c == 0), stop=(c == KC - 1))
                    last.then_inc(S.sem("y"), 1)


def head_stats(dve, link, f2, sm, ss, rn_in, ratio, tmp, heads_n):
    link(dve.tensor_tensor(tmp, sm, sm, ALU.mult))
    link(dve.scalar_tensor_tensor(tmp, tmp, -1.0 / P, ss, ALU.mult, ALU.add))
    link(dve.tensor_scalar(tmp, tmp, 1.0 / (P - 1), None, ALU.mult))
    link(dve.tensor_scalar(ratio, tmp, 1.0, 2.0, ALU.min, ALU.mult))
    link(dve.tensor_scalar(tmp, tmp, 1.0, None, ALU.add))
    link(dve.reciprocal(tmp, tmp))
    link(dve.tensor_tensor(ratio, ratio, tmp, ALU.mult))


def l2_xattn(nc, A, R):
    H, HD = 8, 128
    W = H * HD
    GW = HD + 2
    steps = R.keys // CHUNK // 2
    with Stage(nc, "l2x") as S:
        w = S.sb("w", [P, DC, W])
        bias = S.sb("bias", [P, W])
        fq = S.sb("fq", [P, W])
        qs = S.sb("qs", [P, 5, H])
        wp1 = S.sb("wp1", [P, DC, HD])
        Msb = S.sb("Msb", [P, H, GW])
        with ExitStack() as mem:
            def sb(name, shape, dt=F32):
                return mem.enter_context(nc.sbuf_tensor(f"l2x_{name}", shape, dt))
            xn, nw, nw2 = sb("xn", [P, DIM]), sb("nw", [P, 16]), sb("nw2", [P, 16])
            xn2, xT = sb("xn2", [P, DIM]), sb("xT", [P, DC, P])
            g, b = sb("g", [P, DC]), sb("b", [P, DC])
            bb = sb("bb", [P, DC, P])
            sq = sb("sq", [P, W])
            pt = mem.enter_context(nc.psum_tensor("l2x_pt", [P, BANK], F32))
            pb = mem.enter_context(nc.psum_tensor("l2x_pb", [P, 2, BANK], F32))
            pf = mem.enter_context(nc.psum_tensor("l2x_pf", [P, 2, BANK], F32))
            loads = Loads(S.sem("loads"))
            with nc.Block() as block:
                @block.sync
                def _(sp):
                    loads(sp.dma_start(w[:, :, :], by_rows(A["L2_xattn_w_in"])))
                    loads(sp.dma_start(g[:, :], column(A["L2_xattn_ln_g"]), allow_slow_non_contiguous=True))
                    loads(sp.dma_start(b[:, :], column(A["L2_xattn_ln_b"]), allow_slow_non_contiguous=True))

                @block.scalar
                def _(act):
                    norm_scalar(act, S, "n", nw)
                    norm_scalar(act, S, "m", nw2)
                    act.wait_ge(S.sem("qss"), 1)
                    act.activation(qs[:, 2, :], qs[:, 1, :], ACT.Sqrt).then_inc(S.sem("qn"), 1)

                @block.vector
                def _(dve):
                    link = Link(dve, S.sem("dve_link"))
                    norm_vector(dve, link, S, "n", R.x[:, :], xn[:, :], nw)
                    norm_vector(dve, link, S, "m", xn[:, :], xn2[:, :], nw2)
                    turn_vector(dve, S, "m", xT, pt)
                    dve.wait_ge(S.sem("loads"), loads.total)
                    dve.tensor_copy(bb[:, :, :], b[:, :].unsqueeze(2).broadcast_to([P, DC, P])).then_inc(
                        S.sem("bb"), 1)
                    dve.wait_ge(S.sem("bias_proj"), 1)
                    link(dve.tensor_copy(bias[:, :], pb[:, :, :].rearrange("p a n -> p (a n)")))
                    for c in range(DC):
                        link(dve.tensor_scalar(w[:, c, :], w[:, c, :], g[:, c:c + 1], None, ALU.mult))
                    dve.sem_inc(S.sem("w_folded"), 1)
                    dve.wait_ge(S.sem("q_proj"), 1)
                    link(dve.tensor_tensor(fq[:, :], pf[:, :, :].rearrange("p a n -> p (a n)"), bias[:, :], ALU.add))
                    link(dve.tensor_tensor(sq[:, :], fq[:, :], fq[:, :], ALU.mult))
                    link(dve.tensor_reduce(qs[:, 0, :], fq[:, :].rearrange("p (h d) -> p h d", h=H), AX.X, ALU.add))
                    dve.tensor_reduce(qs[:, 1, :], sq[:, :].rearrange("p (h d) -> p h d", h=H), AX.X, ALU.add).then_inc(
                        S.sem("qss"), 1)
                    dve.wait_ge(S.sem("qss"), 1)
                    head_stats(dve, link, None, qs[:, 0, :], qs[:, 1, :], None, qs[:, 3, :], qs[:, 4, :], H)
                    dve.wait_ge(S.sem("qn"), 1)
                    dve.reciprocal(qs[:, 2, :], qs[:, 2, :])

                @block.tensor
                def _(pe):
                    turn_tensor(pe, S, "m", xn2, pt, R.ident)
                    pe.wait_ge(S.sem("loads"), loads.total)
                    pe.wait_ge(S.sem("bb"), 1)
                    for n in range(2):
                        for c in range(DC):
                            last = pe.matmul(pb[:, n, :], bb[:, c, :], w[:, c, n * BANK:(n + 1) * BANK],
                                             start=(c == 0), stop=(c == DC - 1))
                    last.then_inc(S.sem("bias_proj"), 1)
                    pe.wait_ge(S.sem("w_folded"), 1)
                    pe.wait_ge(S.sem("m_xT"), 1)
                    for n in range(2):
                        for c in range(DC):
                            last = pe.matmul(pf[:, n, :], xT[:, c, :], w[:, c, n * BANK:(n + 1) * BANK],
                                             start=(c == 0), stop=(c == DC - 1))
                    last.then_inc(S.sem("q_proj"), 1)
        with ExitStack() as mem:
            def sb(name, shape, dt=F32):
                return mem.enter_context(nc.sbuf_tensor(f"l2x_{name}", shape, dt))
            nin = [sb(f"nin{b}", [P, DC, CHUNK]) for b in range(2)]
            f = [sb(f"f{b}", [P, TILES, W]) for b in range(2)]
            gk = [sb(f"gk{b}", [P, TILES, H, GW]) for b in range(2)]
            sq = [sb(f"fsq{b}", [P, W]) for b in range(2)]
            ks = [sb(f"ks{b}", [P, 5, TILES, H]) for b in range(2)]
            zl, zr = sb("zl", [P, P]), sb("zr", [P, BANK])
            pf = [mem.enter_context(nc.psum_tensor(f"l2x_kf{b}", [P, 2, BANK], F32)) for b in range(2)]
            pM = mem.enter_context(nc.psum_tensor("l2x_M", [P, 3, BANK], F32))
            src = R.nT.rearrange("c p (n k) -> n p c k", k=CHUNK)

            def use(i, b, t):
                k = b * TILES + t
                return k % 2, i * TILES + k // 2

            with nc.Block() as block:
                @block.sync
                def _(sp):
                    with sp.Fori(0, steps) as i:
                        for b in range(2):
                            sp.wait_ge(S.sem(f"nin_used{b}"), i)
                            sp.dma_start(nin[b][:, :, :], src[bass.ds(i * 2 + b, 1)].squeeze(0)).then_inc(
                                S.sem(f"nin{b}"), 16)

                def squares_sum(dve, i, b, t):
                    u, j = use(i, b, t)
                    dve.wait_ge(S.sem(f"sq{u}"), j + 1)
                    dve.tensor_reduce(ks[b][:, 1, t, :], sq[u][:, :].rearrange("p (h d) -> p h d", h=H), AX.X,
                                      ALU.add).then_inc(S.sem(f"sums{b}"), 1)
                    dve.wait_ge(S.sem(f"sums{b}"), i * 2 * TILES + min(2 * t + 3, 2 * TILES))
                    dve.sem_inc(S.sem(f"sq_read{u}"), 1)

                @block.vector
                def _(dve):
                    dve.memset(zl[:, :], 0.0).then_inc(S.sem("constants"), 1)
                    dve.memset(zr[:, :], 0.0).then_inc(S.sem("constants"), 1)
                    for b in range(2):
                        dve.memset(gk[b][:, :, :, HD + 1:GW], 1.0).then_inc(S.sem("constants"), 1)

                    with dve.Fori(0, steps) as i:
                        for b in range(2):
                            dve.wait_ge(S.sem(f"f_used{b}"), i)
                            for t in range(TILES):
                                u, j = use(i, b, t)
                                dve.wait_ge(S.sem(f"f_proj{u}"), j + 1)
                                dve.tensor_tensor(f[b][:, t, :], pf[u][:, :, :].rearrange("p a n -> p (a n)"),
                                                  bias[:, :], ALU.add).then_inc(S.sem(f"f{u}"), 1)
                                dve.wait_ge(S.sem(f"f{u}"), j + 1)
                                dve.tensor_reduce(ks[b][:, 0, t, :], f[b][:, t, :].rearrange("p (h d) -> p h d", h=H),
                                                  AX.X, ALU.add).then_inc(S.sem(f"sums{b}"), 1)
                                if t:
                                    squares_sum(dve, i, b, t - 1)
                            squares_sum(dve, i, b, TILES - 1)
                            dve.wait_ge(S.sem(f"sums{b}"), (i + 1) * 2 * TILES)
                            dve.sem_inc(S.sem(f"ss{b}"), 1)
                            n0 = 7
                            sm, ss, ratio, tmp = ks[b][:, 0], ks[b][:, 1], gk[b][:, :, :, HD], ks[b][:, 4]

                            def lk(n, ins):
                                ins.then_inc(S.sem(f"stat{b}"), 1)
                                dve.wait_ge(S.sem(f"stat{b}"), i * n0 + n)
                            lk(1, dve.tensor_tensor(tmp, sm, sm, ALU.mult))
                            lk(2, dve.scalar_tensor_tensor(tmp, tmp, -1.0 / P, ss, ALU.mult, ALU.add))
                            lk(3, dve.tensor_scalar(tmp, tmp, 1.0 / (P - 1), None, ALU.mult))
                            lk(4, dve.tensor_scalar(ks[b][:, 3], tmp, 1.0, 2.0, ALU.min, ALU.mult))
                            lk(5, dve.tensor_scalar(tmp, tmp, 1.0, None, ALU.add))
                            lk(6, dve.reciprocal(tmp, tmp))
                            dve.tensor_tensor(ratio, ks[b][:, 3], tmp, ALU.mult).then_inc(S.sem(f"ratio{b}"), 1)
                            dve.wait_ge(S.sem(f"kn{b}"), i + 1)
                            lk(7, dve.reciprocal(ks[b][:, 2], ks[b][:, 2]))
                            dve.sem_inc(S.sem(f"rn{b}"), 1)

                @block.scalar
                def _(act):
                    with act.Fori(0, steps) as i:
                        for b in range(2):
                            for t in range(TILES):
                                u, j = use(i, b, t)
                                act.wait_ge(S.sem(f"f{u}"), j + 1)
                                act.wait_ge(S.sem(f"sq_read{u}"), j)
                                act.activation(sq[u][:, :], f[b][:, t, :], ACT.Square).then_inc(S.sem(f"sq{u}"), 1)
                            act.wait_ge(S.sem(f"ss{b}"), i + 1)
                            act.wait_ge(S.sem(f"gk{b}"), i * TILES)
                            act.activation(ks[b][:, 2], ks[b][:, 1], ACT.Sqrt).then_inc(S.sem(f"kn{b}"), 1)

                @block.gpsimd
                def _(pool):
                    with pool.Fori(0, steps) as i:
                        for b in range(2):
                            pool.wait_ge(S.sem(f"rn{b}"), i + 1)
                            for t in range(TILES):
                                pool.tensor_tensor(gk[b][:, t, :, 0:HD], f[b][:, t, :].rearrange("p (h d) -> p h d", h=H),
                                                   ks[b][:, 2, t, :].unsqueeze(2).broadcast_to([P, H, HD]),
                                                   ALU.mult).then_inc(S.sem(f"gk{b}"), 1)

                @block.tensor
                def _(pe):
                    def project(i, b):
                        pe.wait_ge(S.sem(f"nin{b}"), (i + 1) * 16)
                        for t in range(TILES):
                            u, j = use(i, b, t)
                            pe.wait_ge(S.sem(f"f{u}"), j)
                            for n in range(2):
                                for c in range(DC):
                                    last = pe.matmul(pf[u][:, n, :], nin[b][:, c, t * P:(t + 1) * P],
                                                     w[:, c, n * BANK:(n + 1) * BANK], start=(c == 0),
                                                     stop=(c == DC - 1))
                            last.then_inc(S.sem(f"f_proj{u}"), 1)
                        pe.wait_ge(S.sem(f"f_proj{u}"), j + 1)
                        pe.sem_inc(S.sem(f"nin_used{b}"), 1)

                    def gather(i, b):
                        pe.wait_ge(S.sem(f"ratio{b}"), i + 1)
                        for t in range(TILES):
                            pe.wait_ge(S.sem(f"gk{b}"), i * TILES + t + 1)
                            for h in range(H):
                                last = pe.matmul(pM[:, h // 3, (h % 3) * GW:(h % 3 + 1) * GW],
                                                 f[b][:, t, h * HD:(h + 1) * HD], gk[b][:, t, h, :],
                                                 start=False, stop=False, skip_group_check=True)
                        last.then_inc(S.sem(f"f_used{b}"), 1)

                    pe.wait_ge(S.sem("constants"), 4)
                    for n in range(3):
                        pe.matmul(pM[:, n, :], zl[:, :], zr[:, :], start=True, stop=True)
                    project(0, 0)
                    if steps > 1:
                        with pe.Fori(0, steps - 1) as i:
                            project(i, 1)
                            gather(i, 0)
                            project(i + 1, 0)
                            gather(i, 1)
                    project(steps - 1, 1)
                    gather(steps - 1, 0)
                    gather(steps - 1, 1)
            with nc.Block() as block:
                @block.vector
                def _(dve):
                    for n in range(3):
                        k = min(3, H - 3 * n)
                        dve.tensor_copy(Msb[:, 3 * n:3 * n + k, :],
                                        pM[:, n, 0:k * GW].rearrange("p (h g) -> p h g", g=GW))
        with ExitStack() as mem:
            def sb(name, shape, dt=F32):
                return mem.enter_context(nc.sbuf_tensor(f"l2x_{name}", shape, dt))
            b1, lg, lb = sb("b1", [H, HD]), sb("lg", [H, HD]), sb("lb", [H, HD])
            w2, b2 = sb("w2", [P, 3]), sb("b2", [H, 3])
            wo, bo = sb("wo", [P, H, DIM]), sb("bo", [P, DIM])
            ones, off = sb("ones", [P, P]), sb("off", [P, P])
            qc, corr = sb("qc", [P, H, HD]), sb("corr", [P, H, HD])
            cs, dec = sb("cs", [P, H]), sb("dec", [P, H])
            gT = sb("gT", [P, 2, H])
            h1, nw3, h1T = sb("h1", [H, HD]), sb("nw3", [H, 16]), sb("h1T", [P, H])
            lo, sw, dw = sb("lo", [H, 3]), sb("sw", [H, 4]), sb("dw", [H, H, 3])
            mix = sb("mix", [P, H, 3])
            ca, cb = sb("ca", [P, H]), sb("cb", [P, H])
            cbw = sb("cbw", [P, H, P])
            a, aT, yT, cbT = sb("a", [P, H, HD]), sb("aT", [P, H, P]), sb("yT", [P, H, P]), sb("cbT", [P, H, P])
            p1 = mem.enter_context(nc.psum_tensor("l2x_p1", [P, 2, BANK], F32))
            p2 = mem.enter_context(nc.psum_tensor("l2x_p2", [P, 2, BANK], F32))
            p3, p4, p5, p6 = [mem.enter_context(nc.psum_tensor(f"l2x_p{n}", [P, BANK], F32)) for n in range(3, 7)]
            loads = Loads(S.sem("late_loads"))
            heads = lambda ap: ap.rearrange("p a (b d) -> p (a b) d", d=P)
            with nc.Block() as block:
                @block.sync
                def _(sp):
                    loads(sp.dma_start(wp1[:, :, :], by_rows(A["L2_xattn_wp_w1"])))
                    loads(sp.dma_start(b1[:, :], A["L2_xattn_wp_b1"].partition_broadcast(H)))
                    loads(sp.dma_start(lg[:, :], A["L2_xattn_wp_ln_g"].partition_broadcast(H)))
                    loads(sp.dma_start(lb[:, :], A["L2_xattn_wp_ln_b"].partition_broadcast(H)))
                    loads(sp.dma_start(w2[:, :], A["L2_xattn_wp_w2"]))
                    loads(sp.dma_start(b2[:, :], A["L2_xattn_wp_b2"].partition_broadcast(H)))
                    loads(sp.dma_start(wo[:, :, :], by_rows(A["L2_xattn_w_out"])))
                    loads(sp.dma_start(bo[:, :], A["L2_xattn_b_out"].partition_broadcast(P)))

                @block.scalar
                def _(act):
                    act.wait_ge(S.sem("corr_total"), 1)
                    act.activation(dec[:, :], p3[:, 0:H], ACT.Sqrt).then_inc(S.sem("corr_root"), 1)
                    norm_scalar(act, S, "h", nw3, rows=H)
                    act.wait_ge(S.sem("corr_root"), 1)
                    act.activation(dec[:, :], dec[:, :], ACT.Exp, scale=-5.0 / P / (HD * HD)).then_inc(
                        S.sem("decorr"), 1)
                    act.wait_ge(S.sem("w_shifted"), 1)
                    act.activation(lo[:, :], lo[:, :], ACT.Exp, accum_out=sw[:, 1:2]).then_inc(S.sem("w_exp"), 1)

                @block.vector
                def _(dve):
                    link = Link(dve, S.sem("late_link"))
                    fqh = fq[:, :].rearrange("p (h d) -> p h d", h=H)
                    link(dve.memset(ones[:, :], 1.0))
                    link(dve.tensor_scalar(off[:, :], R.ident[:, :], -1.0, 1.0, ALU.mult, ALU.add))
                    link(dve.tensor_scalar(cs[:, :], qs[:, 0, :], 1.0 / HD, None, ALU.mult))
                    link(dve.tensor_tensor(qc[:, :, :], fqh, cs[:, :].unsqueeze(2).broadcast_to([P, H, HD]),
                                           ALU.subtract))
                    dve.sem_inc(S.sem("qc"), 1)
                    dve.wait_ge(S.sem("corr"), 1)
                    link(dve.tensor_tensor(corr[:, :, :], heads(p1[:, :, :]),
                                           off[:, :].unsqueeze(1).broadcast_to([P, H, P]), ALU.mult))
                    link(dve.tensor_tensor(corr[:, :, :], corr[:, :, :], corr[:, :, :], ALU.mult))
                    link(dve.tensor_reduce(cs[:, :], corr[:, :, :], AX.X, ALU.add))
                    dve.sem_inc(S.sem("corr_sq"), 1)
                    dve.wait_ge(S.sem("q_mean"), 1)
                    link(dve.tensor_scalar(gT[:, 0, :], p4[:, 0:H], 1.0 / P, None, ALU.mult))
                    link(dve.tensor_scalar(gT[:, 1, :], Msb[:, :, HD + 1], 1.0 / R.keys, None, ALU.mult))
                    dve.sem_inc(S.sem("gT"), 1)
                    dve.wait_ge(S.sem("late_loads"), loads.total)
                    dve.wait_ge(S.sem("h1"), 1)
                    link(dve.tensor_tensor(h1[:, :], p5[0:H, 0:HD], b1[:, :], ALU.add))
                    norm_vector(dve, link, S, "h", h1[:, :], h1[:, :], nw3, rows=H)
                    link(dve.tensor_tensor(h1[:, :], h1[:, :], lg[:, :], ALU.mult))
                    link(dve.tensor_tensor(h1[:, :], h1[:, :], lb[:, :], ALU.add))
                    link(dve.tensor_scalar(h1[:, :], h1[:, :], 0.0, None, ALU.max))
                    dve.sem_inc(S.sem("h1_relu"), 1)
                    dve.wait_ge(S.sem("h1_turned"), 1)
                    dve.tensor_copy(h1T[:, :], p5[:, 0:H]).then_inc(S.sem("h1T"), 1)
                    dve.wait_ge(S.sem("logits"), 1)
                    link(dve.tensor_tensor(lo[:, :], p5[0:H, 0:3], b2[:, :], ALU.add))
                    link(dve.tensor_reduce(sw[:, 0:1], lo[:, :], AX.X, ALU.max))
                    dve.tensor_scalar(lo[:, :], lo[:, :], sw[:, 0:1], None, ALU.subtract).then_inc(
                        S.sem("w_shifted"), 1)
                    dve.wait_ge(S.sem("w_exp"), 1)
                    link(dve.reciprocal(sw[:, 2:3], sw[:, 1:2]))
                    link(dve.tensor_scalar(lo[:, :], lo[:, :], sw[:, 2:3], None, ALU.mult))
                    link(dve.tensor_tensor(dw[:, :, :], lo[:, :].unsqueeze(1).broadcast_to([H, H, 3]),
                                           R.ident[0:H, 0:H].unsqueeze(2).broadcast_to([H, H, 3]), ALU.mult))
                    dve.sem_inc(S.sem("dw"), 1)
                    dve.wait_ge(S.sem("mix"), 1)
                    link(dve.tensor_copy(mix[:, :, :], p6[:, 0:3 * H].rearrange("p (h k) -> p h k", k=3)))
                    dve.wait_ge(S.sem("decorr"), 1)
                    link(dve.tensor_tensor(ca[:, :], mix[:, :, 1], dec[:, :], ALU.mult))
                    link(dve.tensor_tensor(ca[:, :], ca[:, :], mix[:, :, 0], ALU.add))
                    link(dve.tensor_tensor(ca[:, :], ca[:, :], qs[:, 2, :], ALU.mult))
                    link(dve.tensor_tensor(cb[:, :], mix[:, :, 2], qs[:, 3, :], ALU.mult))
                    link(dve.tensor_tensor(a[:, :, :], fqh, ca[:, :].unsqueeze(2).broadcast_to([P, H, HD]), ALU.mult))
                    link(dve.tensor_copy(cbw[:, :, :], cb[:, :].unsqueeze(2).broadcast_to([P, H, P])))
                    dve.sem_inc(S.sem("a"), 1)
                    dve.wait_ge(S.sem("a_turned"), 1)
                    link(dve.tensor_copy(aT[:, :, :], heads(p1[:, :, :])))
                    link(dve.tensor_copy(cbT[:, :, :], heads(p2[:, :, :])))
                    dve.sem_inc(S.sem("aT"), 1)
                    for h in range(H):
                        link(dve.tensor_scalar(yT[:, h, :], cbT[:, h, :], Msb[:, h, HD:HD + 1], None, ALU.mult))
                    dve.wait_ge(S.sem("mixed"), 1)
                    link(dve.tensor_tensor(yT[:, :, :], yT[:, :, :], heads(p1[:, :, :]), ALU.add))
                    dve.sem_inc(S.sem("yT"), 1)
                    link(dve.tensor_tensor(R.x[:, :], R.x[:, :], bo[:, :], ALU.add))
                    dve.wait_ge(S.sem("y"), 1)
                    dve.tensor_tensor(R.x[:, :], R.x[:, :], p3[:, 0:DIM], ALU.add)

                @block.tensor
                def _(pe):
                    pe.wait_ge(S.sem("qc"), 1)
                    for h in range(H):
                        last = pe.matmul(p1[:, h // 4, (h % 4) * P:(h % 4 + 1) * P], qc[:, h, :], qc[:, h, :],
                                         start=True, stop=True)
                    last.then_inc(S.sem("corr"), 1)
                    for h in range(H):
                        last = pe.matmul(p4[:, h:h + 1], fq[:, h * HD:(h + 1) * HD], ones[:, 0:1], start=True,
                                         stop=True)
                    last.then_inc(S.sem("q_mean"), 1)
                    pe.wait_ge(S.sem("corr_sq"), 1)
                    pe.matmul(p3[:, 0:H], ones[:, :], cs[:, :], start=True, stop=True).then_inc(
                        S.sem("corr_total"), 1)
                    pe.wait_ge(S.sem("gT"), 1)
                    pe.wait_ge(S.sem("late_loads"), loads.total)
                    for c in range(2):
                        last = pe.matmul(p5[0:H, 0:HD], gT[:, c, :], wp1[:, c, :], start=(c == 0), stop=(c == 1))
                    last.then_inc(S.sem("h1"), 1)
                    pe.wait_ge(S.sem("h1_relu"), 1)
                    pe.transpose(p5[:, 0:H], h1[:, :], R.ident[0:H, 0:H]).then_inc(S.sem("h1_turned"), 1)
                    pe.wait_ge(S.sem("h1T"), 1)
                    pe.matmul(p5[0:H, 0:3], h1T[:, :], w2[:, :], start=True, stop=True).then_inc(S.sem("logits"), 1)
                    pe.wait_ge(S.sem("dw"), 1)
                    pe.matmul(p6[:, 0:3 * H], ones[0:H, :], dw[:, :, :].rearrange("p h k -> p (h k)"),
                              start=True, stop=True).then_inc(S.sem("mix"), 1)
                    pe.wait_ge(S.sem("a"), 1)
                    for h in range(H):
                        pe.transpose(p1[:, h // 4, (h % 4) * P:(h % 4 + 1) * P], a[:, h, :], R.ident[:, :])
                        last = pe.matmul(p2[:, h // 4, (h % 4) * P:(h % 4 + 1) * P], cbw[:, h, :], R.ident[:, :],
                                         start=True, stop=True)
                    last.then_inc(S.sem("a_turned"), 1)
                    pe.wait_ge(S.sem("aT"), 1)
                    for h in range(H):
                        last = pe.matmul(p1[:, h // 4, (h % 4) * P:(h % 4 + 1) * P], Msb[:, h, 0:HD], aT[:, h, :],
                                         start=True, stop=True)
                    last.then_inc(S.sem("mixed"), 1)
                    pe.wait_ge(S.sem("yT"), 1)
                    for h in range(H):
                        last = pe.matmul(p3[:, 0:DIM], yT[:, h, :], wo[:, h, :], start=(h == 0), stop=(h == H - 1))
                    last.then_inc(S.sem("y"), 1)


INNER, STATES, TAPS = 512, 16, 4
IC = INNER // P


def conv_silu_vector(dve, link, S, pad, xc, sx, taps, bias):
    for c in range(IC):
        link(dve.tensor_scalar(xc[:, c, :], pad[:, c, 0:P], taps[:, c, 0:1], None, ALU.mult))
        for k in range(1, TAPS):
            link(dve.scalar_tensor_tensor(xc[:, c, :], pad[:, c, k:k + P], taps[:, c, k:k + 1], xc[:, c, :],
                                          ALU.mult, ALU.add))
        link(dve.tensor_scalar(xc[:, c, :], xc[:, c, :], bias[:, c:c + 1], None, ALU.add))
    dve.sem_inc(S.sem("conv"), 1)
    dve.wait_ge(S.sem("sigmoid"), 1)
    link(dve.tensor_tensor(xc[:, :, :], xc[:, :, :], sx[:, :, :], ALU.mult))


def softplus_vector(dve, link, S, src, mag, delta):
    link(dve.tensor_scalar(mag[:, :, :], src, -1.0, None, ALU.mult))
    dve.tensor_tensor(mag[:, :, :], mag[:, :, :], src, ALU.min).then_inc(S.sem("mag"), 1)
    link(dve.tensor_scalar(delta[:, :, :], src, 0.0, None, ALU.max))
    dve.wait_ge(S.sem("log1p"), 1)
    link(dve.tensor_tensor(delta[:, :, :], delta[:, :, :], mag[:, :, :], ALU.add))


def softplus_scalar(act, S, mag):
    act.wait_ge(S.sem("mag"), 1)
    act.activation(mag[:, :, :], mag[:, :, :], ACT.Exp).then_inc(S.sem("exp_mag"), 1)
    act.wait_ge(S.sem("exp_mag"), 1)
    act.activation(mag[:, :, :], mag[:, :, :], ACT.Ln, bias=1.0).then_inc(S.sem("log1p"), 1)


def mamba(nc, A, R, name, weights, selective):
    N3 = 16 + 2 * STATES
    with Stage(nc, name) as S:
        w_in = S.sb("w_in", [P, DC, 2 * INNER])
        w_out = S.sb("w_out", [P, IC, DIM])
        taps, cbias = S.sb("taps", [P, IC, TAPS]), S.sb("cbias", [P, IC])
        alog, dskip = S.sb("alog", [P, IC, STATES]), S.sb("dskip", [P, IC])
        xn, xT, nw = S.sb("xn", [P, DIM]), S.sb("xT", [P, DC, P]), S.sb("nw", [P, 16])
        pad = S.sb("pad", [P, IC, P + TAPS - 1])
        xc, sx, gate = S.sb("xc", [P, IC, P]), S.sb("sx", [P, IC, P]), S.sb("gate", [P, IC, P])
        mag, delta, u = S.sb("mag", [P, IC, P]), S.sb("delta", [P, IC, P]), S.sb("u", [P, IC, P])
        decay = [S.sb(f"decay{b}", [P, STATES, P]) for b in range(IC)]
        drive = [S.sb(f"drive{b}", [P, STATES, P]) for b in range(2)]
        state = [S.sb(f"state{b}", [P, STATES, P]) for b in range(2)]
        y = S.sb("y", [P, IC, P])
        if selective:
            wx, wdt, bdt = S.sb("wx", [P, IC, N3]), S.sb("wdt", [16, INNER]), S.sb("bdt", [P, IC])
            dbc = S.sb("dbc", [N3, P])
            bc = S.sb("bc", [P, 2 * STATES, P])
            bc_dram = nc.dram_tensor(f"{name}_bc_dram", (2 * STATES, P), F32, kind="Internal").ap()
            px = S.psum("px")
        pt, pi, pg, po = S.psum("pt"), S.psum("pi"), S.psum("pg"), S.psum("po")
        pd = S.psum("pd")
        loads = Loads(S.sem("loads"))
        with S.nc.Block() as block:
            @block.sync
            def _(sp):
                loads(sp.dma_start(w_in[:, :, :], by_rows(A[weights["in"]])))
                loads(sp.dma_start(w_out[:, :, :], by_rows(A[weights["out"]])))
                loads(sp.dma_start(taps[:, :, :], by_rows(A[weights["conv"]])))
                loads(sp.dma_start(cbias[:, :], column(A[weights["conv_b"]]), allow_slow_non_contiguous=True))
                loads(sp.dma_start(alog[:, :, :], by_rows(A[weights["A_log"]])))
                loads(sp.dma_start(dskip[:, :], column(A[weights["D"]]), allow_slow_non_contiguous=True))
                if selective:
                    loads(sp.dma_start(wx[:, :, :], by_rows(A["L2_attn_W_xproj"])))
                    loads(sp.dma_start(wdt[:, :], A["L2_attn_W_dt"]))
                    loads(sp.dma_start(bdt[:, :], column(A["L2_attn_b_dt"]), allow_slow_non_contiguous=True))
                    sp.wait_ge(S.sem("dbc"), 1)
                    sp.dma_start(bc_dram, dbc[16:N3, :]).then_inc(S.sem("bc_out"), 16)
                    sp.wait_ge(S.sem("bc_out"), 16)
                    sp.dma_start(bc[:, :, :], bc_dram.partition_broadcast(P)).then_inc(S.sem("bc"), 16)

            @block.vector
            def _(dve):
                link = Link(dve, S.sem("dve_link"))
                link(dve.memset(pad[:, :, :], 0.0))
                norm_vector(dve, link, S, "n", R.x[:, :], xn[:, :], nw)
                turn_vector(dve, S, "n", xT, pt)
                dve.wait_ge(S.sem("loads"), loads.total)
                dve.wait_ge(S.sem("in_proj"), 1)
                link(dve.tensor_copy(pad[:, :, TAPS - 1:], pi[:, :].rearrange("p (c t) -> p c t", c=IC)))
                conv_silu_vector(dve, link, S, pad, xc, sx, taps, cbias)
                dve.sem_inc(S.sem("xc"), 1)
                if selective:
                    dve.wait_ge(S.sem("x_proj"), 1)
                    dve.tensor_copy(dbc[:, :], px[0:N3, 0:P]).then_inc(S.sem("dbc"), 1)
                    dve.wait_ge(S.sem("dt_proj"), 1)
                    for c in range(IC):
                        link(dve.tensor_scalar(u[:, c, :], pd[:, c * P:(c + 1) * P], bdt[:, c:c + 1], None, ALU.add))
                    softplus_vector(dve, link, S, u[:, :, :], mag, delta)
                    link(dve.tensor_tensor(u[:, :, :], delta[:, :, :], xc[:, :, :], ALU.mult))
                else:
                    softplus_vector(dve, link, S, xc[:, :, :], mag, delta)
                    link(dve.tensor_tensor(u[:, :, :], xc[:, :, :], xc[:, :, :], ALU.mult))
                dve.wait_ge(S.sem("minus_a"), 1)
                for c in range(IC):
                    dve.tensor_tensor(decay[c][:, :, :],
                                      delta[:, c, :].unsqueeze(1).broadcast_to([P, STATES, P]),
                                      alog[:, c, :].unsqueeze(2).broadcast_to([P, STATES, P]),
                                      ALU.mult).then_inc(S.sem("rate"), 1)
                if selective:
                    dve.wait_ge(S.sem("bc"), 16)
                for c in range(IC):
                    b = c % 2
                    ub = u[:, c, :].unsqueeze(1).broadcast_to([P, STATES, P])
                    if selective:
                        link(dve.tensor_tensor(drive[b][:, :, :], ub, bc[:, 0:STATES, :], ALU.mult))
                    else:
                        link(dve.tensor_copy(drive[b][:, :, :], ub))
                    dve.wait_ge(S.sem("decay"), c + 1)
                    link(dve.memset(decay[c][:, :, 0:1], 0.0))
                    flat = lambda ap: ap[:, :, :].rearrange("p n t -> p (n t)")
                    link(dve.tensor_tensor_scan(flat(state[b]), flat(decay[c]), flat(drive[b]), 0.0, ALU.mult,
                                                ALU.add))
                    if selective:
                        link(dve.tensor_tensor(state[b][:, :, :], state[b][:, :, :], bc[:, STATES:, :], ALU.mult))
                    link(dve.tensor_reduce(y[:, c, :], state[b][:, :, :].rearrange("p n t -> p t n"), AX.X, ALU.add))
                dve.wait_ge(S.sem("gate"), 1)
                link(dve.tensor_tensor(gate[:, :, :], gate[:, :, :], pg[:, :].rearrange("p (c t) -> p c t", c=IC),
                                       ALU.mult))
                if selective:
                    for c in range(IC):
                        link(dve.scalar_tensor_tensor(y[:, c, :], xc[:, c, :], dskip[:, c:c + 1], y[:, c, :],
                                                      ALU.mult, ALU.add))
                    link(dve.tensor_tensor(y[:, :, :], y[:, :, :], gate[:, :, :], ALU.mult))
                else:
                    link(dve.tensor_tensor(y[:, :, :], y[:, :, :], xc[:, :, :], ALU.mult))
                    link(dve.tensor_tensor(y[:, :, :], y[:, :, :], gate[:, :, :], ALU.mult))
                    for c in range(IC):
                        link(dve.scalar_tensor_tensor(y[:, c, :], xc[:, c, :], dskip[:, c:c + 1], y[:, c, :],
                                                      ALU.mult, ALU.add))
                dve.sem_inc(S.sem("y"), 1)
                dve.wait_ge(S.sem("out_proj"), 1)
                dve.tensor_tensor(R.x[:, :], R.x[:, :], po[:, 0:DIM], ALU.add)

            @block.scalar
            def _(act):
                norm_scalar(act, S, "n", nw)
                act.wait_ge(S.sem("gate_proj"), 1)
                act.activation(gate[:, :, :], pg[:, :].rearrange("p (c t) -> p c t", c=IC), ACT.Sigmoid).then_inc(
                    S.sem("gate"), 1)
                act.wait_ge(S.sem("conv"), 1)
                act.activation(sx[:, :, :], xc[:, :, :], ACT.Sigmoid).then_inc(S.sem("sigmoid"), 1)
                act.wait_ge(S.sem("loads"), loads.total)
                act.activation(alog[:, :, :], alog[:, :, :], ACT.Exp).then_inc(S.sem("minus_a"), 1)
                softplus_scalar(act, S, mag)
                for c in range(IC):
                    act.wait_ge(S.sem("rate"), c + 1)
                    act.activation(decay[c][:, :, :], decay[c][:, :, :], ACT.Exp, scale=-1.0).then_inc(
                        S.sem("decay"), 1)

            @block.tensor
            def _(pe):
                turn_tensor(pe, S, "n", xn, pt, R.ident)
                pe.wait_ge(S.sem("loads"), loads.total)
                pe.wait_ge(S.sem("n_xT"), 1)
                for side, out, signal in ((0, pi, "in_proj"), (1, pg, "gate_proj")):
                    for o in range(IC):
                        for c in range(DC):
                            at = side * INNER + o * P
                            last = pe.matmul(out[:, o * P:(o + 1) * P], w_in[:, c, at:at + P], xT[:, c, :],
                                             start=(c == 0), stop=(c == DC - 1))
                    last.then_inc(S.sem(signal), 1)
                if selective:
                    pe.wait_ge(S.sem("xc"), 1)
                    for c in range(IC):
                        last = pe.matmul(px[0:N3, 0:P], wx[:, c, :], xc[:, c, :], start=(c == 0),
                                         stop=(c == IC - 1))
                    last.then_inc(S.sem("x_proj"), 1)
                    pe.wait_ge(S.sem("dbc"), 1)
                    for c in range(IC):
                        last = pe.matmul(pd[:, c * P:(c + 1) * P], wdt[:, c * P:(c + 1) * P], dbc[0:16, :],
                                         start=True, stop=True)
                    last.then_inc(S.sem("dt_proj"), 1)
                pe.wait_ge(S.sem("y"), 1)
                for c in range(IC):
                    last = pe.matmul(po[:, 0:DIM], y[:, c, :], w_out[:, c, :], start=(c == 0), stop=(c == IC - 1))
                last.then_inc(S.sem("out_proj"), 1)


def l0_attn(nc, A, R):
    mamba(nc, A, R, "l0a", {"in": "L0_attn_W_in", "out": "L0_attn_W_out", "conv": "L0_attn_conv_w",
                            "conv_b": "L0_attn_conv_b", "A_log": "L0_attn_A_log", "D": "L0_attn_D"}, False)


def l2_attn(nc, A, R):
    mamba(nc, A, R, "l2a", {"in": "L2_attn_W_in", "out": "L2_attn_W_out", "conv": "L2_attn_W_conv",
                            "conv_b": "L2_attn_b_conv", "A_log": "L2_attn_A_log", "D": "L2_attn_D"}, True)


def l1_attn(nc, A, R):
    H, HD = 16, 16
    with Stage(nc, "l1a") as S:
        names = ("r", "k", "v", "g")
        w = S.sb("w", [P, 5, DC, DIM])
        mixc = S.sb("mixc", [P, 4, DC])
        omm = S.sb("omm", [P, 4, DC])
        td, u = S.sb("td", [P, H]), S.sb("u", [P, H])
        lnw, lnb = S.sb("lnw", [P, DIM]), S.sb("lnb", [P, DIM])
        lag, later, hm = S.sb("lag", [P, P]), S.sb("later", [P, P]), S.sb("hm", [P, 8])
        xn, nw = S.sb("xn", [P, DIM]), S.sb("nw", [P, 16])
        xp = S.sb("xp", [P, DC, P + 1])
        xm = S.sb("xm", [P, 4, DC, P])
        rb = [S.sb(f"rb{c}", [P, 8, P]) for c in range(DC)]
        kT, v, g = S.sb("kT", [P, DC, P]), S.sb("v", [P, DIM]), S.sb("g", [P, DIM])
        wm = S.sb("wm", [P, H, P])
        att = S.sb("att", [P, H, P])
        o, oc, sq = S.sb("o", [P, H, HD]), S.sb("oc", [P, H, HD]), S.sb("sq", [P, H, HD])
        m, va = S.sb("m", [P, H]), S.sb("va", [P, H])
        oT = S.sb("oT", [P, DC, P])
        pt, prk, pvg, po = S.psum("pt"), S.psum("prk"), S.psum("pvg"), S.psum("po")
        pa = S.psum("pa", 4)
        loads = Loads(S.sem("loads"))
        with S.nc.Block() as block:
            @block.sync
            def _(sp):
                for n, name in enumerate(names):
                    loads(sp.dma_start(w[:, n, :, :], by_rows(A[f"L1_attn_W_{name}"])))
                    loads(sp.dma_start(mixc[:, n, :], column(A[f"L1_attn_time_mix_{name}"]),
                                       allow_slow_non_contiguous=True))
                loads(sp.dma_start(w[:, 4, :, :], by_rows(A["L1_attn_W_o"])))
                loads(sp.dma_start(td[:, :], A["L1_attn_time_decay"].partition_broadcast(P)))
                loads(sp.dma_start(u[:, :], A["L1_attn_time_faaaa"].partition_broadcast(P)))
                loads(sp.dma_start(lnw[:, :], A["L1_attn_ln_w"].partition_broadcast(P)))
                loads(sp.dma_start(lnb[:, :], A["L1_attn_ln_b"].partition_broadcast(P)))
                loads(sp.dma_start(lag[:, :], A["c_lag"]))
                loads(sp.dma_start(later[:, :], A["c_later"]))
                loads(sp.dma_start(hm[:, :], A["c_head16"]))

            @block.vector
            def _(dve):
                link = Link(dve, S.sem("dve_link"))
                link(dve.memset(xp[:, :, :], 0.0))
                norm_vector(dve, link, S, "n", R.x[:, :], xn[:, :], nw)
                dve.wait_ge(S.sem("n_turned"), 1)
                link(dve.tensor_copy(xp[:, :, 1:], pt[:, 0:DIM].rearrange("p (c t) -> p c t", c=DC)))
                dve.wait_ge(S.sem("loads"), loads.total)
                link(dve.tensor_scalar(omm[:, :, :], mixc[:, :, :], -1.0, 1.0, ALU.mult, ALU.add))
                for n in range(4):
                    for c in range(DC):
                        link(dve.tensor_scalar(xm[:, n, c, :], xp[:, c, 0:P], omm[:, n, c:c + 1], None, ALU.mult))
                        link(dve.scalar_tensor_tensor(xm[:, n, c, :], xp[:, c, 1:], mixc[:, n, c:c + 1],
                                                      xm[:, n, c, :], ALU.mult, ALU.add))
                dve.sem_inc(S.sem("mixed"), 1)
                dve.wait_ge(S.sem("rk"), 1)
                for c in range(DC):
                    link(dve.tensor_tensor(rb[c][:, :, :],
                                           prk[:, c * P:(c + 1) * P].unsqueeze(1).broadcast_to([P, 8, P]),
                                           hm[:, :].unsqueeze(2).broadcast_to([P, 8, P]), ALU.mult))
                link(dve.tensor_copy(kT[:, :, :], prk[:, DIM:2 * DIM].rearrange("p (c t) -> p c t", c=DC)))
                dve.sem_inc(S.sem("rk_ready"), 1)
                dve.wait_ge(S.sem("rates"), 1)
                dve.tensor_scalar(td[:, :], td[:, :], 1e30, -1.0, ALU.min, ALU.mult).then_inc(S.sem("rate"), 1)
                dve.wait_ge(S.sem("powers"), 1)
                link(dve.tensor_tensor(wm[:, :, :], wm[:, :, :],
                                       later[:, :].unsqueeze(1).broadcast_to([P, H, P]), ALU.mult))
                for h in range(H):
                    link(dve.scalar_tensor_tensor(wm[:, h, :], R.ident[:, :], u[:, h:h + 1], wm[:, h, :],
                                                  ALU.mult, ALU.add))
                dve.wait_ge(S.sem("att"), 1)
                link(dve.tensor_tensor(att[:, :, :], pa[:, :, :].rearrange("p a (b q) -> p (a b) q", q=P),
                                       wm[:, :, :], ALU.mult))
                dve.wait_ge(S.sem("vg"), 1)
                dve.tensor_copy(v[:, :], pvg[:, 0:DIM]).then_inc(S.sem("att_ready"), 1)
                dve.wait_ge(S.sem("gate"), 1)
                link(dve.tensor_tensor(g[:, :], g[:, :], pvg[:, DIM:2 * DIM], ALU.mult))
                dve.wait_ge(S.sem("out"), 1)
                link(dve.tensor_scalar(o[:, :, :], po[:, 0:DIM].rearrange("p (h d) -> p h d", h=H), 1.0 / 8.0, None,
                                       ALU.mult))
                link(dve.tensor_reduce(m[:, :], o[:, :, :], AX.X, ALU.add))
                link(dve.tensor_scalar(m[:, :], m[:, :], 1.0 / HD, None, ALU.mult))
                link(dve.tensor_tensor(oc[:, :, :], o[:, :, :], m[:, :].unsqueeze(2).broadcast_to([P, H, HD]),
                                       ALU.subtract))
                link(dve.tensor_tensor(sq[:, :, :], oc[:, :, :], oc[:, :, :], ALU.mult))
                link(dve.tensor_reduce(va[:, :], sq[:, :, :], AX.X, ALU.add))
                dve.tensor_scalar(va[:, :], va[:, :], 1.0 / HD, EPS, ALU.mult, ALU.add).then_inc(S.sem("o_var"), 1)
                dve.wait_ge(S.sem("o_std"), 1)
                link(dve.reciprocal(va[:, :], va[:, :]))
                link(dve.tensor_tensor(oc[:, :, :], oc[:, :, :], va[:, :].unsqueeze(2).broadcast_to([P, H, HD]),
                                       ALU.mult))
                flat = oc[:, :, :].rearrange("p h d -> p (h d)")
                link(dve.tensor_tensor(xn[:, :], flat, lnw[:, :], ALU.mult))
                link(dve.tensor_tensor(xn[:, :], xn[:, :], lnb[:, :], ALU.add))
                dve.tensor_tensor(xn[:, :], xn[:, :], g[:, :], ALU.mult).then_inc(S.sem("gated"), 1)
                turn_vector(dve, S, "o", oT, pt)
                dve.wait_ge(S.sem("y"), 1)
                dve.tensor_tensor(R.x[:, :], R.x[:, :], po[:, DIM:2 * DIM], ALU.add)

            @block.scalar
            def _(act):
                norm_scalar(act, S, "n", nw)
                act.wait_ge(S.sem("loads"), loads.total)
                act.activation(td[:, :], td[:, :], ACT.Exp).then_inc(S.sem("rates"), 1)
                act.wait_ge(S.sem("rate"), 1)
                for h in range(H):
                    last = act.activation(wm[:, h, :], lag[:, :], ACT.Exp, scale=td[:, h:h + 1])
                last.then_inc(S.sem("powers"), 1)
                act.wait_ge(S.sem("vg"), 1)
                act.wait_ge(S.sem("att_ready"), 1)
                act.activation(g[:, :], pvg[:, DIM:2 * DIM], ACT.Sigmoid).then_inc(S.sem("gate"), 1)
                act.wait_ge(S.sem("o_var"), 1)
                act.activation(va[:, :], va[:, :], ACT.Sqrt).then_inc(S.sem("o_std"), 1)

            @block.tensor
            def _(pe):
                turn_tensor(pe, S, "n", xn, pt, R.ident)
                pe.wait_ge(S.sem("loads"), loads.total)
                pe.wait_ge(S.sem("mixed"), 1)
                for n in range(2):
                    for oo in range(DC):
                        for c in range(DC):
                            at = n * DIM + oo * P
                            last = pe.matmul(prk[:, at:at + P], w[:, n, c, oo * P:(oo + 1) * P], xm[:, n, c, :],
                                             start=(c == 0), stop=(c == DC - 1))
                last.then_inc(S.sem("rk"), 1)
                for n in range(2):
                    for c in range(DC):
                        last = pe.matmul(pvg[:, n * DIM:(n + 1) * DIM], xm[:, 2 + n, c, :], w[:, 2 + n, c, :],
                                         start=(c == 0), stop=(c == DC - 1))
                last.then_inc(S.sem("vg"), 1)
                pe.wait_ge(S.sem("rk_ready"), 1)
                for c in range(DC):
                    for half in range(2):
                        last = pe.matmul(pa[:, 2 * c + half, :], kT[:, c, :],
                                         rb[c][:, 4 * half:4 * half + 4, :].rearrange("p h q -> p (h q)"),
                                         start=True, stop=True)
                last.then_inc(S.sem("att"), 1)
                pe.wait_ge(S.sem("att_ready"), 1)
                for h in range(H):
                    last = pe.matmul(po[:, h * HD:(h + 1) * HD], att[:, h, :], v[:, h * HD:(h + 1) * HD],
                                     start=True, stop=True)
                last.then_inc(S.sem("out"), 1)
                turn_tensor(pe, S, "o", xn, pt, R.ident, ready="gated")
                pe.wait_ge(S.sem("o_xT"), 1)
                for c in range(DC):
                    last = pe.matmul(po[:, DIM:2 * DIM], oT[:, c, :], w[:, 4, c, :], start=(c == 0),
                                     stop=(c == DC - 1))
                last.then_inc(S.sem("y"), 1)


def l0_ffn(nc, A, R):
    E, FF = 8, 1024
    FC = FF // P
    with Stage(nc, "l0f") as S:
        w1 = [S.sb(f"w1_{b}", [P, DC, FF]) for b in range(2)]
        w2 = [S.sb(f"w2_{b}", [P, FC, DIM]) for b in range(2)]
        b1, b1r = S.sb("b1", [P, E + 1, FC]), S.sb("b1r", [(E + 1) * FC, P])
        b2, b2s = S.sb("b2", [E, DIM]), S.sb("b2s", [P, DIM])
        wr, br = S.sb("wr", [P, DC, E]), S.sb("br", [P, E])
        xn, xT, nw = S.sb("xn", [P, DIM]), S.sb("xT", [P, DC, P]), S.sb("nw", [P, 16])
        lg, pr, tmp, oh = S.sb("lg", [P, E]), S.sb("pr", [P, E]), S.sb("tmp", [P, E]), S.sb("oh", [P, E + 1])
        oh2, sw, wt = S.sb("oh2", [P, E + 1]), S.sb("sw", [P, 8]), S.sb("wt", [P, E])
        weT = S.sb("weT", [E, P])
        hT = [S.sb(f"hT{b}", [P, FC, P]) for b in range(2)]
        acc = S.sb("acc", [P, DIM])
        pt, pm = S.psum("pt"), S.psum("pm")
        ph = [S.psum(f"ph{b}", 2) for b in range(2)]
        py = [S.psum(f"py{b}") for b in range(2)]
        loads = Loads(S.sem("small"))

        def hidden(pe, b):
            for f in range(FC):
                for c in range(DC):
                    last = pe.matmul(ph[b][:, f // 4, (f % 4) * P:(f % 4 + 1) * P], w1[b][:, c, f * P:(f + 1) * P],
                                     xT[:, c, :], start=(c == 0), stop=(c == DC - 1))
            last.then_inc(S.sem(f"h{b}"), 1)

        def output(pe, b):
            for f in range(FC):
                last = pe.matmul(py[b][:, 0:DIM], hT[b][:, f, :], w2[b][:, f, :], start=(f == 0), stop=(f == FC - 1))
            last.then_inc(S.sem(f"y{b}"), 1)

        def gelu(act, b, bias):
            for f in range(FC):
                last = act.activation(hT[b][:, f, :], ph[b][:, f // 4, (f % 4) * P:(f % 4 + 1) * P], ACT.Gelu,
                                      bias=bias(f))
            last.then_inc(S.sem(f"hT{b}"), 1)

        with S.nc.Block() as block:
            @block.sync
            def _(sp):
                sp.dma_start(w1[0][:, :, :], by_rows(A["L0_ffn_shared_w1"])).then_inc(S.sem("w1_0"), 16)
                sp.dma_start(w2[0][:, :, :], by_rows(A["L0_ffn_shared_w2"])).then_inc(S.sem("w2_0"), 16)
                loads(sp.dma_start(b1r[0:E * FC, :], A["L0_ffn_exp_b1"].rearrange("e (f p) -> (e f) p", p=P)))
                loads(sp.dma_start(b1r[E * FC:, :], A["L0_ffn_shared_b1"].rearrange("(f p) -> f p", p=P)))
                loads(sp.dma_start(b2[:, :], A["L0_ffn_exp_b2"]))
                loads(sp.dma_start(b2s[:, :], A["L0_ffn_shared_b2"].partition_broadcast(P)))
                loads(sp.dma_start(wr[:, :, :], by_rows(A["L0_ffn_router_w"])))
                loads(sp.dma_start(br[:, :], A["L0_ffn_router_b"].partition_broadcast(P)))
                with sp.Fori(0, E // 2) as i:
                    for b in (1, 0):
                        e = i * 2 + (1 - b)
                        sp.wait_ge(S.sem(f"used{b}"), i + (1 - b))
                        sp.dma_start(w1[b][:, :, :], A["L0_ffn_exp_w1"][bass.ds(e, 1)].rearrange(
                            "e (c p) n -> p (e c) n", p=P)).then_inc(S.sem(f"w1_{b}"), 16)
                        sp.dma_start(w2[b][:, :, :], A["L0_ffn_exp_w2"][bass.ds(e, 1)].rearrange(
                            "e (c p) n -> p (e c) n", p=P)).then_inc(S.sem(f"w2_{b}"), 16)

            @block.vector
            def _(dve):
                link = Link(dve, S.sem("dve_link"))
                norm_vector(dve, link, S, "n", R.x[:, :], xn[:, :], nw)
                turn_vector(dve, S, "n", xT, pt)
                dve.wait_ge(S.sem("b1_turned"), 1)
                dve.tensor_copy(b1[:, :, :], pm[:, 0:(E + 1) * FC].rearrange("p (e f) -> p e f", f=FC)).then_inc(
                    S.sem("b1_ready"), 1)
                dve.wait_ge(S.sem("small"), loads.total)
                dve.wait_ge(S.sem("router"), 1)
                link(dve.tensor_tensor(lg[:, :], pt[:, 0:E], br[:, :], ALU.add))
                softmax8_vector(dve, link, S, "r", lg[:, :], pr[:, :], sw)
                first_of_max(dve, link, oh, pr[:, :], sw[:, 3:4], tmp[:, :], R.idx_down[:, :])
                link(dve.scalar_tensor_tensor(lg[:, :], oh[:, 0:E], -2.0, pr[:, :], ALU.mult, ALU.add))
                first_of_max(dve, link, oh2, lg[:, :], sw[:, 4:5], tmp[:, :], R.idx_down[:, :])
                link(dve.tensor_tensor(oh[:, 0:E], oh[:, 0:E], oh2[:, 0:E], ALU.add))
                link(dve.tensor_tensor(sw[:, 5:6], sw[:, 3:4], sw[:, 4:5], ALU.add))
                link(dve.tensor_scalar(sw[:, 5:6], sw[:, 5:6], 1e-9, None, ALU.add))
                link(dve.reciprocal(sw[:, 5:6], sw[:, 5:6]))
                link(dve.tensor_tensor(wt[:, :], pr[:, :], oh[:, 0:E], ALU.mult))
                link(dve.tensor_scalar(wt[:, :], wt[:, :], sw[:, 5:6], None, ALU.mult))
                dve.sem_inc(S.sem("weights_of_experts"), 1)
                dve.wait_ge(S.sem("we_turned"), 1)
                dve.tensor_copy(weT[:, :], pm[0:E, P:2 * P]).then_inc(S.sem("weT_ready"), 1)
                dve.wait_ge(S.sem("b2_mixed"), 1)
                link(dve.tensor_tensor(acc[:, :], pm[:, DIM:2 * DIM], R.x[:, :], ALU.add))
                link(dve.tensor_tensor(acc[:, :], acc[:, :], b2s[:, :], ALU.add))
                dve.wait_ge(S.sem("y0"), 1)
                dve.tensor_tensor(acc[:, :], acc[:, :], py[0][:, 0:DIM], ALU.add).then_inc(S.sem("acc_link"), 1)
                with dve.Fori(0, E // 2) as i:
                    for b in (1, 0):
                        e = i * 2 + (1 - b)
                        dve.wait_ge(S.sem(f"y{b}"), i + (2 - b))
                        dve.wait_ge(S.sem("acc_link"), e + 1)
                        dve.scalar_tensor_tensor(acc[:, :], py[b][:, 0:DIM], wt[:, bass.ds(e, 1)], acc[:, :],
                                                 ALU.mult, ALU.add).then_inc(S.sem("acc_link"), 1)
                dve.wait_ge(S.sem("acc_link"), E + 1)
                dve.tensor_copy(R.x[:, :], acc[:, :])

            @block.scalar
            def _(act):
                norm_scalar(act, S, "n", nw)
                softmax8_scalar(act, S, "r", pr[:, :], sw)
                act.wait_ge(S.sem("b1_ready"), 1)
                act.wait_ge(S.sem("h0"), 1)
                gelu(act, 0, lambda f: b1[:, E, f:f + 1])
                with act.Fori(0, E // 2) as i:
                    for b in (1, 0):
                        e = i * 2 + (1 - b)
                        act.wait_ge(S.sem("b1_ready"), 1)
                        act.wait_ge(S.sem(f"h{b}"), i + (2 - b))
                        act.wait_ge(S.sem(f"y{b}"), i + (1 - b))
                        gelu(act, b, lambda f: b1[:, bass.ds(e, 1), f])

            @block.tensor
            def _(pe):
                turn_tensor(pe, S, "n", xn, pt, R.ident)
                pe.wait_ge(S.sem("small"), loads.total)
                pe.transpose(pm[:, 0:(E + 1) * FC], b1r[:, :], R.ident[0:(E + 1) * FC, 0:(E + 1) * FC]).then_inc(
                    S.sem("b1_turned"), 1)
                pe.wait_ge(S.sem("n_xT"), 1)
                for c in range(DC):
                    last = pe.matmul(pt[:, 0:E], xT[:, c, :], wr[:, c, :], start=(c == 0), stop=(c == DC - 1))
                last.then_inc(S.sem("router"), 1)
                pe.wait_ge(S.sem("w1_0"), 16)
                hidden(pe, 0)
                pe.wait_ge(S.sem("w2_0"), 16)
                pe.wait_ge(S.sem("hT0"), 1)
                output(pe, 0)
                pe.wait_ge(S.sem("y0"), 1)
                pe.sem_inc(S.sem("used0"), 1)
                pe.wait_ge(S.sem("weights_of_experts"), 1)
                pe.wait_ge(S.sem("b1_ready"), 1)
                pe.transpose(pm[0:E, P:2 * P], wt[:, :], R.ident[:, :]).then_inc(S.sem("we_turned"), 1)
                pe.wait_ge(S.sem("weT_ready"), 1)
                pe.matmul(pm[:, DIM:2 * DIM], weT[:, :], b2[:, :], start=True, stop=True).then_inc(
                    S.sem("b2_mixed"), 1)
                with pe.Fori(0, E // 2) as i:
                    for b in (1, 0):
                        pe.wait_ge(S.sem(f"w1_{b}"), (i + (2 - b)) * 16)
                        pe.wait_ge(S.sem(f"hT{b}"), i + (1 - b))
                        hidden(pe, b)
                    for b in (1, 0):
                        pe.wait_ge(S.sem(f"w2_{b}"), (i + (2 - b)) * 16)
                        pe.wait_ge(S.sem(f"hT{b}"), i + (2 - b))
                        pe.wait_ge(S.sem("acc_link"), i * 2 + (1 - b))
                        output(pe, b)
                        pe.wait_ge(S.sem(f"y{b}"), i + (2 - b))
                        pe.sem_inc(S.sem(f"used{b}"), 1)


def l1_ffn(nc, A, R):
    E, FF = 8, 1024
    FC = FF // P
    with Stage(nc, "l1f") as S:
        w1 = [S.sb(f"w1_{b}", [P, DC, FF]) for b in range(2)]
        w2 = [S.sb(f"w2_{b}", [P, FC, DIM]) for b in range(2)]
        b1, b1r, b2 = S.sb("b1", [P, E, FC]), S.sb("b1r", [E * FC, P]), S.sb("b2", [E, DIM])
        wr, br = S.sb("wr", [P, DC, E]), S.sb("br", [P, E])
        xn, xT, nw = S.sb("xn", [P, DIM]), S.sb("xT", [P, DC, P]), S.sb("nw", [P, 16])
        lg, pr, tmp, oh = S.sb("lg", [P, E]), S.sb("pr", [P, E]), S.sb("tmp", [P, E]), S.sb("oh", [P, E + 1])
        sw, ohw, ones = S.sb("sw", [P, 4]), S.sb("ohw", [P, E, P]), S.sb("ones", [E, P])
        xe = S.sb("xe", [P, E, DC, P])
        hT = [S.sb(f"hT{b}", [P, FC, P]) for b in range(2)]
        xv = [S.sb(f"xv{b}", [P, DC, P]) for b in range(2)]
        pt, pb = S.psum("pt"), S.psum("pb", 2)
        ph = [S.psum(f"ph{b}", 2) for b in range(2)]
        py = S.psum("py")
        loads = Loads(S.sem("small"))
        with S.nc.Block() as block:
            @block.sync
            def _(sp):
                loads(sp.dma_start(b1r[:, :], A["L1_ffn_b1"].rearrange("e (f p) -> (e f) p", p=P)))
                loads(sp.dma_start(b2[:, :], A["L1_ffn_b2"]))
                loads(sp.dma_start(wr[:, :, :], by_rows(A["L1_ffn_Wr"])))
                loads(sp.dma_start(br[:, :], A["L1_ffn_br"].partition_broadcast(P)))
                with sp.Fori(0, E // 2) as i:
                    for b in range(2):
                        e = i * 2 + b
                        sp.wait_ge(S.sem(f"used{b}"), i)
                        sp.dma_start(w1[b][:, :, :], A["L1_ffn_W1"][bass.ds(e, 1)].rearrange(
                            "e (c p) n -> p (e c) n", p=P)).then_inc(S.sem(f"w1_{b}"), 16)
                        sp.dma_start(w2[b][:, :, :], A["L1_ffn_W2"][bass.ds(e, 1)].rearrange(
                            "e (c p) n -> p (e c) n", p=P)).then_inc(S.sem(f"w2_{b}"), 16)

            @block.vector
            def _(dve):
                link = Link(dve, S.sem("dve_link"))
                link(dve.memset(ones[:, :], 1.0))
                norm_vector(dve, link, S, "n", R.x[:, :], xn[:, :], nw)
                turn_vector(dve, S, "n", xT, pt)
                dve.wait_ge(S.sem("b1_turned"), 1)
                dve.tensor_copy(b1[:, :, :], pb[:, 0, 0:E * FC].rearrange("p (e f) -> p e f", f=FC)).then_inc(
                    S.sem("b1_ready"), 1)
                dve.wait_ge(S.sem("small"), loads.total)
                dve.wait_ge(S.sem("router"), 1)
                link(dve.tensor_tensor(lg[:, :], pt[:, 0:E], br[:, :], ALU.add))
                softmax8_vector(dve, link, S, "r", lg[:, :], pr[:, :], sw)
                first_of_max(dve, link, oh, pr[:, :], sw[:, 3:4], tmp[:, :], R.idx_down[:, :])
                dve.tensor_copy(ohw[:, :, :], oh[:, 0:E].unsqueeze(2).broadcast_to([P, E, P])).then_inc(
                    S.sem("chosen"), 1)
                dve.wait_ge(S.sem("chosen_rows"), 1)
                for c in range(DC):
                    last = dve.tensor_tensor(xe[:, :, c, :], xT[:, c, :].unsqueeze(1).broadcast_to([P, E, P]),
                                             pb[:, :, :].rearrange("p a (b t) -> p (a b) t", t=P), ALU.mult)
                    link(last)
                dve.sem_inc(S.sem("xe"), 1)
                with dve.Fori(0, E // 2) as i:
                    for b in range(2):
                        dve.wait_ge(S.sem(f"h{b}"), i)
                        dve.tensor_copy(xv[b][:, :, :], xe[:, bass.ds(i * 2 + b, 1)].squeeze(1)).then_inc(
                            S.sem(f"xv{b}"), 1)
                dve.wait_ge(S.sem("y"), 1)
                dve.tensor_tensor(R.x[:, :], R.x[:, :], py[:, 0:DIM], ALU.add)

            @block.scalar
            def _(act):
                norm_scalar(act, S, "n", nw)
                softmax8_scalar(act, S, "r", pr[:, :], sw)
                act.wait_ge(S.sem("b1_ready"), 1)
                with act.Fori(0, E // 2) as i:
                    for b in range(2):
                        act.wait_ge(S.sem("b1_ready"), 1)
                        act.wait_ge(S.sem(f"h{b}"), i + 1)
                        act.wait_ge(S.sem(f"used{b}"), i)
                        for f in range(FC):
                            last = act.activation(hT[b][:, f, :], ph[b][:, f // 4, (f % 4) * P:(f % 4 + 1) * P],
                                                  ACT.Relu, bias=b1[:, bass.ds(i * 2 + b, 1), f])
                        last.then_inc(S.sem(f"hT{b}"), 1)

            @block.tensor
            def _(pe):
                turn_tensor(pe, S, "n", xn, pt, R.ident)
                pe.wait_ge(S.sem("small"), loads.total)
                pe.transpose(pb[:, 0, 0:E * FC], b1r[:, :], R.ident[0:E * FC, 0:E * FC]).then_inc(
                    S.sem("b1_turned"), 1)
                pe.wait_ge(S.sem("n_xT"), 1)
                for c in range(DC):
                    last = pe.matmul(pt[:, 0:E], xT[:, c, :], wr[:, c, :], start=(c == 0), stop=(c == DC - 1))
                last.then_inc(S.sem("router"), 1)
                pe.wait_ge(S.sem("chosen"), 1)
                pe.wait_ge(S.sem("b1_ready"), 1)
                for e in range(E):
                    last = pe.matmul(pb[:, e // 4, (e % 4) * P:(e % 4 + 1) * P], ohw[:, e, :], R.ident[:, :],
                                     start=True, stop=True)
                last.then_inc(S.sem("chosen_rows"), 1)
                pe.matmul(py[:, 0:DIM], ones[:, :], b2[:, :], start=True, stop=False, skip_group_check=True)
                with pe.Fori(0, E // 2) as i:
                    for b in range(2):
                        pe.wait_ge(S.sem(f"w1_{b}"), (i + 1) * 16)
                        pe.wait_ge(S.sem(f"xv{b}"), i + 1)
                        pe.wait_ge(S.sem(f"hT{b}"), i)
                        for f in range(FC):
                            for c in range(DC):
                                last = pe.matmul(ph[b][:, f // 4, (f % 4) * P:(f % 4 + 1) * P],
                                                 w1[b][:, c, f * P:(f + 1) * P], xv[b][:, c, :],
                                                 start=(c == 0), stop=(c == DC - 1))
                        last.then_inc(S.sem(f"h{b}"), 1)
                    for b in range(2):
                        pe.wait_ge(S.sem(f"w2_{b}"), (i + 1) * 16)
                        pe.wait_ge(S.sem(f"hT{b}"), i + 1)
                        for f in range(FC):
                            last = pe.matmul(py[:, 0:DIM], hT[b][:, f, :], w2[b][:, f, :], start=False, stop=False,
                                             skip_group_check=True)
                        last.then_inc(S.sem(f"used{b}"), 1)
                for b in range(2):
                    pe.wait_ge(S.sem(f"used{b}"), E // 2)
                pe.sem_inc(S.sem("y"), 1)


def l2_ffn(nc, A, R):
    E, HID = 8, 128
    with Stage(nc, "l2f") as S:
        w1, b1, w2, b2 = S.sb("w1", [P, DC, HID]), S.sb("b1", [P, 1]), S.sb("w2", [P, E]), S.sb("b2", [P, E])
        we, be = S.sb("we", [P, E, DC, DIM]), S.sb("be", [E, DIM])
        xn, xT, nw = S.sb("xn", [P, DIM]), S.sb("xT", [P, DC, P]), S.sb("nw", [P, 16])
        hT = S.sb("hT", [P, P])
        lg, pr, tmp, oh = S.sb("lg", [P, E]), S.sb("pr", [P, E]), S.sb("tmp", [P, E]), S.sb("oh", [P, E + 1])
        sw, ohw, ohT = S.sb("sw", [P, 4]), S.sb("ohw", [P, E, P]), S.sb("ohT", [E, P])
        xe = S.sb("xe", [P, E, DC, P])
        pt, ph, pl, po, py = [S.psum(n) for n in ("pt", "ph", "pl", "po", "py")]
        pb = S.psum("pb", 2)
        loads = Loads(S.sem("loads"))
        experts = Loads(S.sem("experts"))
        with S.nc.Block() as block:
            @block.sync
            def _(sp):
                loads(sp.dma_start(w1[:, :, :], by_rows(A["L2_ffn_w1"])))
                loads(sp.dma_start(b1[:, :], column(A["L2_ffn_b1"]), allow_slow_non_contiguous=True))
                loads(sp.dma_start(w2[:, :], A["L2_ffn_w2"]))
                loads(sp.dma_start(b2[:, :], A["L2_ffn_b2"].partition_broadcast(P)))
                loads(sp.dma_start(be[:, :], A["L2_ffn_expert_b"]))
                experts(sp.dma_start(we[:, :, :, :].rearrange("p e c n -> p (e c) n"),
                                     A["L2_ffn_expert_W"].rearrange("e (c p) n -> p (e c) n", p=P)))

            @block.vector
            def _(dve):
                link = Link(dve, S.sem("dve_link"))
                norm_vector(dve, link, S, "n", R.x[:, :], xn[:, :], nw)
                turn_vector(dve, S, "n", xT, pt)
                dve.wait_ge(S.sem("loads"), loads.total)
                dve.wait_ge(S.sem("h"), 1)
                dve.tensor_scalar(hT[:, :], ph[:, 0:P], b1[:, 0:1], 0.0, ALU.add, ALU.max).then_inc(S.sem("hT"), 1)
                dve.wait_ge(S.sem("router"), 1)
                link(dve.tensor_tensor(lg[:, :], pl[:, 0:E], b2[:, :], ALU.add))
                softmax8_vector(dve, link, S, "r", lg[:, :], pr[:, :], sw)
                first_of_max(dve, link, oh, pr[:, :], sw[:, 3:4], tmp[:, :], R.idx_down[:, :])
                dve.tensor_copy(ohw[:, :, :], oh[:, 0:E].unsqueeze(2).broadcast_to([P, E, P])).then_inc(
                    S.sem("chosen"), 1)
                dve.wait_ge(S.sem("chosen_rows"), 1)
                dve.tensor_copy(ohT[:, :], po[0:E, 0:P]).then_inc(S.sem("ohT"), 1)
                for c in range(DC):
                    link(dve.tensor_tensor(xe[:, :, c, :], xT[:, c, :].unsqueeze(1).broadcast_to([P, E, P]),
                                           pb[:, :, :].rearrange("p a (b t) -> p (a b) t", t=P), ALU.mult))
                dve.sem_inc(S.sem("xe"), 1)
                dve.wait_ge(S.sem("y"), 1)
                dve.tensor_tensor(R.x[:, :], R.x[:, :], py[:, 0:DIM], ALU.add)

            @block.scalar
            def _(act):
                norm_scalar(act, S, "n", nw)
                softmax8_scalar(act, S, "r", pr[:, :], sw)

            @block.tensor
            def _(pe):
                turn_tensor(pe, S, "n", xn, pt, R.ident)
                pe.wait_ge(S.sem("loads"), loads.total)
                pe.wait_ge(S.sem("n_xT"), 1)
                for c in range(DC):
                    last = pe.matmul(ph[:, 0:P], w1[:, c, :], xT[:, c, :], start=(c == 0), stop=(c == DC - 1))
                last.then_inc(S.sem("h"), 1)
                pe.wait_ge(S.sem("hT"), 1)
                pe.matmul(pl[:, 0:E], hT[:, :], w2[:, :], start=True, stop=True).then_inc(S.sem("router"), 1)
                pe.wait_ge(S.sem("chosen"), 1)
                for e in range(E):
                    pe.matmul(pb[:, e // 4, (e % 4) * P:(e % 4 + 1) * P], ohw[:, e, :], R.ident[:, :],
                              start=True, stop=True)
                pe.transpose(po[0:E, 0:P], oh[:, 0:E], R.ident[:, :]).then_inc(S.sem("chosen_rows"), 1)
                pe.wait_ge(S.sem("ohT"), 1)
                pe.matmul(py[:, 0:DIM], ohT[:, :], be[:, :], start=True, stop=False)
                pe.wait_ge(S.sem("experts"), experts.total)
                pe.wait_ge(S.sem("xe"), 1)
                for e in range(E):
                    for c in range(DC):
                        last = pe.matmul(py[:, 0:DIM], xe[:, e, c, :], we[:, e, c, :], start=False,
                                         stop=(e == E - 1 and c == DC - 1))
                last.then_inc(S.sem("y"), 1)



class Residents:
    pass


def constants(keys):
    f = np.float32
    idx = np.arange(P)
    inv_freq = (1.0 / np.power(f(10000.0), np.arange(0, 64, 2, dtype=f) / f(64))).astype(f)
    theta = (np.arange(keys, dtype=f)[:, None] * inv_freq[None, :]).astype(f)
    cos, sin = np.cos(theta).astype(f).T, np.sin(theta).astype(f).T
    diff = idx[None, :] - idx[:, None]
    head16 = (idx[:, None] // 16 == np.arange(8)[None, :]).astype(f)
    head64 = ((idx[:, None] // 32) % 2 == np.arange(2)[None, :]).astype(f)
    count = np.broadcast_to(np.arange(32, dtype=f), (P, 32))
    return {
        "c_ident": np.eye(P, dtype=f),
        "c_head16": head16, "c_head64": head64,
        "c_count": np.ascontiguousarray(count),
        "c_lag": np.maximum(diff - 1, 0).astype(f), "c_later": (diff > 0).astype(f),
        "c_cos": np.ascontiguousarray(np.tile(cos, (4, 1))), "c_sin": np.ascontiguousarray(np.tile(sin, (4, 1))),
    }


def halves_together(w):
    return w.reshape(w.shape[0], 4, 2, 2, 32).transpose(0, 1, 3, 2, 4).reshape(w.shape[0], 512)


def layout(inputs):
    a = {k: np.asarray(v) for k, v in inputs.items()}
    out = constants(a["ctx_1024"].shape[1])
    flip = ["L0_attn_W_in", "L0_attn_W_out", "L1_xattn_wq", "L1_xattn_wk", "L1_xattn_wv", "L1_attn_W_r",
            "L1_attn_W_k", "L1_attn_W_v", "L1_attn_W_g", "L1_attn_W_o", "L2_xattn_w_in", "L2_xattn_wp_w1",
            "L2_xattn_wp_w2", "L2_xattn_w_out", "L3_attn_Wq", "L3_attn_Wk", "L3_attn_Wv"]
    for k, v in a.items():
        out[k] = v.T if k in flip else v
    out["ctx"] = a["ctx_1024"][0]
    out["ctxT"] = a["ctx_1024"][0].T
    out["L0_xattn_Wq"] = halves_together(a["L0_xattn_Wq"])
    out["L0_xattn_Wk"] = halves_together(a["L0_xattn_Wkv"][:, :512])
    out["L0_xattn_Wv"] = a["L0_xattn_Wkv"][:, 512:]
    out["mask_row"] = a["mask_BxS2_ff1"].reshape(-1, P)
    out["mask_qk"] = a["mask_BxSxS2_bk0"][0]
    for k in ("L0_attn_conv_w", "L2_attn_W_conv"):
        out[k] = a[k][:, 0, :]
    for k in ("k", "v", "r", "g"):
        out[f"L1_attn_time_mix_{k}"] = a[f"L1_attn_time_mix_{k}"].reshape(-1)
    for k in ("x", "ctx_1024", "mask_BxS2_ff1", "mask_BxSxS2_bk0", "L0_xattn_Wkv"):
        out.pop(k, None)
    out["x_in"] = a["x"][0]
    return {k: np.ascontiguousarray(v) for k, v in out.items()}


def program(nc, A, x_name, y_name, layers):
    R = Residents()
    keys = A["ctx"].shape[0]
    R.keys = keys
    with ExitStack() as memory:
        def sb(name, shape, dt=F32):
            return memory.enter_context(nc.sbuf_tensor(name, shape, dt))
        R.x = sb("tokens", [P, DIM])
        R.ident = sb("ident", [P, P])
        R.count = sb("count", [P, 32])
        R.count8 = sb("count8", [P, 8])
        R.idx_down = sb("idx_down", [P, 8])
        R.nT = nc.dram_tensor("scratch_nT", (DC, P, keys), F32, kind="Internal").ap()
        R.KT = nc.dram_tensor("scratch_KT", (4, P, keys), F32, kind="Internal").ap()
        loaded = memory.enter_context(nc.semaphore("loaded"))
        counted = memory.enter_context(nc.semaphore("counted"))
        stored = memory.enter_context(nc.semaphore("stored"))
        with nc.Block() as block:
            @block.sync
            def _(sp):
                sp.dma_start(R.x[:, :], A[x_name]).then_inc(loaded, 16)
                sp.dma_start(R.ident[:, :], A["c_ident"]).then_inc(loaded, 16)
                sp.dma_start(R.count[:, :], A["c_count"]).then_inc(loaded, 16)

            @block.vector
            def _(dve):
                dve.wait_ge(loaded, 48)
                dve.tensor_scalar(R.count8[:, :], R.count[:, 0:8], 8.0, None, ALU.mult)
                dve.tensor_scalar(R.idx_down[:, :], R.count[:, 0:8], -1.0, 8.0, ALU.mult, ALU.add)
        ctx_norm(nc, A, R)
        for layer in layers:
            LAYERS[layer](nc, A, R)
        with nc.Block() as block:
            @block.sync
            def _(sp):
                sp.dma_start(A[y_name], R.x[:, :]).then_inc(stored, 16)
                sp.wait_ge(stored, 16)


LAYERS = {
    "l0_xattn": l0_xattn, "l0_attn": l0_attn, "l0_ffn": l0_ffn,
    "l1_xattn": l1_xattn, "l1_attn": l1_attn, "l1_ffn": l1_ffn,
    "l2_xattn": l2_xattn, "l2_attn": l2_attn, "l2_ffn": l2_ffn,
    "l3_xattn": l3_xattn, "l3_attn": l3_attn, "l3_ffn": l3_ffn,
}



def kernel(**inputs):
    import concourse.bacc as bacc
    from concourse.bass_utils import run_bass_kernel_spmd

    nc = bacc.Bacc("TRN2", target_bir_lowering=False, num_devices=1)
    arrays = layout(inputs)
    A = {name: nc.dram_tensor(name, a.shape, mybir.dt.from_np(a.dtype), kind="ExternalInput").ap()
         for name, a in arrays.items()}
    A["x_out"] = nc.dram_tensor("x_out", (P, DIM), F32, kind="ExternalOutput").ap()
    program(nc, A, "x_in", "x_out", list(LAYERS))
    result = run_bass_kernel_spmd(nc, [arrays], core_ids=[0])
    return result.results[0]["x_out"].reshape(1, P, DIM)
```

```python
from contextlib import ExitStack

import numpy as np

import concourse.bass as bass
from concourse import mybir

P = 128
DIM = 256
DC = DIM // P
BANK = 512
EPS = 1e-5

ALU = mybir.AluOpType
ACT = mybir.ActivationFunctionType
AX = mybir.AxisListType
F32 = mybir.dt.float32
BF16 = mybir.dt.bfloat16
U8 = mybir.dt.uint8

MAX_CHUNK = 448
TILES = 7
CHUNK = TILES * P
MASK_BIG = 952.0 * 2 ** 20


class Stage:

    def __init__(self, nc, name):
        self.nc, self.name = nc, name
        self.memory, self.sems, self.unstarted = ExitStack(), {}, []

    def __enter__(self):
        self.memory.__enter__()
        return self

    def sb(self, name, shape, dt=F32):
        return self.memory.enter_context(self.nc.sbuf_tensor(f"{self.name}_{name}", shape, dt))

    def psum(self, name, banks=1):
        shape = [P, BANK] if banks == 1 else [P, banks, BANK]
        return self.memory.enter_context(self.nc.psum_tensor(f"{self.name}_{name}", shape, F32))

    def sem(self, name):
        if name not in self.sems:
            self.sems[name] = self.memory.enter_context(self.nc.semaphore(f"{self.name}_{name}"))
        return self.sems[name]

    def counted(self, name):
        if name not in self.sems:
            self.unstarted.append(self.sem(name))
        return self.sems[name]

    def __exit__(self, *e):
        if e[0] is None:
            for s in self.sems.values():
                self.nc.gpsimd.sem_clear(s)
            self.nc.all_engine_barrier()
        return self.memory.__exit__(*e)


def start_counts(eng, S):
    for s in S.unstarted:
        eng.sem_inc(s, 1)
    S.unstarted = []


def after(eng, sem, n):
    eng.wait_ge(sem, n + 1)


class Link:

    def __init__(self, eng, sem):
        self.eng, self.sem, self.n = eng, sem, 0

    def __call__(self, ins):
        self.n += 1
        ins.then_inc(self.sem, 1)
        self.eng.wait_ge(self.sem, self.n)


class Loads:

    def __init__(self, sem):
        self.sem, self.total = sem, 0

    def __call__(self, ins):
        ins.then_inc(self.sem, 16)
        self.total += 16



def norm_vector(dve, link, S, tag, x, xn, w, rows=P):
    link(dve.bn_stats(w[:rows, 0:6], x))
    link(dve.bn_aggr(w[:rows, 6:8], w[:rows, 0:6]))
    dve.tensor_scalar(w[:rows, 8:9], w[:rows, 7:8], EPS, None, ALU.add).then_inc(S.sem(tag + "_var"), 1)
    dve.wait_ge(S.sem(tag + "_std"), 1)
    link(dve.reciprocal(w[:rows, 10:11], w[:rows, 9:10]))
    dve.tensor_scalar(xn, x, w[:rows, 6:7], w[:rows, 10:11], ALU.subtract, ALU.mult).then_inc(
        S.sem(tag + "_xn"), 1)
    dve.wait_ge(S.sem(tag + "_xn"), 1)


def norm_scalar(act, S, tag, w, rows=P):
    act.wait_ge(S.sem(tag + "_var"), 1)
    act.activation(w[:rows, 9:10], w[:rows, 8:9], ACT.Sqrt).then_inc(S.sem(tag + "_std"), 1)


def turn_tensor(pe, S, tag, xn, ps, ident, ready=None):
    pe.wait_ge(S.sem(ready or tag + "_xn"), 1)
    for c in range(DC):
        last = pe.transpose(ps[:, c * P:(c + 1) * P], xn[:, c * P:(c + 1) * P], ident[:, :])
    last.then_inc(S.sem(tag + "_turned"), 1)


def turn_vector(dve, S, tag, xT, ps):
    dve.wait_ge(S.sem(tag + "_turned"), 1)
    dve.tensor_copy(xT[:, :, :], ps[:, 0:DIM].rearrange("p (c t) -> p c t", c=DC)).then_inc(
        S.sem(tag + "_xT"), 1)
    dve.wait_ge(S.sem(tag + "_xT"), 1)


def by_rows(w):
    return w.rearrange("(c p) n -> p c n", p=P)


def column(v):
    return v.rearrange("(c p) -> p c", p=P)


def first_of_max(dve, link, onehot, vals, top, tmp, idx_down):
    link(dve.tensor_reduce(top, vals, AX.X, ALU.max))
    link(dve.tensor_scalar(tmp, vals, top, None, ALU.is_equal))
    link(dve.tensor_tensor(tmp, tmp, idx_down, ALU.mult))
    link(dve.tensor_reduce(onehot[:, 0:1], tmp, AX.X, ALU.max))
    link(dve.tensor_scalar(onehot[:, 8:9], onehot[:, 0:1], 0.0, None, ALU.add))
    link(dve.tensor_scalar(onehot[:, 0:8], tmp, onehot[:, 8:9], None, ALU.is_equal))


def softmax8_vector(dve, link, S, tag, logits, probs, w):
    link(dve.tensor_reduce(w[:, 0:1], logits, AX.X, ALU.max))
    dve.tensor_scalar(probs, logits, w[:, 0:1], None, ALU.subtract).then_inc(S.sem(tag + "_shifted"), 1)
    dve.wait_ge(S.sem(tag + "_exp"), 1)
    link(dve.reciprocal(w[:, 2:3], w[:, 1:2]))
    link(dve.tensor_scalar(probs, probs, w[:, 2:3], None, ALU.mult))


def softmax8_scalar(act, S, tag, probs, w):
    act.wait_ge(S.sem(tag + "_shifted"), 1)
    act.activation(probs, probs, ACT.Exp, accum_out=w[:, 1:2]).then_inc(S.sem(tag + "_exp"), 1)


def l3_attn(nc, A, R):
    H, HD = 16, 16
    with Stage(nc, "l3a") as S:
        w = S.sb("w", [P, DC, 3 * DIM])
        bias = S.sb("bias", [P, 3 * DIM])
        xn, xT, nw = S.sb("xn", [P, DIM]), S.sb("xT", [P, DC, P]), S.sb("nw", [P, 16])
        qkv = S.sb("qkv", [P, 3 * DIM])
        qk, s, e, top = S.sb("qk", [P, DIM]), S.sb("s", [P, H]), S.sb("e", [P, H]), S.sb("top", [P, H])
        pt, pqk, pv = S.psum("pt"), S.psum("pqk"), S.psum("pv")
        loads = Loads(S.sem("weights"))
        block = S.nc.Block()
        with block as block:
            @block.sync
            def _(sp):
                for n, name in enumerate(("Wq", "Wk", "Wv")):
                    loads(sp.dma_start(w[:, :, n * DIM:(n + 1) * DIM], by_rows(A[f"L3_attn_{name}"])))
                for n, name in enumerate(("bq", "bk", "bv")):
                    loads(sp.dma_start(bias[:, n * DIM:(n + 1) * DIM],
                                       A[f"L3_attn_{name}"].partition_broadcast(P)))

            @block.vector
            def _(dve):
                link = Link(dve, S.sem("dve_link"))
                norm_vector(dve, link, S, "n", R.x[:, :], xn[:, :], nw)
                turn_vector(dve, S, "n", xT, pt)
                dve.wait_ge(S.sem("weights"), loads.total)
                dve.wait_ge(S.sem("projected"), 1)
                link(dve.tensor_tensor(qkv[:, 0:2 * DIM], pqk[:, :], bias[:, 0:2 * DIM], ALU.add))
                link(dve.tensor_tensor(qkv[:, 2 * DIM:], pv[:, 0:DIM], bias[:, 2 * DIM:], ALU.add))
                link(dve.tensor_tensor(qk[:, :], qkv[:, 0:DIM], qkv[:, DIM:2 * DIM], ALU.mult))
                link(dve.tensor_reduce(s[:, :], qk[:, :].rearrange("p (h d) -> p h d", h=H), AX.X, ALU.add))
                link(dve.tensor_scalar(s[:, :], s[:, :], HD ** -0.5, None, ALU.mult))
                link(dve.tensor_reduce(top[:, :], s[:, :].unsqueeze(2), AX.X, ALU.max))
                dve.tensor_tensor(e[:, :], s[:, :], top[:, :], ALU.subtract).then_inc(S.sem("shifted"), 1)
                dve.wait_ge(S.sem("exp"), 1)
                link(dve.tensor_scalar(s[:, :], e[:, :], 1.0, None, ALU.add))
                link(dve.reciprocal(s[:, :], s[:, :]))
                link(dve.tensor_tensor(e[:, :], e[:, :], s[:, :], ALU.mult))
                link(dve.tensor_tensor(qk[:, :].rearrange("p (h d) -> p h d", h=H),
                                       qkv[:, 2 * DIM:].rearrange("p (h d) -> p h d", h=H),
                                       e[:, :].unsqueeze(2).broadcast_to([P, H, HD]), ALU.mult))
                link(dve.tensor_tensor(R.x[:, :], R.x[:, :], qk[:, :], ALU.add))

            @block.scalar
            def _(act):
                norm_scalar(act, S, "n", nw)
                act.wait_ge(S.sem("shifted"), 1)
                act.activation(e[:, :], e[:, :], ACT.Exp).then_inc(S.sem("exp"), 1)

            @block.tensor
            def _(pe):
                turn_tensor(pe, S, "n", xn, pt, R.ident)
                pe.wait_ge(S.sem("weights"), loads.total)
                pe.wait_ge(S.sem("n_xT"), 1)
                for c in range(DC):
                    pe.matmul(pqk[:, :], xT[:, c, :], w[:, c, 0:2 * DIM], start=(c == 0), stop=(c == DC - 1))
                for c in range(DC):
                    last = pe.matmul(pv[:, 0:DIM], xT[:, c, :], w[:, c, 2 * DIM:], start=(c == 0),
                                     stop=(c == DC - 1))
                last.then_inc(S.sem("projected"), 1)


def l3_ffn(nc, A, R):
    E, FF = 8, 1024
    FC = FF // P
    LIM = 24
    with Stage(nc, "l3f") as S:
        w1 = [S.sb(f"w1_{b}", [P, DC, FF]) for b in range(2)]
        w2 = [S.sb(f"w2_{b}", [P, FC, DIM]) for b in range(2)]
        b1 = S.sb("b1", [P, E, FC])
        b1r = S.sb("b1r", [E * FC, P])
        b2 = S.sb("b2", [E, DIM])
        xn, xT, nw = S.sb("xn", [P, DIM]), S.sb("xT", [P, DC, P]), S.sb("nw", [P, 16])
        steps = S.sb("steps", [P, 2, LIM])
        r = S.sb("r", [P, 8])
        we, wt = S.sb("we", [P, E]), S.sb("wt", [P, E])
        weT = S.sb("weT", [E, P])
        hT = [S.sb(f"hT{b}", [P, FC, P]) for b in range(2)]
        acc = S.sb("acc", [P, DIM])
        pt, pm = S.psum("pt"), S.psum("pm")
        ph = [S.psum(f"ph{b}", 2) for b in range(2)]
        py = [S.psum(f"py{b}") for b in range(2)]
        loads = Loads(S.sem("small"))
        with S.nc.Block() as block:
            @block.sync
            def _(sp):
                loads(sp.dma_start(b1r[:, :], A["L3_ffn_b1"].rearrange("e (f p) -> (e f) p", p=P)))
                loads(sp.dma_start(b2[:, :], A["L3_ffn_b2"]))
                with sp.Fori(0, E // 2) as i:
                    for b in range(2):
                        e = 2 * i + b
                        after(sp, S.counted(f"used{b}"), i)
                        sp.dma_start(w1[b][:, :, :], A["L3_ffn_W1"][bass.ds(e, 1)].rearrange(
                            "e (c p) n -> p (e c) n", p=P)).then_inc(S.counted(f"w1_{b}"), 16)
                        sp.dma_start(w2[b][:, :, :], A["L3_ffn_W2"][bass.ds(e, 1)].rearrange(
                            "e (c p) n -> p (e c) n", p=P)).then_inc(S.counted(f"w2_{b}"), 16)

            @block.vector
            def _(dve):
                link = Link(dve, S.sem("dve_link"))
                norm_vector(dve, link, S, "n", R.x[:, :], xn[:, :], nw)
                turn_vector(dve, S, "n", xT, pt)
                link(dve.tensor_tensor(r[:, 0:1], xn[:, 0:1], xn[:, 1:2], ALU.add))
                link(dve.tensor_scalar(r[:, 1:2], r[:, 0:1], -1.0, None, ALU.mult))
                for side in range(2):
                    link(dve.tensor_scalar(steps[:, side, :], R.count[:, 1:LIM + 1],
                                           r[:, side:side + 1], None, ALU.is_le))
                    link(dve.tensor_reduce(r[:, 2 + side:3 + side], steps[:, side, :], AX.X, ALU.add))
                link(dve.tensor_tensor(r[:, 4:5], r[:, 2:3], r[:, 3:4], ALU.subtract))
                link(dve.tensor_scalar(r[:, 4:5], r[:, 4:5], float(LIM), None, ALU.add))
                link(dve.tensor_scalar(steps[:, 0, 0:2 * LIM // 8], R.count8[:, 1:2 * LIM // 8 + 1],
                                       r[:, 4:5], None, ALU.is_le))
                link(dve.tensor_reduce(r[:, 5:6], steps[:, 0, 0:2 * LIM // 8], AX.X, ALU.add))
                link(dve.tensor_scalar(r[:, 5:6], r[:, 5:6], -8.0, r[:, 4:5], ALU.mult, ALU.add))
                link(dve.tensor_scalar(we[:, :], R.count[:, 0:E], r[:, 5:6], None, ALU.subtract))
                link(dve.tensor_scalar(wt[:, :], we[:, :], 0.0, 0.5, ALU.is_equal, ALU.mult))
                for off in (1.0, -7.0):
                    link(dve.tensor_scalar(acc[:, 0:E], we[:, :], off, 0.5, ALU.is_equal, ALU.mult))
                    link(dve.tensor_tensor(wt[:, :], wt[:, :], acc[:, 0:E], ALU.add))
                dve.sem_inc(S.sem("weights_of_experts"), 1)
                dve.wait_ge(S.sem("b1_turned"), 1)
                dve.tensor_copy(b1[:, :, :], pm[:, 0:E * FC].rearrange("p (e f) -> p e f", e=E)).then_inc(
                    S.sem("b1_ready"), 1)
                dve.wait_ge(S.sem("we_turned"), 1)
                dve.tensor_copy(weT[:, :], pm[0:E, P:2 * P]).then_inc(S.sem("weT_ready"), 1)
                dve.wait_ge(S.sem("b2_mixed"), 1)
                link(dve.tensor_tensor(acc[:, :], pm[:, DIM:2 * DIM], R.x[:, :], ALU.add))
                dve.sem_inc(S.counted("acc_link"), 1)
                with dve.Fori(0, E // 2) as i:
                    for b in range(2):
                        after(dve, S.counted(f"y{b}"), i + 1)
                        after(dve, S.counted("acc_link"), i * 2 + b + 1)
                        dve.scalar_tensor_tensor(acc[:, :], py[b][:, 0:DIM], wt[:, bass.ds(i * 2 + b, 1)],
                                                 acc[:, :], ALU.mult, ALU.add).then_inc(
                            S.counted("acc_link"), 1)
                after(dve, S.counted("acc_link"), E + 1)
                dve.tensor_copy(R.x[:, :], acc[:, :])

            @block.scalar
            def _(act):
                norm_scalar(act, S, "n", nw)
                act.wait_ge(S.sem("b1_ready"), 1)
                with act.Fori(0, E // 2) as i:
                    for b in range(2):
                        act.wait_ge(S.sem("b1_ready"), 1)
                        after(act, S.counted(f"h{b}"), i + 1)
                        after(act, S.counted(f"y{b}"), i)
                        for f in range(FC):
                            last = act.activation(hT[b][:, f, :], ph[b][:, f // 4, (f % 4) * P:(f % 4 + 1) * P],
                                                  ACT.Relu, bias=b1[:, bass.ds(i * 2 + b, 1), f])
                        last.then_inc(S.counted(f"hT{b}"), 1)

            @block.tensor
            def _(pe):
                turn_tensor(pe, S, "n", xn, pt, R.ident)
                pe.wait_ge(S.sem("small"), loads.total)
                pe.transpose(pm[:, 0:E * FC], b1r[:, :], R.ident[0:E * FC, 0:E * FC]).then_inc(
                    S.sem("b1_turned"), 1)
                pe.wait_ge(S.sem("weights_of_experts"), 1)
                pe.wait_ge(S.sem("b1_ready"), 1)
                pe.transpose(pm[0:E, P:2 * P], wt[:, :], R.ident[:, :]).then_inc(S.sem("we_turned"), 1)
                pe.wait_ge(S.sem("weT_ready"), 1)
                pe.matmul(pm[:, DIM:2 * DIM], weT[:, :], b2[:, :], start=True, stop=True).then_inc(
                    S.sem("b2_mixed"), 1)
                pe.wait_ge(S.sem("n_xT"), 1)
                with pe.Fori(0, E // 2) as i:
                    for b in range(2):
                        after(pe, S.counted(f"w1_{b}"), (i + 1) * 16)
                        after(pe, S.counted(f"hT{b}"), i)
                        for f in range(FC):
                            for c in range(DC):
                                last = pe.matmul(ph[b][:, f // 4, (f % 4) * P:(f % 4 + 1) * P],
                                                 w1[b][:, c, f * P:(f + 1) * P], xT[:, c, :],
                                                 start=(c == 0), stop=(c == DC - 1))
                        last.then_inc(S.counted(f"h{b}"), 1)
                    for b in range(2):
                        after(pe, S.counted(f"w2_{b}"), (i + 1) * 16)
                        after(pe, S.counted(f"hT{b}"), i + 1)
                        after(pe, S.counted("acc_link"), i * 2 + b)
                        for f in range(FC):
                            last = pe.matmul(py[b][:, 0:DIM], hT[b][:, f, :], w2[b][:, f, :],
                                             start=(f == 0), stop=(f == FC - 1))
                        last.then_inc(S.counted(f"y{b}"), 1)
                        after(pe, S.counted(f"y{b}"), i + 1)
                        pe.sem_inc(S.counted(f"used{b}"), 1)

            @block.gpsimd
            def _(pool):
                start_counts(pool, S)



def ctx_norm(nc, A, R):
    steps = R.keys // CHUNK // 2
    rows = A["ctx"].rearrange("(n t p) d -> n p t d", t=TILES, p=P)
    turned = R.nT.rearrange("c p (n k) -> n p c k", k=CHUNK)
    with Stage(nc, "norm") as S:
        raw = [S.sb(f"raw{b}", [P, TILES, DIM]) for b in range(2)]
        xn = [S.sb(f"xn{b}", [P, TILES, DIM]) for b in range(2)]
        out = [S.sb(f"out{b}", [P, DC, CHUNK]) for b in range(2)]
        st = [S.sb(f"st{b}", [P, TILES, 6]) for b in range(2)]
        mv = [S.sb(f"mv{b}", [P, TILES, 2]) for b in range(2)]
        ve = [S.sb(f"ve{b}", [P, TILES]) for b in range(2)]
        sd = [S.sb(f"sd{b}", [P, TILES]) for b in range(2)]
        pt = [S.psum(f"pt{b}", 4) for b in range(2)]
        with S.nc.Block() as block:
            @block.sync
            def _(sp):
                def load(b, i):
                    sp.dma_start(raw[b][:, :, :], rows[bass.ds(i * 2 + b, 1)].squeeze(0)).then_inc(
                        S.counted(f"raw{b}"), 16)

                def store(b, i):
                    after(sp, S.counted(f"out{b}"), i + 1)
                    sp.dma_start(turned[bass.ds(i * 2 + b, 1)].squeeze(0), out[b][:, :, :]).then_inc(
                        S.counted(f"stored{b}"), 16)

                load(0, 0)
                load(1, 0)
                with sp.Fori(0, steps - 1) as i:
                    for b in range(2):
                        after(sp, S.counted(f"normed{b}"), i + 1)
                        load(b, i + 1)
                    store(0, i)
                    store(1, i)
                for b in range(2):
                    store(b, steps - 1)
                for b in range(2):
                    after(sp, S.counted(f"stored{b}"), steps * 16)

            @block.vector
            def _(dve):
                def stats(b, i):
                    after(dve, S.counted(f"raw{b}"), (i + 1) * 16)
                    for t in range(TILES):
                        last = dve.bn_stats(st[b][:, t, :], raw[b][:, t, :])
                    last.then_inc(S.counted(f"st{b}"), 1)
                    after(dve, S.counted(f"st{b}"), i + 1)
                    dve.sem_inc(S.sem("stats_seen"), 1)
                    for t in range(TILES):
                        last = dve.bn_aggr(mv[b][:, t, :], st[b][:, t, :])
                    last.then_inc(S.counted(f"mv{b}"), 1)
                    after(dve, S.counted(f"mv{b}"), i + 1)
                    dve.tensor_scalar(ve[b][:, :], mv[b][:, :, 1], EPS, None, ALU.add).then_inc(
                        S.counted(f"ve{b}"), 1)

                def scale(b, i):
                    after(dve, S.counted(f"sd{b}"), i + 1)
                    dve.reciprocal(sd[b][:, :], sd[b][:, :]).then_inc(S.counted(f"rs{b}"), 1)
                    after(dve, S.counted(f"rs{b}"), i + 1)
                    after(dve, S.counted(f"turned{b}"), i)
                    for t in range(TILES):
                        last = dve.tensor_scalar(xn[b][:, t, :], raw[b][:, t, :], mv[b][:, t, 0:1],
                                                 sd[b][:, t:t + 1], ALU.subtract, ALU.mult)
                    last.then_inc(S.counted(f"normed{b}"), 1)

                with dve.Fori(0, steps) as i:
                    stats(0, i)
                    stats(1, i)
                    scale(0, i)
                    scale(1, i)

            @block.scalar
            def _(act):
                with act.Fori(0, steps) as i:
                    for b in range(2):
                        after(act, S.counted(f"ve{b}"), i + 1)
                        act.activation(sd[b][:, :], ve[b][:, :], ACT.Sqrt).then_inc(S.counted(f"sd{b}"), 1)
                    for b in range(2):
                        after(act, S.counted(f"turned{b}"), i + 1)
                        after(act, S.counted(f"stored{b}"), i * 16)
                        for c in range(DC):
                            act.activation(out[b][:, c, 0:BANK], pt[b][:, 2 * c, :], ACT.Copy)
                            last = act.activation(out[b][:, c, BANK:CHUNK], pt[b][:, 2 * c + 1, 0:CHUNK - BANK],
                                                  ACT.Copy)
                        last.then_inc(S.counted(f"out{b}"), 1)

            @block.tensor
            def _(pe):
                with pe.Fori(0, steps) as i:
                    for b in range(2):
                        after(pe, S.counted(f"normed{b}"), i + 1)
                        after(pe, S.counted(f"out{b}"), i)
                        for t in range(TILES):
                            for c in range(DC):
                                last = pe.transpose(pt[b][:, 2 * c + t // 4, (t % 4) * P:(t % 4 + 1) * P],
                                                    xn[b][:, t, c * P:(c + 1) * P], R.ident[:, :])
                        last.then_inc(S.counted(f"turned{b}"), 1)

            @block.gpsimd
            def _(pool):
                start_counts(pool, S)


def run_ahead(eng, steps, first, both, second):
    first(0, 0)
    with eng.Fori(0, steps - 1) as i:
        both((1, i), (0, i))
        both((0, i + 1), (1, i))
    both((1, steps - 1), (0, steps - 1))
    second(1, steps - 1)


def find_maximum(nc, S, A, R, heads, kc, per_chunk, qb, source, project, w_k, bias_k, top, masks, split):
    nc = S.nc
    steps = R.keys // MAX_CHUNK // 2
    src = source.rearrange("c p (n k) -> n p c k", k=MAX_CHUNK)
    rope = project == "rope"
    mem = ExitStack()
    with mem:
        def sb(name, shape, dt=F32):
            return mem.enter_context(nc.sbuf_tensor(f"{S.name}_max_{name}", shape, dt))
        xin = [sb(f"xin{b}", [P, DC, MAX_CHUNK]) for b in range(2)]
        kf = [sb(f"kf{b}", [P, kc, MAX_CHUNK]) for b in range(2)] if project else xin
        n_parts = 3 if split else 1
        kp = [sb(f"kp{b}", [P, n_parts, kc, MAX_CHUNK], BF16) for b in range(2)]
        if split:
            rest = [sb(f"rest{b}", [P, kc, MAX_CHUNK]) for b in range(2)]
        red = [sb(f"red{b}", [P, heads]) for b in range(2)]
        if rope:
            cs = [sb(f"cs{b}", [P, 2, MAX_CHUNK]) for b in range(2)]
            ks = [sb(f"ks{b}", [P, kc, MAX_CHUNK]) for b in range(2)]
            kt = [sb(f"kt{b}", [P, kc, MAX_CHUNK]) for b in range(2)]
            cos = A["c_cos"].rearrange("p (n k) -> n p k", k=MAX_CHUNK)
            sin = A["c_sin"].rearrange("p (n k) -> n p k", k=MAX_CHUNK)
        kt_dram = (R.KS if split else R.KT[0:kc]).rearrange("c p (n k) -> n p c k", k=MAX_CHUNK)
        if masks == "query_key":
            mq = [sb(f"mq{b}", [P, MAX_CHUNK], U8) for b in range(2)]
            mb = [sb(f"mb{b}", [P, MAX_CHUNK], BF16) for b in range(2)]
            one = sb("one", [P, 1])
            mask_src = A["mask_qk"].rearrange("q (n k) -> n q k", k=MAX_CHUNK)
        n_ps = 2 if project else 4
        psc = [mem.enter_context(nc.psum_tensor(f"{S.name}_max_ps{u}", [P, 2, BANK], F32)) for u in range(n_ps)]
        pk = [mem.enter_context(nc.psum_tensor(f"{S.name}_max_pk{c}", [P, BANK], F32)) for c in range(kc if project else 0)]
        sem = lambda n: S.counted("max_" + n)
        pairs = heads // 2
        per_piece = pairs // kc
        per = pairs // n_ps

        def pair_counts(b, i, pr):
            return pr % n_ps, i * (2 * per) + b * per + pr // n_ps

        with nc.Block() as block:
            @block.sync
            def _(sp):
                def load(b, i):
                    sp.dma_start(xin[b][:, :, :], src[bass.ds(i * 2 + b, 1)].squeeze(0)).then_inc(sem(f"xin{b}"), 16)
                    if rope:
                        sp.dma_start(cs[b][:, 0, :], cos[bass.ds(i * 2 + b, 1)].squeeze(0)).then_inc(
                            sem(f"cs{b}"), 16)
                        sp.dma_start(cs[b][:, 1, :], sin[bass.ds(i * 2 + b, 1)].squeeze(0)).then_inc(
                            sem(f"cs{b}"), 16)
                    if masks == "query_key":
                        sp.dma_start(mq[b][:, :], mask_src[bass.ds(i * 2 + b, 1)].squeeze(0)).then_inc(
                            sem(f"mq{b}"), 16)

                def spill(b, i):
                    if split:
                        after(sp, sem(f"low{b}"), i + 1)
                        sp.dma_start(kt_dram[bass.ds(i * 2 + b, 1)].squeeze(0),
                                     kp[b][:, :, :, :].rearrange("p s c k -> p (s c) k")).then_inc(
                            sem(f"spilled{b}"), 16)
                    else:
                        after(sp, sem(f"kf{b}"), (i + 1) * kc)
                        sp.dma_start(kt_dram[bass.ds(i * 2 + b, 1)].squeeze(0), kf[b][:, :, :]).then_inc(
                            sem(f"spilled{b}"), 16)

                for b in range(2):
                    load(b, 0)
                with sp.Fori(0, steps - 1) as i:
                    for b in range(2):
                        if project:
                            after(sp, sem(f"xin_used{b}"), i + 1)
                        else:
                            after(sp, sem(f"rest{b}"), i + 1)
                            after(sp, sem(f"kb{b}"), (i + 1) * kc)
                        if rope:
                            after(sp, sem(f"turned{b}"), (i + 1) * kc)
                        if masks == "query_key":
                            after(sp, sem(f"mb{b}"), i + 1)
                        load(b, i + 1)
                        spill(b, i)
                for b in range(2):
                    spill(b, steps - 1)
                for b in range(2):
                    after(sp, sem(f"spilled{b}"), steps * 16)

            @block.vector
            def _(dve):
                dve.memset(top[:, :], -3.0e38).then_inc(sem("top"), 1)
                if masks == "query_key":
                    dve.memset(one[:, :], 1.0).then_inc(S.sem("one"), 1)

                def bias_cos(b, i, c):
                    if c == 0:
                        after(dve, sem(f"cs{b}"), (i + 1) * 32)
                        after(dve, sem(f"kf{b}"), i * kc)
                    after(dve, sem(f"k_proj{c}"), i * 2 + b + 1)
                    dve.scalar_tensor_tensor(kt[b][:, c, :], pk[c][:, 0:MAX_CHUNK], bias_k[:, c:c + 1],
                                             cs[b][:, 0, :], ALU.add, ALU.mult).then_inc(sem(f"k_read{c}"), 1)

                def times_sin(b, i, c):
                    after(dve, sem(f"k_swapped{c}"), i * 2 + b + 1)
                    dve.tensor_tensor(ks[b][:, c, :], ks[b][:, c, :], cs[b][:, 1, :], ALU.mult).then_inc(
                        sem(f"turned{b}"), 1)

                def turn(b, i):
                    for c in range(kc):
                        bias_cos(b, i, c)
                        times_sin(b, i, c)

                def maximum(b, i, pr):
                    u, j = pair_counts(b, i, pr)
                    after(dve, sem(f"scores{u}"), j + 1)
                    dve.tensor_reduce(red[b][:, 2 * pr:2 * pr + 2], psc[u][:, :, 0:MAX_CHUNK], AX.X,
                                      ALU.max).then_inc(sem(f"scores_read{u}"), 1)

                def merge(b, i):
                    for u in range(n_ps):
                        after(dve, sem(f"scores_read{u}"), i * (2 * per) + (b + 1) * per)
                    after(dve, sem("top"), i * 2 + b + 1)
                    dve.tensor_tensor(top[:, :], top[:, :], red[b][:, :], ALU.max).then_inc(sem("top"), 1)
                    after(dve, sem("top"), i * 2 + b + 2)

                def reduce(b, i):
                    for pr in range(pairs):
                        maximum(b, i, pr)
                    merge(b, i)

                def turn_and_reduce(ahead, now):
                    for c in range(kc):
                        bias_cos(*ahead, c)
                        maximum(*now, c)
                        times_sin(*ahead, c)
                    merge(*now)

                if rope:
                    run_ahead(dve, steps, turn, turn_and_reduce, reduce)
                else:
                    with dve.Fori(0, steps) as i:
                        reduce(0, i)
                        reduce(1, i)

            @block.scalar
            def _(act):
                def evacuate(b, i, c):
                    if rope:
                        if c == 0:
                            after(act, sem(f"turned{b}"), i * kc)
                            after(act, sem(f"kf{b}"), i * kc)
                        after(act, sem(f"k_read{c}"), i * 2 + b + 1)
                        act.activation(ks[b][0:64, c, :], pk[c][64:P, 0:MAX_CHUNK], ACT.Identity,
                                       scale=-1.0, bias=R.nbias_k[0:64, c:c + 1])
                        act.activation(ks[b][64:P, c, :], pk[c][0:64, 0:MAX_CHUNK], ACT.Identity,
                                       bias=R.nbias_k[64:P, c:c + 1]).then_inc(sem(f"k_swapped{c}"), 1)
                    else:
                        if c == 0:
                            after(act, sem(f"rest{b}"), i)
                        after(act, sem(f"k_proj{c}"), i * 2 + b + 1)
                        act.activation(kf[b][:, c, :], pk[c][:, 0:MAX_CHUNK], ACT.Identity,
                                       bias=bias_k[:, c:c + 1]).then_inc(sem(f"k_swapped{c}"), 1)
                        after(act, sem(f"k_swapped{c}"), i * 2 + b + 1)

                def copy(b, i, c):
                    if c == 0:
                        after(act, sem(f"scored{b}"), i)
                        if split:
                            after(act, sem(f"spilled{b}"), i * 16)
                        if not project:
                            after(act, sem(f"xin{b}"), (i + 1) * 16)
                    if rope:
                        after(act, sem(f"kf{b}"), i * kc + c + 1)
                    act.activation(kp[b][:, 0, c, :], kf[b][:, c, :], ACT.Copy).then_inc(sem(f"kb{b}"), 1)

                if masks == "query_key":
                    act.wait_ge(S.sem("one"), 1)
                with act.Fori(0, steps) as i:
                    for b in range(2):
                        if rope:
                            for c in range(kc):
                                evacuate(b, i, c)
                                if c:
                                    copy(b, i, c - 1)
                            copy(b, i, kc - 1)
                        else:
                            for c in range(kc):
                                if project:
                                    evacuate(b, i, c)
                                copy(b, i, c)
                        if masks == "query_key":
                            after(act, sem(f"mq{b}"), (i + 1) * 16)
                            act.activation(mb[b][:, :], mq[b][:, :], ACT.Identity, scale=-1.0,
                                           bias=one[:, :]).then_inc(sem(f"mb{b}"), 1)
                        if split:
                            after(act, sem(f"rest{b}"), i + 1)
                            act.activation(kp[b][:, 1], rest[b][:, :, :], ACT.Copy).then_inc(sem(f"mid{b}"), 1)

            @block.tensor
            def _(pe):
                def proj(b, i, c):
                    if c == 0:
                        after(pe, sem(f"xin{b}"), (i + 1) * 16)
                    after(pe, sem(f"k_swapped{c}"), i * 2 + b)
                    for d in range(DC):
                        last = pe.matmul(pk[c][:, 0:MAX_CHUNK], w_k[:, d, c * P:(c + 1) * P], xin[b][:, d, :],
                                         start=(d == 0), stop=(d == DC - 1))
                    last.then_inc(sem(f"k_proj{c}"), 1)
                    if c == kc - 1:
                        after(pe, sem(f"k_proj{c}"), i * 2 + b + 1)
                        pe.sem_inc(sem(f"xin_used{b}"), 1)

                def score(b, i, pr):
                    if pr % per_piece == 0:
                        after(pe, sem(f"kb{b}"), i * kc + pr // per_piece + 1)
                        if masks == "query_key" and pr == 0:
                            after(pe, sem(f"mb{b}"), i + 1)
                    u, j = pair_counts(b, i, pr)
                    after(pe, sem(f"scores_read{u}"), j)
                    for n in range(2):
                        h = 2 * pr + n
                        c = h // per_chunk
                        out = psc[u][:, n, 0:MAX_CHUNK]
                        last = pe.matmul(out, qb[c][:, h % per_chunk, :], kp[b][:, 0, c, :], start=True,
                                         stop=(masks is None))
                        if masks == "query_key":
                            last = pe.matmul(out, R.neg_big[:, :], mb[b][:, :], start=False, stop=True)
                        if masks == "key":
                            last = pe.matmul(out, R.ones3[:, :],
                                             R.mask3[:, bass.ds(i * (2 * MAX_CHUNK) + b * MAX_CHUNK, MAX_CHUNK)],
                                             start=False, stop=True)
                    last.then_inc(sem(f"scores{u}"), 1)
                    if pr == pairs - 1:
                        after(pe, sem(f"scores{u}"), j + 1)
                        pe.sem_inc(sem(f"scored{b}"), 1)

                def project_all(b, i):
                    for c in range(kc):
                        proj(b, i, c)

                def score_all(b, i):
                    for pr in range(pairs):
                        score(b, i, pr)

                def project_and_score(ahead, now):
                    for c in range(kc):
                        for n in range(per_piece):
                            if n == per_piece // 2:
                                proj(*ahead, c)
                            score(*now, c * per_piece + n)

                if project:
                    run_ahead(pe, steps, project_all, project_and_score, score_all)
                else:
                    with pe.Fori(0, steps) as i:
                        score_all(0, i)
                        score_all(1, i)

            @block.gpsimd
            def _(pool):
                start_counts(pool, S)
                with pool.Fori(0, steps) as i:
                    for b in range(2):
                        if rope:
                            for c in range(kc):
                                if c == 0:
                                    after(pool, sem(f"kb{b}"), i * kc)
                                    after(pool, sem(f"spilled{b}"), i * 16)
                                after(pool, sem(f"turned{b}"), i * kc + c + 1)
                                pool.tensor_tensor(kf[b][:, c, :], kt[b][:, c, :], ks[b][:, c, :],
                                                   ALU.add).then_inc(sem(f"kf{b}"), 1)
                        else:
                            after(pool, sem(f"kb{b}"), (i + 1) * kc)
                            after(pool, sem(f"low{b}"), i)
                            pool.tensor_tensor(rest[b][:, :, :], kf[b][:, :, :], kp[b][:, 0],
                                               ALU.subtract).then_inc(sem(f"rest{b}"), 1)
                            after(pool, sem(f"mid{b}"), i + 1)
                            pool.tensor_tensor(kp[b][:, 2], rest[b][:, :, :], kp[b][:, 1],
                                               ALU.subtract).then_inc(sem(f"low{b}"), 1)


def split_rows(nc, S, R, name, top, heads, m3):
    scratch = nc.dram_tensor(f"{S.name}_{name}_rows", (3, heads, P), BF16, kind="Internal").ap()
    mem = ExitStack()
    with mem:
        tT = mem.enter_context(nc.sbuf_tensor(f"{S.name}_topT", [heads, P], F32))
        parts = [mem.enter_context(nc.sbuf_tensor(f"{S.name}_part{n}", [heads, P], BF16)) for n in range(3)]
        ps = mem.enter_context(nc.psum_tensor(f"{S.name}_topps", [P, BANK], F32))
        with nc.Block() as block:
            @block.tensor
            def _(pe):
                pe.transpose(ps[0:heads, 0:P], top[:, :], R.ident[:, :]).then_inc(S.sem("top_turned"), 1)

            @block.vector
            def _(dve):
                link = Link(dve, S.sem("split_link"))
                dve.wait_ge(S.sem("top_turned"), 1)
                link(dve.tensor_scalar(tT[:, :], ps[0:heads, 0:P], -1.0, None, ALU.mult))
                for n in range(3):
                    link(dve.tensor_copy(parts[n][:, :], tT[:, :]))
                    link(dve.tensor_tensor(tT[:, :], tT[:, :], parts[n][:, :], ALU.subtract))
                dve.sem_inc(S.sem("split"), 1)

            @block.sync
            def _(sp):
                sp.wait_ge(S.sem("split"), 1)
                for n in range(3):
                    sp.dma_start(scratch[n], parts[n][:, :]).then_inc(S.sem("rows_out"), 16)
                sp.wait_ge(S.sem("rows_out"), 48)
                sp.dma_start(m3, scratch.rearrange("n h q -> n (h q)")).then_inc(S.sem("rows_in"), 16)
                sp.wait_ge(S.sem("rows_in"), 16)


PARTS_OF_K, PARTS_OF_Q = (0, 0, 0, 1, 1, 2), (0, 1, 2, 0, 1, 0)
STACK = 16 * len(PARTS_OF_K)


def parts_to_rows(eng, rows, parts, which, sem):
    for n, s in enumerate(which):
        eng.dma_start(rows[16 * n:16 * n + 16], parts[2 * s:2 * s + 2].rearrange(
            "c (h d) k -> d (c h) k", d=16)).then_inc(sem, 16)


def split_queries(nc, S, qT, scale):
    qs = S.sb("qs", [STACK + 3, 16, P], BF16)
    scratch = nc.dram_tensor(f"{S.name}_q_parts", (3 * DC, P, P), BF16, kind="Internal").ap()
    with ExitStack() as mem:
        rest = mem.enter_context(nc.sbuf_tensor(f"{S.name}_qrest", [P, DC * P], F32))
        parts = mem.enter_context(nc.sbuf_tensor(f"{S.name}_qparts", [P, 3, DC * P], BF16))
        with nc.Block() as block:
            @block.vector
            def _(dve):
                link = Link(dve, S.sem("q_split_link"))
                link(dve.tensor_scalar(rest[:, :], qT, scale, None, ALU.mult))
                for n in range(3):
                    link(dve.tensor_copy(parts[:, n, :], rest[:, :]))
                    link(dve.tensor_tensor(rest[:, :], rest[:, :], parts[:, n, :], ALU.subtract))
                dve.sem_inc(S.sem("q_split"), 1)

            @block.sync
            def _(sp):
                sp.wait_ge(S.sem("q_split"), 1)
                sp.dma_start(scratch.rearrange("c p t -> p c t"), parts[:, :, :].rearrange(
                    "p s (c t) -> p (s c) t", c=DC)).then_inc(S.sem("q_out"), 16)
                sp.wait_ge(S.sem("q_out"), 16)
                parts_to_rows(sp, qs, scratch, PARTS_OF_Q, S.sem("q_in"))
                sp.wait_ge(S.sem("q_in"), 16 * len(PARTS_OF_Q))
    return qs


def attend(nc, S, A, R, heads, kc, per_chunk, q, kt_src, v_src, w_v, bias_v, m3, masks, O, sums, last_tile=None):
    nc = S.nc
    wide = heads == 8
    vd = DIM // heads * (2 if wide else 1)
    steps = R.keys // CHUNK // 2
    octets = heads // 8
    mem = ExitStack()
    kt_src = kt_src.rearrange("c p (n k) -> n p c k" if wide else "c p (n k) -> n c p k", k=CHUNK)
    project = w_v is not None
    if project:
        v_src = v_src.rearrange("c p (n k) -> n p c k", k=CHUNK)
    else:
        v_src = v_src.rearrange("(n t p) d -> n p t d", t=TILES, p=P)
    with mem:
        def sb(name, shape, dt=F32):
            return mem.enter_context(nc.sbuf_tensor(f"{S.name}_att_{name}", shape, dt))
        kt = [sb(f"kt{b}", [P, kc, CHUNK]) if wide else sb(f"kt{b}", [STACK + 3, 16, CHUNK], BF16) for b in range(2)]
        kt_count = 16 if wide else 16 * len(PARTS_OF_K)
        vin = [sb(f"vin{b}", [P, DC, CHUNK] if project else [P, TILES, DIM]) for b in range(2)]
        if wide:
            v = [sb(f"v{b}", [P, heads, vd]) for b in range(2)]
        else:
            v = [sb(f"v{b}", [P, heads, vd + 1]) for b in range(2)]
        pt = [sb(f"pt{b}", [P, 8, P]) for b in range(2)]
        ones3 = sb("ones3", [P, P], BF16)
        zl, zr = sb("zl", [P, P]), sb("zr", [P, BANK])
        if masks == "query_key":
            mq = [sb(f"mq{b}", [P, CHUNK], U8) for b in range(2)]
            mb = [sb(f"mb{b}", [P, CHUNK], BF16) for b in range(2)]
            mask_src = A["mask_qk"].rearrange("q (n k) -> n q k", k=CHUNK)
        psc = [mem.enter_context(nc.psum_tensor(f"{S.name}_att_ps{b}", [P, 2, BANK], F32)) for b in range(2)]
        pv = [mem.enter_context(nc.psum_tensor(f"{S.name}_att_pv{b}", [P, BANK], F32)) for b in range(2)]
        sem = lambda n: S.counted("att_" + n)
        per_body = 2 * TILES
        uses = per_body * octets // 2
        vuses = per_body // 2

        def octet_counts(i, t, o):
            k = t * octets + o
            return k % 2, i * uses + k // 2

        def tile_counts(i, t):
            return t % 2, i * vuses + t // 2

        with nc.Block() as block:
            @block.sync
            def _(sp):
                if not wide:
                    for b in range(2):
                        sp.dma_start(kt[b][STACK:STACK + 3, :, :], R.ones_row.unsqueeze(0).broadcast_to(
                            [3, 16, CHUNK])).then_inc(S.sem("ones_rows"), 16)
                with sp.Fori(0, steps) as i:
                    for b in range(2):
                        n = i * 2 + b
                        after(sp, sem(f"chunk_used{b}"), i)
                        if wide:
                            sp.dma_start(kt[b][:, :, :], kt_src[bass.ds(n, 1)].squeeze(0)).then_inc(
                                sem(f"kt{b}"), 16)
                        else:
                            parts_to_rows(sp, kt[b], kt_src[bass.ds(n, 1)].squeeze(0), PARTS_OF_K, sem(f"kt{b}"))
                        if not project:
                            after(sp, sem(f"v_copied{b}"), i)
                        sp.dma_start(vin[b][:, :, :], v_src[bass.ds(n, 1)].squeeze(0)).then_inc(
                            sem(f"vin{b}"), 16)
                        if masks == "query_key":
                            after(sp, sem(f"mb{b}"), i)
                            sp.dma_start(mq[b][:, :], mask_src[bass.ds(n, 1)].squeeze(0)).then_inc(
                                sem(f"mq{b}"), 16)

            @block.vector
            def _(dve):
                dve.memset(zl[:, :], 0.0)
                dve.memset(zr[:, :], 0.0)
                if wide:
                    dve.memset(sums[:, :, :], 0.0)
                else:
                    for b in range(2):
                        dve.memset(v[b][:, :, vd:vd + 1], 1.0)
                dve.memset(ones3[:, :], 0.0).then_inc(sem("ones_zero"), 1)
                after(dve, sem("ones_zero"), 1)
                dve.memset(ones3[0:3, :], 1.0).then_inc(sem("constants"), 1)
                after(dve, sem("constants"), 1)

                def weights_sum(i, t):
                    u, j = octet_counts(i, t, 0)
                    after(dve, sem(f"probs{u}"), j + 1)
                    after(dve, sem(f"summed{1 - u}"), j + (1 if u else 0))
                    dve.tensor_tensor(sums[:, :, :], sums[:, :, :], pt[u][:, :, :], ALU.add).then_inc(
                        sem(f"summed{u}"), 1)

                def tile(i, t):
                    b, s = t // TILES, t % TILES
                    vb, j = tile_counts(i, t)
                    if masks == "query_key" and s == 0:
                        after(dve, sem(f"mq{b}"), (i + 1) * 16)
                        after(dve, sem(f"chunk_used{b}"), i)
                        dve.tensor_scalar(mb[b][:, :], mq[b][:, :], -1.0, 1.0, ALU.mult, ALU.add).then_inc(
                            sem(f"mb{b}"), 1)
                    after(dve, sem(f"v_used{vb}"), j)
                    if project:
                        after(dve, sem(f"v_proj{vb}"), j + 1)
                        dve.tensor_tensor(v[vb][:, :, 0:vd],
                                          pv[vb][:, 0:heads * vd].rearrange("p (h d) -> p h d", h=heads),
                                          bias_v[:, :].rearrange("p (h d) -> p h d", h=heads),
                                          ALU.add).then_inc(sem(f"v{vb}"), 1)
                    else:
                        after(dve, sem(f"vin{b}"), (i + 1) * 16)
                        dve.tensor_copy(v[vb][:, :, 0:vd],
                                        vin[b][:, s, :].rearrange("p (h d) -> p h d", h=heads)).then_inc(
                            sem(f"v{vb}"), 1)
                        if s == TILES - 1:
                            after(dve, sem(f"v{vb}"), j + 1)
                            dve.sem_inc(sem(f"v_copied{b}"), 1)

                with dve.Fori(0, steps) as i:
                    for t in range(per_body):
                        tile(i, t)
                        if wide and t:
                            weights_sum(i, t - 1)
                    if wide:
                        weights_sum(i, per_body - 1)
                if last_tile:
                    weights_sum(steps, 0)

            @block.scalar
            def _(act):
                def exps(i, t, o):
                    u, j = octet_counts(i, t, o)
                    if masks == "key":
                        act.wait_ge(S.sem("mask_split"), 1)
                    after(act, sem(f"scores{u}"), j + 1)
                    after(act, sem(f"pv{u}"), j)
                    if wide:
                        after(act, sem(f"summed{u}"), j)
                    if masks == "key":
                        tile_ap = R.mask_col[:, bass.ds(i * per_body + t, 1)]
                        ins = act.activation(pt[u][:, :, :], psc[u][:, :, :].rearrange("p a (b q) -> p (a b) q", q=P),
                                             ACT.Exp, bias=tile_ap)
                    else:
                        ins = act.activation(pt[u][:, :, :], psc[u][:, :, :].rearrange("p a (b q) -> p (a b) q", q=P),
                                             ACT.Exp)
                    ins.then_inc(sem(f"probs{u}"), 1)

                with act.Fori(0, steps) as i:
                    for t in range(per_body):
                        for o in range(octets):
                            exps(i, t, o)
                if last_tile:
                    exps(steps, 0, 0)

            @block.tensor
            def _(pe):
                after(pe, sem("constants"), 1)
                if not wide:
                    pe.wait_ge(S.sem("ones_rows"), 32)
                pe.matmul(O[:, :], zl[:, :], zr[:, :], start=True, stop=True)

                def values(i, t):
                    b, s = t // TILES, t % TILES
                    vb, j = tile_counts(i, t)
                    after(pe, sem(f"vin{b}"), (i + 1) * 16)
                    after(pe, sem(f"v{vb}"), j)
                    for d in range(DC):
                        last = pe.matmul(pv[vb][:, 0:heads * vd], vin[b][:, d, s * P:(s + 1) * P], w_v[:, d, :],
                                         start=(d == 0), stop=(d == DC - 1))
                    last.then_inc(sem(f"v_proj{vb}"), 1)

                def scores(i, t, o, keys=None):
                    b, s = t // TILES, t % TILES
                    u, j = octet_counts(i, t, o)
                    if o == 0 and s == 0 and keys is None:
                        after(pe, sem(f"kt{b}"), (i + 1) * kt_count)
                        if masks == "query_key":
                            after(pe, sem(f"mb{b}"), i + 1)
                    after(pe, sem(f"probs{u}"), j)
                    for half in range(2):
                        h0 = 8 * o + 4 * half
                        for k in range(4):
                            h = h0 + k
                            out = psc[u][:, half, k * P:(k + 1) * P]
                            if wide:
                                c = h // per_chunk
                                lhs = kt[b][:, c, s * P:(s + 1) * P] if keys is None else keys[:, c, :]
                                pe.matmul(out, lhs, q[c][:, h % per_chunk, :],
                                          start=(k == 0), stop=False, skip_group_check=True)
                            else:
                                last = pe.matmul(out, kt[b][:, h, s * P:(s + 1) * P], q[:, h, :], start=(k == 0),
                                                 stop=(masks != "query_key" and k == 3), skip_group_check=True)
                        if masks == "query_key":
                            last = pe.matmul(psc[u][:, half, :].rearrange("p (k q) -> p k q", k=4),
                                             mb[b][:, s * P:(s + 1) * P],
                                             R.neg_big[:, :].unsqueeze(1).broadcast_to([P, 4, P]),
                                             start=False, stop=True, skip_group_check=True)
                        if wide:
                            last = pe.matmul(psc[u][:, half, :], ones3[:, :], m3[:, h0 * P:(h0 + 4) * P],
                                             start=False, stop=True, skip_group_check=True)
                    last.then_inc(sem(f"scores{u}"), 1)

                def weigh(i, t, o, vals=None):
                    u, j = octet_counts(i, t, o)
                    vb, jv = tile_counts(i, t)
                    after(pe, sem(f"probs{u}"), j + 1)
                    if vals is None:
                        after(pe, sem(f"v{vb}"), jv + 1)
                    vv = v[vb] if vals is None else vals
                    for k in range(8):
                        h = 8 * o + k
                        if wide:
                            out = O[64 * (h % 2):64 * (h % 2) + vd, (h // 2) * P:(h // 2 + 1) * P]
                            lhs = vv[:, h, :]
                        else:
                            out = O[32 * (h % 4):32 * (h % 4) + vd + 1, (h // 4) * P:(h // 4 + 1) * P]
                            lhs = vv[:, h, :]
                        last = pe.matmul(out, lhs, pt[u][:, k, :], start=False, stop=False, skip_group_check=True)
                    last.then_inc(sem(f"pv{u}"), 1)
                    if o == octets - 1:
                        after(pe, sem(f"pv{u}"), j + 1)
                        if vals is None:
                            pe.sem_inc(sem(f"v_used{vb}"), 1)
                        if t % TILES == TILES - 1 and vals is None:
                            pe.sem_inc(sem(f"chunk_used{t // TILES}"), 1)

                with pe.Fori(0, steps) as i:
                    order = [(t, o) for t in range(per_body) for o in range(octets)]
                    if project:
                        values(i, 0)
                    for n, (t, o) in enumerate(order):
                        scores(i, t, o)
                        if project and o == 0 and t + 1 < per_body:
                            values(i, t + 1)
                        if n:
                            weigh(i, *order[n - 1])
                    weigh(i, *order[-1])
                if last_tile:
                    scores(steps, 0, 0, keys=last_tile[0])
                    weigh(steps, 0, 0, vals=last_tile[1])

            @block.gpsimd
            def _(pool):
                start_counts(pool, S)


def finish_heads16(nc, S, A, R, O, bias=None):
    with ExitStack() as mem:
        o_sb = mem.enter_context(nc.sbuf_tensor(f"{S.name}_o", [P, 4, P], F32))
        rec = mem.enter_context(nc.sbuf_tensor(f"{S.name}_rec", [P, 16], F32))
        out = mem.enter_context(nc.sbuf_tensor(f"{S.name}_out", [P, 16, 16], F32))
        ps = mem.enter_context(nc.psum_tensor(f"{S.name}_ops", [P, BANK], F32))
        with nc.Block() as block:
            @block.tensor
            def _(pe):
                pe.wait_ge(S.sem("o_copied"), 1)
                for s in range(4):
                    last = pe.transpose(ps[:, s * P:(s + 1) * P], o_sb[:, s, :], R.ident[:, :])
                last.then_inc(S.sem("o_turned"), 1)

            @block.vector
            def _(dve):
                link = Link(dve, S.sem("finish_link"))
                dve.tensor_copy(o_sb[:, :, :], O[:, :].rearrange("p (s q) -> p s q", s=4)).then_inc(
                    S.sem("o_copied"), 1)
                dve.wait_ge(S.sem("o_turned"), 1)
                rows = ps[:, :].rearrange("p (h f) -> p h f", f=32)
                link(dve.reciprocal(rec[:, :], rows[:, :, 16]))
                link(dve.tensor_tensor(out[:, :, :], rows[:, :, 0:16],
                                       rec[:, :].unsqueeze(2).broadcast_to([P, 16, 16]), ALU.mult))
                link(dve.tensor_tensor(R.x[:, :], R.x[:, :], out[:, :, :].rearrange("p h d -> p (h d)"), ALU.add))


def l3_xattn(nc, A, R):
    H = 16
    with Stage(nc, "l3x") as S:
        xn, nw = S.sb("xn", [P, DIM]), S.sb("nw", [P, 16])
        qb = [S.sb(f"qb{c}", [P, 8, P], BF16) for c in range(DC)]
        hm = S.sb("hm", [P, 8])
        R.neg_big = S.sb("neg_big", [P, P], BF16)
        top = S.sb("top", [P, H])
        qT = S.sb("qT", [P, DC * P])
        with ExitStack() as mem:
            pt = mem.enter_context(nc.psum_tensor("l3x_pt", [P, BANK], F32))
            with nc.Block() as block:
                @block.sync
                def _(sp):
                    sp.dma_start(hm[:, :], A["c_head16"]).then_inc(S.sem("hm"), 16)

                @block.scalar
                def _(act):
                    norm_scalar(act, S, "n", nw)

                @block.vector
                def _(dve):
                    link = Link(dve, S.sem("dve_link"))
                    norm_vector(dve, link, S, "n", R.x[:, :], xn[:, :], nw)
                    link(dve.tensor_scalar(R.neg_big[:, :], R.ident[:, :], -MASK_BIG, None, ALU.mult))
                    dve.wait_ge(S.sem("n_turned"), 1)
                    dve.wait_ge(S.sem("hm"), 16)
                    link(dve.tensor_copy(qT[:, :], pt[:, 0:DC * P]))
                    spread_queries(dve, link, qT, None, qb, hm, 8, 0.25)

                @block.tensor
                def _(pe):
                    turn_tensor(pe, S, "n", xn, pt, R.ident)
        ctxT = A["ctxT"].rearrange("(c p) n -> c p n", p=P)
        qs = split_queries(nc, S, qT[:, :], 0.25)
        find_maximum(nc, S, A, R, H, DC, 8, qb, ctxT, None, None, None, top, "query_key", split=True)
        split_rows(nc, S, R, "m3", top, H, qs[STACK:STACK + 3].rearrange("n h q -> n (h q)"))
        O = S.psum("O")
        attend(nc, S, A, R, H, DC, 8, qs, R.KS, A["ctx"], None, None, None, "query_key", O, None)
        finish_heads16(nc, S, A, R, O)


def spread_queries(dve, link, qT, q, qb, head_mask, per_chunk, scale):
    for c in range(len(qb)):
        link(dve.scalar_tensor_tensor(
            (qb if q is None else q)[c][:, :, :],
            qT[:, c * P:(c + 1) * P].unsqueeze(1).broadcast_to([P, per_chunk, P]), scale,
            head_mask[:, :].unsqueeze(2).broadcast_to([P, per_chunk, P]), ALU.mult, ALU.mult))
        if q is not None:
            link(dve.tensor_copy(qb[c][:, :, :], q[c][:, :, :]))


def l1_xattn(nc, A, R):
    H = 16
    n_tiles = R.keys // P
    with Stage(nc, "l1x") as S:
        xn, xT, nw = S.sb("xn", [P, DIM]), S.sb("xT", [P, DC, P]), S.sb("nw", [P, 16])
        qb = [S.sb(f"qb{c}", [P, 8, P], BF16) for c in range(DC)]
        hm = S.sb("hm", [P, 8])
        top = S.sb("top", [P, H])
        w = S.sb("w", [P, 3, DC, DIM])
        bq, bk, bv = S.sb("bq", [P, DC]), S.sb("bk", [P, DC]), S.sb("bv", [P, DIM])
        qT = S.sb("qT", [P, DC * P])
        R.mask_col = S.sb("mask_col", [P, n_tiles])
        R.ones3 = S.sb("ones3", [P, P], BF16)
        with ExitStack() as mem:
            mask = mem.enter_context(nc.sbuf_tensor("l1x_mask", [n_tiles, P], F32))
            parts = [mem.enter_context(nc.sbuf_tensor(f"l1x_mpart{n}", [n_tiles, P], BF16)) for n in range(3)]
            pt, pq, pm = [mem.enter_context(nc.psum_tensor(f"l1x_p{n}", [P, BANK], F32)) for n in range(3)]
            scratch = nc.dram_tensor("l1x_mask_rows", (3, n_tiles, P), BF16, kind="Internal").ap()
            loads = Loads(S.sem("loads"))
            with nc.Block() as block:
                @block.sync
                def _(sp):
                    loads(sp.dma_start(mask[:, :], A["mask_row"]))
                    loads(sp.dma_start(hm[:, :], A["c_head16"]))
                    for n, name in enumerate(("wq", "wk", "wv")):
                        loads(sp.dma_start(w[:, n, :, :], by_rows(A[f"L1_xattn_{name}"])))
                    loads(sp.dma_start(bv[:, :], A["L1_xattn_bv"].partition_broadcast(P)))
                    loads(sp.dma_start(bq[:, :], column(A["L1_xattn_bq"]), allow_slow_non_contiguous=True))
                    loads(sp.dma_start(bk[:, :], column(A["L1_xattn_bk"]), allow_slow_non_contiguous=True))
                    sp.wait_ge(S.sem("mask_split"), 1)
                    for n in range(3):
                        sp.dma_start(scratch[n], parts[n][:, :]).then_inc(S.sem("mask_out"), 16)
                    sp.wait_ge(S.sem("mask_out"), 48)

                @block.scalar
                def _(act):
                    norm_scalar(act, S, "n", nw)

                @block.vector
                def _(dve):
                    link = Link(dve, S.sem("dve_link"))
                    link(dve.memset(R.ones3[:, :], 0.0))
                    link(dve.memset(R.ones3[0:3, :], 1.0))
                    norm_vector(dve, link, S, "n", R.x[:, :], xn[:, :], nw)
                    turn_vector(dve, S, "n", xT, pt)
                    dve.wait_ge(S.sem("loads"), loads.total)
                    link(dve.tensor_scalar(mask[:, :], mask[:, :], -1.0, 1.0, ALU.mult, ALU.add))
                    dve.tensor_scalar(mask[:, :], mask[:, :], -10000.0, None, ALU.mult).then_inc(
                        S.sem("mask_bias"), 1)
                    dve.wait_ge(S.sem("mask_turned"), 1)
                    link(dve.tensor_copy(R.mask_col[:, :], pm[:, 0:n_tiles]))
                    for n in range(3):
                        link(dve.tensor_copy(parts[n][:, :], mask[:, :]))
                        link(dve.tensor_tensor(mask[:, :], mask[:, :], parts[n][:, :], ALU.subtract))
                    dve.sem_inc(S.sem("mask_split"), 1)
                    dve.wait_ge(S.sem("q_proj"), 1)
                    for c in range(DC):
                        link(dve.tensor_scalar(qT[:, c * P:(c + 1) * P], pq[:, c * P:(c + 1) * P], bq[:, c:c + 1],
                                               None, ALU.add))
                    spread_queries(dve, link, qT, None, qb, hm, 8, 0.25)

                @block.tensor
                def _(pe):
                    turn_tensor(pe, S, "n", xn, pt, R.ident)
                    pe.wait_ge(S.sem("mask_bias"), 1)
                    pe.transpose(pm[:, 0:n_tiles], mask[:, :], R.ident[0:n_tiles, 0:n_tiles]).then_inc(
                        S.sem("mask_turned"), 1)
                    pe.wait_ge(S.sem("n_xT"), 1)
                    pe.wait_ge(S.sem("loads"), loads.total)
                    for o in range(DC):
                        for c in range(DC):
                            last = pe.matmul(pq[:, o * P:(o + 1) * P], w[:, 0, c, o * P:(o + 1) * P], xT[:, c, :],
                                             start=(c == 0), stop=(c == DC - 1))
                    last.then_inc(S.sem("q_proj"), 1)
        qs = split_queries(nc, S, qT[:, :], 0.25)
        ctxT = A["ctxT"].rearrange("(c p) n -> c p n", p=P)
        with ExitStack() as mem:
            R.mask3 = mem.enter_context(nc.sbuf_tensor("l1x_mask3", [P, R.keys], BF16))
            with nc.Block() as block:
                @block.gpsimd
                def _(pool):
                    pool.memset(R.mask3[:, :], 0.0).then_inc(S.sem("mask_zero"), 1)

                @block.sync
                def _(sp):
                    sp.wait_ge(S.sem("mask_zero"), 1)
                    sp.dma_start(R.mask3[0:3, :], scratch.rearrange("n t p -> n (t p)")).then_inc(S.sem("mask_in"), 16)
                    sp.wait_ge(S.sem("mask_in"), 16)
            find_maximum(nc, S, A, R, H, DC, 8, qb, ctxT, "plain", w[:, 1, :, :], bk, top, "key", split=True)
        split_rows(nc, S, R, "m3", top, H, qs[STACK:STACK + 3].rearrange("n h q -> n (h q)"))
        O = S.psum("O")
        attend(nc, S, A, R, H, DC, 8, qs, R.KS, ctxT, w[:, 2, :, :], bv, None, "key", O, None)
        finish_heads16(nc, S, A, R, O)


def l0_xattn(nc, A, R):
    H, HD, KC = 8, 64, 4
    INNER = H * HD
    with Stage(nc, "l0x") as S:
        q = [S.sb(f"q{c}", [P, 2, P]) for c in range(KC)]
        qb = [S.sb(f"qb{c}", [P, 2, P], BF16) for c in range(KC)]
        hm = S.sb("hm", [P, 2])
        top = S.sb("top", [P, H])
        wk, wv = S.sb("wk", [P, DC, INNER]), S.sb("wv", [P, DC, INNER])
        bias_k, bias_v = S.sb("bias_k", [P, KC]), S.sb("bias_v", [P, INNER])
        R.nbias_k = S.sb("nbias_k", [P, KC])
        kl, vl = S.sb("kl", [P, KC, P]), S.sb("vl", [P, H, HD])
        klb = S.sb("klb", [P, KC, P], BF16)
        ltop = S.sb("ltop", [P, H])
        with ExitStack() as mem:
            def sb(name, shape, dt=F32):
                return mem.enter_context(nc.sbuf_tensor(f"l0x_{name}", shape, dt))
            xn, nw, nw2 = sb("xn", [P, DIM]), sb("nw", [P, 16]), sb("nw2", [P, 16])
            ln, lT = sb("ln", [P, DIM]), sb("lT", [P, DC, P])
            wq = sb("wq", [P, DC, INNER])
            gl, bl = sb("gl", [P, DIM]), sb("bl", [P, DIM])
            gx, bx = sb("gx", [P, DC]), sb("bx", [P, DC])
            bxb = sb("bxb", [P, DC, P])
            pq, pk, pv, pbk, pbv, ps0, ps1, pt = [
                mem.enter_context(nc.psum_tensor(f"l0x_p{n}", [P, BANK], F32)) for n in range(8)]
            loads = Loads(S.sem("loads"))
            with nc.Block() as block:
                @block.sync
                def _(sp):
                    loads(sp.dma_start(hm[:, :], A["c_head64"]))
                    loads(sp.dma_start(gl[:, :], A["L0_xattn_gamma_l"].partition_broadcast(P)))
                    loads(sp.dma_start(bl[:, :], A["L0_xattn_beta_l"].partition_broadcast(P)))
                    loads(sp.dma_start(gx[:, :], column(A["L0_xattn_gamma_x"]), allow_slow_non_contiguous=True))
                    loads(sp.dma_start(bx[:, :], column(A["L0_xattn_beta_x"]), allow_slow_non_contiguous=True))
                    loads(sp.dma_start(wq[:, :, :], by_rows(A["L0_xattn_Wq"])))
                    loads(sp.dma_start(wk[:, :, :], by_rows(A["L0_xattn_Wk"])))
                    loads(sp.dma_start(wv[:, :, :], by_rows(A["L0_xattn_Wv"])))

                @block.scalar
                def _(act):
                    norm_scalar(act, S, "n", nw)
                    norm_scalar(act, S, "m", nw2)

                @block.vector
                def _(dve):
                    link = Link(dve, S.sem("dve_link"))
                    norm_vector(dve, link, S, "n", R.x[:, :], xn[:, :], nw)
                    norm_vector(dve, link, S, "m", xn[:, :], ln[:, :], nw2)
                    dve.wait_ge(S.sem("loads"), loads.total)
                    link(dve.tensor_tensor(ln[:, :], ln[:, :], gl[:, :], ALU.mult))
                    dve.tensor_tensor(ln[:, :], ln[:, :], bl[:, :], ALU.add).then_inc(S.sem("ln"), 1)
                    turn_vector(dve, S, "l", lT, pt)
                    link(dve.tensor_copy(bxb[:, :, :], bx[:, :].unsqueeze(2).broadcast_to([P, DC, P])))
                    dve.sem_inc(S.sem("bxb"), 1)
                    dve.wait_ge(S.sem("q_proj"), 1)
                    spread_queries(dve, link, pq, q, qb, hm, 2, HD ** -0.5)
                    dve.sem_inc(S.sem("q"), 1)
                    dve.wait_ge(S.sem("latents_proj"), 1)
                    link(dve.tensor_copy(kl[:, :, :], pk[:, :].rearrange("p (c t) -> p c t", c=KC)))
                    dve.tensor_copy(klb[:, :, :], kl[:, :, :]).then_inc(S.sem("klb"), 1)
                    dve.tensor_copy(vl[:, :, :], pv[:, :].rearrange("p (h d) -> p h d", h=H))
                    dve.wait_ge(S.sem("bias_proj"), 1)
                    link(dve.tensor_copy(bias_k[:, :], pbk[:, 0:KC]))
                    dve.tensor_copy(R.nbias_k[64:P, :], pbk[0:64, 0:KC])
                    dve.tensor_scalar(R.nbias_k[0:64, :], pbk[64:P, 0:KC], -1.0, None, ALU.mult)
                    dve.tensor_copy(bias_v[:, :], pbv[:, :])
                    for c in range(DC):
                        dve.tensor_scalar(wk[:, c, :], wk[:, c, :], gx[:, c:c + 1], None, ALU.mult)
                        dve.tensor_scalar(wv[:, c, :], wv[:, c, :], gx[:, c:c + 1], None, ALU.mult)
                    dve.wait_ge(S.sem("latent_scores"), 1)
                    dve.tensor_reduce(ltop[:, 0:4], ps0[:, :].rearrange("p (h k) -> p h k", h=4), AX.X, ALU.max)
                    dve.tensor_reduce(ltop[:, 4:8], ps1[:, :].rearrange("p (h k) -> p h k", h=4), AX.X, ALU.max)

                @block.tensor
                def _(pe):
                    turn_tensor(pe, S, "l", ln, pt, R.ident, ready="ln")
                    pe.wait_ge(S.sem("l_xT"), 1)
                    pe.wait_ge(S.sem("loads"), loads.total)
                    for o in range(KC):
                        for c in range(DC):
                            last = pe.matmul(pq[:, o * P:(o + 1) * P], wq[:, c, o * P:(o + 1) * P], lT[:, c, :],
                                             start=(c == 0), stop=(c == DC - 1))
                    last.then_inc(S.sem("q_proj"), 1)
                    for o in range(KC):
                        for c in range(DC):
                            pe.matmul(pk[:, o * P:(o + 1) * P], wk[:, c, o * P:(o + 1) * P], lT[:, c, :],
                                      start=(c == 0), stop=(c == DC - 1))
                    for c in range(DC):
                        last = pe.matmul(pv[:, :], lT[:, c, :], wv[:, c, :], start=(c == 0), stop=(c == DC - 1))
                    last.then_inc(S.sem("latents_proj"), 1)
                    pe.wait_ge(S.sem("bxb"), 1)
                    for o in range(KC):
                        for c in range(DC):
                            pe.matmul(pbk[:, o:o + 1], wk[:, c, o * P:(o + 1) * P], bx[:, c:c + 1],
                                      start=(c == 0), stop=(c == DC - 1))
                    for c in range(DC):
                        last = pe.matmul(pbv[:, :], bxb[:, c, :], wv[:, c, :], start=(c == 0), stop=(c == DC - 1))
                    last.then_inc(S.sem("bias_proj"), 1)
                    pe.wait_ge(S.sem("q"), 1)
                    pe.wait_ge(S.sem("klb"), 1)
                    for h in range(H):
                        last = pe.matmul((ps0 if h < 4 else ps1)[:, (h % 4) * P:(h % 4 + 1) * P],
                                         qb[h // 2][:, h % 2, :], klb[:, h // 2, :], start=True, stop=True)
                    last.then_inc(S.sem("latent_scores"), 1)
        find_maximum(nc, S, A, R, H, KC, 2, qb, R.nT, "rope", wk, bias_k, top, None, split=False)
        m3 = S.sb("m3", [P, H * P], BF16)
        with nc.Block() as block:
            @block.vector
            def _(dve):
                dve.memset(m3[:, :], 0.0)
                dve.tensor_tensor(top[:, :], top[:, :], ltop[:, :], ALU.max)
        split_rows(nc, S, R, "m3", top, H, m3[0:3, :])
        O = S.psum("O")
        sums = S.sb("sums", [P, H, P])
        attend(nc, S, A, R, H, KC, 2, q, R.KT, R.nT, wv, bias_v, m3, None, O, sums, last_tile=(kl, vl))
        with ExitStack() as mem:
            def sb(name, shape, dt=F32):
                return mem.enter_context(nc.sbuf_tensor(f"l0x_{name}", shape, dt))
            ones = sb("ones", [P, P])
            rec = sb("rec", [P, H, P])
            oT = sb("oT", [P, KC, P])
            wo = sb("wo", [P, KC, DIM])
            pr = [mem.enter_context(nc.psum_tensor(f"l0x_pr{n}", [P, BANK], F32)) for n in range(2)]
            py = mem.enter_context(nc.psum_tensor("l0x_py", [P, BANK], F32))
            with nc.Block() as block:
                @block.sync
                def _(sp):
                    sp.dma_start(wo[:, :, :], by_rows(A["L0_xattn_Wo"])).then_inc(S.sem("wo"), 16)

                @block.vector
                def _(dve):
                    link = Link(dve, S.sem("finish_link"))
                    dve.memset(ones[:, :], 1.0).then_inc(S.sem("ones"), 1)
                    dve.wait_ge(S.sem("totals"), 1)
                    for n in range(2):
                        link(dve.reciprocal(rec[:, 4 * n:4 * n + 4, :], pr[n][:, :].rearrange("p (h q) -> p h q", h=4)))
                    for g in range(2):
                        rows = slice(64 * g, 64 * g + 64)
                        last = dve.tensor_tensor(oT[rows, :, :], O[rows, :].rearrange("p (s q) -> p s q", s=KC),
                                                 rec[rows, g:H:2, :], ALU.mult)
                        link(last)
                    dve.sem_inc(S.sem("oT"), 1)
                    dve.wait_ge(S.sem("y"), 1)
                    dve.tensor_tensor(R.x[:, :], R.x[:, :], py[:, 0:DIM], ALU.add)

                @block.tensor
                def _(pe):
                    pe.wait_ge(S.sem("ones"), 1)
                    for n in range(2):
                        last = pe.matmul(pr[n][:, :], ones[:, :],
                                         sums[:, 4 * n:4 * n + 4, :].rearrange("p h q -> p (h q)"), start=True, stop=True)
                    last.then_inc(S.sem("totals"), 1)
                    pe.wait_ge(S.sem("oT"), 1)
                    pe.wait_ge(S.sem("wo"), 16)
                    for c in range(KC):
                        last = pe.matmul(py[:, 0:DIM], oT[:, c, :], wo[:, c, :], start=(c == 0), stop=(c == KC - 1))
                    last.then_inc(S.sem("y"), 1)


def head_stats(dve, link, f2, sm, ss, rn_in, ratio, tmp, heads_n):
    link(dve.tensor_tensor(tmp, sm, sm, ALU.mult))
    link(dve.scalar_tensor_tensor(tmp, tmp, -1.0 / P, ss, ALU.mult, ALU.add))
    link(dve.tensor_scalar(tmp, tmp, 1.0 / (P - 1), None, ALU.mult))
    link(dve.tensor_scalar(ratio, tmp, 1.0, 2.0, ALU.min, ALU.mult))
    link(dve.tensor_scalar(tmp, tmp, 1.0, None, ALU.add))
    link(dve.reciprocal(tmp, tmp))
    link(dve.tensor_tensor(ratio, ratio, tmp, ALU.mult))


def l2_xattn(nc, A, R):
    H, HD = 8, 128
    W = H * HD
    GW = HD + 2
    steps = R.keys // CHUNK // 2
    with Stage(nc, "l2x") as S:
        w = S.sb("w", [P, DC, W])
        bias = S.sb("bias", [P, W])
        fq = S.sb("fq", [P, W])
        qs = S.sb("qs", [P, 5, H])
        wp1 = S.sb("wp1", [P, DC, HD])
        Msb = S.sb("Msb", [P, H, GW])
        with ExitStack() as mem:
            def sb(name, shape, dt=F32):
                return mem.enter_context(nc.sbuf_tensor(f"l2x_{name}", shape, dt))
            xn, nw, nw2 = sb("xn", [P, DIM]), sb("nw", [P, 16]), sb("nw2", [P, 16])
            xn2, xT = sb("xn2", [P, DIM]), sb("xT", [P, DC, P])
            g, b = sb("g", [P, DC]), sb("b", [P, DC])
            bb = sb("bb", [P, DC, P])
            sq = sb("sq", [P, W])
            pt = mem.enter_context(nc.psum_tensor("l2x_pt", [P, BANK], F32))
            pb = mem.enter_context(nc.psum_tensor("l2x_pb", [P, 2, BANK], F32))
            pf = mem.enter_context(nc.psum_tensor("l2x_pf", [P, 2, BANK], F32))
            loads = Loads(S.sem("loads"))
            with nc.Block() as block:
                @block.sync
                def _(sp):
                    loads(sp.dma_start(w[:, :, :], by_rows(A["L2_xattn_w_in"])))
                    loads(sp.dma_start(g[:, :], column(A["L2_xattn_ln_g"]), allow_slow_non_contiguous=True))
                    loads(sp.dma_start(b[:, :], column(A["L2_xattn_ln_b"]), allow_slow_non_contiguous=True))

                @block.scalar
                def _(act):
                    norm_scalar(act, S, "n", nw)
                    norm_scalar(act, S, "m", nw2)
                    act.wait_ge(S.sem("qss"), 1)
                    act.activation(qs[:, 2, :], qs[:, 1, :], ACT.Sqrt).then_inc(S.sem("qn"), 1)

                @block.vector
                def _(dve):
                    link = Link(dve, S.sem("dve_link"))
                    norm_vector(dve, link, S, "n", R.x[:, :], xn[:, :], nw)
                    norm_vector(dve, link, S, "m", xn[:, :], xn2[:, :], nw2)
                    turn_vector(dve, S, "m", xT, pt)
                    dve.wait_ge(S.sem("loads"), loads.total)
                    dve.tensor_copy(bb[:, :, :], b[:, :].unsqueeze(2).broadcast_to([P, DC, P])).then_inc(
                        S.sem("bb"), 1)
                    dve.wait_ge(S.sem("bias_proj"), 1)
                    link(dve.tensor_copy(bias[:, :], pb[:, :, :].rearrange("p a n -> p (a n)")))
                    for c in range(DC):
                        link(dve.tensor_scalar(w[:, c, :], w[:, c, :], g[:, c:c + 1], None, ALU.mult))
                    dve.sem_inc(S.sem("w_folded"), 1)
                    dve.wait_ge(S.sem("q_proj"), 1)
                    link(dve.tensor_tensor(fq[:, :], pf[:, :, :].rearrange("p a n -> p (a n)"), bias[:, :], ALU.add))
                    link(dve.tensor_tensor(sq[:, :], fq[:, :], fq[:, :], ALU.mult))
                    link(dve.tensor_reduce(qs[:, 0, :], fq[:, :].rearrange("p (h d) -> p h d", h=H), AX.X, ALU.add))
                    dve.tensor_reduce(qs[:, 1, :], sq[:, :].rearrange("p (h d) -> p h d", h=H), AX.X, ALU.add).then_inc(
                        S.sem("qss"), 1)
                    dve.wait_ge(S.sem("qss"), 1)
                    head_stats(dve, link, None, qs[:, 0, :], qs[:, 1, :], None, qs[:, 3, :], qs[:, 4, :], H)
                    dve.wait_ge(S.sem("qn"), 1)
                    dve.reciprocal(qs[:, 2, :], qs[:, 2, :])

                @block.tensor
                def _(pe):
                    turn_tensor(pe, S, "m", xn2, pt, R.ident)
                    pe.wait_ge(S.sem("loads"), loads.total)
                    pe.wait_ge(S.sem("bb"), 1)
                    for n in range(2):
                        for c in range(DC):
                            last = pe.matmul(pb[:, n, :], bb[:, c, :], w[:, c, n * BANK:(n + 1) * BANK],
                                             start=(c == 0), stop=(c == DC - 1))
                    last.then_inc(S.sem("bias_proj"), 1)
                    pe.wait_ge(S.sem("w_folded"), 1)
                    pe.wait_ge(S.sem("m_xT"), 1)
                    for n in range(2):
                        for c in range(DC):
                            last = pe.matmul(pf[:, n, :], xT[:, c, :], w[:, c, n * BANK:(n + 1) * BANK],
                                             start=(c == 0), stop=(c == DC - 1))
                    last.then_inc(S.sem("q_proj"), 1)
        with ExitStack() as mem:
            def sb(name, shape, dt=F32):
                return mem.enter_context(nc.sbuf_tensor(f"l2x_{name}", shape, dt))
            nin = [sb(f"nin{b}", [P, DC, CHUNK]) for b in range(2)]
            f = [sb(f"f{b}", [P, TILES, W]) for b in range(2)]
            gk = [sb(f"gk{b}", [P, TILES, H, GW]) for b in range(2)]
            sq = [sb(f"fsq{b}", [P, W]) for b in range(2)]
            ks = [sb(f"ks{b}", [P, 5, TILES, H]) for b in range(2)]
            zl, zr = sb("zl", [P, P]), sb("zr", [P, BANK])
            pf = [mem.enter_context(nc.psum_tensor(f"l2x_kf{b}", [P, 2, BANK], F32)) for b in range(2)]
            pM = mem.enter_context(nc.psum_tensor("l2x_M", [P, 3, BANK], F32))
            src = R.nT.rearrange("c p (n k) -> n p c k", k=CHUNK)

            def use(i, b, t):
                k = b * TILES + t
                return k % 2, i * TILES + k // 2

            with nc.Block() as block:
                @block.sync
                def _(sp):
                    with sp.Fori(0, steps) as i:
                        for b in range(2):
                            after(sp, S.counted(f"nin_used{b}"), i)
                            sp.dma_start(nin[b][:, :, :], src[bass.ds(i * 2 + b, 1)].squeeze(0)).then_inc(
                                S.counted(f"nin{b}"), 16)

                def squares_sum(dve, i, b, t):
                    u, j = use(i, b, t)
                    after(dve, S.counted(f"sq{u}"), j + 1)
                    dve.tensor_reduce(ks[b][:, 1, t, :], sq[u][:, :].rearrange("p (h d) -> p h d", h=H), AX.X,
                                      ALU.add).then_inc(S.counted(f"sums{b}"), 1)
                    after(dve, S.counted(f"sums{b}"), i * 2 * TILES + min(2 * t + 3, 2 * TILES))
                    dve.sem_inc(S.counted(f"sq_read{u}"), 1)

                @block.vector
                def _(dve):
                    dve.memset(zl[:, :], 0.0).then_inc(S.sem("constants"), 1)
                    dve.memset(zr[:, :], 0.0).then_inc(S.sem("constants"), 1)
                    for b in range(2):
                        dve.memset(gk[b][:, :, :, HD + 1:GW], 1.0).then_inc(S.sem("constants"), 1)

                    with dve.Fori(0, steps) as i:
                        for b in range(2):
                            after(dve, S.counted(f"f_used{b}"), i)
                            for t in range(TILES):
                                u, j = use(i, b, t)
                                after(dve, S.counted(f"f_proj{u}"), j + 1)
                                dve.tensor_tensor(f[b][:, t, :], pf[u][:, :, :].rearrange("p a n -> p (a n)"),
                                                  bias[:, :], ALU.add).then_inc(S.counted(f"f{u}"), 1)
                                after(dve, S.counted(f"f{u}"), j + 1)
                                dve.tensor_reduce(ks[b][:, 0, t, :], f[b][:, t, :].rearrange("p (h d) -> p h d", h=H),
                                                  AX.X, ALU.add).then_inc(S.counted(f"sums{b}"), 1)
                                if t:
                                    squares_sum(dve, i, b, t - 1)
                            squares_sum(dve, i, b, TILES - 1)
                            after(dve, S.counted(f"sums{b}"), (i + 1) * 2 * TILES)
                            dve.sem_inc(S.counted(f"ss{b}"), 1)
                            n0 = 7
                            sm, ss, ratio, tmp = ks[b][:, 0], ks[b][:, 1], gk[b][:, :, :, HD], ks[b][:, 4]

                            def lk(n, ins):
                                ins.then_inc(S.counted(f"stat{b}"), 1)
                                after(dve, S.counted(f"stat{b}"), i * n0 + n)
                            lk(1, dve.tensor_tensor(tmp, sm, sm, ALU.mult))
                            lk(2, dve.scalar_tensor_tensor(tmp, tmp, -1.0 / P, ss, ALU.mult, ALU.add))
                            lk(3, dve.tensor_scalar(tmp, tmp, 1.0 / (P - 1), None, ALU.mult))
                            lk(4, dve.tensor_scalar(ks[b][:, 3], tmp, 1.0, 2.0, ALU.min, ALU.mult))
                            lk(5, dve.tensor_scalar(tmp, tmp, 1.0, None, ALU.add))
                            lk(6, dve.reciprocal(tmp, tmp))
                            dve.tensor_tensor(ratio, ks[b][:, 3], tmp, ALU.mult).then_inc(S.counted(f"ratio{b}"), 1)
                            after(dve, S.counted(f"kn{b}"), i + 1)
                            lk(7, dve.reciprocal(ks[b][:, 2], ks[b][:, 2]))
                            dve.sem_inc(S.counted(f"rn{b}"), 1)

                @block.scalar
                def _(act):
                    with act.Fori(0, steps) as i:
                        for b in range(2):
                            for t in range(TILES):
                                u, j = use(i, b, t)
                                after(act, S.counted(f"f{u}"), j + 1)
                                after(act, S.counted(f"sq_read{u}"), j)
                                act.activation(sq[u][:, :], f[b][:, t, :], ACT.Square).then_inc(S.counted(f"sq{u}"), 1)
                            after(act, S.counted(f"ss{b}"), i + 1)
                            after(act, S.counted(f"gk{b}"), i * TILES)
                            act.activation(ks[b][:, 2], ks[b][:, 1], ACT.Sqrt).then_inc(S.counted(f"kn{b}"), 1)

                @block.tensor
                def _(pe):
                    def project(i, b):
                        after(pe, S.counted(f"nin{b}"), (i + 1) * 16)
                        for t in range(TILES):
                            u, j = use(i, b, t)
                            after(pe, S.counted(f"f{u}"), j)
                            for n in range(2):
                                for c in range(DC):
                                    last = pe.matmul(pf[u][:, n, :], nin[b][:, c, t * P:(t + 1) * P],
                                                     w[:, c, n * BANK:(n + 1) * BANK], start=(c == 0),
                                                     stop=(c == DC - 1))
                            last.then_inc(S.counted(f"f_proj{u}"), 1)
                        after(pe, S.counted(f"f_proj{u}"), j + 1)
                        pe.sem_inc(S.counted(f"nin_used{b}"), 1)

                    def gather(i, b):
                        after(pe, S.counted(f"ratio{b}"), i + 1)
                        for t in range(TILES):
                            after(pe, S.counted(f"gk{b}"), i * TILES + t + 1)
                            for h in range(H):
                                last = pe.matmul(pM[:, h // 3, (h % 3) * GW:(h % 3 + 1) * GW],
                                                 f[b][:, t, h * HD:(h + 1) * HD], gk[b][:, t, h, :],
                                                 start=False, stop=False, skip_group_check=True)
                        last.then_inc(S.counted(f"f_used{b}"), 1)

                    pe.wait_ge(S.sem("constants"), 4)
                    for n in range(3):
                        pe.matmul(pM[:, n, :], zl[:, :], zr[:, :], start=True, stop=True)
                    project(0, 0)
                    if steps > 1:
                        with pe.Fori(0, steps - 1) as i:
                            project(i, 1)
                            gather(i, 0)
                            project(i + 1, 0)
                            gather(i, 1)
                    project(steps - 1, 1)
                    gather(steps - 1, 0)
                    gather(steps - 1, 1)

                @block.gpsimd
                def _(pool):
                    start_counts(pool, S)
                    with pool.Fori(0, steps) as i:
                        for b in range(2):
                            after(pool, S.counted(f"rn{b}"), i + 1)
                            for t in range(TILES):
                                pool.tensor_tensor(gk[b][:, t, :, 0:HD], f[b][:, t, :].rearrange("p (h d) -> p h d", h=H),
                                                   ks[b][:, 2, t, :].unsqueeze(2).broadcast_to([P, H, HD]),
                                                   ALU.mult).then_inc(S.counted(f"gk{b}"), 1)
            with nc.Block() as block:
                @block.vector
                def _(dve):
                    for n in range(3):
                        k = min(3, H - 3 * n)
                        dve.tensor_copy(Msb[:, 3 * n:3 * n + k, :],
                                        pM[:, n, 0:k * GW].rearrange("p (h g) -> p h g", g=GW))
        with ExitStack() as mem:
            def sb(name, shape, dt=F32):
                return mem.enter_context(nc.sbuf_tensor(f"l2x_{name}", shape, dt))
            b1, lg, lb = sb("b1", [H, HD]), sb("lg", [H, HD]), sb("lb", [H, HD])
            w2, b2 = sb("w2", [P, 3]), sb("b2", [H, 3])
            wo, bo = sb("wo", [P, H, DIM]), sb("bo", [P, DIM])
            ones, off = sb("ones", [P, P]), sb("off", [P, P])
            qc, corr = sb("qc", [P, H, HD]), sb("corr", [P, H, HD])
            cs, dec = sb("cs", [P, H]), sb("dec", [P, H])
            gT = sb("gT", [P, 2, H])
            h1, nw3, h1T = sb("h1", [H, HD]), sb("nw3", [H, 16]), sb("h1T", [P, H])
            lo, sw, dw = sb("lo", [H, 3]), sb("sw", [H, 4]), sb("dw", [H, H, 3])
            mix = sb("mix", [P, H, 3])
            ca, cb = sb("ca", [P, H]), sb("cb", [P, H])
            cbw = sb("cbw", [P, H, P])
            a, aT, yT, cbT = sb("a", [P, H, HD]), sb("aT", [P, H, P]), sb("yT", [P, H, P]), sb("cbT", [P, H, P])
            p1 = mem.enter_context(nc.psum_tensor("l2x_p1", [P, 2, BANK], F32))
            p2 = mem.enter_context(nc.psum_tensor("l2x_p2", [P, 2, BANK], F32))
            p3, p4, p5, p6 = [mem.enter_context(nc.psum_tensor(f"l2x_p{n}", [P, BANK], F32)) for n in range(3, 7)]
            loads = Loads(S.sem("late_loads"))
            heads = lambda ap: ap.rearrange("p a (b d) -> p (a b) d", d=P)
            with nc.Block() as block:
                @block.sync
                def _(sp):
                    loads(sp.dma_start(wp1[:, :, :], by_rows(A["L2_xattn_wp_w1"])))
                    loads(sp.dma_start(b1[:, :], A["L2_xattn_wp_b1"].partition_broadcast(H)))
                    loads(sp.dma_start(lg[:, :], A["L2_xattn_wp_ln_g"].partition_broadcast(H)))
                    loads(sp.dma_start(lb[:, :], A["L2_xattn_wp_ln_b"].partition_broadcast(H)))
                    loads(sp.dma_start(w2[:, :], A["L2_xattn_wp_w2"]))
                    loads(sp.dma_start(b2[:, :], A["L2_xattn_wp_b2"].partition_broadcast(H)))
                    loads(sp.dma_start(wo[:, :, :], by_rows(A["L2_xattn_w_out"])))
                    loads(sp.dma_start(bo[:, :], A["L2_xattn_b_out"].partition_broadcast(P)))

                @block.scalar
                def _(act):
                    act.wait_ge(S.sem("corr_total"), 1)
                    act.activation(dec[:, :], p3[:, 0:H], ACT.Sqrt).then_inc(S.sem("corr_root"), 1)
                    norm_scalar(act, S, "h", nw3, rows=H)
                    act.wait_ge(S.sem("corr_root"), 1)
                    act.activation(dec[:, :], dec[:, :], ACT.Exp, scale=-5.0 / P / (HD * HD)).then_inc(
                        S.sem("decorr"), 1)
                    act.wait_ge(S.sem("w_shifted"), 1)
                    act.activation(lo[:, :], lo[:, :], ACT.Exp, accum_out=sw[:, 1:2]).then_inc(S.sem("w_exp"), 1)

                @block.vector
                def _(dve):
                    link = Link(dve, S.sem("late_link"))
                    fqh = fq[:, :].rearrange("p (h d) -> p h d", h=H)
                    link(dve.memset(ones[:, :], 1.0))
                    link(dve.tensor_scalar(off[:, :], R.ident[:, :], -1.0, 1.0, ALU.mult, ALU.add))
                    link(dve.tensor_scalar(cs[:, :], qs[:, 0, :], 1.0 / HD, None, ALU.mult))
                    link(dve.tensor_tensor(qc[:, :, :], fqh, cs[:, :].unsqueeze(2).broadcast_to([P, H, HD]),
                                           ALU.subtract))
                    dve.sem_inc(S.sem("qc"), 1)
                    dve.wait_ge(S.sem("corr"), 1)
                    link(dve.tensor_tensor(corr[:, :, :], heads(p1[:, :, :]),
                                           off[:, :].unsqueeze(1).broadcast_to([P, H, P]), ALU.mult))
                    link(dve.tensor_tensor(corr[:, :, :], corr[:, :, :], corr[:, :, :], ALU.mult))
                    link(dve.tensor_reduce(cs[:, :], corr[:, :, :], AX.X, ALU.add))
                    dve.sem_inc(S.sem("corr_sq"), 1)
                    dve.wait_ge(S.sem("q_mean"), 1)
                    link(dve.tensor_scalar(gT[:, 0, :], p4[:, 0:H], 1.0 / P, None, ALU.mult))
                    link(dve.tensor_scalar(gT[:, 1, :], Msb[:, :, HD + 1], 1.0 / R.keys, None, ALU.mult))
                    dve.sem_inc(S.sem("gT"), 1)
                    dve.wait_ge(S.sem("late_loads"), loads.total)
                    dve.wait_ge(S.sem("h1"), 1)
                    link(dve.tensor_tensor(h1[:, :], p5[0:H, 0:HD], b1[:, :], ALU.add))
                    norm_vector(dve, link, S, "h", h1[:, :], h1[:, :], nw3, rows=H)
                    link(dve.tensor_tensor(h1[:, :], h1[:, :], lg[:, :], ALU.mult))
                    link(dve.tensor_tensor(h1[:, :], h1[:, :], lb[:, :], ALU.add))
                    link(dve.tensor_scalar(h1[:, :], h1[:, :], 0.0, None, ALU.max))
                    dve.sem_inc(S.sem("h1_relu"), 1)
                    dve.wait_ge(S.sem("h1_turned"), 1)
                    dve.tensor_copy(h1T[:, :], p5[:, 0:H]).then_inc(S.sem("h1T"), 1)
                    dve.wait_ge(S.sem("logits"), 1)
                    link(dve.tensor_tensor(lo[:, :], p5[0:H, 0:3], b2[:, :], ALU.add))
                    link(dve.tensor_reduce(sw[:, 0:1], lo[:, :], AX.X, ALU.max))
                    dve.tensor_scalar(lo[:, :], lo[:, :], sw[:, 0:1], None, ALU.subtract).then_inc(
                        S.sem("w_shifted"), 1)
                    dve.wait_ge(S.sem("w_exp"), 1)
                    link(dve.reciprocal(sw[:, 2:3], sw[:, 1:2]))
                    link(dve.tensor_scalar(lo[:, :], lo[:, :], sw[:, 2:3], None, ALU.mult))
                    link(dve.tensor_tensor(dw[:, :, :], lo[:, :].unsqueeze(1).broadcast_to([H, H, 3]),
                                           R.ident[0:H, 0:H].unsqueeze(2).broadcast_to([H, H, 3]), ALU.mult))
                    dve.sem_inc(S.sem("dw"), 1)
                    dve.wait_ge(S.sem("mix"), 1)
                    link(dve.tensor_copy(mix[:, :, :], p6[:, 0:3 * H].rearrange("p (h k) -> p h k", k=3)))
                    dve.wait_ge(S.sem("decorr"), 1)
                    link(dve.tensor_tensor(ca[:, :], mix[:, :, 1], dec[:, :], ALU.mult))
                    link(dve.tensor_tensor(ca[:, :], ca[:, :], mix[:, :, 0], ALU.add))
                    link(dve.tensor_tensor(ca[:, :], ca[:, :], qs[:, 2, :], ALU.mult))
                    link(dve.tensor_tensor(cb[:, :], mix[:, :, 2], qs[:, 3, :], ALU.mult))
                    link(dve.tensor_tensor(a[:, :, :], fqh, ca[:, :].unsqueeze(2).broadcast_to([P, H, HD]), ALU.mult))
                    link(dve.tensor_copy(cbw[:, :, :], cb[:, :].unsqueeze(2).broadcast_to([P, H, P])))
                    dve.sem_inc(S.sem("a"), 1)
                    dve.wait_ge(S.sem("a_turned"), 1)
                    link(dve.tensor_copy(aT[:, :, :], heads(p1[:, :, :])))
                    link(dve.tensor_copy(cbT[:, :, :], heads(p2[:, :, :])))
                    dve.sem_inc(S.sem("aT"), 1)
                    for h in range(H):
                        link(dve.tensor_scalar(yT[:, h, :], cbT[:, h, :], Msb[:, h, HD:HD + 1], None, ALU.mult))
                    dve.wait_ge(S.sem("mixed"), 1)
                    link(dve.tensor_tensor(yT[:, :, :], yT[:, :, :], heads(p1[:, :, :]), ALU.add))
                    dve.sem_inc(S.sem("yT"), 1)
                    link(dve.tensor_tensor(R.x[:, :], R.x[:, :], bo[:, :], ALU.add))
                    dve.wait_ge(S.sem("y"), 1)
                    dve.tensor_tensor(R.x[:, :], R.x[:, :], p3[:, 0:DIM], ALU.add)

                @block.tensor
                def _(pe):
                    pe.wait_ge(S.sem("qc"), 1)
                    for h in range(H):
                        last = pe.matmul(p1[:, h // 4, (h % 4) * P:(h % 4 + 1) * P], qc[:, h, :], qc[:, h, :],
                                         start=True, stop=True)
                    last.then_inc(S.sem("corr"), 1)
                    for h in range(H):
                        last = pe.matmul(p4[:, h:h + 1], fq[:, h * HD:(h + 1) * HD], ones[:, 0:1], start=True,
                                         stop=True)
                    last.then_inc(S.sem("q_mean"), 1)
                    pe.wait_ge(S.sem("corr_sq"), 1)
                    pe.matmul(p3[:, 0:H], ones[:, :], cs[:, :], start=True, stop=True).then_inc(
                        S.sem("corr_total"), 1)
                    pe.wait_ge(S.sem("gT"), 1)
                    pe.wait_ge(S.sem("late_loads"), loads.total)
                    for c in range(2):
                        last = pe.matmul(p5[0:H, 0:HD], gT[:, c, :], wp1[:, c, :], start=(c == 0), stop=(c == 1))
                    last.then_inc(S.sem("h1"), 1)
                    pe.wait_ge(S.sem("h1_relu"), 1)
                    pe.transpose(p5[:, 0:H], h1[:, :], R.ident[0:H, 0:H]).then_inc(S.sem("h1_turned"), 1)
                    pe.wait_ge(S.sem("h1T"), 1)
                    pe.matmul(p5[0:H, 0:3], h1T[:, :], w2[:, :], start=True, stop=True).then_inc(S.sem("logits"), 1)
                    pe.wait_ge(S.sem("dw"), 1)
                    pe.matmul(p6[:, 0:3 * H], ones[0:H, :], dw[:, :, :].rearrange("p h k -> p (h k)"),
                              start=True, stop=True).then_inc(S.sem("mix"), 1)
                    pe.wait_ge(S.sem("a"), 1)
                    for h in range(H):
                        pe.transpose(p1[:, h // 4, (h % 4) * P:(h % 4 + 1) * P], a[:, h, :], R.ident[:, :])
                        last = pe.matmul(p2[:, h // 4, (h % 4) * P:(h % 4 + 1) * P], cbw[:, h, :], R.ident[:, :],
                                         start=True, stop=True)
                    last.then_inc(S.sem("a_turned"), 1)
                    pe.wait_ge(S.sem("aT"), 1)
                    for h in range(H):
                        last = pe.matmul(p1[:, h // 4, (h % 4) * P:(h % 4 + 1) * P], Msb[:, h, 0:HD], aT[:, h, :],
                                         start=True, stop=True)
                    last.then_inc(S.sem("mixed"), 1)
                    pe.wait_ge(S.sem("yT"), 1)
                    for h in range(H):
                        last = pe.matmul(p3[:, 0:DIM], yT[:, h, :], wo[:, h, :], start=(h == 0), stop=(h == H - 1))
                    last.then_inc(S.sem("y"), 1)


INNER, STATES, TAPS = 512, 16, 4
IC = INNER // P


def conv_silu_vector(dve, link, S, pad, xc, sx, taps, bias):
    for c in range(IC):
        link(dve.tensor_scalar(xc[:, c, :], pad[:, c, 0:P], taps[:, c, 0:1], None, ALU.mult))
        for k in range(1, TAPS):
            link(dve.scalar_tensor_tensor(xc[:, c, :], pad[:, c, k:k + P], taps[:, c, k:k + 1], xc[:, c, :],
                                          ALU.mult, ALU.add))
        link(dve.tensor_scalar(xc[:, c, :], xc[:, c, :], bias[:, c:c + 1], None, ALU.add))
    dve.sem_inc(S.sem("conv"), 1)
    dve.wait_ge(S.sem("sigmoid"), 1)
    link(dve.tensor_tensor(xc[:, :, :], xc[:, :, :], sx[:, :, :], ALU.mult))


def softplus_vector(dve, link, S, src, mag, delta):
    link(dve.tensor_scalar(mag[:, :, :], src, -1.0, None, ALU.mult))
    dve.tensor_tensor(mag[:, :, :], mag[:, :, :], src, ALU.min).then_inc(S.sem("mag"), 1)
    link(dve.tensor_scalar(delta[:, :, :], src, 0.0, None, ALU.max))
    dve.wait_ge(S.sem("log1p"), 1)
    link(dve.tensor_tensor(delta[:, :, :], delta[:, :, :], mag[:, :, :], ALU.add))


def softplus_scalar(act, S, mag):
    act.wait_ge(S.sem("mag"), 1)
    act.activation(mag[:, :, :], mag[:, :, :], ACT.Exp).then_inc(S.sem("exp_mag"), 1)
    act.wait_ge(S.sem("exp_mag"), 1)
    act.activation(mag[:, :, :], mag[:, :, :], ACT.Ln, bias=1.0).then_inc(S.sem("log1p"), 1)


def mamba(nc, A, R, name, weights, selective):
    N3 = 16 + 2 * STATES
    with Stage(nc, name) as S:
        w_in = S.sb("w_in", [P, DC, 2 * INNER])
        w_out = S.sb("w_out", [P, IC, DIM])
        taps, cbias = S.sb("taps", [P, IC, TAPS]), S.sb("cbias", [P, IC])
        alog, dskip = S.sb("alog", [P, IC, STATES]), S.sb("dskip", [P, IC])
        xn, xT, nw = S.sb("xn", [P, DIM]), S.sb("xT", [P, DC, P]), S.sb("nw", [P, 16])
        pad = S.sb("pad", [P, IC, P + TAPS - 1])
        xc, sx, gate = S.sb("xc", [P, IC, P]), S.sb("sx", [P, IC, P]), S.sb("gate", [P, IC, P])
        mag, delta, u = S.sb("mag", [P, IC, P]), S.sb("delta", [P, IC, P]), S.sb("u", [P, IC, P])
        decay = [S.sb(f"decay{b}", [P, STATES, P]) for b in range(IC)]
        drive = [S.sb(f"drive{b}", [P, STATES, P]) for b in range(2)]
        state = [S.sb(f"state{b}", [P, STATES, P]) for b in range(2)]
        y = S.sb("y", [P, IC, P])
        if selective:
            wx, wdt, bdt = S.sb("wx", [P, IC, N3]), S.sb("wdt", [16, INNER]), S.sb("bdt", [P, IC])
            dbc = S.sb("dbc", [N3, P])
            bc = S.sb("bc", [P, 2 * STATES, P])
            bc_dram = nc.dram_tensor(f"{name}_bc_dram", (2 * STATES, P), F32, kind="Internal").ap()
            px = S.psum("px")
        pt, pi, pg, po = S.psum("pt"), S.psum("pi"), S.psum("pg"), S.psum("po")
        pd = S.psum("pd")
        loads = Loads(S.sem("loads"))
        with S.nc.Block() as block:
            @block.sync
            def _(sp):
                loads(sp.dma_start(w_in[:, :, :], by_rows(A[weights["in"]])))
                loads(sp.dma_start(w_out[:, :, :], by_rows(A[weights["out"]])))
                loads(sp.dma_start(taps[:, :, :], by_rows(A[weights["conv"]])))
                loads(sp.dma_start(cbias[:, :], column(A[weights["conv_b"]]), allow_slow_non_contiguous=True))
                loads(sp.dma_start(alog[:, :, :], by_rows(A[weights["A_log"]])))
                loads(sp.dma_start(dskip[:, :], column(A[weights["D"]]), allow_slow_non_contiguous=True))
                if selective:
                    loads(sp.dma_start(wx[:, :, :], by_rows(A["L2_attn_W_xproj"])))
                    loads(sp.dma_start(wdt[:, :], A["L2_attn_W_dt"]))
                    loads(sp.dma_start(bdt[:, :], column(A["L2_attn_b_dt"]), allow_slow_non_contiguous=True))
                    sp.wait_ge(S.sem("dbc"), 1)
                    sp.dma_start(bc_dram, dbc[16:N3, :]).then_inc(S.sem("bc_out"), 16)
                    sp.wait_ge(S.sem("bc_out"), 16)
                    sp.dma_start(bc[:, :, :], bc_dram.partition_broadcast(P)).then_inc(S.sem("bc"), 16)

            @block.vector
            def _(dve):
                link = Link(dve, S.sem("dve_link"))
                link(dve.memset(pad[:, :, :], 0.0))
                norm_vector(dve, link, S, "n", R.x[:, :], xn[:, :], nw)
                turn_vector(dve, S, "n", xT, pt)
                dve.wait_ge(S.sem("loads"), loads.total)
                dve.wait_ge(S.sem("in_proj"), 1)
                link(dve.tensor_copy(pad[:, :, TAPS - 1:], pi[:, :].rearrange("p (c t) -> p c t", c=IC)))
                conv_silu_vector(dve, link, S, pad, xc, sx, taps, cbias)
                dve.sem_inc(S.sem("xc"), 1)
                if selective:
                    dve.wait_ge(S.sem("x_proj"), 1)
                    dve.tensor_copy(dbc[:, :], px[0:N3, 0:P]).then_inc(S.sem("dbc"), 1)
                    dve.wait_ge(S.sem("dt_proj"), 1)
                    for c in range(IC):
                        link(dve.tensor_scalar(u[:, c, :], pd[:, c * P:(c + 1) * P], bdt[:, c:c + 1], None, ALU.add))
                    softplus_vector(dve, link, S, u[:, :, :], mag, delta)
                    link(dve.tensor_tensor(u[:, :, :], delta[:, :, :], xc[:, :, :], ALU.mult))
                else:
                    softplus_vector(dve, link, S, xc[:, :, :], mag, delta)
                    link(dve.tensor_tensor(u[:, :, :], xc[:, :, :], xc[:, :, :], ALU.mult))
                dve.wait_ge(S.sem("minus_a"), 1)
                for c in range(IC):
                    dve.tensor_tensor(decay[c][:, :, :],
                                      delta[:, c, :].unsqueeze(1).broadcast_to([P, STATES, P]),
                                      alog[:, c, :].unsqueeze(2).broadcast_to([P, STATES, P]),
                                      ALU.mult).then_inc(S.sem("rate"), 1)
                if selective:
                    dve.wait_ge(S.sem("bc"), 16)
                for c in range(IC):
                    b = c % 2
                    ub = u[:, c, :].unsqueeze(1).broadcast_to([P, STATES, P])
                    if selective:
                        link(dve.tensor_tensor(drive[b][:, :, :], ub, bc[:, 0:STATES, :], ALU.mult))
                    else:
                        link(dve.tensor_copy(drive[b][:, :, :], ub))
                    dve.wait_ge(S.sem("decay"), c + 1)
                    link(dve.memset(decay[c][:, :, 0:1], 0.0))
                    flat = lambda ap: ap[:, :, :].rearrange("p n t -> p (n t)")
                    link(dve.tensor_tensor_scan(flat(state[b]), flat(decay[c]), flat(drive[b]), 0.0, ALU.mult,
                                                ALU.add))
                    if selective:
                        link(dve.tensor_tensor(state[b][:, :, :], state[b][:, :, :], bc[:, STATES:, :], ALU.mult))
                    link(dve.tensor_reduce(y[:, c, :], state[b][:, :, :].rearrange("p n t -> p t n"), AX.X, ALU.add))
                dve.wait_ge(S.sem("gate"), 1)
                link(dve.tensor_tensor(gate[:, :, :], gate[:, :, :], pg[:, :].rearrange("p (c t) -> p c t", c=IC),
                                       ALU.mult))
                if selective:
                    for c in range(IC):
                        link(dve.scalar_tensor_tensor(y[:, c, :], xc[:, c, :], dskip[:, c:c + 1], y[:, c, :],
                                                      ALU.mult, ALU.add))
                    link(dve.tensor_tensor(y[:, :, :], y[:, :, :], gate[:, :, :], ALU.mult))
                else:
                    link(dve.tensor_tensor(y[:, :, :], y[:, :, :], xc[:, :, :], ALU.mult))
                    link(dve.tensor_tensor(y[:, :, :], y[:, :, :], gate[:, :, :], ALU.mult))
                    for c in range(IC):
                        link(dve.scalar_tensor_tensor(y[:, c, :], xc[:, c, :], dskip[:, c:c + 1], y[:, c, :],
                                                      ALU.mult, ALU.add))
                dve.sem_inc(S.sem("y"), 1)
                dve.wait_ge(S.sem("out_proj"), 1)
                dve.tensor_tensor(R.x[:, :], R.x[:, :], po[:, 0:DIM], ALU.add)

            @block.scalar
            def _(act):
                norm_scalar(act, S, "n", nw)
                act.wait_ge(S.sem("gate_proj"), 1)
                act.activation(gate[:, :, :], pg[:, :].rearrange("p (c t) -> p c t", c=IC), ACT.Sigmoid).then_inc(
                    S.sem("gate"), 1)
                act.wait_ge(S.sem("conv"), 1)
                act.activation(sx[:, :, :], xc[:, :, :], ACT.Sigmoid).then_inc(S.sem("sigmoid"), 1)
                act.wait_ge(S.sem("loads"), loads.total)
                act.activation(alog[:, :, :], alog[:, :, :], ACT.Exp).then_inc(S.sem("minus_a"), 1)
                softplus_scalar(act, S, mag)
                for c in range(IC):
                    act.wait_ge(S.sem("rate"), c + 1)
                    act.activation(decay[c][:, :, :], decay[c][:, :, :], ACT.Exp, scale=-1.0).then_inc(
                        S.sem("decay"), 1)

            @block.tensor
            def _(pe):
                turn_tensor(pe, S, "n", xn, pt, R.ident)
                pe.wait_ge(S.sem("loads"), loads.total)
                pe.wait_ge(S.sem("n_xT"), 1)
                for side, out, signal in ((0, pi, "in_proj"), (1, pg, "gate_proj")):
                    for o in range(IC):
                        for c in range(DC):
                            at = side * INNER + o * P
                            last = pe.matmul(out[:, o * P:(o + 1) * P], w_in[:, c, at:at + P], xT[:, c, :],
                                             start=(c == 0), stop=(c == DC - 1))
                    last.then_inc(S.sem(signal), 1)
                if selective:
                    pe.wait_ge(S.sem("xc"), 1)
                    for c in range(IC):
                        last = pe.matmul(px[0:N3, 0:P], wx[:, c, :], xc[:, c, :], start=(c == 0),
                                         stop=(c == IC - 1))
                    last.then_inc(S.sem("x_proj"), 1)
                    pe.wait_ge(S.sem("dbc"), 1)
                    for c in range(IC):
                        last = pe.matmul(pd[:, c * P:(c + 1) * P], wdt[:, c * P:(c + 1) * P], dbc[0:16, :],
                                         start=True, stop=True)
                    last.then_inc(S.sem("dt_proj"), 1)
                pe.wait_ge(S.sem("y"), 1)
                for c in range(IC):
                    last = pe.matmul(po[:, 0:DIM], y[:, c, :], w_out[:, c, :], start=(c == 0), stop=(c == IC - 1))
                last.then_inc(S.sem("out_proj"), 1)


def l0_attn(nc, A, R):
    mamba(nc, A, R, "l0a", {"in": "L0_attn_W_in", "out": "L0_attn_W_out", "conv": "L0_attn_conv_w",
                            "conv_b": "L0_attn_conv_b", "A_log": "L0_attn_A_log", "D": "L0_attn_D"}, False)


def l2_attn(nc, A, R):
    mamba(nc, A, R, "l2a", {"in": "L2_attn_W_in", "out": "L2_attn_W_out", "conv": "L2_attn_W_conv",
                            "conv_b": "L2_attn_b_conv", "A_log": "L2_attn_A_log", "D": "L2_attn_D"}, True)


def l1_attn(nc, A, R):
    H, HD = 16, 16
    with Stage(nc, "l1a") as S:
        names = ("r", "k", "v", "g")
        w = S.sb("w", [P, 5, DC, DIM])
        mixc = S.sb("mixc", [P, 4, DC])
        omm = S.sb("omm", [P, 4, DC])
        td, u = S.sb("td", [P, H]), S.sb("u", [P, H])
        lnw, lnb = S.sb("lnw", [P, DIM]), S.sb("lnb", [P, DIM])
        lag, later, hm = S.sb("lag", [P, P]), S.sb("later", [P, P]), S.sb("hm", [P, 8])
        xn, nw = S.sb("xn", [P, DIM]), S.sb("nw", [P, 16])
        xp = S.sb("xp", [P, DC, P + 1])
        xm = S.sb("xm", [P, 4, DC, P])
        rb = [S.sb(f"rb{c}", [P, 8, P]) for c in range(DC)]
        kT, v, g = S.sb("kT", [P, DC, P]), S.sb("v", [P, DIM]), S.sb("g", [P, DIM])
        wm = S.sb("wm", [P, H, P])
        att = S.sb("att", [P, H, P])
        o, oc, sq = S.sb("o", [P, H, HD]), S.sb("oc", [P, H, HD]), S.sb("sq", [P, H, HD])
        m, va = S.sb("m", [P, H]), S.sb("va", [P, H])
        oT = S.sb("oT", [P, DC, P])
        pt, prk, pvg, po = S.psum("pt"), S.psum("prk"), S.psum("pvg"), S.psum("po")
        pa = S.psum("pa", 4)
        loads = Loads(S.sem("loads"))
        with S.nc.Block() as block:
            @block.sync
            def _(sp):
                for n, name in enumerate(names):
                    loads(sp.dma_start(w[:, n, :, :], by_rows(A[f"L1_attn_W_{name}"])))
                    loads(sp.dma_start(mixc[:, n, :], column(A[f"L1_attn_time_mix_{name}"]),
                                       allow_slow_non_contiguous=True))
                loads(sp.dma_start(w[:, 4, :, :], by_rows(A["L1_attn_W_o"])))
                loads(sp.dma_start(td[:, :], A["L1_attn_time_decay"].partition_broadcast(P)))
                loads(sp.dma_start(u[:, :], A["L1_attn_time_faaaa"].partition_broadcast(P)))
                loads(sp.dma_start(lnw[:, :], A["L1_attn_ln_w"].partition_broadcast(P)))
                loads(sp.dma_start(lnb[:, :], A["L1_attn_ln_b"].partition_broadcast(P)))
                loads(sp.dma_start(lag[:, :], A["c_lag"]))
                loads(sp.dma_start(later[:, :], A["c_later"]))
                loads(sp.dma_start(hm[:, :], A["c_head16"]))

            @block.vector
            def _(dve):
                link = Link(dve, S.sem("dve_link"))
                link(dve.memset(xp[:, :, :], 0.0))
                norm_vector(dve, link, S, "n", R.x[:, :], xn[:, :], nw)
                dve.wait_ge(S.sem("n_turned"), 1)
                link(dve.tensor_copy(xp[:, :, 1:], pt[:, 0:DIM].rearrange("p (c t) -> p c t", c=DC)))
                dve.wait_ge(S.sem("loads"), loads.total)
                link(dve.tensor_scalar(omm[:, :, :], mixc[:, :, :], -1.0, 1.0, ALU.mult, ALU.add))
                for n in range(4):
                    for c in range(DC):
                        link(dve.tensor_scalar(xm[:, n, c, :], xp[:, c, 0:P], omm[:, n, c:c + 1], None, ALU.mult))
                        link(dve.scalar_tensor_tensor(xm[:, n, c, :], xp[:, c, 1:], mixc[:, n, c:c + 1],
                                                      xm[:, n, c, :], ALU.mult, ALU.add))
                dve.sem_inc(S.sem("mixed"), 1)
                dve.wait_ge(S.sem("rk"), 1)
                for c in range(DC):
                    link(dve.tensor_tensor(rb[c][:, :, :],
                                           prk[:, c * P:(c + 1) * P].unsqueeze(1).broadcast_to([P, 8, P]),
                                           hm[:, :].unsqueeze(2).broadcast_to([P, 8, P]), ALU.mult))
                link(dve.tensor_copy(kT[:, :, :], prk[:, DIM:2 * DIM].rearrange("p (c t) -> p c t", c=DC)))
                dve.sem_inc(S.sem("rk_ready"), 1)
                dve.wait_ge(S.sem("rates"), 1)
                dve.tensor_scalar(td[:, :], td[:, :], 1e30, -1.0, ALU.min, ALU.mult).then_inc(S.sem("rate"), 1)
                dve.wait_ge(S.sem("powers"), 1)
                link(dve.tensor_tensor(wm[:, :, :], wm[:, :, :],
                                       later[:, :].unsqueeze(1).broadcast_to([P, H, P]), ALU.mult))
                for h in range(H):
                    link(dve.scalar_tensor_tensor(wm[:, h, :], R.ident[:, :], u[:, h:h + 1], wm[:, h, :],
                                                  ALU.mult, ALU.add))
                dve.wait_ge(S.sem("att"), 1)
                link(dve.tensor_tensor(att[:, :, :], pa[:, :, :].rearrange("p a (b q) -> p (a b) q", q=P),
                                       wm[:, :, :], ALU.mult))
                dve.wait_ge(S.sem("vg"), 1)
                dve.tensor_copy(v[:, :], pvg[:, 0:DIM]).then_inc(S.sem("att_ready"), 1)
                dve.wait_ge(S.sem("gate"), 1)
                link(dve.tensor_tensor(g[:, :], g[:, :], pvg[:, DIM:2 * DIM], ALU.mult))
                dve.wait_ge(S.sem("out"), 1)
                link(dve.tensor_scalar(o[:, :, :], po[:, 0:DIM].rearrange("p (h d) -> p h d", h=H), 1.0 / 8.0, None,
                                       ALU.mult))
                link(dve.tensor_reduce(m[:, :], o[:, :, :], AX.X, ALU.add))
                link(dve.tensor_scalar(m[:, :], m[:, :], 1.0 / HD, None, ALU.mult))
                link(dve.tensor_tensor(oc[:, :, :], o[:, :, :], m[:, :].unsqueeze(2).broadcast_to([P, H, HD]),
                                       ALU.subtract))
                link(dve.tensor_tensor(sq[:, :, :], oc[:, :, :], oc[:, :, :], ALU.mult))
                link(dve.tensor_reduce(va[:, :], sq[:, :, :], AX.X, ALU.add))
                dve.tensor_scalar(va[:, :], va[:, :], 1.0 / HD, EPS, ALU.mult, ALU.add).then_inc(S.sem("o_var"), 1)
                dve.wait_ge(S.sem("o_std"), 1)
                link(dve.reciprocal(va[:, :], va[:, :]))
                link(dve.tensor_tensor(oc[:, :, :], oc[:, :, :], va[:, :].unsqueeze(2).broadcast_to([P, H, HD]),
                                       ALU.mult))
                flat = oc[:, :, :].rearrange("p h d -> p (h d)")
                link(dve.tensor_tensor(xn[:, :], flat, lnw[:, :], ALU.mult))
                link(dve.tensor_tensor(xn[:, :], xn[:, :], lnb[:, :], ALU.add))
                dve.tensor_tensor(xn[:, :], xn[:, :], g[:, :], ALU.mult).then_inc(S.sem("gated"), 1)
                turn_vector(dve, S, "o", oT, pt)
                dve.wait_ge(S.sem("y"), 1)
                dve.tensor_tensor(R.x[:, :], R.x[:, :], po[:, DIM:2 * DIM], ALU.add)

            @block.scalar
            def _(act):
                norm_scalar(act, S, "n", nw)
                act.wait_ge(S.sem("loads"), loads.total)
                act.activation(td[:, :], td[:, :], ACT.Exp).then_inc(S.sem("rates"), 1)
                act.wait_ge(S.sem("rate"), 1)
                for h in range(H):
                    last = act.activation(wm[:, h, :], lag[:, :], ACT.Exp, scale=td[:, h:h + 1])
                last.then_inc(S.sem("powers"), 1)
                act.wait_ge(S.sem("vg"), 1)
                act.wait_ge(S.sem("att_ready"), 1)
                act.activation(g[:, :], pvg[:, DIM:2 * DIM], ACT.Sigmoid).then_inc(S.sem("gate"), 1)
                act.wait_ge(S.sem("o_var"), 1)
                act.activation(va[:, :], va[:, :], ACT.Sqrt).then_inc(S.sem("o_std"), 1)

            @block.tensor
            def _(pe):
                turn_tensor(pe, S, "n", xn, pt, R.ident)
                pe.wait_ge(S.sem("loads"), loads.total)
                pe.wait_ge(S.sem("mixed"), 1)
                for n in range(2):
                    for oo in range(DC):
                        for c in range(DC):
                            at = n * DIM + oo * P
                            last = pe.matmul(prk[:, at:at + P], w[:, n, c, oo * P:(oo + 1) * P], xm[:, n, c, :],
                                             start=(c == 0), stop=(c == DC - 1))
                last.then_inc(S.sem("rk"), 1)
                for n in range(2):
                    for c in range(DC):
                        last = pe.matmul(pvg[:, n * DIM:(n + 1) * DIM], xm[:, 2 + n, c, :], w[:, 2 + n, c, :],
                                         start=(c == 0), stop=(c == DC - 1))
                last.then_inc(S.sem("vg"), 1)
                pe.wait_ge(S.sem("rk_ready"), 1)
                for c in range(DC):
                    for half in range(2):
                        last = pe.matmul(pa[:, 2 * c + half, :], kT[:, c, :],
                                         rb[c][:, 4 * half:4 * half + 4, :].rearrange("p h q -> p (h q)"),
                                         start=True, stop=True)
                last.then_inc(S.sem("att"), 1)
                pe.wait_ge(S.sem("att_ready"), 1)
                for h in range(H):
                    last = pe.matmul(po[:, h * HD:(h + 1) * HD], att[:, h, :], v[:, h * HD:(h + 1) * HD],
                                     start=True, stop=True)
                last.then_inc(S.sem("out"), 1)
                turn_tensor(pe, S, "o", xn, pt, R.ident, ready="gated")
                pe.wait_ge(S.sem("o_xT"), 1)
                for c in range(DC):
                    last = pe.matmul(po[:, DIM:2 * DIM], oT[:, c, :], w[:, 4, c, :], start=(c == 0),
                                     stop=(c == DC - 1))
                last.then_inc(S.sem("y"), 1)


def l0_ffn(nc, A, R):
    E, FF = 8, 1024
    FC = FF // P
    with Stage(nc, "l0f") as S:
        w1 = [S.sb(f"w1_{b}", [P, DC, FF]) for b in range(2)]
        w2 = [S.sb(f"w2_{b}", [P, FC, DIM]) for b in range(2)]
        b1, b1r = S.sb("b1", [P, E + 1, FC]), S.sb("b1r", [(E + 1) * FC, P])
        b2, b2s = S.sb("b2", [E, DIM]), S.sb("b2s", [P, DIM])
        wr, br = S.sb("wr", [P, DC, E]), S.sb("br", [P, E])
        xn, xT, nw = S.sb("xn", [P, DIM]), S.sb("xT", [P, DC, P]), S.sb("nw", [P, 16])
        lg, pr, tmp, oh = S.sb("lg", [P, E]), S.sb("pr", [P, E]), S.sb("tmp", [P, E]), S.sb("oh", [P, E + 1])
        oh2, sw, wt = S.sb("oh2", [P, E + 1]), S.sb("sw", [P, 8]), S.sb("wt", [P, E])
        weT = S.sb("weT", [E, P])
        hT = [S.sb(f"hT{b}", [P, FC, P]) for b in range(2)]
        acc = S.sb("acc", [P, DIM])
        pt, pm = S.psum("pt"), S.psum("pm")
        ph = [S.psum(f"ph{b}", 2) for b in range(2)]
        py = [S.psum(f"py{b}") for b in range(2)]
        loads = Loads(S.sem("small"))

        def hidden(pe, b):
            for f in range(FC):
                for c in range(DC):
                    last = pe.matmul(ph[b][:, f // 4, (f % 4) * P:(f % 4 + 1) * P], w1[b][:, c, f * P:(f + 1) * P],
                                     xT[:, c, :], start=(c == 0), stop=(c == DC - 1))
            last.then_inc(S.counted(f"h{b}"), 1)

        def output(pe, b):
            for f in range(FC):
                last = pe.matmul(py[b][:, 0:DIM], hT[b][:, f, :], w2[b][:, f, :], start=(f == 0), stop=(f == FC - 1))
            last.then_inc(S.counted(f"y{b}"), 1)

        def gelu(act, b, bias):
            for f in range(FC):
                last = act.activation(hT[b][:, f, :], ph[b][:, f // 4, (f % 4) * P:(f % 4 + 1) * P], ACT.Gelu,
                                      bias=bias(f))
            last.then_inc(S.counted(f"hT{b}"), 1)

        with S.nc.Block() as block:
            @block.sync
            def _(sp):
                sp.dma_start(w1[0][:, :, :], by_rows(A["L0_ffn_shared_w1"])).then_inc(S.counted("w1_0"), 16)
                sp.dma_start(w2[0][:, :, :], by_rows(A["L0_ffn_shared_w2"])).then_inc(S.counted("w2_0"), 16)
                loads(sp.dma_start(b1r[0:E * FC, :], A["L0_ffn_exp_b1"].rearrange("e (f p) -> (e f) p", p=P)))
                loads(sp.dma_start(b1r[E * FC:, :], A["L0_ffn_shared_b1"].rearrange("(f p) -> f p", p=P)))
                loads(sp.dma_start(b2[:, :], A["L0_ffn_exp_b2"]))
                loads(sp.dma_start(b2s[:, :], A["L0_ffn_shared_b2"].partition_broadcast(P)))
                loads(sp.dma_start(wr[:, :, :], by_rows(A["L0_ffn_router_w"])))
                loads(sp.dma_start(br[:, :], A["L0_ffn_router_b"].partition_broadcast(P)))
                with sp.Fori(0, E // 2) as i:
                    for b in (1, 0):
                        e = i * 2 + (1 - b)
                        after(sp, S.counted(f"used{b}"), i + (1 - b))
                        sp.dma_start(w1[b][:, :, :], A["L0_ffn_exp_w1"][bass.ds(e, 1)].rearrange(
                            "e (c p) n -> p (e c) n", p=P)).then_inc(S.counted(f"w1_{b}"), 16)
                        sp.dma_start(w2[b][:, :, :], A["L0_ffn_exp_w2"][bass.ds(e, 1)].rearrange(
                            "e (c p) n -> p (e c) n", p=P)).then_inc(S.counted(f"w2_{b}"), 16)

            @block.vector
            def _(dve):
                link = Link(dve, S.sem("dve_link"))
                norm_vector(dve, link, S, "n", R.x[:, :], xn[:, :], nw)
                turn_vector(dve, S, "n", xT, pt)
                dve.wait_ge(S.sem("b1_turned"), 1)
                dve.tensor_copy(b1[:, :, :], pm[:, 0:(E + 1) * FC].rearrange("p (e f) -> p e f", f=FC)).then_inc(
                    S.sem("b1_ready"), 1)
                dve.wait_ge(S.sem("small"), loads.total)
                dve.wait_ge(S.sem("router"), 1)
                link(dve.tensor_tensor(lg[:, :], pt[:, 0:E], br[:, :], ALU.add))
                softmax8_vector(dve, link, S, "r", lg[:, :], pr[:, :], sw)
                first_of_max(dve, link, oh, pr[:, :], sw[:, 3:4], tmp[:, :], R.idx_down[:, :])
                link(dve.scalar_tensor_tensor(lg[:, :], oh[:, 0:E], -2.0, pr[:, :], ALU.mult, ALU.add))
                first_of_max(dve, link, oh2, lg[:, :], sw[:, 4:5], tmp[:, :], R.idx_down[:, :])
                link(dve.tensor_tensor(oh[:, 0:E], oh[:, 0:E], oh2[:, 0:E], ALU.add))
                link(dve.tensor_tensor(sw[:, 5:6], sw[:, 3:4], sw[:, 4:5], ALU.add))
                link(dve.tensor_scalar(sw[:, 5:6], sw[:, 5:6], 1e-9, None, ALU.add))
                link(dve.reciprocal(sw[:, 5:6], sw[:, 5:6]))
                link(dve.tensor_tensor(wt[:, :], pr[:, :], oh[:, 0:E], ALU.mult))
                link(dve.tensor_scalar(wt[:, :], wt[:, :], sw[:, 5:6], None, ALU.mult))
                dve.sem_inc(S.sem("weights_of_experts"), 1)
                dve.wait_ge(S.sem("we_turned"), 1)
                dve.tensor_copy(weT[:, :], pm[0:E, P:2 * P]).then_inc(S.sem("weT_ready"), 1)
                dve.wait_ge(S.sem("b2_mixed"), 1)
                link(dve.tensor_tensor(acc[:, :], pm[:, DIM:2 * DIM], R.x[:, :], ALU.add))
                link(dve.tensor_tensor(acc[:, :], acc[:, :], b2s[:, :], ALU.add))
                after(dve, S.counted("y0"), 1)
                dve.tensor_tensor(acc[:, :], acc[:, :], py[0][:, 0:DIM], ALU.add).then_inc(S.counted("acc_link"), 1)
                with dve.Fori(0, E // 2) as i:
                    for b in (1, 0):
                        e = i * 2 + (1 - b)
                        after(dve, S.counted(f"y{b}"), i + (2 - b))
                        after(dve, S.counted("acc_link"), e + 1)
                        dve.scalar_tensor_tensor(acc[:, :], py[b][:, 0:DIM], wt[:, bass.ds(e, 1)], acc[:, :],
                                                 ALU.mult, ALU.add).then_inc(S.counted("acc_link"), 1)
                after(dve, S.counted("acc_link"), E + 1)
                dve.tensor_copy(R.x[:, :], acc[:, :])

            @block.scalar
            def _(act):
                norm_scalar(act, S, "n", nw)
                softmax8_scalar(act, S, "r", pr[:, :], sw)
                act.wait_ge(S.sem("b1_ready"), 1)
                after(act, S.counted("h0"), 1)
                gelu(act, 0, lambda f: b1[:, E, f:f + 1])
                with act.Fori(0, E // 2) as i:
                    for b in (1, 0):
                        e = i * 2 + (1 - b)
                        act.wait_ge(S.sem("b1_ready"), 1)
                        after(act, S.counted(f"h{b}"), i + (2 - b))
                        after(act, S.counted(f"y{b}"), i + (1 - b))
                        gelu(act, b, lambda f: b1[:, bass.ds(e, 1), f])

            @block.tensor
            def _(pe):
                turn_tensor(pe, S, "n", xn, pt, R.ident)
                pe.wait_ge(S.sem("small"), loads.total)
                pe.transpose(pm[:, 0:(E + 1) * FC], b1r[:, :], R.ident[0:(E + 1) * FC, 0:(E + 1) * FC]).then_inc(
                    S.sem("b1_turned"), 1)
                pe.wait_ge(S.sem("n_xT"), 1)
                for c in range(DC):
                    last = pe.matmul(pt[:, 0:E], xT[:, c, :], wr[:, c, :], start=(c == 0), stop=(c == DC - 1))
                last.then_inc(S.sem("router"), 1)
                after(pe, S.counted("w1_0"), 16)
                hidden(pe, 0)
                after(pe, S.counted("w2_0"), 16)
                after(pe, S.counted("hT0"), 1)
                output(pe, 0)
                after(pe, S.counted("y0"), 1)
                pe.sem_inc(S.counted("used0"), 1)
                pe.wait_ge(S.sem("weights_of_experts"), 1)
                pe.wait_ge(S.sem("b1_ready"), 1)
                pe.transpose(pm[0:E, P:2 * P], wt[:, :], R.ident[:, :]).then_inc(S.sem("we_turned"), 1)
                pe.wait_ge(S.sem("weT_ready"), 1)
                pe.matmul(pm[:, DIM:2 * DIM], weT[:, :], b2[:, :], start=True, stop=True).then_inc(
                    S.sem("b2_mixed"), 1)
                with pe.Fori(0, E // 2) as i:
                    for b in (1, 0):
                        after(pe, S.counted(f"w1_{b}"), (i + (2 - b)) * 16)
                        after(pe, S.counted(f"hT{b}"), i + (1 - b))
                        hidden(pe, b)
                    for b in (1, 0):
                        after(pe, S.counted(f"w2_{b}"), (i + (2 - b)) * 16)
                        after(pe, S.counted(f"hT{b}"), i + (2 - b))
                        after(pe, S.counted("acc_link"), i * 2 + (1 - b))
                        output(pe, b)
                        after(pe, S.counted(f"y{b}"), i + (2 - b))
                        pe.sem_inc(S.counted(f"used{b}"), 1)

            @block.gpsimd
            def _(pool):
                start_counts(pool, S)


def l1_ffn(nc, A, R):
    E, FF = 8, 1024
    FC = FF // P
    with Stage(nc, "l1f") as S:
        w1 = [S.sb(f"w1_{b}", [P, DC, FF]) for b in range(2)]
        w2 = [S.sb(f"w2_{b}", [P, FC, DIM]) for b in range(2)]
        b1, b1r, b2 = S.sb("b1", [P, E, FC]), S.sb("b1r", [E * FC, P]), S.sb("b2", [E, DIM])
        wr, br = S.sb("wr", [P, DC, E]), S.sb("br", [P, E])
        xn, xT, nw = S.sb("xn", [P, DIM]), S.sb("xT", [P, DC, P]), S.sb("nw", [P, 16])
        lg, pr, tmp, oh = S.sb("lg", [P, E]), S.sb("pr", [P, E]), S.sb("tmp", [P, E]), S.sb("oh", [P, E + 1])
        sw, ohw, ones = S.sb("sw", [P, 4]), S.sb("ohw", [P, E, P]), S.sb("ones", [E, P])
        xe = S.sb("xe", [P, E, DC, P])
        hT = [S.sb(f"hT{b}", [P, FC, P]) for b in range(2)]
        xv = [S.sb(f"xv{b}", [P, DC, P]) for b in range(2)]
        pt, pb = S.psum("pt"), S.psum("pb", 2)
        ph = [S.psum(f"ph{b}", 2) for b in range(2)]
        py = S.psum("py")
        loads = Loads(S.sem("small"))
        with S.nc.Block() as block:
            @block.sync
            def _(sp):
                loads(sp.dma_start(b1r[:, :], A["L1_ffn_b1"].rearrange("e (f p) -> (e f) p", p=P)))
                loads(sp.dma_start(b2[:, :], A["L1_ffn_b2"]))
                loads(sp.dma_start(wr[:, :, :], by_rows(A["L1_ffn_Wr"])))
                loads(sp.dma_start(br[:, :], A["L1_ffn_br"].partition_broadcast(P)))
                with sp.Fori(0, E // 2) as i:
                    for b in range(2):
                        e = i * 2 + b
                        after(sp, S.counted(f"used{b}"), i)
                        sp.dma_start(w1[b][:, :, :], A["L1_ffn_W1"][bass.ds(e, 1)].rearrange(
                            "e (c p) n -> p (e c) n", p=P)).then_inc(S.counted(f"w1_{b}"), 16)
                        sp.dma_start(w2[b][:, :, :], A["L1_ffn_W2"][bass.ds(e, 1)].rearrange(
                            "e (c p) n -> p (e c) n", p=P)).then_inc(S.counted(f"w2_{b}"), 16)

            @block.vector
            def _(dve):
                link = Link(dve, S.sem("dve_link"))
                link(dve.memset(ones[:, :], 1.0))
                norm_vector(dve, link, S, "n", R.x[:, :], xn[:, :], nw)
                turn_vector(dve, S, "n", xT, pt)
                dve.wait_ge(S.sem("b1_turned"), 1)
                dve.tensor_copy(b1[:, :, :], pb[:, 0, 0:E * FC].rearrange("p (e f) -> p e f", f=FC)).then_inc(
                    S.sem("b1_ready"), 1)
                dve.wait_ge(S.sem("small"), loads.total)
                dve.wait_ge(S.sem("router"), 1)
                link(dve.tensor_tensor(lg[:, :], pt[:, 0:E], br[:, :], ALU.add))
                softmax8_vector(dve, link, S, "r", lg[:, :], pr[:, :], sw)
                first_of_max(dve, link, oh, pr[:, :], sw[:, 3:4], tmp[:, :], R.idx_down[:, :])
                dve.tensor_copy(ohw[:, :, :], oh[:, 0:E].unsqueeze(2).broadcast_to([P, E, P])).then_inc(
                    S.sem("chosen"), 1)
                dve.wait_ge(S.sem("chosen_rows"), 1)
                for c in range(DC):
                    last = dve.tensor_tensor(xe[:, :, c, :], xT[:, c, :].unsqueeze(1).broadcast_to([P, E, P]),
                                             pb[:, :, :].rearrange("p a (b t) -> p (a b) t", t=P), ALU.mult)
                    link(last)
                dve.sem_inc(S.sem("xe"), 1)
                with dve.Fori(0, E // 2) as i:
                    for b in range(2):
                        after(dve, S.counted(f"h{b}"), i)
                        dve.tensor_copy(xv[b][:, :, :], xe[:, bass.ds(i * 2 + b, 1)].squeeze(1)).then_inc(
                            S.counted(f"xv{b}"), 1)
                dve.wait_ge(S.sem("y"), 1)
                dve.tensor_tensor(R.x[:, :], R.x[:, :], py[:, 0:DIM], ALU.add)

            @block.scalar
            def _(act):
                norm_scalar(act, S, "n", nw)
                softmax8_scalar(act, S, "r", pr[:, :], sw)
                act.wait_ge(S.sem("b1_ready"), 1)
                with act.Fori(0, E // 2) as i:
                    for b in range(2):
                        act.wait_ge(S.sem("b1_ready"), 1)
                        after(act, S.counted(f"h{b}"), i + 1)
                        after(act, S.counted(f"used{b}"), i)
                        for f in range(FC):
                            last = act.activation(hT[b][:, f, :], ph[b][:, f // 4, (f % 4) * P:(f % 4 + 1) * P],
                                                  ACT.Relu, bias=b1[:, bass.ds(i * 2 + b, 1), f])
                        last.then_inc(S.counted(f"hT{b}"), 1)

            @block.tensor
            def _(pe):
                turn_tensor(pe, S, "n", xn, pt, R.ident)
                pe.wait_ge(S.sem("small"), loads.total)
                pe.transpose(pb[:, 0, 0:E * FC], b1r[:, :], R.ident[0:E * FC, 0:E * FC]).then_inc(
                    S.sem("b1_turned"), 1)
                pe.wait_ge(S.sem("n_xT"), 1)
                for c in range(DC):
                    last = pe.matmul(pt[:, 0:E], xT[:, c, :], wr[:, c, :], start=(c == 0), stop=(c == DC - 1))
                last.then_inc(S.sem("router"), 1)
                pe.wait_ge(S.sem("chosen"), 1)
                pe.wait_ge(S.sem("b1_ready"), 1)
                for e in range(E):
                    last = pe.matmul(pb[:, e // 4, (e % 4) * P:(e % 4 + 1) * P], ohw[:, e, :], R.ident[:, :],
                                     start=True, stop=True)
                last.then_inc(S.sem("chosen_rows"), 1)
                pe.matmul(py[:, 0:DIM], ones[:, :], b2[:, :], start=True, stop=False, skip_group_check=True)
                with pe.Fori(0, E // 2) as i:
                    for b in range(2):
                        after(pe, S.counted(f"w1_{b}"), (i + 1) * 16)
                        after(pe, S.counted(f"xv{b}"), i + 1)
                        after(pe, S.counted(f"hT{b}"), i)
                        for f in range(FC):
                            for c in range(DC):
                                last = pe.matmul(ph[b][:, f // 4, (f % 4) * P:(f % 4 + 1) * P],
                                                 w1[b][:, c, f * P:(f + 1) * P], xv[b][:, c, :],
                                                 start=(c == 0), stop=(c == DC - 1))
                        last.then_inc(S.counted(f"h{b}"), 1)
                    for b in range(2):
                        after(pe, S.counted(f"w2_{b}"), (i + 1) * 16)
                        after(pe, S.counted(f"hT{b}"), i + 1)
                        for f in range(FC):
                            last = pe.matmul(py[:, 0:DIM], hT[b][:, f, :], w2[b][:, f, :], start=False, stop=False,
                                             skip_group_check=True)
                        last.then_inc(S.counted(f"used{b}"), 1)
                for b in range(2):
                    after(pe, S.counted(f"used{b}"), E // 2)
                pe.sem_inc(S.sem("y"), 1)

            @block.gpsimd
            def _(pool):
                start_counts(pool, S)


def l2_ffn(nc, A, R):
    E, HID = 8, 128
    with Stage(nc, "l2f") as S:
        w1, b1, w2, b2 = S.sb("w1", [P, DC, HID]), S.sb("b1", [P, 1]), S.sb("w2", [P, E]), S.sb("b2", [P, E])
        we, be = S.sb("we", [P, E, DC, DIM]), S.sb("be", [E, DIM])
        xn, xT, nw = S.sb("xn", [P, DIM]), S.sb("xT", [P, DC, P]), S.sb("nw", [P, 16])
        hT = S.sb("hT", [P, P])
        lg, pr, tmp, oh = S.sb("lg", [P, E]), S.sb("pr", [P, E]), S.sb("tmp", [P, E]), S.sb("oh", [P, E + 1])
        sw, ohw, ohT = S.sb("sw", [P, 4]), S.sb("ohw", [P, E, P]), S.sb("ohT", [E, P])
        xe = S.sb("xe", [P, E, DC, P])
        pt, ph, pl, po, py = [S.psum(n) for n in ("pt", "ph", "pl", "po", "py")]
        pb = S.psum("pb", 2)
        loads = Loads(S.sem("loads"))
        experts = Loads(S.sem("experts"))
        with S.nc.Block() as block:
            @block.sync
            def _(sp):
                loads(sp.dma_start(w1[:, :, :], by_rows(A["L2_ffn_w1"])))
                loads(sp.dma_start(b1[:, :], column(A["L2_ffn_b1"]), allow_slow_non_contiguous=True))
                loads(sp.dma_start(w2[:, :], A["L2_ffn_w2"]))
                loads(sp.dma_start(b2[:, :], A["L2_ffn_b2"].partition_broadcast(P)))
                loads(sp.dma_start(be[:, :], A["L2_ffn_expert_b"]))
                experts(sp.dma_start(we[:, :, :, :].rearrange("p e c n -> p (e c) n"),
                                     A["L2_ffn_expert_W"].rearrange("e (c p) n -> p (e c) n", p=P)))

            @block.vector
            def _(dve):
                link = Link(dve, S.sem("dve_link"))
                norm_vector(dve, link, S, "n", R.x[:, :], xn[:, :], nw)
                turn_vector(dve, S, "n", xT, pt)
                dve.wait_ge(S.sem("loads"), loads.total)
                dve.wait_ge(S.sem("h"), 1)
                dve.tensor_scalar(hT[:, :], ph[:, 0:P], b1[:, 0:1], 0.0, ALU.add, ALU.max).then_inc(S.sem("hT"), 1)
                dve.wait_ge(S.sem("router"), 1)
                link(dve.tensor_tensor(lg[:, :], pl[:, 0:E], b2[:, :], ALU.add))
                softmax8_vector(dve, link, S, "r", lg[:, :], pr[:, :], sw)
                first_of_max(dve, link, oh, pr[:, :], sw[:, 3:4], tmp[:, :], R.idx_down[:, :])
                dve.tensor_copy(ohw[:, :, :], oh[:, 0:E].unsqueeze(2).broadcast_to([P, E, P])).then_inc(
                    S.sem("chosen"), 1)
                dve.wait_ge(S.sem("chosen_rows"), 1)
                dve.tensor_copy(ohT[:, :], po[0:E, 0:P]).then_inc(S.sem("ohT"), 1)
                for c in range(DC):
                    link(dve.tensor_tensor(xe[:, :, c, :], xT[:, c, :].unsqueeze(1).broadcast_to([P, E, P]),
                                           pb[:, :, :].rearrange("p a (b t) -> p (a b) t", t=P), ALU.mult))
                dve.sem_inc(S.sem("xe"), 1)
                dve.wait_ge(S.sem("y"), 1)
                dve.tensor_tensor(R.x[:, :], R.x[:, :], py[:, 0:DIM], ALU.add)

            @block.scalar
            def _(act):
                norm_scalar(act, S, "n", nw)
                softmax8_scalar(act, S, "r", pr[:, :], sw)

            @block.tensor
            def _(pe):
                turn_tensor(pe, S, "n", xn, pt, R.ident)
                pe.wait_ge(S.sem("loads"), loads.total)
                pe.wait_ge(S.sem("n_xT"), 1)
                for c in range(DC):
                    last = pe.matmul(ph[:, 0:P], w1[:, c, :], xT[:, c, :], start=(c == 0), stop=(c == DC - 1))
                last.then_inc(S.sem("h"), 1)
                pe.wait_ge(S.sem("hT"), 1)
                pe.matmul(pl[:, 0:E], hT[:, :], w2[:, :], start=True, stop=True).then_inc(S.sem("router"), 1)
                pe.wait_ge(S.sem("chosen"), 1)
                for e in range(E):
                    pe.matmul(pb[:, e // 4, (e % 4) * P:(e % 4 + 1) * P], ohw[:, e, :], R.ident[:, :],
                              start=True, stop=True)
                pe.transpose(po[0:E, 0:P], oh[:, 0:E], R.ident[:, :]).then_inc(S.sem("chosen_rows"), 1)
                pe.wait_ge(S.sem("ohT"), 1)
                pe.matmul(py[:, 0:DIM], ohT[:, :], be[:, :], start=True, stop=False)
                pe.wait_ge(S.sem("experts"), experts.total)
                pe.wait_ge(S.sem("xe"), 1)
                for e in range(E):
                    for c in range(DC):
                        last = pe.matmul(py[:, 0:DIM], xe[:, e, c, :], we[:, e, c, :], start=False,
                                         stop=(e == E - 1 and c == DC - 1))
                last.then_inc(S.sem("y"), 1)



class Residents:
    pass


def constants(keys):
    f = np.float32
    idx = np.arange(P)
    inv_freq = (1.0 / np.power(f(10000.0), np.arange(0, 64, 2, dtype=f) / f(64))).astype(f)
    theta = (np.arange(keys, dtype=f)[:, None] * inv_freq[None, :]).astype(f)
    cos, sin = np.cos(theta).astype(f).T, np.sin(theta).astype(f).T
    diff = idx[None, :] - idx[:, None]
    head16 = (idx[:, None] // 16 == np.arange(8)[None, :]).astype(f)
    head64 = ((idx[:, None] // 32) % 2 == np.arange(2)[None, :]).astype(f)
    count = np.broadcast_to(np.arange(32, dtype=f), (P, 32))
    return {
        "c_ident": np.eye(P, dtype=f),
        "c_head16": head16, "c_head64": head64,
        "c_count": np.ascontiguousarray(count),
        "c_lag": np.maximum(diff - 1, 0).astype(f), "c_later": (diff > 0).astype(f),
        "c_cos": np.ascontiguousarray(np.tile(cos, (4, 1))), "c_sin": np.ascontiguousarray(np.tile(sin, (4, 1))),
    }


def halves_together(w):
    return w.reshape(w.shape[0], 4, 2, 2, 32).transpose(0, 1, 3, 2, 4).reshape(w.shape[0], 512)


def layout(inputs):
    a = {k: np.asarray(v) for k, v in inputs.items()}
    out = constants(a["ctx_1024"].shape[1])
    flip = ["L0_attn_W_in", "L0_attn_W_out", "L1_xattn_wq", "L1_xattn_wk", "L1_xattn_wv", "L1_attn_W_r",
            "L1_attn_W_k", "L1_attn_W_v", "L1_attn_W_g", "L1_attn_W_o", "L2_xattn_w_in", "L2_xattn_wp_w1",
            "L2_xattn_wp_w2", "L2_xattn_w_out", "L3_attn_Wq", "L3_attn_Wk", "L3_attn_Wv"]
    for k, v in a.items():
        out[k] = v.T if k in flip else v
    out["ctx"] = a["ctx_1024"][0]
    out["ctxT"] = a["ctx_1024"][0].T
    out["L0_xattn_Wq"] = halves_together(a["L0_xattn_Wq"])
    out["L0_xattn_Wk"] = halves_together(a["L0_xattn_Wkv"][:, :512])
    out["L0_xattn_Wv"] = a["L0_xattn_Wkv"][:, 512:]
    out["mask_row"] = a["mask_BxS2_ff1"].reshape(-1, P)
    out["mask_qk"] = a["mask_BxSxS2_bk0"][0]
    for k in ("L0_attn_conv_w", "L2_attn_W_conv"):
        out[k] = a[k][:, 0, :]
    for k in ("k", "v", "r", "g"):
        out[f"L1_attn_time_mix_{k}"] = a[f"L1_attn_time_mix_{k}"].reshape(-1)
    for k in ("x", "ctx_1024", "mask_BxS2_ff1", "mask_BxSxS2_bk0", "L0_xattn_Wkv"):
        out.pop(k, None)
    out["x_in"] = a["x"][0]
    return {k: np.ascontiguousarray(v) for k, v in out.items()}


def program(nc, A, x_name, y_name, layers):
    R = Residents()
    keys = A["ctx"].shape[0]
    R.keys = keys
    with ExitStack() as memory:
        def sb(name, shape, dt=F32):
            return memory.enter_context(nc.sbuf_tensor(name, shape, dt))
        R.x = sb("tokens", [P, DIM])
        R.ident = sb("ident", [P, P])
        R.count = sb("count", [P, 32])
        R.count8 = sb("count8", [P, 8])
        R.idx_down = sb("idx_down", [P, 8])
        R.nT = nc.dram_tensor("scratch_nT", (DC, P, keys), F32, kind="Internal").ap()
        R.KT = nc.dram_tensor("scratch_KT", (4, P, keys), F32, kind="Internal").ap()
        R.KS = nc.dram_tensor("scratch_KS", (3 * DC, P, keys), BF16, kind="Internal").ap()
        R.ones_row = nc.dram_tensor("scratch_ones", (1, CHUNK), BF16, kind="Internal").ap()
        ones = sb("ones_row", [1, CHUNK], BF16)
        loaded = memory.enter_context(nc.semaphore("loaded"))
        counted = memory.enter_context(nc.semaphore("counted"))
        stored = memory.enter_context(nc.semaphore("stored"))
        with nc.Block() as block:
            @block.sync
            def _(sp):
                sp.dma_start(R.x[:, :], A[x_name]).then_inc(loaded, 16)
                sp.dma_start(R.ident[:, :], A["c_ident"]).then_inc(loaded, 16)
                sp.dma_start(R.count[:, :], A["c_count"]).then_inc(loaded, 16)
                sp.wait_ge(counted, 1)
                sp.dma_start(R.ones_row, ones[:, :]).then_inc(stored, 16)
                sp.wait_ge(stored, 16)

            @block.vector
            def _(dve):
                dve.memset(ones[:, :], 1.0).then_inc(counted, 1)
                dve.wait_ge(loaded, 48)
                dve.tensor_scalar(R.count8[:, :], R.count[:, 0:8], 8.0, None, ALU.mult)
                dve.tensor_scalar(R.idx_down[:, :], R.count[:, 0:8], -1.0, 8.0, ALU.mult, ALU.add)
        ctx_norm(nc, A, R)
        for layer in layers:
            LAYERS[layer](nc, A, R)
        with nc.Block() as block:
            @block.sync
            def _(sp):
                sp.dma_start(A[y_name], R.x[:, :]).then_inc(stored, 16)
                sp.wait_ge(stored, 32)


LAYERS = {
    "l0_xattn": l0_xattn, "l0_attn": l0_attn, "l0_ffn": l0_ffn,
    "l1_xattn": l1_xattn, "l1_attn": l1_attn, "l1_ffn": l1_ffn,
    "l2_xattn": l2_xattn, "l2_attn": l2_attn, "l2_ffn": l2_ffn,
    "l3_xattn": l3_xattn, "l3_attn": l3_attn, "l3_ffn": l3_ffn,
}



def kernel(**inputs):
    import concourse.bacc as bacc
    from concourse.bass_utils import run_bass_kernel_spmd

    nc = bacc.Bacc("TRN2", target_bir_lowering=False, num_devices=1)
    arrays = layout(inputs)
    A = {name: nc.dram_tensor(name, a.shape, mybir.dt.from_np(a.dtype), kind="ExternalInput").ap()
         for name, a in arrays.items()}
    A["x_out"] = nc.dram_tensor("x_out", (P, DIM), F32, kind="ExternalOutput").ap()
    program(nc, A, "x_in", "x_out", list(LAYERS))
    result = run_bass_kernel_spmd(nc, [arrays], core_ids=[0])
    return result.results[0]["x_out"].reshape(1, P, DIM)
```

```python
from contextlib import ExitStack

import numpy as np

import concourse.bass as bass
from concourse import mybir

P = 128
DIM = 256
DC = DIM // P
BANK = 512
EPS = 1e-5

ALU = mybir.AluOpType
ACT = mybir.ActivationFunctionType
AX = mybir.AxisListType
F32 = mybir.dt.float32
BF16 = mybir.dt.bfloat16
U8 = mybir.dt.uint8

MAX_CHUNK = 448
TILES = 7
CHUNK = TILES * P
MASK_BIG = 952.0 * 2 ** 20


MASK_ROW = 96
MASK_HEAD = MASK_ROW // 16


class Stage:

    def __init__(self, nc, name):
        self.nc, self.name = nc, name
        self.memory, self.sems, self.unstarted = ExitStack(), {}, []

    def __enter__(self):
        self.memory.__enter__()
        return self

    def sb(self, name, shape, dt=F32):
        return self.memory.enter_context(self.nc.sbuf_tensor(f"{self.name}_{name}", shape, dt))

    def psum(self, name, banks=1):
        shape = [P, BANK] if banks == 1 else [P, banks, BANK]
        return self.memory.enter_context(self.nc.psum_tensor(f"{self.name}_{name}", shape, F32))

    def sem(self, name):
        if name not in self.sems:
            self.sems[name] = self.memory.enter_context(self.nc.semaphore(f"{self.name}_{name}"))
        return self.sems[name]

    def counted(self, name):
        if name not in self.sems:
            self.unstarted.append(self.sem(name))
        return self.sems[name]

    def __exit__(self, *e):
        if e[0] is None:
            engines = (self.nc.gpsimd, self.nc.sync, self.nc.scalar, self.nc.vector, self.nc.tensor)
            for n, s in enumerate(self.sems.values()):
                engines[n % len(engines)].sem_clear(s)
            self.nc.all_engine_barrier()
        return self.memory.__exit__(*e)


def start_counts(eng, S):
    for s in S.unstarted:
        eng.sem_inc(s, 1)
    S.unstarted = []


def after(eng, sem, n):
    eng.wait_ge(sem, n + 1)


class Link:

    def __init__(self, eng, sem):
        self.eng, self.sem, self.n = eng, sem, 0

    def __call__(self, ins):
        self.n += 1
        ins.then_inc(self.sem, 1)
        self.eng.wait_ge(self.sem, self.n)


class Loads:

    def __init__(self, sem):
        self.sem, self.total = sem, 0

    def __call__(self, ins):
        ins.then_inc(self.sem, 16)
        self.total += 16


def run_ahead(eng, steps, first, both, second, started=False):
    if not started:
        first(0, 0)
    with eng.Fori(0, steps - 1) as i:
        both((1, i), (0, i))
        both((0, i + 1), (1, i))
    both((1, steps - 1), (0, steps - 1))
    second(1, steps - 1)



def norm_vector(dve, link, S, tag, x, xn, w, rows=P):
    link(dve.bn_stats(w[:rows, 0:6], x))
    link(dve.bn_aggr(w[:rows, 6:8], w[:rows, 0:6]))
    dve.tensor_scalar(w[:rows, 8:9], w[:rows, 7:8], EPS, None, ALU.add).then_inc(S.sem(tag + "_var"), 1)
    dve.wait_ge(S.sem(tag + "_std"), 1)
    link(dve.reciprocal(w[:rows, 10:11], w[:rows, 9:10]))
    dve.tensor_scalar(xn, x, w[:rows, 6:7], w[:rows, 10:11], ALU.subtract, ALU.mult).then_inc(
        S.sem(tag + "_xn"), 1)
    dve.wait_ge(S.sem(tag + "_xn"), 1)


def norm_scalar(act, S, tag, w, rows=P):
    act.wait_ge(S.sem(tag + "_var"), 1)
    act.activation(w[:rows, 9:10], w[:rows, 8:9], ACT.Sqrt).then_inc(S.sem(tag + "_std"), 1)


def turn_tensor(pe, S, tag, xn, ps, ident, ready=None):
    pe.wait_ge(S.sem(ready or tag + "_xn"), 1)
    for c in range(DC):
        last = pe.transpose(ps[:, c * P:(c + 1) * P], xn[:, c * P:(c + 1) * P], ident[:, :])
    last.then_inc(S.sem(tag + "_turned"), 1)


def turn_vector(dve, S, tag, xT, ps):
    dve.wait_ge(S.sem(tag + "_turned"), 1)
    dve.tensor_copy(xT[:, :, :], ps[:, 0:DIM].rearrange("p (c t) -> p c t", c=DC)).then_inc(
        S.sem(tag + "_xT"), 1)
    dve.wait_ge(S.sem(tag + "_xT"), 1)


def by_rows(w):
    return w.rearrange("(c p) n -> p c n", p=P)


def column(v):
    return v.rearrange("(c p) -> p c", p=P)


def first_of_max(dve, link, onehot, vals, top, tmp, idx_down):
    link(dve.tensor_reduce(top, vals, AX.X, ALU.max))
    link(dve.tensor_scalar(tmp, vals, top, None, ALU.is_equal))
    link(dve.tensor_tensor(tmp, tmp, idx_down, ALU.mult))
    link(dve.tensor_reduce(onehot[:, 0:1], tmp, AX.X, ALU.max))
    link(dve.tensor_scalar(onehot[:, 8:9], onehot[:, 0:1], 0.0, None, ALU.add))
    link(dve.tensor_scalar(onehot[:, 0:8], tmp, onehot[:, 8:9], None, ALU.is_equal))


def softmax8_vector(dve, link, S, tag, logits, probs, w):
    link(dve.tensor_reduce(w[:, 0:1], logits, AX.X, ALU.max))
    dve.tensor_scalar(probs, logits, w[:, 0:1], None, ALU.subtract).then_inc(S.sem(tag + "_shifted"), 1)
    dve.wait_ge(S.sem(tag + "_exp"), 1)
    link(dve.reciprocal(w[:, 2:3], w[:, 1:2]))
    link(dve.tensor_scalar(probs, probs, w[:, 2:3], None, ALU.mult))


def softmax8_scalar(act, S, tag, probs, w):
    act.wait_ge(S.sem(tag + "_shifted"), 1)
    act.activation(probs, probs, ACT.Exp, accum_out=w[:, 1:2]).then_inc(S.sem(tag + "_exp"), 1)


def l3_attn(nc, A, R):
    H, HD = 16, 16
    with Stage(nc, "l3a") as S:
        w = S.sb("w", [P, DC, 3 * DIM])
        bias = S.sb("bias", [P, 3 * DIM])
        xn, xT, nw = S.sb("xn", [P, DIM]), S.sb("xT", [P, DC, P]), S.sb("nw", [P, 16])
        qkv = S.sb("qkv", [P, 3 * DIM])
        qk, s, e, top = S.sb("qk", [P, DIM]), S.sb("s", [P, H]), S.sb("e", [P, H]), S.sb("top", [P, H])
        pt, pqk, pv = S.psum("pt"), S.psum("pqk"), S.psum("pv")
        loads = Loads(S.sem("weights"))
        block = S.nc.Block()
        with block as block:
            @block.sync
            def _(sp):
                for n, name in enumerate(("Wq", "Wk", "Wv")):
                    loads(sp.dma_start(w[:, :, n * DIM:(n + 1) * DIM], by_rows(A[f"L3_attn_{name}"])))
                for n, name in enumerate(("bq", "bk", "bv")):
                    loads(sp.dma_start(bias[:, n * DIM:(n + 1) * DIM],
                                       A[f"L3_attn_{name}"].partition_broadcast(P)))

            @block.vector
            def _(dve):
                link = Link(dve, S.sem("dve_link"))
                norm_vector(dve, link, S, "n", R.x[:, :], xn[:, :], nw)
                turn_vector(dve, S, "n", xT, pt)
                dve.wait_ge(S.sem("weights"), loads.total)
                dve.wait_ge(S.sem("projected"), 1)
                link(dve.tensor_tensor(qkv[:, 0:2 * DIM], pqk[:, :], bias[:, 0:2 * DIM], ALU.add))
                link(dve.tensor_tensor(qkv[:, 2 * DIM:], pv[:, 0:DIM], bias[:, 2 * DIM:], ALU.add))
                link(dve.tensor_tensor(qk[:, :], qkv[:, 0:DIM], qkv[:, DIM:2 * DIM], ALU.mult))
                link(dve.tensor_reduce(s[:, :], qk[:, :].rearrange("p (h d) -> p h d", h=H), AX.X, ALU.add))
                link(dve.tensor_scalar(s[:, :], s[:, :], HD ** -0.5, None, ALU.mult))
                link(dve.tensor_reduce(top[:, :], s[:, :].unsqueeze(2), AX.X, ALU.max))
                dve.tensor_tensor(e[:, :], s[:, :], top[:, :], ALU.subtract).then_inc(S.sem("shifted"), 1)
                dve.wait_ge(S.sem("exp"), 1)
                link(dve.tensor_scalar(s[:, :], e[:, :], 1.0, None, ALU.add))
                link(dve.reciprocal(s[:, :], s[:, :]))
                link(dve.tensor_tensor(e[:, :], e[:, :], s[:, :], ALU.mult))
                link(dve.tensor_tensor(qk[:, :].rearrange("p (h d) -> p h d", h=H),
                                       qkv[:, 2 * DIM:].rearrange("p (h d) -> p h d", h=H),
                                       e[:, :].unsqueeze(2).broadcast_to([P, H, HD]), ALU.mult))
                link(dve.tensor_tensor(R.x[:, :], R.x[:, :], qk[:, :], ALU.add))

            @block.scalar
            def _(act):
                norm_scalar(act, S, "n", nw)
                act.wait_ge(S.sem("shifted"), 1)
                act.activation(e[:, :], e[:, :], ACT.Exp).then_inc(S.sem("exp"), 1)

            @block.tensor
            def _(pe):
                turn_tensor(pe, S, "n", xn, pt, R.ident)
                pe.wait_ge(S.sem("weights"), loads.total)
                pe.wait_ge(S.sem("n_xT"), 1)
                for c in range(DC):
                    pe.matmul(pqk[:, :], xT[:, c, :], w[:, c, 0:2 * DIM], start=(c == 0), stop=(c == DC - 1))
                for c in range(DC):
                    last = pe.matmul(pv[:, 0:DIM], xT[:, c, :], w[:, c, 2 * DIM:], start=(c == 0),
                                     stop=(c == DC - 1))
                last.then_inc(S.sem("projected"), 1)


def l3_ffn(nc, A, R):
    E, FF = 8, 1024
    FC = FF // P
    LIM = 24
    with Stage(nc, "l3f") as S:
        w1 = [S.sb(f"w1_{b}", [P, DC, FF]) for b in range(2)]
        w2 = [S.sb(f"w2_{b}", [P, FC, DIM]) for b in range(2)]
        b1 = S.sb("b1", [P, E, FC])
        b1r = S.sb("b1r", [E * FC, P])
        b2 = S.sb("b2", [E, DIM])
        xn, xT, nw = S.sb("xn", [P, DIM]), S.sb("xT", [P, DC, P]), S.sb("nw", [P, 16])
        steps = S.sb("steps", [P, 2, LIM])
        r = S.sb("r", [P, 8])
        we, wt = S.sb("we", [P, E]), S.sb("wt", [P, E])
        weT = S.sb("weT", [E, P])
        hT = [S.sb(f"hT{b}", [P, FC, P]) for b in range(2)]
        acc = S.sb("acc", [P, DIM])
        pt, pm = S.psum("pt"), S.psum("pm")
        ph = [S.psum(f"ph{b}", 2) for b in range(2)]
        py = [S.psum(f"py{b}") for b in range(2)]
        loads = Loads(S.sem("small"))
        with S.nc.Block() as block:
            @block.sync
            def _(sp):
                loads(sp.dma_start(b1r[:, :], A["L3_ffn_b1"].rearrange("e (f p) -> (e f) p", p=P)))
                loads(sp.dma_start(b2[:, :], A["L3_ffn_b2"]))
                with sp.Fori(0, E // 2) as i:
                    for b in range(2):
                        e = 2 * i + b
                        after(sp, S.counted(f"h{b}"), i)
                        sp.dma_start(w1[b][:, :, :], A["L3_ffn_W1"][bass.ds(e, 1)].rearrange(
                            "e (c p) n -> p (e c) n", p=P)).then_inc(S.counted(f"w1_{b}"), 16)
                        after(sp, S.counted(f"y{b}"), i)
                        sp.dma_start(w2[b][:, :, :], A["L3_ffn_W2"][bass.ds(e, 1)].rearrange(
                            "e (c p) n -> p (e c) n", p=P)).then_inc(S.counted(f"w2_{b}"), 16)

            @block.vector
            def _(dve):
                link = Link(dve, S.sem("dve_link"))
                norm_vector(dve, link, S, "n", R.x[:, :], xn[:, :], nw)
                turn_vector(dve, S, "n", xT, pt)
                link(dve.tensor_tensor(r[:, 0:1], xn[:, 0:1], xn[:, 1:2], ALU.add))
                link(dve.tensor_scalar(r[:, 1:2], r[:, 0:1], -1.0, None, ALU.mult))
                for side in range(2):
                    link(dve.tensor_scalar(steps[:, side, :], R.count[:, 1:LIM + 1],
                                           r[:, side:side + 1], None, ALU.is_le))
                    link(dve.tensor_reduce(r[:, 2 + side:3 + side], steps[:, side, :], AX.X, ALU.add))
                link(dve.tensor_tensor(r[:, 4:5], r[:, 2:3], r[:, 3:4], ALU.subtract))
                link(dve.tensor_scalar(r[:, 4:5], r[:, 4:5], float(LIM), None, ALU.add))
                link(dve.tensor_scalar(steps[:, 0, 0:2 * LIM // 8], R.count8[:, 1:2 * LIM // 8 + 1],
                                       r[:, 4:5], None, ALU.is_le))
                link(dve.tensor_reduce(r[:, 5:6], steps[:, 0, 0:2 * LIM // 8], AX.X, ALU.add))
                link(dve.tensor_scalar(r[:, 5:6], r[:, 5:6], -8.0, r[:, 4:5], ALU.mult, ALU.add))
                link(dve.tensor_scalar(we[:, :], R.count[:, 0:E], r[:, 5:6], None, ALU.subtract))
                link(dve.tensor_scalar(wt[:, :], we[:, :], 0.0, 0.5, ALU.is_equal, ALU.mult))
                for off in (1.0, -7.0):
                    link(dve.tensor_scalar(acc[:, 0:E], we[:, :], off, 0.5, ALU.is_equal, ALU.mult))
                    link(dve.tensor_tensor(wt[:, :], wt[:, :], acc[:, 0:E], ALU.add))
                dve.sem_inc(S.sem("weights_of_experts"), 1)
                dve.wait_ge(S.sem("b1_turned"), 1)
                dve.tensor_copy(b1[:, :, :], pm[:, 0:E * FC].rearrange("p (e f) -> p e f", e=E)).then_inc(
                    S.sem("b1_ready"), 1)
                dve.wait_ge(S.sem("we_turned"), 1)
                dve.tensor_copy(weT[:, :], pm[0:E, P:2 * P]).then_inc(S.sem("weT_ready"), 1)
                dve.wait_ge(S.sem("b2_mixed"), 1)
                link(dve.tensor_tensor(acc[:, :], pm[:, DIM:2 * DIM], R.x[:, :], ALU.add))
                with dve.Fori(0, E // 2) as i:
                    for b in range(2):
                        after(dve, S.counted(f"y{b}"), i + 1)
                        after(dve, S.counted(f"added{1 - b}"), i + b)
                        dve.scalar_tensor_tensor(acc[:, :], py[b][:, 0:DIM], wt[:, bass.ds(i * 2 + b, 1)],
                                                 acc[:, :], ALU.mult, ALU.add).then_inc(
                            S.counted(f"added{b}"), 1)
                after(dve, S.counted("added1"), E // 2)
                dve.tensor_copy(R.x[:, :], acc[:, :])

            @block.scalar
            def _(act):
                norm_scalar(act, S, "n", nw)
                act.wait_ge(S.sem("b1_ready"), 1)
                with act.Fori(0, E // 2) as i:
                    for b in range(2):
                        act.wait_ge(S.sem("b1_ready"), 1)
                        after(act, S.counted(f"h{b}"), i + 1)
                        after(act, S.counted(f"y{b}"), i)
                        for f in range(FC):
                            last = act.activation(hT[b][:, f, :], ph[b][:, f // 4, (f % 4) * P:(f % 4 + 1) * P],
                                                  ACT.Relu, bias=b1[:, bass.ds(i * 2 + b, 1), f])
                        last.then_inc(S.counted(f"hT{b}"), 1)

            @block.tensor
            def _(pe):
                turn_tensor(pe, S, "n", xn, pt, R.ident)
                pe.wait_ge(S.sem("small"), loads.total)
                pe.transpose(pm[:, 0:E * FC], b1r[:, :], R.ident[0:E * FC, 0:E * FC]).then_inc(
                    S.sem("b1_turned"), 1)

                def hidden(b, i):
                    after(pe, S.counted(f"w1_{b}"), (i + 1) * 16)
                    after(pe, S.counted(f"hT{b}"), i)
                    for f in range(FC):
                        for c in range(DC):
                            last = pe.matmul(ph[b][:, f // 4, (f % 4) * P:(f % 4 + 1) * P],
                                             w1[b][:, c, f * P:(f + 1) * P], xT[:, c, :],
                                             start=(c == 0), stop=(c == DC - 1))
                    last.then_inc(S.counted(f"h{b}"), 1)

                def output(b, i):
                    after(pe, S.counted(f"w2_{b}"), (i + 1) * 16)
                    after(pe, S.counted(f"hT{b}"), i + 1)
                    after(pe, S.counted(f"added{b}"), i)
                    for f in range(FC):
                        last = pe.matmul(py[b][:, 0:DIM], hT[b][:, f, :], w2[b][:, f, :],
                                         start=(f == 0), stop=(f == FC - 1))
                    last.then_inc(S.counted(f"y{b}"), 1)

                pe.wait_ge(S.sem("n_xT"), 1)
                hidden(0, 0)
                pe.wait_ge(S.sem("weights_of_experts"), 1)
                pe.wait_ge(S.sem("b1_ready"), 1)
                pe.transpose(pm[0:E, P:2 * P], wt[:, :], R.ident[:, :]).then_inc(S.sem("we_turned"), 1)
                pe.wait_ge(S.sem("weT_ready"), 1)
                pe.matmul(pm[:, DIM:2 * DIM], weT[:, :], b2[:, :], start=True, stop=True).then_inc(
                    S.sem("b2_mixed"), 1)
                run_ahead(pe, E // 2, hidden, lambda ahead, now: (hidden(*ahead), output(*now)), output,
                          started=True)

            @block.gpsimd
            def _(pool):
                start_counts(pool, S)



def ctx_norm(nc, A, R):
    steps = R.keys // CHUNK // 2
    rows = A["ctx"].rearrange("(n t p) d -> n p t d", t=TILES, p=P)
    turned = R.nT.rearrange("c p (n k) -> n p c k", k=CHUNK)
    with Stage(nc, "norm") as S:
        raw = [S.sb(f"raw{b}", [P, TILES, DIM]) for b in range(2)]
        xn = [S.sb(f"xn{b}", [P, TILES, DIM]) for b in range(2)]
        out = [S.sb(f"out{b}", [P, DC, CHUNK]) for b in range(2)]
        st = [S.sb(f"st{b}", [P, TILES, 6]) for b in range(2)]
        mv = [S.sb(f"mv{b}", [P, TILES, 2]) for b in range(2)]
        ve = [S.sb(f"ve{b}", [P, TILES]) for b in range(2)]
        sd = [S.sb(f"sd{b}", [P, TILES]) for b in range(2)]
        pt = [S.psum(f"pt{b}", 4) for b in range(2)]
        with S.nc.Block() as block:
            @block.sync
            def _(sp):
                def load(b, i):
                    sp.dma_start(raw[b][:, :, :], rows[bass.ds(i * 2 + b, 1)].squeeze(0)).then_inc(
                        S.counted(f"raw{b}"), 16)

                def store(b, i):
                    after(sp, S.counted(f"out{b}"), i + 1)
                    sp.dma_start(turned[bass.ds(i * 2 + b, 1)].squeeze(0), out[b][:, :, :]).then_inc(
                        S.counted(f"stored{b}"), 16)

                load(0, 0)
                load(1, 0)
                with sp.Fori(0, steps - 1) as i:
                    for b in range(2):
                        after(sp, S.counted(f"normed{b}"), i + 1)
                        load(b, i + 1)
                    store(0, i)
                    store(1, i)
                for b in range(2):
                    store(b, steps - 1)
                for b in range(2):
                    after(sp, S.counted(f"stored{b}"), steps * 16)

            @block.vector
            def _(dve):
                def stats(b, i):
                    after(dve, S.counted(f"raw{b}"), (i + 1) * 16)
                    for t in range(TILES):
                        last = dve.bn_stats(st[b][:, t, :], raw[b][:, t, :])
                    last.then_inc(S.counted(f"st{b}"), 1)
                    after(dve, S.counted(f"st{b}"), i + 1)
                    dve.sem_inc(S.sem("stats_seen"), 1)
                    for t in range(TILES):
                        last = dve.bn_aggr(mv[b][:, t, :], st[b][:, t, :])
                    last.then_inc(S.counted(f"mv{b}"), 1)
                    after(dve, S.counted(f"mv{b}"), i + 1)
                    dve.tensor_scalar(ve[b][:, :], mv[b][:, :, 1], EPS, None, ALU.add).then_inc(
                        S.counted(f"ve{b}"), 1)

                def scale(b, i):
                    after(dve, S.counted(f"sd{b}"), i + 1)
                    dve.reciprocal(sd[b][:, :], sd[b][:, :]).then_inc(S.counted(f"rs{b}"), 1)
                    after(dve, S.counted(f"rs{b}"), i + 1)
                    after(dve, S.counted(f"turned{b}"), i)
                    for t in range(TILES):
                        last = dve.tensor_scalar(xn[b][:, t, :], raw[b][:, t, :], mv[b][:, t, 0:1],
                                                 sd[b][:, t:t + 1], ALU.subtract, ALU.mult)
                    last.then_inc(S.counted(f"normed{b}"), 1)

                with dve.Fori(0, steps) as i:
                    stats(0, i)
                    scale(0, i)
                    stats(1, i)
                    scale(1, i)

            @block.scalar
            def _(act):
                def root(b, i):
                    after(act, S.counted(f"ve{b}"), i + 1)
                    act.activation(sd[b][:, :], ve[b][:, :], ACT.Sqrt).then_inc(S.counted(f"sd{b}"), 1)

                def copy(b, i):
                    after(act, S.counted(f"turned{b}"), i + 1)
                    after(act, S.counted(f"stored{b}"), i * 16)
                    for c in range(DC):
                        act.activation(out[b][:, c, 0:BANK], pt[b][:, 2 * c, :], ACT.Copy)
                        last = act.activation(out[b][:, c, BANK:CHUNK], pt[b][:, 2 * c + 1, 0:CHUNK - BANK],
                                              ACT.Copy)
                    last.then_inc(S.counted(f"out{b}"), 1)

                run_ahead(act, steps, root, lambda ahead, now: (root(*ahead), copy(*now)), copy)

            @block.tensor
            def _(pe):
                with pe.Fori(0, steps) as i:
                    for b in range(2):
                        after(pe, S.counted(f"normed{b}"), i + 1)
                        after(pe, S.counted(f"out{b}"), i)
                        for t in range(TILES):
                            for c in range(DC):
                                last = pe.transpose(pt[b][:, 2 * c + t // 4, (t % 4) * P:(t % 4 + 1) * P],
                                                    xn[b][:, t, c * P:(c + 1) * P], R.ident[:, :])
                        last.then_inc(S.counted(f"turned{b}"), 1)

            @block.gpsimd
            def _(pool):
                start_counts(pool, S)


def find_maximum(nc, S, A, R, heads, kc, per_chunk, qb, source, project, w_k, bias_k, top, masks, split, chunks, seed=None):
    nc = S.nc
    steps = R.keys // MAX_CHUNK // 2
    src = source.rearrange("c p (n k) -> n p c k", k=MAX_CHUNK)
    rope = project == "rope"
    mem = ExitStack()
    with mem:
        def sb(name, shape, dt=F32):
            return mem.enter_context(nc.sbuf_tensor(f"{S.name}_max_{name}", shape, dt))
        xin = [sb(f"xin{b}", [P, DC, MAX_CHUNK]) for b in range(2)]
        kf = [sb(f"kf{b}", [P, kc, MAX_CHUNK]) for b in range(2)] if project else xin
        n_parts = 3 if split else 1
        kp = [sb(f"kp{b}", [P, n_parts, kc, MAX_CHUNK], BF16) for b in range(2)]
        if masks == "key":
            ka = [sb(f"ka{b}", [P, kc, MAX_CHUNK], BF16) for b in range(2)]
        if split:
            rest = [sb(f"rest{b}", [P, kc, MAX_CHUNK]) for b in range(2)]
        red = [sb(f"red{b}", [P, heads]) for b in range(2)]
        if rope:
            cs = [sb(f"cs{b}", [P, 2, MAX_CHUNK]) for b in range(2)]
            ks = [sb(f"ks{b}", [P, kc, MAX_CHUNK]) for b in range(2)]
            kt = [sb(f"kt{b}", [P, kc, MAX_CHUNK]) for b in range(2)]
            cos = A["c_cos"].rearrange("p (n k) -> n p k", k=MAX_CHUNK)
            sin = A["c_sin"].rearrange("p (n k) -> n p k", k=MAX_CHUNK)
        kt_dram = (R.KS if split else R.KT[0:kc]).rearrange("c p (n k) -> n p c k", k=MAX_CHUNK)
        if masks == "query_key":
            mq = [sb(f"mq{b}", [P, MAX_CHUNK], U8) for b in range(2)]
            mb = [sb(f"mb{b}", [P, MAX_CHUNK], BF16) for b in range(2)]
            one = sb("one", [P, 1])
            mask_src = A["mask_qk"].rearrange("q (n k) -> n q k", k=MAX_CHUNK)
        n_ps = 2 if rope else 3 if project else 4
        psc = [mem.enter_context(nc.psum_tensor(f"{S.name}_max_ps{u}", [P, 2, BANK], F32)) for u in range(n_ps)]
        pk = [mem.enter_context(nc.psum_tensor(f"{S.name}_max_pk{c}", [P, BANK], F32)) for c in range(kc if project else 0)]
        sem = lambda n: S.counted("max_" + n)
        copied = {None: (), "key": (5,), "query_key": (2, 4, 6)}[masks]
        near = {pr: [sb(f"near{pr}_{b}", [P, 2, MAX_CHUNK], BF16) for b in range(2)] for pr in copied}
        running = {pr: sb(f"running{pr}", [P, 2, MAX_CHUNK], BF16) for pr in copied}
        pairs = heads // 2
        per_piece = pairs // kc
        per = [len(range(u, pairs, n_ps)) for u in range(n_ps)]

        def pair_counts(b, i, pr):
            u = pr % n_ps
            return u, i * (2 * per[u]) + b * per[u] + pr // n_ps

        with nc.Block() as block:
            @block.sync
            def _(sp):
                def load(b, i):
                    sp.dma_start(xin[b][:, :, :], src[bass.ds(i * 2 + b, 1)].squeeze(0)).then_inc(sem(f"xin{b}"), 16)
                    if rope:
                        sp.dma_start(cs[b][:, 0, :], cos[bass.ds(i * 2 + b, 1)].squeeze(0)).then_inc(
                            sem(f"cs{b}"), 16)
                        sp.dma_start(cs[b][:, 1, :], sin[bass.ds(i * 2 + b, 1)].squeeze(0)).then_inc(
                            sem(f"cs{b}"), 16)
                    if masks == "query_key":
                        sp.dma_start(mq[b][:, :], mask_src[bass.ds(i * 2 + b, 1)].squeeze(0)).then_inc(
                            sem(f"mq{b}"), 16)

                def spill(b, i):
                    if split:
                        after(sp, sem(f"low{b}"), i + 1)
                        sp.dma_start(kt_dram[bass.ds(i * 2 + b, 1)].squeeze(0),
                                     kp[b][:, :, :, :].rearrange("p s c k -> p (s c) k")).then_inc(
                            sem(f"spilled{b}"), 16)
                    else:
                        after(sp, sem(f"kf{b}"), (i + 1) * kc)
                        sp.dma_start(kt_dram[bass.ds(i * 2 + b, 1)].squeeze(0), kf[b][:, :, :]).then_inc(
                            sem(f"spilled{b}"), 16)

                for b in range(2):
                    load(b, 0)
                def load_and_spill(i):
                    for b in range(2):
                        if project:
                            after(sp, sem(f"xin_used{b}"), i + 1)
                        else:
                            after(sp, sem(f"rest{b}"), i + 1)
                            after(sp, sem(f"kb{b}"), (i + 1) * kc)
                        if rope:
                            after(sp, sem(f"turned{b}"), (i + 1) * kc)
                        if masks == "query_key":
                            after(sp, sem(f"mb{b}"), i + 1)
                        load(b, i + 1)
                        spill(b, i)

                ahead = min(steps - 1, 2)
                if steps - 1 > ahead:
                    with sp.Fori(0, steps - 1 - ahead) as i:
                        load_and_spill(i)
                else:
                    for i in range(0, steps - 1 - ahead + 1):
                        load_and_spill(i)
                    ahead -= 1
                for b in range(2):
                    after(sp, sem(f"spilled{b}"), (steps - 1 - ahead) * 16)
                chunks.load(sp, 0, 0)
                for i in range(steps - 1 - ahead, steps - 1):
                    load_and_spill(i)
                for b in range(2):
                    spill(b, steps - 1)
                for b in range(2):
                    after(sp, sem(f"spilled{b}"), steps * 16)

            @block.vector
            def _(dve):
                if seed is None:
                    dve.memset(top[:, :], -3.0e38).then_inc(sem("top"), 1)
                else:
                    dve.tensor_copy(top[:, :], seed[:, :]).then_inc(sem("top"), 1)
                if masks == "query_key":
                    dve.memset(one[:, :], 1.0).then_inc(S.sem("one"), 1)
                for pr in copied:
                    dve.memset(running[pr][:, :, :], -3.0e38).then_inc(sem(f"folded{pr}"), 1)
                for b in range(2):
                    dve.memset(red[b][:, :], -3.0e38).then_inc(S.sem("red_begun"), 1)
                dve.wait_ge(S.sem("red_begun"), 2)

                def bias_cos(b, i, c):
                    if c == 0:
                        after(dve, sem(f"cs{b}"), (i + 1) * 32)
                        after(dve, sem(f"kf{b}"), i * kc)
                    after(dve, sem(f"k_proj{c}"), i * 2 + b + 1)
                    dve.scalar_tensor_tensor(kt[b][:, c, :], pk[c][:, 0:MAX_CHUNK], bias_k[:, c:c + 1],
                                             cs[b][:, 0, :], ALU.add, ALU.mult).then_inc(sem(f"k_read{c}"), 1)

                def times_sin(b, i, c):
                    after(dve, sem(f"k_swapped{c}"), i * 2 + b + 1)
                    dve.tensor_tensor(ks[b][:, c, :], ks[b][:, c, :], cs[b][:, 1, :], ALU.mult).then_inc(
                        sem(f"turned{b}"), 1)

                def turn(b, i):
                    for c in range(kc):
                        bias_cos(b, i, c)
                        times_sin(b, i, c)

                def maximum(b, i, pr):
                    u, j = pair_counts(b, i, pr)
                    if pr == 0:
                        after(dve, sem("top"), i * 2 + b + 1)
                    after(dve, sem(f"scores{u}"), j + 1)
                    dve.tensor_reduce(red[b][:, 2 * pr:2 * pr + 2], psc[u][:, :, 0:MAX_CHUNK], AX.X,
                                      ALU.max).then_inc(sem(f"scores_read{u}"), 1)

                def merge_before(b, i):
                    for u in range(n_ps):
                        after(dve, sem(f"scores_read{u}"), i * (2 * per[u]) + b * per[u])
                    after(dve, sem("top"), i * 2 + b + 1)
                    dve.tensor_tensor(top[:, :], top[:, :], red[1 - b][:, :], ALU.max).then_inc(sem("top"), 1)

                def fold(b, i, pr):
                    u, j = pair_counts(b, i, pr)
                    after(dve, sem(f"scores_read{u}"), j + 1)
                    after(dve, sem(f"folded{pr}"), i * 2 + b + 1)
                    dve.tensor_tensor(running[pr][:, :, :], running[pr][:, :, :], near[pr][b][:, :, :],
                                      ALU.max).then_inc(sem(f"folded{pr}"), 1)

                def reduce(b, i):
                    for pr in range(pairs):
                        if pr not in copied:
                            maximum(b, i, pr)
                        if pr == 1:
                            merge_before(b, i)
                        if pr - 1 in copied:
                            fold(b, i, pr - 1)

                def turn_and_reduce(ahead, now):
                    for c in range(kc):
                        bias_cos(*ahead, c)
                        if c:
                            times_sin(*ahead, c - 1)
                        maximum(*now, c)
                        if c == 1:
                            merge_before(*now)
                    times_sin(*ahead, kc - 1)

                if rope:
                    run_ahead(dve, steps, turn, turn_and_reduce, reduce)
                else:
                    with dve.Fori(0, steps) as i:
                        reduce(0, i)
                        reduce(1, i)
                merge_before(0, steps)
                if copied:
                    after(dve, sem("top"), 2 * steps + 2)
                for pr in copied:
                    after(dve, sem(f"folded{pr}"), 2 * steps + 1)
                    dve.tensor_reduce(red[0][:, 2 * pr:2 * pr + 2], running[pr][:, :, :], AX.X, ALU.max).then_inc(
                        sem("top"), 1)
                if copied:
                    after(dve, sem("top"), 2 * steps + 2 + len(copied))
                    dve.tensor_tensor(top[:, :], top[:, :], red[0][:, :], ALU.max).then_inc(sem("top"), 1)

            @block.scalar
            def _(act):
                def evacuate(b, i, c):
                    if rope:
                        if c == 0:
                            after(act, sem(f"turned{b}"), i * kc)
                            after(act, sem(f"kf{b}"), i * kc)
                        after(act, sem(f"k_read{c}"), i * 2 + b + 1)
                        act.activation(ks[b][0:64, c, :], pk[c][64:P, 0:MAX_CHUNK], ACT.Identity,
                                       scale=-1.0, bias=R.nbias_k[0:64, c:c + 1])
                        act.activation(ks[b][64:P, c, :], pk[c][0:64, 0:MAX_CHUNK], ACT.Identity,
                                       bias=R.nbias_k[64:P, c:c + 1]).then_inc(sem(f"k_swapped{c}"), 1)
                    else:
                        if c == 0:
                            after(act, sem(f"rest{b}"), i)
                        after(act, sem(f"k_proj{c}"), i * 2 + b + 1)
                        act.activation(kf[b][:, c, :], pk[c][:, 0:MAX_CHUNK], ACT.Identity,
                                       bias=bias_k[:, c:c + 1]).then_inc(sem(f"k_swapped{c}"), 1)
                        after(act, sem(f"k_swapped{c}"), i * 2 + b + 1)

                def copy(b, i, c):
                    if c == 0:
                        after(act, sem(f"scored{b}"), i)
                        if split:
                            after(act, sem(f"spilled{b}"), i * 16)
                        if not project:
                            after(act, sem(f"xin{b}"), (i + 1) * 16)
                    if rope:
                        after(act, sem(f"kf{b}"), i * kc + c + 1)
                    act.activation(kp[b][:, 0, c, :], kf[b][:, c, :], ACT.Copy).then_inc(sem(f"kb{b}"), 1)
                    if masks == "key":
                        act.activation(ka[b][:, c, :], kf[b][:, c, :], ACT.Copy).then_inc(sem(f"ka_full{b}"), 1)
                        after(act, sem(f"ka_full{b}"), i * kc + c + 1)
                        act.sem_inc(S.sem("rows_begun"), 1)
                        act.activation(ka[b][MASK_ROW:MASK_ROW + 3, c, :],
                                       R.mask3[MASK_ROW:MASK_ROW + 3, bass.ds((2 * i + b) * MAX_CHUNK, MAX_CHUNK)],
                                       ACT.Copy).then_inc(sem(f"ka{b}"), 1)

                if masks == "key":
                    act.wait_ge(S.sem("mask_in"), 16)
                if masks == "query_key":
                    act.wait_ge(S.sem("one"), 1)
                def copy_scores(b, i, pr):
                    u, j = pair_counts(b, i, pr)
                    after(act, sem(f"scores{u}"), j + 1)
                    after(act, sem(f"folded{pr}"), i * 2 + b)
                    act.activation(near[pr][b][:, :, :], psc[u][:, :, 0:MAX_CHUNK], ACT.Copy).then_inc(
                        sem(f"scores_read{u}"), 1)

                def prepare(b, i, c):
                    if project:
                        evacuate(b, i, c)
                    copy(b, i, c)

                def mask_and_middle(b, i):
                    if masks == "query_key":
                        after(act, sem(f"mq{b}"), (i + 1) * 16)
                        act.activation(mb[b][:, :], mq[b][:, :], ACT.Identity, scale=-1.0,
                                       bias=one[:, :]).then_inc(sem(f"mb{b}"), 1)
                    after(act, sem(f"rest{b}"), i + 1)
                    act.activation(kp[b][:, 1], rest[b][:, :, :], ACT.Copy).then_inc(sem(f"mid{b}"), 1)

                def prepare_all(b, i):
                    for c in range(kc):
                        prepare(b, i, c)
                    mask_and_middle(b, i)

                def prepare_and_copy(ahead, now):
                    prepare(*ahead, 0)
                    copy_scores(*now, copied[0])
                    prepare(*ahead, 1)
                    for pr in copied[1:2]:
                        copy_scores(*now, pr)
                    mask_and_middle(*ahead)
                    for pr in copied[2:]:
                        copy_scores(*now, pr)

                def copy_all(b, i):
                    for pr in copied:
                        copy_scores(b, i, pr)

                if rope:
                    with act.Fori(0, steps) as i:
                        for b in range(2):
                            for c in range(kc):
                                evacuate(b, i, c)
                                if c:
                                    copy(b, i, c - 1)
                            copy(b, i, kc - 1)
                elif copied:
                    run_ahead(act, steps, prepare_all, prepare_and_copy, copy_all)
                else:
                    with act.Fori(0, steps) as i:
                        prepare_all(0, i)
                        prepare_all(1, i)

            @block.tensor
            def _(pe):
                def proj(b, i, c):
                    if c == 0:
                        after(pe, sem(f"xin{b}"), (i + 1) * 16)
                    after(pe, sem(f"k_swapped{c}"), i * 2 + b)
                    for d in range(DC):
                        last = pe.matmul(pk[c][:, 0:MAX_CHUNK], w_k[:, d, c * P:(c + 1) * P], xin[b][:, d, :],
                                         start=(d == 0), stop=(d == DC - 1))
                    last.then_inc(sem(f"k_proj{c}"), 1)
                    if c == kc - 1:
                        after(pe, sem(f"k_proj{c}"), i * 2 + b + 1)
                        pe.sem_inc(sem(f"xin_used{b}"), 1)

                def score(b, i, pr):
                    if pr % per_piece == 0:
                        after(pe, sem(f"kb{b}"), i * kc + pr // per_piece + 1)
                        if masks == "key":
                            after(pe, sem(f"ka{b}"), i * kc + pr // per_piece + 1)
                        if masks == "query_key" and pr == 0:
                            after(pe, sem(f"mb{b}"), i + 1)
                    u, j = pair_counts(b, i, pr)
                    after(pe, sem(f"scores_read{u}"), j)
                    for n in range(2):
                        h = 2 * pr + n
                        c = h // per_chunk
                        out = psc[u][:, n, 0:MAX_CHUNK]
                        in_rows = masks == "key" and h % per_chunk != MASK_HEAD
                        last = pe.matmul(out, qb[c][:, h % per_chunk, :], (ka[b] if in_rows else kp[b][:, 0])[:, c, :],
                                         start=True, stop=(masks is None or in_rows))
                        if masks == "query_key":
                            last = pe.matmul(out, R.neg_big[:, :], mb[b][:, :], start=False, stop=True)
                        if masks == "key" and not in_rows:
                            last = pe.matmul(out, R.ones3[:, :],
                                             R.mask3[:, bass.ds(i * (2 * MAX_CHUNK) + b * MAX_CHUNK, MAX_CHUNK)],
                                             start=False, stop=True)
                    last.then_inc(sem(f"scores{u}"), 1)
                    if pr == pairs - 1:
                        after(pe, sem(f"scores{u}"), j + 1)
                        pe.sem_inc(sem(f"scored{b}"), 1)

                def project_all(b, i):
                    for c in range(kc):
                        proj(b, i, c)

                def score_all(b, i):
                    for pr in range(pairs):
                        score(b, i, pr)

                def project_and_score(ahead, now):
                    for c in range(kc):
                        for n in range(per_piece):
                            if n == min(1, per_piece - 1):
                                proj(*ahead, c)
                            score(*now, c * per_piece + n)

                if masks == "key":
                    pe.wait_ge(S.sem("mask_in"), 16)
                if project:
                    run_ahead(pe, steps, project_all, project_and_score, score_all)
                else:
                    with pe.Fori(0, steps) as i:
                        score_all(0, i)
                        score_all(1, i)

            @block.gpsimd
            def _(pool):
                start_counts(pool, S)
                with pool.Fori(0, steps) as i:
                    for b in range(2):
                        if rope:
                            for c in range(kc):
                                if c == 0:
                                    after(pool, sem(f"kb{b}"), i * kc)
                                    after(pool, sem(f"spilled{b}"), i * 16)
                                after(pool, sem(f"turned{b}"), i * kc + c + 1)
                                pool.tensor_tensor(kf[b][:, c, :], kt[b][:, c, :], ks[b][:, c, :],
                                                   ALU.add).then_inc(sem(f"kf{b}"), 1)
                        else:
                            after(pool, sem(f"kb{b}"), (i + 1) * kc)
                            after(pool, sem(f"low{b}"), i)
                            pool.tensor_tensor(rest[b][:, :, :], kf[b][:, :, :], kp[b][:, 0],
                                               ALU.subtract).then_inc(sem(f"rest{b}"), 1)
                            after(pool, sem(f"mid{b}"), i + 1)
                            pool.tensor_tensor(kp[b][:, 2], rest[b][:, :, :], kp[b][:, 1],
                                               ALU.subtract).then_inc(sem(f"low{b}"), 1)


class TopRows:

    def __init__(self, nc, S, mem, R, top, heads, rows):
        self.S, self.R, self.top, self.heads, self.rows = S, R, top, heads, rows
        self.scratch = nc.dram_tensor(f"{S.name}_top_rows", (3, heads, P), BF16, kind="Internal").ap()
        self.topT = mem.enter_context(nc.sbuf_tensor(f"{S.name}_topT", [heads, P], F32))
        self.parts = mem.enter_context(nc.sbuf_tensor(f"{S.name}_top_parts", [heads, 3, P], BF16))
        self.ps = mem.enter_context(nc.psum_tensor(f"{S.name}_topps", [P, BANK], F32))

    def tensor(self, pe):
        pe.transpose(self.ps[0:self.heads, 0:P], self.top[:, :], self.R.ident[:, :]).then_inc(
            self.S.sem("top_turned"), 1)

    def vector(self, dve):
        link = Link(dve, self.S.sem("split_link"))
        dve.wait_ge(self.S.sem("top_turned"), 1)
        link(dve.tensor_scalar(self.topT[:, :], self.ps[0:self.heads, 0:P], -1.0, None, ALU.mult))
        for n in range(3):
            link(dve.tensor_copy(self.parts[:, n, :], self.topT[:, :]))
            link(dve.tensor_tensor(self.topT[:, :], self.topT[:, :], self.parts[:, n, :], ALU.subtract))
        dve.sem_inc(self.S.sem("split"), 1)

    def sync(self, sp):
        sp.wait_ge(self.S.sem("split"), 1)
        sp.dma_start(self.scratch.rearrange("n h q -> h n q"), self.parts[:, :, :]).then_inc(
            self.S.sem("rows_out"), 16)
        sp.wait_ge(self.S.sem("rows_out"), 16)
        sp.dma_start(self.rows, self.scratch.rearrange("n h q -> n (h q)")).then_inc(self.S.sem("rows_in"), 16)

    def wait(self, eng):
        eng.wait_ge(self.S.sem("rows_in"), 16)


PARTS_OF_K, PARTS_OF_Q = (0, 0, 0, 1, 1, 2), (0, 1, 2, 0, 1, 0)
STACK = 16 * len(PARTS_OF_K)


def parts_to_rows(eng, rows, parts, which, sem):
    for n, s in enumerate(which):
        eng.dma_start(rows[16 * n:16 * n + 16], parts[2 * s:2 * s + 2].rearrange(
            "c (h d) k -> d (c h) k", d=16)).then_inc(sem, 16)


class QueryRows:

    def __init__(self, nc, S, mem, rows):
        self.S, self.rows = S, rows
        self.scratch = nc.dram_tensor(f"{S.name}_q_parts", (3 * DC, P, P), BF16, kind="Internal").ap()
        self.rest = mem.enter_context(nc.sbuf_tensor(f"{S.name}_q_rest", [P, DC * P], F32))
        self.parts = mem.enter_context(nc.sbuf_tensor(f"{S.name}_q_parts_sb", [P, 3, DC * P], BF16))

    def vector(self, dve, link, qT, scale):
        link(dve.tensor_scalar(self.rest[:, :], qT, scale, None, ALU.mult))
        for n in range(3):
            link(dve.tensor_copy(self.parts[:, n, :], self.rest[:, :]))
            if n < 2:
                link(dve.tensor_tensor(self.rest[:, :], self.rest[:, :], self.parts[:, n, :], ALU.subtract))
        dve.sem_inc(self.S.sem("q_split"), 1)

    def sync(self, sp):
        sp.wait_ge(self.S.sem("q_split"), 1)
        sp.dma_start(self.scratch.rearrange("c p t -> p c t"), self.parts[:, :, :].rearrange(
            "p s (c t) -> p (s c) t", c=DC)).then_inc(self.S.sem("q_out"), 16)
        sp.wait_ge(self.S.sem("q_out"), 16)
        parts_to_rows(sp, self.rows, self.scratch, PARTS_OF_Q, self.S.sem("q_in"))

    def wait(self, eng):
        eng.wait_ge(self.S.sem("q_in"), 16 * len(PARTS_OF_Q))


class KeyChunks:

    def __init__(self, nc, S, A, R, mem, heads, kc, kt_src, v_src, project, masks):
        def sb(name, shape, dt=F32):
            return mem.enter_context(nc.sbuf_tensor(f"{S.name}_att_{name}", shape, dt))
        self.S, self.masks, self.wide = S, masks, heads == 8
        self.kt_src = kt_src.rearrange("c p (n k) -> n p c k" if self.wide else "c p (n k) -> n c p k", k=CHUNK)
        self.v_src = v_src.rearrange("c p (n k) -> n p c k", k=CHUNK) if project else v_src.rearrange(
            "(n t p) d -> n p t d", t=TILES, p=P)
        self.kt = [sb(f"kt{b}", [P, kc, CHUNK]) if self.wide else sb(f"kt{b}", [STACK + 3, 16, CHUNK], BF16)
                   for b in range(2)]
        self.kt_count = 16 if self.wide else 16 * len(PARTS_OF_K)
        self.vin = [sb(f"vin{b}", [P, DC, CHUNK] if project else [P, TILES, DIM]) for b in range(2)]
        if masks == "query_key":
            self.mq = [sb(f"mq{b}", [P, CHUNK], U8) for b in range(2)]
            self.mask_src = A["mask_qk"].rearrange("q (n k) -> n q k", k=CHUNK)

    def load(self, sp, b, i):
        sem = lambda n: self.S.counted("att_" + n)
        n = i * 2 + b
        if self.wide:
            sp.dma_start(self.kt[b][:, :, :], self.kt_src[bass.ds(n, 1)].squeeze(0)).then_inc(sem(f"kt{b}"), 16)
        else:
            parts_to_rows(sp, self.kt[b], self.kt_src[bass.ds(n, 1)].squeeze(0), PARTS_OF_K, sem(f"kt{b}"))
        sp.dma_start(self.vin[b][:, :, :], self.v_src[bass.ds(n, 1)].squeeze(0)).then_inc(sem(f"vin{b}"), 16)
        if self.masks == "query_key":
            sp.dma_start(self.mq[b][:, :], self.mask_src[bass.ds(n, 1)].squeeze(0)).then_inc(sem(f"mq{b}"), 16)


def attend(nc, S, R, heads, per_chunk, q, chunks, w_v, bias_v, top, masks, O, sums, last_tile=None):
    nc = S.nc
    wide = heads == 8
    vd = DIM // heads * (2 if wide else 1)
    steps = R.keys // CHUNK // 2
    octets = heads // 8
    mem = ExitStack()
    project = w_v is not None
    kt, vin, kt_count = chunks.kt, chunks.vin, chunks.kt_count
    with mem:
        def sb(name, shape, dt=F32):
            return mem.enter_context(nc.sbuf_tensor(f"{S.name}_att_{name}", shape, dt))
        if wide:
            v = [sb(f"v{b}", [P, heads, vd]) for b in range(2)]
        else:
            v = [sb(f"v{b}", [P, heads, vd + 1]) for b in range(2)]
        pt = [sb(f"pt{b}", [P, 8, P]) for b in range(2)]
        zl, zr = sb("zl", [P, P]), sb("zr", [P, BANK])
        if masks == "query_key":
            mq = chunks.mq
            mb = [sb(f"mb{b}", [P, CHUNK], BF16) for b in range(2)]
        if wide:
            tops = sb("tops", [P, heads, P])
            top_wide = sb("top_wide", [P, heads, P])
        else:
            shift = TopRows(nc, S, mem, R, top, heads, q.rows[STACK:STACK + 3].rearrange("n h q -> n (h q)"))
        psc = [mem.enter_context(nc.psum_tensor(f"{S.name}_att_ps{b}", [P, 2, BANK], F32)) for b in range(2)]
        pv = [mem.enter_context(nc.psum_tensor(f"{S.name}_att_pv{b}", [P, BANK], F32)) for b in range(2)]
        sem = lambda n: S.counted("att_" + n)
        per_body = 2 * TILES
        uses = per_body * octets // 2
        vuses = per_body // 2

        def octet_counts(i, t, o):
            k = t * octets + o
            return k % 2, i * uses + k // 2

        def tile_counts(i, t):
            return t % 2, i * vuses + t // 2

        def weighed(i, t, o):
            if wide or o:
                return sem(f"weighed{t % 2}"), i * vuses + t // 2
            return sem("weighed_first"), i * per_body + t

        def weighed_before(i, t, o):
            if wide or o == 0:
                return weighed(i, t, o)
            return sem(f"weighed{(t + 1) % 2}"), i * vuses + (t + 1) // 2

        with nc.Block() as block:
            @block.sync
            def _(sp):
                if not wide:
                    for b in range(2):
                        sp.dma_start(kt[b][STACK:STACK + 3, :, :], R.ones_row.unsqueeze(0).broadcast_to(
                            [3, 16, CHUNK])).then_inc(S.sem("ones_rows"), 16)
                    shift.sync(sp)
                chunks.load(sp, 1, 0)
                with sp.Fori(0, steps - 1) as i:
                    for b in range(2):
                        after(sp, sem(f"chunk_used{b}"), i + 1)
                        if not project:
                            after(sp, sem(f"v_copied{b}"), i + 1)
                        if masks == "query_key":
                            after(sp, sem(f"mb{b}"), i + 1)
                        chunks.load(sp, b, i + 1)

            @block.vector
            def _(dve):
                dve.memset(zl[:, :], 0.0)
                if wide:
                    dve.memset(sums[:, :, :], 0.0)
                else:
                    for b in range(2):
                        dve.memset(v[b][:, :, vd:vd + 1], 1.0)
                dve.memset(zr[:, :], 0.0).then_inc(S.sem("constants"), 1)
                dve.wait_ge(S.sem("constants"), 1)
                if wide:
                    dve.tensor_copy(top_wide[:, :, :], top[:, :].unsqueeze(2).broadcast_to([P, heads, P])).then_inc(
                        S.sem("top_wide"), 1)
                    dve.wait_ge(S.sem("tops_made"), 1)
                    dve.tensor_copy(tops[:, :, :], psc[1][:, :, :].rearrange("p a (b q) -> p (a b) q", q=P)).then_inc(
                        S.sem("tops"), 1)
                    dve.wait_ge(S.sem("tops"), 1)
                else:
                    shift.vector(dve)

                def subtract(i, t):
                    u, j = octet_counts(i, t, 0)
                    after(dve, sem(f"scores{u}"), j + 1)
                    after(dve, *weighed(i, t, 0))
                    after(dve, sem(f"summed{u}"), j)
                    dve.tensor_tensor(pt[u][:, :, :], psc[u][:, :, :].rearrange("p a (b q) -> p (a b) q", q=P),
                                      tops[:, :, :], ALU.subtract).then_inc(sem(f"shifted{u}"), 1)

                def weights_sum(i, t):
                    u, j = octet_counts(i, t, 0)
                    after(dve, sem(f"probs{u}"), j + 1)
                    after(dve, sem(f"summed{1 - u}"), j + (1 if u else 0))
                    dve.tensor_tensor(sums[:, :, :], sums[:, :, :], pt[u][:, :, :], ALU.add).then_inc(
                        sem(f"summed{u}"), 1)

                def tile(i, t):
                    b, s = t // TILES, t % TILES
                    vb, j = tile_counts(i, t)
                    if masks == "query_key" and s == 0:
                        after(dve, sem(f"mq{b}"), (i + 1) * 16)
                        after(dve, sem(f"chunk_used{b}"), i)
                        dve.tensor_scalar(mb[b][:, :], mq[b][:, :], -1.0, 1.0, ALU.mult, ALU.add).then_inc(
                            sem(f"mb{b}"), 1)
                    after(dve, sem(f"weighed{vb}"), j)
                    if project:
                        after(dve, sem(f"v_proj{vb}"), j + 1)
                        dve.tensor_tensor(v[vb][:, :, 0:vd],
                                          pv[vb][:, 0:heads * vd].rearrange("p (h d) -> p h d", h=heads),
                                          bias_v[:, :].rearrange("p (h d) -> p h d", h=heads),
                                          ALU.add).then_inc(sem(f"v{vb}"), 1)
                    else:
                        after(dve, sem(f"vin{b}"), (i + 1) * 16)
                        dve.tensor_copy(v[vb][:, :, 0:vd],
                                        vin[b][:, s, :].rearrange("p (h d) -> p h d", h=heads)).then_inc(
                            sem(f"v{vb}"), 1)
                        if s == TILES - 1:
                            after(dve, sem(f"v{vb}"), j + 1)
                            dve.sem_inc(sem(f"v_copied{b}"), 1)

                with dve.Fori(0, steps) as i:
                    for t in range(per_body):
                        tile(i, t)
                        if wide:
                            subtract(i, t)
                        if wide and t:
                            weights_sum(i, t - 1)
                    if wide:
                        weights_sum(i, per_body - 1)
                if last_tile:
                    subtract(steps, 0)
                    weights_sum(steps, 0)

            @block.scalar
            def _(act):
                def exps(i, t, o):
                    u, j = octet_counts(i, t, o)
                    if wide:
                        after(act, sem(f"shifted{u}"), j + 1)
                        act.activation(pt[u][:, :, :], pt[u][:, :, :], ACT.Exp).then_inc(sem(f"probs{u}"), 1)
                        return
                    after(act, sem(f"scores{u}"), j + 1)
                    after(act, *weighed_before(i, t, o))
                    if masks == "key":
                        act.sem_inc(S.sem("exps_begun"), 1)
                        tile_ap = R.mask_col[:, bass.ds(i * per_body + t, 1)]
                        ins = act.activation(pt[u][:, :, :], psc[u][:, :, :].rearrange("p a (b q) -> p (a b) q", q=P),
                                             ACT.Exp, bias=tile_ap)
                    else:
                        ins = act.activation(pt[u][:, :, :], psc[u][:, :, :].rearrange("p a (b q) -> p (a b) q", q=P),
                                             ACT.Exp)
                    ins.then_inc(sem(f"probs{u}"), 1)

                with act.Fori(0, steps) as i:
                    for t in range(per_body):
                        for o in range(octets):
                            exps(i, t, o)
                if last_tile:
                    exps(steps, 0, 0)

            @block.tensor
            def _(pe):
                if not wide:
                    shift.tensor(pe)
                pe.wait_ge(S.sem("constants"), 1)
                if not wide:
                    pe.wait_ge(S.sem("ones_rows"), 32)
                pe.matmul(O[:, :], zl[:, :], zr[:, :], start=True, stop=True)

                def values(i, t):
                    b, s = t // TILES, t % TILES
                    vb, j = tile_counts(i, t)
                    after(pe, sem(f"vin{b}"), (i + 1) * 16)
                    after(pe, sem(f"v{vb}"), j)
                    for d in range(DC):
                        last = pe.matmul(pv[vb][:, 0:heads * vd], vin[b][:, d, s * P:(s + 1) * P], w_v[:, d, :],
                                         start=(d == 0), stop=(d == DC - 1))
                    last.then_inc(sem(f"v_proj{vb}"), 1)

                def scores(i, t, o, keys=None):
                    b, s = t // TILES, t % TILES
                    u, j = octet_counts(i, t, o)
                    if o == 0 and s == 0 and keys is None:
                        after(pe, sem(f"kt{b}"), (i + 1) * kt_count)
                        if masks == "query_key":
                            after(pe, sem(f"mb{b}"), i + 1)
                    after(pe, sem(f"shifted{u}" if wide else f"probs{u}"), j)
                    for half in range(2):
                        h0 = 8 * o + 4 * half
                        for k in range(4):
                            h = h0 + k
                            out = psc[u][:, half, k * P:(k + 1) * P]
                            if wide:
                                c = h // per_chunk
                                lhs = kt[b][:, c, s * P:(s + 1) * P] if keys is None else keys[:, c, :]
                                last = pe.matmul(out, lhs, q[c][:, h % per_chunk, :], start=(k == 0),
                                                 stop=(k == 3), skip_group_check=True)
                            else:
                                last = pe.matmul(out, kt[b][:, h, s * P:(s + 1) * P], q.rows[:, h, :], start=(k == 0),
                                                 stop=(masks != "query_key" and k == 3), skip_group_check=True)
                        if masks == "query_key":
                            last = pe.matmul(psc[u][:, half, :].rearrange("p (k q) -> p k q", k=4),
                                             mb[b][:, s * P:(s + 1) * P],
                                             R.neg_big[:, :].unsqueeze(1).broadcast_to([P, 4, P]),
                                             start=False, stop=True, skip_group_check=True)
                    last.then_inc(sem(f"scores{u}"), 1)

                def weigh(i, t, o, vals=None):
                    u, j = octet_counts(i, t, o)
                    vb, jv = tile_counts(i, t)
                    after(pe, sem(f"probs{u}"), j + 1)
                    if vals is None:
                        after(pe, sem(f"v{vb}"), jv + 1)
                    vv = v[vb] if vals is None else vals
                    for k in range(8):
                        h = 8 * o + k
                        if wide:
                            out = O[64 * (h % 2):64 * (h % 2) + vd, (h // 2) * P:(h // 2 + 1) * P]
                            lhs = vv[:, h, :]
                        else:
                            out = O[32 * (h % 4):32 * (h % 4) + vd + 1, (h // 4) * P:(h // 4 + 1) * P]
                            lhs = vv[:, h, :]
                        last = pe.matmul(out, lhs, pt[u][:, k, :], start=False, stop=False, skip_group_check=True)
                    done, n = weighed(i, t, o)
                    last.then_inc(done, 1)
                    if o == octets - 1 and t % TILES == TILES - 1 and vals is None:
                        after(pe, done, n + 1)
                        pe.sem_inc(sem(f"chunk_used{t // TILES}"), 1)

                if wide:
                    pe.wait_ge(S.sem("top_wide"), 1)
                    for h in range(heads):
                        last = pe.matmul(psc[1][:, h // 4, (h % 4) * P:(h % 4 + 1) * P], top_wide[:, h, :],
                                         R.ident[:, :], start=True, stop=True)
                    last.then_inc(S.sem("tops_made"), 1)
                    pe.wait_ge(S.sem("tops"), 1)
                else:
                    shift.wait(pe)
                    q.wait(pe)
                order = [(t, o) for t in range(per_body) for o in range(octets)]

                def start(i, t, o, last_body):
                    scores(i, t, o)
                    if project and o == 0:
                        if t + 1 < per_body:
                            values(i, t + 1)
                        elif not last_body:
                            values(i + 1, 0)

                def body(i, last_body):
                    for n, (t, o) in enumerate(order):
                        if n + 1 < len(order):
                            start(i, *order[n + 1], last_body)
                        elif not last_body:
                            start(i + 1, *order[0], False)
                        weigh(i, t, o)

                if project:
                    values(0, 0)
                start(0, 0, 0, steps == 1)
                if steps > 1:
                    with pe.Fori(0, steps - 1) as i:
                        body(i, False)
                body(steps - 1, True)
                if last_tile:
                    scores(steps, 0, 0, keys=last_tile[0])
                    weigh(steps, 0, 0, vals=last_tile[1])

            @block.gpsimd
            def _(pool):
                start_counts(pool, S)


def finish_heads16(nc, S, A, R, O, bias=None):
    with ExitStack() as mem:
        o_sb = mem.enter_context(nc.sbuf_tensor(f"{S.name}_o", [P, 4, P], F32))
        rec = mem.enter_context(nc.sbuf_tensor(f"{S.name}_rec", [P, 16], F32))
        out = mem.enter_context(nc.sbuf_tensor(f"{S.name}_out", [P, 16, 16], F32))
        ps = mem.enter_context(nc.psum_tensor(f"{S.name}_ops", [P, BANK], F32))
        with nc.Block() as block:
            @block.tensor
            def _(pe):
                pe.wait_ge(S.sem("o_copied"), 1)
                for s in range(4):
                    last = pe.transpose(ps[:, s * P:(s + 1) * P], o_sb[:, s, :], R.ident[:, :])
                last.then_inc(S.sem("o_turned"), 1)

            @block.vector
            def _(dve):
                link = Link(dve, S.sem("finish_link"))
                dve.tensor_copy(o_sb[:, :, :], O[:, :].rearrange("p (s q) -> p s q", s=4)).then_inc(
                    S.sem("o_copied"), 1)
                dve.wait_ge(S.sem("o_turned"), 1)
                rows = ps[:, :].rearrange("p (h f) -> p h f", f=32)
                link(dve.reciprocal(rec[:, :], rows[:, :, 16]))
                link(dve.tensor_tensor(out[:, :, :], rows[:, :, 0:16],
                                       rec[:, :].unsqueeze(2).broadcast_to([P, 16, 16]), ALU.mult))
                link(dve.tensor_tensor(R.x[:, :], R.x[:, :], out[:, :, :].rearrange("p h d -> p (h d)"), ALU.add))


def l3_xattn(nc, A, R):
    H = 16
    with Stage(nc, "l3x") as S:
        xn, nw = S.sb("xn", [P, DIM]), S.sb("nw", [P, 16])
        qb = [S.sb(f"qb{c}", [P, 8, P], BF16) for c in range(DC)]
        hm = S.sb("hm", [P, 8])
        R.neg_big = S.sb("neg_big", [P, P], BF16)
        top = S.sb("top", [P, H])
        qT = S.sb("qT", [P, DC * P])
        q_rows = S.sb("q_rows", [STACK + 3, 16, P], BF16)
        with ExitStack() as mem:
            q = QueryRows(nc, S, mem, q_rows)
            pt = mem.enter_context(nc.psum_tensor("l3x_pt", [P, BANK], F32))
            with nc.Block() as block:
                @block.sync
                def _(sp):
                    sp.dma_start(hm[:, :], A["c_head16"]).then_inc(S.sem("hm"), 16)
                    q.sync(sp)

                @block.scalar
                def _(act):
                    norm_scalar(act, S, "n", nw)

                @block.vector
                def _(dve):
                    link = Link(dve, S.sem("dve_link"))
                    norm_vector(dve, link, S, "n", R.x[:, :], xn[:, :], nw)
                    link(dve.tensor_scalar(R.neg_big[:, :], R.ident[:, :], -MASK_BIG, None, ALU.mult))
                    dve.wait_ge(S.sem("n_turned"), 1)
                    dve.wait_ge(S.sem("hm"), 16)
                    link(dve.tensor_copy(qT[:, :], pt[:, 0:DC * P]))
                    q.vector(dve, link, qT[:, :], 0.25)
                    spread_queries(dve, link, qT, None, qb, hm, 8, 0.25)

                @block.tensor
                def _(pe):
                    turn_tensor(pe, S, "n", xn, pt, R.ident)
        ctxT = A["ctxT"].rearrange("(c p) n -> c p n", p=P)
        with ExitStack() as mem:
            chunks = KeyChunks(nc, S, A, R, mem, H, DC, R.KS, A["ctx"], False, "query_key")
            find_maximum(nc, S, A, R, H, DC, 8, qb, ctxT, None, None, None, top, "query_key", True, chunks)
            O = S.psum("O")
            attend(nc, S, R, H, 8, q, chunks, None, None, top, "query_key", O, None)
        finish_heads16(nc, S, A, R, O)


def spread_queries(dve, link, qT, q, qb, head_mask, per_chunk, scale):
    for c in range(len(qb)):
        link(dve.scalar_tensor_tensor(
            (qb if q is None else q)[c][:, :, :],
            qT[:, c * P:(c + 1) * P].unsqueeze(1).broadcast_to([P, per_chunk, P]), scale,
            head_mask[:, :].unsqueeze(2).broadcast_to([P, per_chunk, P]), ALU.mult, ALU.mult))
        if q is not None:
            link(dve.tensor_copy(qb[c][:, :, :], q[c][:, :, :]))


def l1_xattn(nc, A, R):
    H = 16
    n_tiles = R.keys // P
    with Stage(nc, "l1x") as S:
        xn, xT, nw = S.sb("xn", [P, DIM]), S.sb("xT", [P, DC, P]), S.sb("nw", [P, 16])
        qb = [S.sb(f"qb{c}", [P, 8, P], BF16) for c in range(DC)]
        hm = S.sb("hm", [P, 8])
        top = S.sb("top", [P, H])
        w = S.sb("w", [P, 3, DC, DIM])
        bq, bk, bv = S.sb("bq", [P, DC]), S.sb("bk", [P, DC]), S.sb("bv", [P, DIM])
        qT = S.sb("qT", [P, DC * P])
        R.mask_col = S.sb("mask_col", [P, n_tiles])
        R.ones3 = S.sb("ones3", [P, P], BF16)
        q_rows = S.sb("q_rows", [STACK + 3, 16, P], BF16)
        keep = ExitStack()
        chunks = KeyChunks(nc, S, A, R, keep, H, DC, R.KS, A["ctxT"].rearrange("(c p) n -> c p n", p=P), True, "key")
        mask_memory = ExitStack()
        R.mask3 = mask_memory.enter_context(nc.sbuf_tensor("l1x_mask3", [P, R.keys], BF16))
        with ExitStack() as mem:
            q = QueryRows(nc, S, mem, q_rows)
            mask = mem.enter_context(nc.sbuf_tensor("l1x_mask", [n_tiles, P], F32))
            parts = [mem.enter_context(nc.sbuf_tensor(f"l1x_mpart{n}", [n_tiles, P], BF16)) for n in range(3)]
            pt, pq, pm = [mem.enter_context(nc.psum_tensor(f"l1x_p{n}", [P, BANK], F32)) for n in range(3)]
            scratch = nc.dram_tensor("l1x_mask_rows", (3, n_tiles, P), BF16, kind="Internal").ap()
            loads = Loads(S.sem("loads"))
            with nc.Block() as block:
                @block.sync
                def _(sp):
                    loads(sp.dma_start(mask[:, :], A["mask_row"]))
                    loads(sp.dma_start(hm[:, :], A["c_head16"]))
                    for n, name in enumerate(("wq", "wk", "wv")):
                        loads(sp.dma_start(w[:, n, :, :], by_rows(A[f"L1_xattn_{name}"])))
                    loads(sp.dma_start(bv[:, :], A["L1_xattn_bv"].partition_broadcast(P)))
                    loads(sp.dma_start(bq[:, :], column(A["L1_xattn_bq"]), allow_slow_non_contiguous=True))
                    loads(sp.dma_start(bk[:, :], column(A["L1_xattn_bk"]), allow_slow_non_contiguous=True))
                    sp.wait_ge(S.sem("mask_split"), 1)
                    for n in range(3):
                        sp.dma_start(scratch[n], parts[n][:, :]).then_inc(S.sem("mask_out"), 16)
                    sp.wait_ge(S.sem("mask_out"), 48)
                    sp.wait_ge(S.sem("mask_zero"), 1)
                    sp.dma_start(R.mask3[MASK_ROW:MASK_ROW + 3, :], scratch.rearrange("n t p -> n (t p)")).then_inc(S.sem("mask_in"), 16)
                    q.sync(sp)

                @block.gpsimd
                def _(pool):
                    pool.memset(R.mask3[:, :], 0.0).then_inc(S.sem("mask_zero"), 1)

                @block.scalar
                def _(act):
                    norm_scalar(act, S, "n", nw)

                @block.vector
                def _(dve):
                    link = Link(dve, S.sem("dve_link"))
                    link(dve.memset(R.ones3[:, :], 0.0))
                    link(dve.memset(R.ones3[MASK_ROW:MASK_ROW + 3, :], 1.0))
                    norm_vector(dve, link, S, "n", R.x[:, :], xn[:, :], nw)
                    turn_vector(dve, S, "n", xT, pt)
                    dve.wait_ge(S.sem("loads"), loads.total)
                    link(dve.tensor_scalar(mask[:, :], mask[:, :], -1.0, 1.0, ALU.mult, ALU.add))
                    dve.tensor_scalar(mask[:, :], mask[:, :], -10000.0, None, ALU.mult).then_inc(
                        S.sem("mask_bias"), 1)
                    dve.wait_ge(S.sem("mask_turned"), 1)
                    link(dve.tensor_copy(R.mask_col[:, :], pm[:, 0:n_tiles]))
                    for n in range(3):
                        link(dve.tensor_copy(parts[n][:, :], mask[:, :]))
                        link(dve.tensor_tensor(mask[:, :], mask[:, :], parts[n][:, :], ALU.subtract))
                    dve.sem_inc(S.sem("mask_split"), 1)
                    dve.wait_ge(S.sem("q_proj"), 1)
                    for c in range(DC):
                        link(dve.tensor_scalar(qT[:, c * P:(c + 1) * P], pq[:, c * P:(c + 1) * P], bq[:, c:c + 1],
                                               None, ALU.add))
                    q.vector(dve, link, qT[:, :], 0.25)
                    spread_queries(dve, link, qT, None, qb, hm, 8, 0.25)
                    for c in range(DC):
                        dve.memset(qb[c][MASK_ROW:MASK_ROW + 3, 0:MASK_HEAD, :], 1.0)
                        dve.memset(qb[c][MASK_ROW:MASK_ROW + 3, MASK_HEAD + 1:, :], 1.0)

                @block.tensor
                def _(pe):
                    turn_tensor(pe, S, "n", xn, pt, R.ident)
                    pe.wait_ge(S.sem("mask_bias"), 1)
                    pe.transpose(pm[:, 0:n_tiles], mask[:, :], R.ident[0:n_tiles, 0:n_tiles]).then_inc(
                        S.sem("mask_turned"), 1)
                    pe.wait_ge(S.sem("n_xT"), 1)
                    pe.wait_ge(S.sem("loads"), loads.total)
                    for o in range(DC):
                        for c in range(DC):
                            last = pe.matmul(pq[:, o * P:(o + 1) * P], w[:, 0, c, o * P:(o + 1) * P], xT[:, c, :],
                                             start=(c == 0), stop=(c == DC - 1))
                    last.then_inc(S.sem("q_proj"), 1)
        ctxT = A["ctxT"].rearrange("(c p) n -> c p n", p=P)
        with mask_memory:
            find_maximum(nc, S, A, R, H, DC, 8, qb, ctxT, "plain", w[:, 1, :, :], bk, top, "key", True, chunks)
        O = S.psum("O")
        with keep:
            attend(nc, S, R, H, 8, q, chunks, w[:, 2, :, :], bv, top, "key", O, None)
        finish_heads16(nc, S, A, R, O)


def l0_xattn(nc, A, R):
    H, HD, KC = 8, 64, 4
    INNER = H * HD
    with Stage(nc, "l0x") as S:
        q = [S.sb(f"q{c}", [P, 2, P]) for c in range(KC)]
        qb = [S.sb(f"qb{c}", [P, 2, P], BF16) for c in range(KC)]
        hm = S.sb("hm", [P, 2])
        top = S.sb("top", [P, H])
        wk, wv = S.sb("wk", [P, DC, INNER]), S.sb("wv", [P, DC, INNER])
        bias_k, bias_v = S.sb("bias_k", [P, KC]), S.sb("bias_v", [P, INNER])
        R.nbias_k = S.sb("nbias_k", [P, KC])
        kl, vl = S.sb("kl", [P, KC, P]), S.sb("vl", [P, H, HD])
        klb = S.sb("klb", [P, KC, P], BF16)
        ltop = S.sb("ltop", [P, H])
        with ExitStack() as mem:
            def sb(name, shape, dt=F32):
                return mem.enter_context(nc.sbuf_tensor(f"l0x_{name}", shape, dt))
            xn, nw, nw2 = sb("xn", [P, DIM]), sb("nw", [P, 16]), sb("nw2", [P, 16])
            ln, lT = sb("ln", [P, DIM]), sb("lT", [P, DC, P])
            wq = sb("wq", [P, DC, INNER])
            gl, bl = sb("gl", [P, DIM]), sb("bl", [P, DIM])
            gx, bx = sb("gx", [P, DC]), sb("bx", [P, DC])
            bxb = sb("bxb", [P, DC, P])
            pq, pk, pv, pbk, pbv, ps0, ps1, pt = [
                mem.enter_context(nc.psum_tensor(f"l0x_p{n}", [P, BANK], F32)) for n in range(8)]
            loads = Loads(S.sem("loads"))
            with nc.Block() as block:
                @block.sync
                def _(sp):
                    loads(sp.dma_start(hm[:, :], A["c_head64"]))
                    loads(sp.dma_start(gl[:, :], A["L0_xattn_gamma_l"].partition_broadcast(P)))
                    loads(sp.dma_start(bl[:, :], A["L0_xattn_beta_l"].partition_broadcast(P)))
                    loads(sp.dma_start(gx[:, :], column(A["L0_xattn_gamma_x"]), allow_slow_non_contiguous=True))
                    loads(sp.dma_start(bx[:, :], column(A["L0_xattn_beta_x"]), allow_slow_non_contiguous=True))
                    loads(sp.dma_start(wq[:, :, :], by_rows(A["L0_xattn_Wq"])))
                    loads(sp.dma_start(wk[:, :, :], by_rows(A["L0_xattn_Wk"])))
                    loads(sp.dma_start(wv[:, :, :], by_rows(A["L0_xattn_Wv"])))

                @block.scalar
                def _(act):
                    norm_scalar(act, S, "n", nw)
                    norm_scalar(act, S, "m", nw2)

                @block.vector
                def _(dve):
                    link = Link(dve, S.sem("dve_link"))
                    norm_vector(dve, link, S, "n", R.x[:, :], xn[:, :], nw)
                    norm_vector(dve, link, S, "m", xn[:, :], ln[:, :], nw2)
                    dve.wait_ge(S.sem("loads"), loads.total)
                    link(dve.tensor_tensor(ln[:, :], ln[:, :], gl[:, :], ALU.mult))
                    dve.tensor_tensor(ln[:, :], ln[:, :], bl[:, :], ALU.add).then_inc(S.sem("ln"), 1)
                    turn_vector(dve, S, "l", lT, pt)
                    link(dve.tensor_copy(bxb[:, :, :], bx[:, :].unsqueeze(2).broadcast_to([P, DC, P])))
                    dve.sem_inc(S.sem("bxb"), 1)
                    dve.wait_ge(S.sem("q_proj"), 1)
                    spread_queries(dve, link, pq, q, qb, hm, 2, HD ** -0.5)
                    dve.sem_inc(S.sem("q"), 1)
                    dve.wait_ge(S.sem("latents_proj"), 1)
                    link(dve.tensor_copy(kl[:, :, :], pk[:, :].rearrange("p (c t) -> p c t", c=KC)))
                    dve.tensor_copy(klb[:, :, :], kl[:, :, :]).then_inc(S.sem("klb"), 1)
                    dve.tensor_copy(vl[:, :, :], pv[:, :].rearrange("p (h d) -> p h d", h=H))
                    dve.wait_ge(S.sem("bias_proj"), 1)
                    link(dve.tensor_copy(bias_k[:, :], pbk[:, 0:KC]))
                    dve.tensor_copy(R.nbias_k[64:P, :], pbk[0:64, 0:KC])
                    dve.tensor_scalar(R.nbias_k[0:64, :], pbk[64:P, 0:KC], -1.0, None, ALU.mult)
                    dve.tensor_copy(bias_v[:, :], pbv[:, :])
                    for c in range(DC):
                        dve.tensor_scalar(wk[:, c, :], wk[:, c, :], gx[:, c:c + 1], None, ALU.mult)
                        dve.tensor_scalar(wv[:, c, :], wv[:, c, :], gx[:, c:c + 1], None, ALU.mult)
                    dve.wait_ge(S.sem("latent_scores"), 1)
                    dve.tensor_reduce(ltop[:, 0:4], ps0[:, :].rearrange("p (h k) -> p h k", h=4), AX.X, ALU.max)
                    dve.tensor_reduce(ltop[:, 4:8], ps1[:, :].rearrange("p (h k) -> p h k", h=4), AX.X, ALU.max)

                @block.tensor
                def _(pe):
                    turn_tensor(pe, S, "l", ln, pt, R.ident, ready="ln")
                    pe.wait_ge(S.sem("l_xT"), 1)
                    pe.wait_ge(S.sem("loads"), loads.total)
                    for o in range(KC):
                        for c in range(DC):
                            last = pe.matmul(pq[:, o * P:(o + 1) * P], wq[:, c, o * P:(o + 1) * P], lT[:, c, :],
                                             start=(c == 0), stop=(c == DC - 1))
                    last.then_inc(S.sem("q_proj"), 1)
                    for o in range(KC):
                        for c in range(DC):
                            pe.matmul(pk[:, o * P:(o + 1) * P], wk[:, c, o * P:(o + 1) * P], lT[:, c, :],
                                      start=(c == 0), stop=(c == DC - 1))
                    for c in range(DC):
                        last = pe.matmul(pv[:, :], lT[:, c, :], wv[:, c, :], start=(c == 0), stop=(c == DC - 1))
                    last.then_inc(S.sem("latents_proj"), 1)
                    pe.wait_ge(S.sem("bxb"), 1)
                    for o in range(KC):
                        for c in range(DC):
                            pe.matmul(pbk[:, o:o + 1], wk[:, c, o * P:(o + 1) * P], bx[:, c:c + 1],
                                      start=(c == 0), stop=(c == DC - 1))
                    for c in range(DC):
                        last = pe.matmul(pbv[:, :], bxb[:, c, :], wv[:, c, :], start=(c == 0), stop=(c == DC - 1))
                    last.then_inc(S.sem("bias_proj"), 1)
                    pe.wait_ge(S.sem("q"), 1)
                    pe.wait_ge(S.sem("klb"), 1)
                    for h in range(H):
                        last = pe.matmul((ps0 if h < 4 else ps1)[:, (h % 4) * P:(h % 4 + 1) * P],
                                         qb[h // 2][:, h % 2, :], klb[:, h // 2, :], start=True, stop=True)
                    last.then_inc(S.sem("latent_scores"), 1)
        sums = S.sb("sums", [P, H, P])
        with ExitStack() as mem:
            chunks = KeyChunks(nc, S, A, R, mem, H, KC, R.KT, R.nT, True, None)
            find_maximum(nc, S, A, R, H, KC, 2, qb, R.nT, "rope", wk, bias_k, top, None, False, chunks, seed=ltop)
            O = S.psum("O")
            attend(nc, S, R, H, 2, q, chunks, wv, bias_v, top, None, O, sums, last_tile=(kl, vl))
        with ExitStack() as mem:
            def sb(name, shape, dt=F32):
                return mem.enter_context(nc.sbuf_tensor(f"l0x_{name}", shape, dt))
            ones = sb("ones", [P, P])
            rec = sb("rec", [P, H, P])
            oT = sb("oT", [P, KC, P])
            wo = sb("wo", [P, KC, DIM])
            pr = [mem.enter_context(nc.psum_tensor(f"l0x_pr{n}", [P, BANK], F32)) for n in range(2)]
            py = mem.enter_context(nc.psum_tensor("l0x_py", [P, BANK], F32))
            with nc.Block() as block:
                @block.sync
                def _(sp):
                    sp.dma_start(wo[:, :, :], by_rows(A["L0_xattn_Wo"])).then_inc(S.sem("wo"), 16)

                @block.vector
                def _(dve):
                    link = Link(dve, S.sem("finish_link"))
                    dve.memset(ones[:, :], 1.0).then_inc(S.sem("ones"), 1)
                    dve.wait_ge(S.sem("totals"), 1)
                    for n in range(2):
                        link(dve.reciprocal(rec[:, 4 * n:4 * n + 4, :], pr[n][:, :].rearrange("p (h q) -> p h q", h=4)))
                    for g in range(2):
                        rows = slice(64 * g, 64 * g + 64)
                        last = dve.tensor_tensor(oT[rows, :, :], O[rows, :].rearrange("p (s q) -> p s q", s=KC),
                                                 rec[rows, g:H:2, :], ALU.mult)
                        link(last)
                    dve.sem_inc(S.sem("oT"), 1)
                    dve.wait_ge(S.sem("y"), 1)
                    dve.tensor_tensor(R.x[:, :], R.x[:, :], py[:, 0:DIM], ALU.add)

                @block.tensor
                def _(pe):
                    pe.wait_ge(S.sem("ones"), 1)
                    for n in range(2):
                        last = pe.matmul(pr[n][:, :], ones[:, :],
                                         sums[:, 4 * n:4 * n + 4, :].rearrange("p h q -> p (h q)"), start=True, stop=True)
                    last.then_inc(S.sem("totals"), 1)
                    pe.wait_ge(S.sem("oT"), 1)
                    pe.wait_ge(S.sem("wo"), 16)
                    for c in range(KC):
                        last = pe.matmul(py[:, 0:DIM], oT[:, c, :], wo[:, c, :], start=(c == 0), stop=(c == KC - 1))
                    last.then_inc(S.sem("y"), 1)


def head_stats(dve, link, f2, sm, ss, rn_in, ratio, tmp, heads_n):
    link(dve.tensor_tensor(tmp, sm, sm, ALU.mult))
    link(dve.scalar_tensor_tensor(tmp, tmp, -1.0 / P, ss, ALU.mult, ALU.add))
    link(dve.tensor_scalar(tmp, tmp, 1.0 / (P - 1), None, ALU.mult))
    link(dve.tensor_scalar(ratio, tmp, 1.0, 2.0, ALU.min, ALU.mult))
    link(dve.tensor_scalar(tmp, tmp, 1.0, None, ALU.add))
    link(dve.reciprocal(tmp, tmp))
    link(dve.tensor_tensor(ratio, ratio, tmp, ALU.mult))


def l2_xattn(nc, A, R):
    H, HD = 8, 128
    W = H * HD
    GW = HD + 2
    steps = R.keys // CHUNK // 2
    with Stage(nc, "l2x") as S:
        w = S.sb("w", [P, DC, W])
        bias = S.sb("bias", [P, W])
        fq = S.sb("fq", [P, W])
        qs = S.sb("qs", [P, 5, H])
        wp1 = S.sb("wp1", [P, DC, HD])
        Msb = S.sb("Msb", [P, H, GW])
        with ExitStack() as mem:
            def sb(name, shape, dt=F32):
                return mem.enter_context(nc.sbuf_tensor(f"l2x_{name}", shape, dt))
            xn, nw, nw2 = sb("xn", [P, DIM]), sb("nw", [P, 16]), sb("nw2", [P, 16])
            xn2, xT = sb("xn2", [P, DIM]), sb("xT", [P, DC, P])
            g, b = sb("g", [P, DC]), sb("b", [P, DC])
            bb = sb("bb", [P, DC, P])
            sq = sb("sq", [P, W])
            pt = mem.enter_context(nc.psum_tensor("l2x_pt", [P, BANK], F32))
            pb = mem.enter_context(nc.psum_tensor("l2x_pb", [P, 2, BANK], F32))
            pf = mem.enter_context(nc.psum_tensor("l2x_pf", [P, 2, BANK], F32))
            loads = Loads(S.sem("loads"))
            with nc.Block() as block:
                @block.sync
                def _(sp):
                    loads(sp.dma_start(w[:, :, :], by_rows(A["L2_xattn_w_in"])))
                    loads(sp.dma_start(g[:, :], column(A["L2_xattn_ln_g"]), allow_slow_non_contiguous=True))
                    loads(sp.dma_start(b[:, :], column(A["L2_xattn_ln_b"]), allow_slow_non_contiguous=True))

                @block.scalar
                def _(act):
                    norm_scalar(act, S, "n", nw)
                    norm_scalar(act, S, "m", nw2)
                    act.wait_ge(S.sem("qss"), 1)
                    act.activation(qs[:, 2, :], qs[:, 1, :], ACT.Sqrt).then_inc(S.sem("qn"), 1)

                @block.vector
                def _(dve):
                    link = Link(dve, S.sem("dve_link"))
                    norm_vector(dve, link, S, "n", R.x[:, :], xn[:, :], nw)
                    norm_vector(dve, link, S, "m", xn[:, :], xn2[:, :], nw2)
                    turn_vector(dve, S, "m", xT, pt)
                    dve.wait_ge(S.sem("loads"), loads.total)
                    dve.tensor_copy(bb[:, :, :], b[:, :].unsqueeze(2).broadcast_to([P, DC, P])).then_inc(
                        S.sem("bb"), 1)
                    dve.wait_ge(S.sem("bias_proj"), 1)
                    link(dve.tensor_copy(bias[:, :], pb[:, :, :].rearrange("p a n -> p (a n)")))
                    for c in range(DC):
                        link(dve.tensor_scalar(w[:, c, :], w[:, c, :], g[:, c:c + 1], None, ALU.mult))
                    dve.sem_inc(S.sem("w_folded"), 1)
                    dve.wait_ge(S.sem("q_proj"), 1)
                    link(dve.tensor_tensor(fq[:, :], pf[:, :, :].rearrange("p a n -> p (a n)"), bias[:, :], ALU.add))
                    link(dve.tensor_tensor(sq[:, :], fq[:, :], fq[:, :], ALU.mult))
                    link(dve.tensor_reduce(qs[:, 0, :], fq[:, :].rearrange("p (h d) -> p h d", h=H), AX.X, ALU.add))
                    dve.tensor_reduce(qs[:, 1, :], sq[:, :].rearrange("p (h d) -> p h d", h=H), AX.X, ALU.add).then_inc(
                        S.sem("qss"), 1)
                    dve.wait_ge(S.sem("qss"), 1)
                    head_stats(dve, link, None, qs[:, 0, :], qs[:, 1, :], None, qs[:, 3, :], qs[:, 4, :], H)
                    dve.wait_ge(S.sem("qn"), 1)
                    dve.reciprocal(qs[:, 2, :], qs[:, 2, :])

                @block.tensor
                def _(pe):
                    turn_tensor(pe, S, "m", xn2, pt, R.ident)
                    pe.wait_ge(S.sem("loads"), loads.total)
                    pe.wait_ge(S.sem("bb"), 1)
                    for n in range(2):
                        for c in range(DC):
                            last = pe.matmul(pb[:, n, :], bb[:, c, :], w[:, c, n * BANK:(n + 1) * BANK],
                                             start=(c == 0), stop=(c == DC - 1))
                    last.then_inc(S.sem("bias_proj"), 1)
                    pe.wait_ge(S.sem("w_folded"), 1)
                    pe.wait_ge(S.sem("m_xT"), 1)
                    for n in range(2):
                        for c in range(DC):
                            last = pe.matmul(pf[:, n, :], xT[:, c, :], w[:, c, n * BANK:(n + 1) * BANK],
                                             start=(c == 0), stop=(c == DC - 1))
                    last.then_inc(S.sem("q_proj"), 1)
        with ExitStack() as mem:
            def sb(name, shape, dt=F32):
                return mem.enter_context(nc.sbuf_tensor(f"l2x_{name}", shape, dt))
            nin = [sb(f"nin{b}", [P, DC, CHUNK]) for b in range(2)]
            f = [sb(f"f{b}", [P, TILES, W]) for b in range(2)]
            gk = [sb(f"gk{b}", [P, TILES, H, GW]) for b in range(2)]
            sq = [sb(f"fsq{b}", [P, W]) for b in range(2)]
            ks = [sb(f"ks{b}", [P, 5, TILES, H]) for b in range(2)]
            zl, zr = sb("zl", [P, P]), sb("zr", [P, BANK])
            pf = [mem.enter_context(nc.psum_tensor(f"l2x_kf{b}", [P, 2, BANK], F32)) for b in range(2)]
            pM = mem.enter_context(nc.psum_tensor("l2x_M", [P, 3, BANK], F32))
            src = R.nT.rearrange("c p (n k) -> n p c k", k=CHUNK)

            def use(i, b, t):
                k = b * TILES + t
                return k % 2, i * TILES + k // 2

            with nc.Block() as block:
                @block.sync
                def _(sp):
                    with sp.Fori(0, steps) as i:
                        for b in range(2):
                            after(sp, S.counted(f"nin_used{b}"), i)
                            sp.dma_start(nin[b][:, :, :], src[bass.ds(i * 2 + b, 1)].squeeze(0)).then_inc(
                                S.counted(f"nin{b}"), 16)

                def squares_sum(dve, i, b, t):
                    u, j = use(i, b, t)
                    after(dve, S.counted(f"sq{u}"), j + 1)
                    dve.tensor_reduce(ks[b][:, 1, t, :], sq[u][:, :].rearrange("p (h d) -> p h d", h=H), AX.X,
                                      ALU.add).then_inc(S.counted(f"sums{b}"), 1)
                    after(dve, S.counted(f"sums{b}"), i * 2 * TILES + min(2 * t + 3, 2 * TILES))
                    dve.sem_inc(S.counted(f"sq_read{u}"), 1)

                @block.vector
                def _(dve):
                    dve.memset(zl[:, :], 0.0).then_inc(S.sem("constants"), 1)
                    dve.memset(zr[:, :], 0.0).then_inc(S.sem("constants"), 1)
                    for b in range(2):
                        dve.memset(gk[b][:, :, :, HD + 1:GW], 1.0).then_inc(S.sem("constants"), 1)

                    with dve.Fori(0, steps) as i:
                        for b in range(2):
                            after(dve, S.counted(f"f_used{b}"), i)
                            for t in range(TILES):
                                u, j = use(i, b, t)
                                after(dve, S.counted(f"f_proj{u}"), j + 1)
                                dve.tensor_tensor(f[b][:, t, :], pf[u][:, :, :].rearrange("p a n -> p (a n)"),
                                                  bias[:, :], ALU.add).then_inc(S.counted(f"f{u}"), 1)
                                after(dve, S.counted(f"f{u}"), j + 1)
                                dve.tensor_reduce(ks[b][:, 0, t, :], f[b][:, t, :].rearrange("p (h d) -> p h d", h=H),
                                                  AX.X, ALU.add).then_inc(S.counted(f"sums{b}"), 1)
                                if t:
                                    squares_sum(dve, i, b, t - 1)
                            squares_sum(dve, i, b, TILES - 1)
                            after(dve, S.counted(f"sums{b}"), (i + 1) * 2 * TILES)
                            dve.sem_inc(S.counted(f"ss{b}"), 1)
                            n0 = 7
                            sm, ss, ratio, tmp = ks[b][:, 0], ks[b][:, 1], gk[b][:, :, :, HD], ks[b][:, 4]

                            def lk(n, ins):
                                ins.then_inc(S.counted(f"stat{b}"), 1)
                                after(dve, S.counted(f"stat{b}"), i * n0 + n)
                            lk(1, dve.tensor_tensor(tmp, sm, sm, ALU.mult))
                            lk(2, dve.scalar_tensor_tensor(tmp, tmp, -1.0 / P, ss, ALU.mult, ALU.add))
                            lk(3, dve.tensor_scalar(tmp, tmp, 1.0 / (P - 1), None, ALU.mult))
                            lk(4, dve.tensor_scalar(ks[b][:, 3], tmp, 1.0, 2.0, ALU.min, ALU.mult))
                            lk(5, dve.tensor_scalar(tmp, tmp, 1.0, None, ALU.add))
                            lk(6, dve.reciprocal(tmp, tmp))
                            dve.tensor_tensor(ratio, ks[b][:, 3], tmp, ALU.mult).then_inc(S.counted(f"ratio{b}"), 1)
                            after(dve, S.counted(f"kn{b}"), i + 1)
                            lk(7, dve.reciprocal(ks[b][:, 2], ks[b][:, 2]))
                            dve.sem_inc(S.counted(f"rn{b}"), 1)

                @block.scalar
                def _(act):
                    with act.Fori(0, steps) as i:
                        for b in range(2):
                            for t in range(TILES):
                                u, j = use(i, b, t)
                                after(act, S.counted(f"f{u}"), j + 1)
                                after(act, S.counted(f"sq_read{u}"), j)
                                act.activation(sq[u][:, :], f[b][:, t, :], ACT.Square).then_inc(S.counted(f"sq{u}"), 1)
                            after(act, S.counted(f"ss{b}"), i + 1)
                            after(act, S.counted(f"gk{b}"), i * TILES)
                            act.activation(ks[b][:, 2], ks[b][:, 1], ACT.Sqrt).then_inc(S.counted(f"kn{b}"), 1)

                @block.tensor
                def _(pe):
                    def project(i, b):
                        after(pe, S.counted(f"nin{b}"), (i + 1) * 16)
                        for t in range(TILES):
                            u, j = use(i, b, t)
                            after(pe, S.counted(f"f{u}"), j)
                            for n in range(2):
                                for c in range(DC):
                                    last = pe.matmul(pf[u][:, n, :], nin[b][:, c, t * P:(t + 1) * P],
                                                     w[:, c, n * BANK:(n + 1) * BANK], start=(c == 0),
                                                     stop=(c == DC - 1))
                            last.then_inc(S.counted(f"f_proj{u}"), 1)
                        after(pe, S.counted(f"f_proj{u}"), j + 1)
                        pe.sem_inc(S.counted(f"nin_used{b}"), 1)

                    def gather(i, b):
                        after(pe, S.counted(f"ratio{b}"), i + 1)
                        for t in range(TILES):
                            after(pe, S.counted(f"gk{b}"), i * TILES + t + 1)
                            for h in range(H):
                                last = pe.matmul(pM[:, h // 3, (h % 3) * GW:(h % 3 + 1) * GW],
                                                 f[b][:, t, h * HD:(h + 1) * HD], gk[b][:, t, h, :],
                                                 start=False, stop=False, skip_group_check=True)
                        last.then_inc(S.counted(f"f_used{b}"), 1)

                    pe.wait_ge(S.sem("constants"), 4)
                    for n in range(3):
                        pe.matmul(pM[:, n, :], zl[:, :], zr[:, :], start=True, stop=True)
                    project(0, 0)
                    if steps > 1:
                        with pe.Fori(0, steps - 1) as i:
                            project(i, 1)
                            gather(i, 0)
                            project(i + 1, 0)
                            gather(i, 1)
                    project(steps - 1, 1)
                    gather(steps - 1, 0)
                    gather(steps - 1, 1)

                @block.gpsimd
                def _(pool):
                    start_counts(pool, S)
                    with pool.Fori(0, steps) as i:
                        for b in range(2):
                            after(pool, S.counted(f"rn{b}"), i + 1)
                            for t in range(TILES):
                                pool.tensor_tensor(gk[b][:, t, :, 0:HD], f[b][:, t, :].rearrange("p (h d) -> p h d", h=H),
                                                   ks[b][:, 2, t, :].unsqueeze(2).broadcast_to([P, H, HD]),
                                                   ALU.mult).then_inc(S.counted(f"gk{b}"), 1)
            with nc.Block() as block:
                @block.vector
                def _(dve):
                    for n in range(3):
                        k = min(3, H - 3 * n)
                        dve.tensor_copy(Msb[:, 3 * n:3 * n + k, :],
                                        pM[:, n, 0:k * GW].rearrange("p (h g) -> p h g", g=GW))
        with ExitStack() as mem:
            def sb(name, shape, dt=F32):
                return mem.enter_context(nc.sbuf_tensor(f"l2x_{name}", shape, dt))
            b1, lg, lb = sb("b1", [H, HD]), sb("lg", [H, HD]), sb("lb", [H, HD])
            w2, b2 = sb("w2", [P, 3]), sb("b2", [H, 3])
            wo, bo = sb("wo", [P, H, DIM]), sb("bo", [P, DIM])
            ones, off = sb("ones", [P, P]), sb("off", [P, P])
            qc, corr = sb("qc", [P, H, HD]), sb("corr", [P, H, HD])
            cs, dec = sb("cs", [P, H]), sb("dec", [P, H])
            gT = sb("gT", [P, 2, H])
            h1, nw3, h1T = sb("h1", [H, HD]), sb("nw3", [H, 16]), sb("h1T", [P, H])
            lo, sw, dw = sb("lo", [H, 3]), sb("sw", [H, 4]), sb("dw", [H, H, 3])
            mix = sb("mix", [P, H, 3])
            ca, cb = sb("ca", [P, H]), sb("cb", [P, H])
            cbw = sb("cbw", [P, H, P])
            a, aT, yT, cbT = sb("a", [P, H, HD]), sb("aT", [P, H, P]), sb("yT", [P, H, P]), sb("cbT", [P, H, P])
            p1 = mem.enter_context(nc.psum_tensor("l2x_p1", [P, 2, BANK], F32))
            p2 = mem.enter_context(nc.psum_tensor("l2x_p2", [P, 2, BANK], F32))
            p3, p4, p5, p6 = [mem.enter_context(nc.psum_tensor(f"l2x_p{n}", [P, BANK], F32)) for n in range(3, 7)]
            loads = Loads(S.sem("late_loads"))
            heads = lambda ap: ap.rearrange("p a (b d) -> p (a b) d", d=P)
            with nc.Block() as block:
                @block.sync
                def _(sp):
                    loads(sp.dma_start(wp1[:, :, :], by_rows(A["L2_xattn_wp_w1"])))
                    loads(sp.dma_start(b1[:, :], A["L2_xattn_wp_b1"].partition_broadcast(H)))
                    loads(sp.dma_start(lg[:, :], A["L2_xattn_wp_ln_g"].partition_broadcast(H)))
                    loads(sp.dma_start(lb[:, :], A["L2_xattn_wp_ln_b"].partition_broadcast(H)))
                    loads(sp.dma_start(w2[:, :], A["L2_xattn_wp_w2"]))
                    loads(sp.dma_start(b2[:, :], A["L2_xattn_wp_b2"].partition_broadcast(H)))
                    loads(sp.dma_start(wo[:, :, :], by_rows(A["L2_xattn_w_out"])))
                    loads(sp.dma_start(bo[:, :], A["L2_xattn_b_out"].partition_broadcast(P)))

                @block.scalar
                def _(act):
                    act.wait_ge(S.sem("corr_total"), 1)
                    act.activation(dec[:, :], p3[:, 0:H], ACT.Sqrt).then_inc(S.sem("corr_root"), 1)
                    norm_scalar(act, S, "h", nw3, rows=H)
                    act.wait_ge(S.sem("corr_root"), 1)
                    act.activation(dec[:, :], dec[:, :], ACT.Exp, scale=-5.0 / P / (HD * HD)).then_inc(
                        S.sem("decorr"), 1)
                    act.wait_ge(S.sem("w_shifted"), 1)
                    act.activation(lo[:, :], lo[:, :], ACT.Exp, accum_out=sw[:, 1:2]).then_inc(S.sem("w_exp"), 1)

                @block.vector
                def _(dve):
                    link = Link(dve, S.sem("late_link"))
                    fqh = fq[:, :].rearrange("p (h d) -> p h d", h=H)
                    link(dve.memset(ones[:, :], 1.0))
                    link(dve.tensor_scalar(off[:, :], R.ident[:, :], -1.0, 1.0, ALU.mult, ALU.add))
                    link(dve.tensor_scalar(cs[:, :], qs[:, 0, :], 1.0 / HD, None, ALU.mult))
                    link(dve.tensor_tensor(qc[:, :, :], fqh, cs[:, :].unsqueeze(2).broadcast_to([P, H, HD]),
                                           ALU.subtract))
                    dve.sem_inc(S.sem("qc"), 1)
                    dve.wait_ge(S.sem("corr"), 1)
                    link(dve.tensor_tensor(corr[:, :, :], heads(p1[:, :, :]),
                                           off[:, :].unsqueeze(1).broadcast_to([P, H, P]), ALU.mult))
                    link(dve.tensor_tensor(corr[:, :, :], corr[:, :, :], corr[:, :, :], ALU.mult))
                    link(dve.tensor_reduce(cs[:, :], corr[:, :, :], AX.X, ALU.add))
                    dve.sem_inc(S.sem("corr_sq"), 1)
                    dve.wait_ge(S.sem("q_mean"), 1)
                    link(dve.tensor_scalar(gT[:, 0, :], p4[:, 0:H], 1.0 / P, None, ALU.mult))
                    link(dve.tensor_scalar(gT[:, 1, :], Msb[:, :, HD + 1], 1.0 / R.keys, None, ALU.mult))
                    dve.sem_inc(S.sem("gT"), 1)
                    dve.wait_ge(S.sem("late_loads"), loads.total)
                    dve.wait_ge(S.sem("h1"), 1)
                    link(dve.tensor_tensor(h1[:, :], p5[0:H, 0:HD], b1[:, :], ALU.add))
                    norm_vector(dve, link, S, "h", h1[:, :], h1[:, :], nw3, rows=H)
                    link(dve.tensor_tensor(h1[:, :], h1[:, :], lg[:, :], ALU.mult))
                    link(dve.tensor_tensor(h1[:, :], h1[:, :], lb[:, :], ALU.add))
                    link(dve.tensor_scalar(h1[:, :], h1[:, :], 0.0, None, ALU.max))
                    dve.sem_inc(S.sem("h1_relu"), 1)
                    dve.wait_ge(S.sem("h1_turned"), 1)
                    dve.tensor_copy(h1T[:, :], p5[:, 0:H]).then_inc(S.sem("h1T"), 1)
                    dve.wait_ge(S.sem("logits"), 1)
                    link(dve.tensor_tensor(lo[:, :], p5[0:H, 0:3], b2[:, :], ALU.add))
                    link(dve.tensor_reduce(sw[:, 0:1], lo[:, :], AX.X, ALU.max))
                    dve.tensor_scalar(lo[:, :], lo[:, :], sw[:, 0:1], None, ALU.subtract).then_inc(
                        S.sem("w_shifted"), 1)
                    dve.wait_ge(S.sem("w_exp"), 1)
                    link(dve.reciprocal(sw[:, 2:3], sw[:, 1:2]))
                    link(dve.tensor_scalar(lo[:, :], lo[:, :], sw[:, 2:3], None, ALU.mult))
                    link(dve.tensor_tensor(dw[:, :, :], lo[:, :].unsqueeze(1).broadcast_to([H, H, 3]),
                                           R.ident[0:H, 0:H].unsqueeze(2).broadcast_to([H, H, 3]), ALU.mult))
                    dve.sem_inc(S.sem("dw"), 1)
                    dve.wait_ge(S.sem("mix"), 1)
                    link(dve.tensor_copy(mix[:, :, :], p6[:, 0:3 * H].rearrange("p (h k) -> p h k", k=3)))
                    dve.wait_ge(S.sem("decorr"), 1)
                    link(dve.tensor_tensor(ca[:, :], mix[:, :, 1], dec[:, :], ALU.mult))
                    link(dve.tensor_tensor(ca[:, :], ca[:, :], mix[:, :, 0], ALU.add))
                    link(dve.tensor_tensor(ca[:, :], ca[:, :], qs[:, 2, :], ALU.mult))
                    link(dve.tensor_tensor(cb[:, :], mix[:, :, 2], qs[:, 3, :], ALU.mult))
                    link(dve.tensor_tensor(a[:, :, :], fqh, ca[:, :].unsqueeze(2).broadcast_to([P, H, HD]), ALU.mult))
                    link(dve.tensor_copy(cbw[:, :, :], cb[:, :].unsqueeze(2).broadcast_to([P, H, P])))
                    dve.sem_inc(S.sem("a"), 1)
                    dve.wait_ge(S.sem("a_turned"), 1)
                    link(dve.tensor_copy(aT[:, :, :], heads(p1[:, :, :])))
                    link(dve.tensor_copy(cbT[:, :, :], heads(p2[:, :, :])))
                    dve.sem_inc(S.sem("aT"), 1)
                    for h in range(H):
                        link(dve.tensor_scalar(yT[:, h, :], cbT[:, h, :], Msb[:, h, HD:HD + 1], None, ALU.mult))
                    dve.wait_ge(S.sem("mixed"), 1)
                    link(dve.tensor_tensor(yT[:, :, :], yT[:, :, :], heads(p1[:, :, :]), ALU.add))
                    dve.sem_inc(S.sem("yT"), 1)
                    link(dve.tensor_tensor(R.x[:, :], R.x[:, :], bo[:, :], ALU.add))
                    dve.wait_ge(S.sem("y"), 1)
                    dve.tensor_tensor(R.x[:, :], R.x[:, :], p3[:, 0:DIM], ALU.add)

                @block.tensor
                def _(pe):
                    pe.wait_ge(S.sem("qc"), 1)
                    for h in range(H):
                        last = pe.matmul(p1[:, h // 4, (h % 4) * P:(h % 4 + 1) * P], qc[:, h, :], qc[:, h, :],
                                         start=True, stop=True)
                    last.then_inc(S.sem("corr"), 1)
                    for h in range(H):
                        last = pe.matmul(p4[:, h:h + 1], fq[:, h * HD:(h + 1) * HD], ones[:, 0:1], start=True,
                                         stop=True)
                    last.then_inc(S.sem("q_mean"), 1)
                    pe.wait_ge(S.sem("corr_sq"), 1)
                    pe.matmul(p3[:, 0:H], ones[:, :], cs[:, :], start=True, stop=True).then_inc(
                        S.sem("corr_total"), 1)
                    pe.wait_ge(S.sem("gT"), 1)
                    pe.wait_ge(S.sem("late_loads"), loads.total)
                    for c in range(2):
                        last = pe.matmul(p5[0:H, 0:HD], gT[:, c, :], wp1[:, c, :], start=(c == 0), stop=(c == 1))
                    last.then_inc(S.sem("h1"), 1)
                    pe.wait_ge(S.sem("h1_relu"), 1)
                    pe.transpose(p5[:, 0:H], h1[:, :], R.ident[0:H, 0:H]).then_inc(S.sem("h1_turned"), 1)
                    pe.wait_ge(S.sem("h1T"), 1)
                    pe.matmul(p5[0:H, 0:3], h1T[:, :], w2[:, :], start=True, stop=True).then_inc(S.sem("logits"), 1)
                    pe.wait_ge(S.sem("dw"), 1)
                    pe.matmul(p6[:, 0:3 * H], ones[0:H, :], dw[:, :, :].rearrange("p h k -> p (h k)"),
                              start=True, stop=True).then_inc(S.sem("mix"), 1)
                    pe.wait_ge(S.sem("a"), 1)
                    for h in range(H):
                        pe.transpose(p1[:, h // 4, (h % 4) * P:(h % 4 + 1) * P], a[:, h, :], R.ident[:, :])
                        last = pe.matmul(p2[:, h // 4, (h % 4) * P:(h % 4 + 1) * P], cbw[:, h, :], R.ident[:, :],
                                         start=True, stop=True)
                    last.then_inc(S.sem("a_turned"), 1)
                    pe.wait_ge(S.sem("aT"), 1)
                    for h in range(H):
                        last = pe.matmul(p1[:, h // 4, (h % 4) * P:(h % 4 + 1) * P], Msb[:, h, 0:HD], aT[:, h, :],
                                         start=True, stop=True)
                    last.then_inc(S.sem("mixed"), 1)
                    pe.wait_ge(S.sem("yT"), 1)
                    for h in range(H):
                        last = pe.matmul(p3[:, 0:DIM], yT[:, h, :], wo[:, h, :], start=(h == 0), stop=(h == H - 1))
                    last.then_inc(S.sem("y"), 1)


INNER, STATES, TAPS = 512, 16, 4
IC = INNER // P


def conv_silu_vector(dve, link, S, pad, xc, sx, taps, bias):
    for c in range(IC):
        last = dve.tensor_scalar(xc[:, c, :], pad[:, c, 0:P], taps[:, c, 0:1], None, ALU.mult)
    link(last)
    for k in range(1, TAPS):
        for c in range(IC):
            last = dve.scalar_tensor_tensor(xc[:, c, :], pad[:, c, k:k + P], taps[:, c, k:k + 1], xc[:, c, :],
                                            ALU.mult, ALU.add)
        link(last)
    for c in range(IC):
        last = dve.tensor_scalar(xc[:, c, :], xc[:, c, :], bias[:, c:c + 1], None, ALU.add)
    link(last)
    dve.sem_inc(S.sem("conv"), 1)
    dve.wait_ge(S.sem("sigmoid"), 1)
    link(dve.tensor_tensor(xc[:, :, :], xc[:, :, :], sx[:, :, :], ALU.mult))


def softplus_vector(dve, link, S, src, mag, delta):
    link(dve.tensor_scalar(mag[:, :, :], src, -1.0, None, ALU.mult))
    dve.tensor_tensor(mag[:, :, :], mag[:, :, :], src, ALU.min).then_inc(S.sem("mag"), 1)
    link(dve.tensor_scalar(delta[:, :, :], src, 0.0, None, ALU.max))
    dve.wait_ge(S.sem("log1p"), 1)
    link(dve.tensor_tensor(delta[:, :, :], delta[:, :, :], mag[:, :, :], ALU.add))


def softplus_scalar(act, S, mag):
    act.wait_ge(S.sem("mag"), 1)
    act.activation(mag[:, :, :], mag[:, :, :], ACT.Exp).then_inc(S.sem("exp_mag"), 1)
    act.wait_ge(S.sem("exp_mag"), 1)
    act.activation(mag[:, :, :], mag[:, :, :], ACT.Ln, bias=1.0).then_inc(S.sem("log1p"), 1)


def mamba(nc, A, R, name, weights, selective):
    N3 = 16 + 2 * STATES
    with Stage(nc, name) as S:
        w_in = S.sb("w_in", [P, DC, 2 * INNER])
        w_out = S.sb("w_out", [P, IC, DIM])
        taps, cbias = S.sb("taps", [P, IC, TAPS]), S.sb("cbias", [P, IC])
        alog, dskip = S.sb("alog", [P, IC, STATES]), S.sb("dskip", [P, IC])
        xn, xT, nw = S.sb("xn", [P, DIM]), S.sb("xT", [P, DC, P]), S.sb("nw", [P, 16])
        pad = S.sb("pad", [P, IC, P + TAPS - 1])
        xc, sx, gate = S.sb("xc", [P, IC, P]), S.sb("sx", [P, IC, P]), S.sb("gate", [P, IC, P])
        mag, delta, u = S.sb("mag", [P, IC, P]), S.sb("delta", [P, IC, P]), S.sb("u", [P, IC, P])
        decay = [S.sb(f"decay{b}", [P, STATES, P]) for b in range(IC)]
        drive = [S.sb(f"drive{b}", [P, STATES, P]) for b in range(2)]
        state = [S.sb(f"state{b}", [P, STATES, P]) for b in range(2)]
        y = S.sb("y", [P, IC, P])
        if selective:
            wx, wdt, bdt = S.sb("wx", [P, IC, N3]), S.sb("wdt", [16, INNER]), S.sb("bdt", [P, IC])
            dbc = S.sb("dbc", [N3, P])
            bc = S.sb("bc", [P, 2 * STATES, P])
            bc_dram = nc.dram_tensor(f"{name}_bc_dram", (2 * STATES, P), F32, kind="Internal").ap()
            px = S.psum("px")
        pt, pi, pg, po = S.psum("pt"), S.psum("pi"), S.psum("pg"), S.psum("po")
        pd, py = S.psum("pd"), S.psum("py")
        loads = Loads(S.sem("loads"))
        with S.nc.Block() as block:
            @block.sync
            def _(sp):
                sp.dma_start(w_in[:, :, :], by_rows(A[weights["in"]])).then_inc(S.sem("w_in"), 16)
                loads(sp.dma_start(taps[:, :, :], by_rows(A[weights["conv"]])))
                loads(sp.dma_start(cbias[:, :], column(A[weights["conv_b"]]), allow_slow_non_contiguous=True))
                loads(sp.dma_start(alog[:, :, :], by_rows(A[weights["A_log"]])))
                loads(sp.dma_start(dskip[:, :], column(A[weights["D"]]), allow_slow_non_contiguous=True))
                loads(sp.dma_start(w_out[:, :, :], by_rows(A[weights["out"]])))
                if selective:
                    loads(sp.dma_start(wx[:, :, :], by_rows(A["L2_attn_W_xproj"])))
                    loads(sp.dma_start(wdt[:, :], A["L2_attn_W_dt"]))
                    loads(sp.dma_start(bdt[:, :], column(A["L2_attn_b_dt"]), allow_slow_non_contiguous=True))
                    sp.wait_ge(S.sem("dbc"), 1)
                    sp.dma_start(bc_dram, dbc[16:N3, :]).then_inc(S.sem("bc_out"), 16)
                    sp.wait_ge(S.sem("bc_out"), 16)
                    sp.dma_start(bc[:, :, :], bc_dram.partition_broadcast(P)).then_inc(S.sem("bc"), 16)

            @block.vector
            def _(dve):
                link = Link(dve, S.sem("dve_link"))
                link(dve.memset(pad[:, :, :], 0.0))
                norm_vector(dve, link, S, "n", R.x[:, :], xn[:, :], nw)
                turn_vector(dve, S, "n", xT, pt)
                dve.wait_ge(S.sem("loads"), loads.total)
                dve.wait_ge(S.sem("in_proj"), 1)
                link(dve.tensor_copy(pad[:, :, TAPS - 1:], pi[:, :].rearrange("p (c t) -> p c t", c=IC)))
                conv_silu_vector(dve, link, S, pad, xc, sx, taps, cbias)
                dve.sem_inc(S.sem("xc"), 1)
                if selective:
                    dve.wait_ge(S.sem("x_proj"), 1)
                    dve.tensor_copy(dbc[:, :], px[0:N3, 0:P]).then_inc(S.sem("dbc"), 1)
                    dve.wait_ge(S.sem("dt_proj"), 1)
                    for c in range(IC):
                        link(dve.tensor_scalar(u[:, c, :], pd[:, c * P:(c + 1) * P], bdt[:, c:c + 1], None, ALU.add))
                    softplus_vector(dve, link, S, u[:, :, :], mag, delta)
                    link(dve.tensor_tensor(u[:, :, :], delta[:, :, :], xc[:, :, :], ALU.mult))
                else:
                    softplus_vector(dve, link, S, xc[:, :, :], mag, delta)
                    link(dve.tensor_tensor(u[:, :, :], xc[:, :, :], xc[:, :, :], ALU.mult))
                dve.wait_ge(S.sem("minus_a"), 1)
                def rate(c):
                    dve.tensor_tensor(decay[c][:, :, :],
                                      delta[:, c, :].unsqueeze(1).broadcast_to([P, STATES, P]),
                                      alog[:, c, :].unsqueeze(2).broadcast_to([P, STATES, P]),
                                      ALU.mult).then_inc(S.sem("rate"), 1)

                dve.sem_inc(S.sem("u"), 1)
                rate(0)
                rate(1)
                if selective:
                    dve.wait_ge(S.sem("bc"), 16)
                for c in range(IC):
                    b = c % 2
                    dve.wait_ge(S.sem("decay"), c + 1)
                    link(dve.memset(decay[c][:, :, 0:1], 0.0))
                    flat = lambda ap: ap[:, :, :].rearrange("p n t -> p (n t)")
                    dve.wait_ge(S.sem("drive"), c + 1)
                    if c >= 2:
                        dve.wait_ge(S.sem("summed"), c - 1)
                    link(dve.tensor_tensor_scan(flat(state[b]), flat(decay[c]), flat(drive[b]), 0.0, ALU.mult,
                                                ALU.add))
                    if selective:
                        link(dve.tensor_tensor(state[b][:, :, :], state[b][:, :, :], bc[:, STATES:, :], ALU.mult))
                    dve.sem_inc(S.sem("state"), 1)
                    if c + 2 < IC:
                        rate(c + 2)
                dve.wait_ge(S.sem("summed"), IC)
                link(dve.tensor_copy(y[:, :, :], py[:, :].rearrange("p (c t) -> p c t", c=IC)))
                dve.wait_ge(S.sem("gate"), 1)
                link(dve.tensor_tensor(gate[:, :, :], gate[:, :, :], pg[:, :].rearrange("p (c t) -> p c t", c=IC),
                                       ALU.mult))
                if selective:
                    for c in range(IC):
                        link(dve.scalar_tensor_tensor(y[:, c, :], xc[:, c, :], dskip[:, c:c + 1], y[:, c, :],
                                                      ALU.mult, ALU.add))
                    link(dve.tensor_tensor(y[:, :, :], y[:, :, :], gate[:, :, :], ALU.mult))
                else:
                    link(dve.tensor_tensor(y[:, :, :], y[:, :, :], xc[:, :, :], ALU.mult))
                    link(dve.tensor_tensor(y[:, :, :], y[:, :, :], gate[:, :, :], ALU.mult))
                    for c in range(IC):
                        link(dve.scalar_tensor_tensor(y[:, c, :], xc[:, c, :], dskip[:, c:c + 1], y[:, c, :],
                                                      ALU.mult, ALU.add))
                dve.sem_inc(S.sem("y"), 1)
                dve.wait_ge(S.sem("out_proj"), 1)
                dve.tensor_tensor(R.x[:, :], R.x[:, :], po[:, 0:DIM], ALU.add)

            @block.scalar
            def _(act):
                norm_scalar(act, S, "n", nw)
                act.wait_ge(S.sem("gate_proj"), 1)
                act.activation(gate[:, :, :], pg[:, :].rearrange("p (c t) -> p c t", c=IC), ACT.Sigmoid).then_inc(
                    S.sem("gate"), 1)
                act.wait_ge(S.sem("conv"), 1)
                act.activation(sx[:, :, :], xc[:, :, :], ACT.Sigmoid).then_inc(S.sem("sigmoid"), 1)
                act.wait_ge(S.sem("loads"), loads.total)
                act.activation(alog[:, :, :], alog[:, :, :], ACT.Exp).then_inc(S.sem("minus_a"), 1)
                softplus_scalar(act, S, mag)
                if not selective:
                    act.wait_ge(S.sem("u"), 1)
                for c in range(IC):
                    if not selective:
                        if c >= 2:
                            act.wait_ge(S.sem("state"), c - 1)
                        act.activation(drive[c % 2][:, :, :], u[:, c, :].unsqueeze(1).broadcast_to([P, STATES, P]),
                                       ACT.Copy).then_inc(S.sem("drive"), 1)
                    act.wait_ge(S.sem("rate"), c + 1)
                    act.activation(decay[c][:, :, :], decay[c][:, :, :], ACT.Exp, scale=-1.0).then_inc(
                        S.sem("decay"), 1)

            @block.tensor
            def _(pe):
                turn_tensor(pe, S, "n", xn, pt, R.ident)
                pe.wait_ge(S.sem("w_in"), 16)
                pe.wait_ge(S.sem("n_xT"), 1)
                for side, out, signal in ((0, pi, "in_proj"), (1, pg, "gate_proj")):
                    for o in range(IC):
                        for c in range(DC):
                            at = side * INNER + o * P
                            last = pe.matmul(out[:, o * P:(o + 1) * P], w_in[:, c, at:at + P], xT[:, c, :],
                                             start=(c == 0), stop=(c == DC - 1))
                    last.then_inc(S.sem(signal), 1)
                pe.wait_ge(S.sem("loads"), loads.total)
                if selective:
                    pe.wait_ge(S.sem("xc"), 1)
                    for c in range(IC):
                        last = pe.matmul(px[0:N3, 0:P], wx[:, c, :], xc[:, c, :], start=(c == 0),
                                         stop=(c == IC - 1))
                    last.then_inc(S.sem("x_proj"), 1)
                    pe.wait_ge(S.sem("dbc"), 1)
                    for c in range(IC):
                        last = pe.matmul(pd[:, c * P:(c + 1) * P], wdt[:, c * P:(c + 1) * P], dbc[0:16, :],
                                         start=True, stop=True)
                    last.then_inc(S.sem("dt_proj"), 1)
                for c in range(IC):
                    pe.wait_ge(S.sem("state"), c + 1)
                    for n in range(STATES):
                        last = pe.matmul(py[:, c * P:(c + 1) * P], R.ident[:, :], state[c % 2][:, n, :],
                                         start=(n == 0), stop=(n == STATES - 1))
                    last.then_inc(S.sem("summed"), 1)
                pe.wait_ge(S.sem("y"), 1)
                for c in range(IC):
                    last = pe.matmul(po[:, 0:DIM], y[:, c, :], w_out[:, c, :], start=(c == 0), stop=(c == IC - 1))
                last.then_inc(S.sem("out_proj"), 1)

            if selective:
                @block.gpsimd
                def _(pool):
                    pool.wait_ge(S.sem("u"), 1)
                    pool.wait_ge(S.sem("bc"), 16)
                    for c in range(IC):
                        if c >= 2:
                            pool.wait_ge(S.sem("state"), c - 1)
                        pool.tensor_tensor(drive[c % 2][:, :, :], u[:, c, :].unsqueeze(1).broadcast_to([P, STATES, P]),
                                           bc[:, 0:STATES, :], ALU.mult).then_inc(S.sem("drive"), 1)


def l0_attn(nc, A, R):
    mamba(nc, A, R, "l0a", {"in": "L0_attn_W_in", "out": "L0_attn_W_out", "conv": "L0_attn_conv_w",
                            "conv_b": "L0_attn_conv_b", "A_log": "L0_attn_A_log", "D": "L0_attn_D"}, False)


def l2_attn(nc, A, R):
    mamba(nc, A, R, "l2a", {"in": "L2_attn_W_in", "out": "L2_attn_W_out", "conv": "L2_attn_W_conv",
                            "conv_b": "L2_attn_b_conv", "A_log": "L2_attn_A_log", "D": "L2_attn_D"}, True)


def l1_attn(nc, A, R):
    H, HD = 16, 16
    with Stage(nc, "l1a") as S:
        names = ("r", "k", "v", "g")
        w = S.sb("w", [P, 5, DC, DIM])
        mixc = S.sb("mixc", [P, 4, DC])
        omm = S.sb("omm", [P, 4, DC])
        td, u = S.sb("td", [P, H]), S.sb("u", [P, H])
        lnw, lnb = S.sb("lnw", [P, DIM]), S.sb("lnb", [P, DIM])
        lag, later, hm = S.sb("lag", [P, P]), S.sb("later", [P, P]), S.sb("hm", [P, 8])
        xn, nw = S.sb("xn", [P, DIM]), S.sb("nw", [P, 16])
        xp = S.sb("xp", [P, DC, P + 1])
        xm = S.sb("xm", [P, 4, DC, P])
        rb = [S.sb(f"rb{c}", [P, 8, P]) for c in range(DC)]
        kT, v, g = S.sb("kT", [P, DC, P]), S.sb("v", [P, DIM]), S.sb("g", [P, DIM])
        wm = S.sb("wm", [P, H, P])
        att = S.sb("att", [P, H, P])
        o, oc, sq = S.sb("o", [P, H, HD]), S.sb("oc", [P, H, HD]), S.sb("sq", [P, H, HD])
        m, va = S.sb("m", [P, H]), S.sb("va", [P, H])
        oT = S.sb("oT", [P, DC, P])
        pt, prk, pvg, po = S.psum("pt"), S.psum("prk"), S.psum("pvg"), S.psum("po")
        pa = S.psum("pa", 4)
        loads = Loads(S.sem("loads"))
        with S.nc.Block() as block:
            @block.sync
            def _(sp):
                for n, name in enumerate(names):
                    loads(sp.dma_start(w[:, n, :, :], by_rows(A[f"L1_attn_W_{name}"])))
                    loads(sp.dma_start(mixc[:, n, :], column(A[f"L1_attn_time_mix_{name}"]),
                                       allow_slow_non_contiguous=True))
                loads(sp.dma_start(w[:, 4, :, :], by_rows(A["L1_attn_W_o"])))
                loads(sp.dma_start(td[:, :], A["L1_attn_time_decay"].partition_broadcast(P)))
                loads(sp.dma_start(u[:, :], A["L1_attn_time_faaaa"].partition_broadcast(P)))
                loads(sp.dma_start(lnw[:, :], A["L1_attn_ln_w"].partition_broadcast(P)))
                loads(sp.dma_start(lnb[:, :], A["L1_attn_ln_b"].partition_broadcast(P)))
                loads(sp.dma_start(lag[:, :], A["c_lag"]))
                loads(sp.dma_start(later[:, :], A["c_later"]))
                loads(sp.dma_start(hm[:, :], A["c_head16"]))

            @block.vector
            def _(dve):
                link = Link(dve, S.sem("dve_link"))
                link(dve.memset(xp[:, :, :], 0.0))
                norm_vector(dve, link, S, "n", R.x[:, :], xn[:, :], nw)
                dve.wait_ge(S.sem("n_turned"), 1)
                link(dve.tensor_copy(xp[:, :, 1:], pt[:, 0:DIM].rearrange("p (c t) -> p c t", c=DC)))
                dve.wait_ge(S.sem("loads"), loads.total)
                link(dve.tensor_scalar(omm[:, :, :], mixc[:, :, :], -1.0, 1.0, ALU.mult, ALU.add))
                for n in range(4):
                    for c in range(DC):
                        link(dve.tensor_scalar(xm[:, n, c, :], xp[:, c, 0:P], omm[:, n, c:c + 1], None, ALU.mult))
                        link(dve.scalar_tensor_tensor(xm[:, n, c, :], xp[:, c, 1:], mixc[:, n, c:c + 1],
                                                      xm[:, n, c, :], ALU.mult, ALU.add))
                dve.sem_inc(S.sem("mixed"), 1)
                dve.wait_ge(S.sem("rk"), 1)
                for c in range(DC):
                    link(dve.tensor_tensor(rb[c][:, :, :],
                                           prk[:, c * P:(c + 1) * P].unsqueeze(1).broadcast_to([P, 8, P]),
                                           hm[:, :].unsqueeze(2).broadcast_to([P, 8, P]), ALU.mult))
                link(dve.tensor_copy(kT[:, :, :], prk[:, DIM:2 * DIM].rearrange("p (c t) -> p c t", c=DC)))
                dve.sem_inc(S.sem("rk_ready"), 1)
                dve.wait_ge(S.sem("rates"), 1)
                dve.tensor_scalar(td[:, :], td[:, :], 1e30, -1.0, ALU.min, ALU.mult).then_inc(S.sem("rate"), 1)
                dve.wait_ge(S.sem("powers"), 1)
                link(dve.tensor_tensor(wm[:, :, :], wm[:, :, :],
                                       later[:, :].unsqueeze(1).broadcast_to([P, H, P]), ALU.mult))
                for h in range(H):
                    link(dve.scalar_tensor_tensor(wm[:, h, :], R.ident[:, :], u[:, h:h + 1], wm[:, h, :],
                                                  ALU.mult, ALU.add))
                dve.wait_ge(S.sem("att"), 1)
                link(dve.tensor_tensor(att[:, :, :], pa[:, :, :].rearrange("p a (b q) -> p (a b) q", q=P),
                                       wm[:, :, :], ALU.mult))
                dve.wait_ge(S.sem("vg"), 1)
                dve.tensor_copy(v[:, :], pvg[:, 0:DIM]).then_inc(S.sem("att_ready"), 1)
                dve.wait_ge(S.sem("gate"), 1)
                link(dve.tensor_tensor(g[:, :], g[:, :], pvg[:, DIM:2 * DIM], ALU.mult))
                dve.wait_ge(S.sem("out"), 1)
                link(dve.tensor_scalar(o[:, :, :], po[:, 0:DIM].rearrange("p (h d) -> p h d", h=H), 1.0 / 8.0, None,
                                       ALU.mult))
                link(dve.tensor_reduce(m[:, :], o[:, :, :], AX.X, ALU.add))
                link(dve.tensor_scalar(m[:, :], m[:, :], 1.0 / HD, None, ALU.mult))
                link(dve.tensor_tensor(oc[:, :, :], o[:, :, :], m[:, :].unsqueeze(2).broadcast_to([P, H, HD]),
                                       ALU.subtract))
                link(dve.tensor_tensor(sq[:, :, :], oc[:, :, :], oc[:, :, :], ALU.mult))
                link(dve.tensor_reduce(va[:, :], sq[:, :, :], AX.X, ALU.add))
                dve.tensor_scalar(va[:, :], va[:, :], 1.0 / HD, EPS, ALU.mult, ALU.add).then_inc(S.sem("o_var"), 1)
                dve.wait_ge(S.sem("o_std"), 1)
                link(dve.reciprocal(va[:, :], va[:, :]))
                link(dve.tensor_tensor(oc[:, :, :], oc[:, :, :], va[:, :].unsqueeze(2).broadcast_to([P, H, HD]),
                                       ALU.mult))
                flat = oc[:, :, :].rearrange("p h d -> p (h d)")
                link(dve.tensor_tensor(xn[:, :], flat, lnw[:, :], ALU.mult))
                link(dve.tensor_tensor(xn[:, :], xn[:, :], lnb[:, :], ALU.add))
                dve.tensor_tensor(xn[:, :], xn[:, :], g[:, :], ALU.mult).then_inc(S.sem("gated"), 1)
                turn_vector(dve, S, "o", oT, pt)
                dve.wait_ge(S.sem("y"), 1)
                dve.tensor_tensor(R.x[:, :], R.x[:, :], po[:, DIM:2 * DIM], ALU.add)

            @block.scalar
            def _(act):
                norm_scalar(act, S, "n", nw)
                act.wait_ge(S.sem("loads"), loads.total)
                act.activation(td[:, :], td[:, :], ACT.Exp).then_inc(S.sem("rates"), 1)
                act.wait_ge(S.sem("rate"), 1)
                for h in range(H):
                    last = act.activation(wm[:, h, :], lag[:, :], ACT.Exp, scale=td[:, h:h + 1])
                last.then_inc(S.sem("powers"), 1)
                act.wait_ge(S.sem("vg"), 1)
                act.wait_ge(S.sem("att_ready"), 1)
                act.activation(g[:, :], pvg[:, DIM:2 * DIM], ACT.Sigmoid).then_inc(S.sem("gate"), 1)
                act.wait_ge(S.sem("o_var"), 1)
                act.activation(va[:, :], va[:, :], ACT.Sqrt).then_inc(S.sem("o_std"), 1)

            @block.tensor
            def _(pe):
                turn_tensor(pe, S, "n", xn, pt, R.ident)
                pe.wait_ge(S.sem("loads"), loads.total)
                pe.wait_ge(S.sem("mixed"), 1)
                for n in range(2):
                    for oo in range(DC):
                        for c in range(DC):
                            at = n * DIM + oo * P
                            last = pe.matmul(prk[:, at:at + P], w[:, n, c, oo * P:(oo + 1) * P], xm[:, n, c, :],
                                             start=(c == 0), stop=(c == DC - 1))
                last.then_inc(S.sem("rk"), 1)
                for n in range(2):
                    for c in range(DC):
                        last = pe.matmul(pvg[:, n * DIM:(n + 1) * DIM], xm[:, 2 + n, c, :], w[:, 2 + n, c, :],
                                         start=(c == 0), stop=(c == DC - 1))
                last.then_inc(S.sem("vg"), 1)
                pe.wait_ge(S.sem("rk_ready"), 1)
                for c in range(DC):
                    for half in range(2):
                        last = pe.matmul(pa[:, 2 * c + half, :], kT[:, c, :],
                                         rb[c][:, 4 * half:4 * half + 4, :].rearrange("p h q -> p (h q)"),
                                         start=True, stop=True)
                last.then_inc(S.sem("att"), 1)
                pe.wait_ge(S.sem("att_ready"), 1)
                for h in range(H):
                    last = pe.matmul(po[:, h * HD:(h + 1) * HD], att[:, h, :], v[:, h * HD:(h + 1) * HD],
                                     start=True, stop=True)
                last.then_inc(S.sem("out"), 1)
                turn_tensor(pe, S, "o", xn, pt, R.ident, ready="gated")
                pe.wait_ge(S.sem("o_xT"), 1)
                for c in range(DC):
                    last = pe.matmul(po[:, DIM:2 * DIM], oT[:, c, :], w[:, 4, c, :], start=(c == 0),
                                     stop=(c == DC - 1))
                last.then_inc(S.sem("y"), 1)


def l0_ffn(nc, A, R):
    E, FF = 8, 1024
    FC = FF // P
    with Stage(nc, "l0f") as S:
        w1 = [S.sb(f"w1_{b}", [P, DC, FF]) for b in range(2)]
        w2 = [S.sb(f"w2_{b}", [P, FC, DIM]) for b in range(2)]
        b1, b1r = S.sb("b1", [P, E + 1, FC]), S.sb("b1r", [(E + 1) * FC, P])
        b2, b2s = S.sb("b2", [E, DIM]), S.sb("b2s", [P, DIM])
        wr, br = S.sb("wr", [P, DC, E]), S.sb("br", [P, E])
        xn, xT, nw = S.sb("xn", [P, DIM]), S.sb("xT", [P, DC, P]), S.sb("nw", [P, 16])
        lg, pr, tmp, oh = S.sb("lg", [P, E]), S.sb("pr", [P, E]), S.sb("tmp", [P, E]), S.sb("oh", [P, E + 1])
        oh2, sw, wt = S.sb("oh2", [P, E + 1]), S.sb("sw", [P, 8]), S.sb("wt", [P, E])
        weT = S.sb("weT", [E, P])
        hT = [S.sb(f"hT{b}", [P, FC, P]) for b in range(2)]
        acc = S.sb("acc", [P, DIM])
        pt, pm = S.psum("pt"), S.psum("pm")
        ph = [S.psum(f"ph{b}", 2) for b in range(2)]
        py = [S.psum(f"py{b}") for b in range(2)]
        loads = Loads(S.sem("small"))

        def hidden(pe, b):
            for f in range(FC):
                for c in range(DC):
                    last = pe.matmul(ph[b][:, f // 4, (f % 4) * P:(f % 4 + 1) * P], w1[b][:, c, f * P:(f + 1) * P],
                                     xT[:, c, :], start=(c == 0), stop=(c == DC - 1))
            last.then_inc(S.counted(f"h{b}"), 1)

        def output(pe, b):
            for f in range(FC):
                last = pe.matmul(py[b][:, 0:DIM], hT[b][:, f, :], w2[b][:, f, :], start=(f == 0), stop=(f == FC - 1))
            last.then_inc(S.counted(f"y{b}"), 1)

        def gelu(act, b, bias):
            for f in range(FC):
                last = act.activation(hT[b][:, f, :], ph[b][:, f // 4, (f % 4) * P:(f % 4 + 1) * P], ACT.Gelu,
                                      bias=bias(f))
            last.then_inc(S.counted(f"hT{b}"), 1)

        with S.nc.Block() as block:
            @block.sync
            def _(sp):
                sp.dma_start(w1[0][:, :, :], by_rows(A["L0_ffn_shared_w1"])).then_inc(S.counted("w1_0"), 16)
                sp.dma_start(w2[0][:, :, :], by_rows(A["L0_ffn_shared_w2"])).then_inc(S.counted("w2_0"), 16)
                loads(sp.dma_start(b1r[0:E * FC, :], A["L0_ffn_exp_b1"].rearrange("e (f p) -> (e f) p", p=P)))
                loads(sp.dma_start(b1r[E * FC:, :], A["L0_ffn_shared_b1"].rearrange("(f p) -> f p", p=P)))
                loads(sp.dma_start(b2[:, :], A["L0_ffn_exp_b2"]))
                loads(sp.dma_start(b2s[:, :], A["L0_ffn_shared_b2"].partition_broadcast(P)))
                loads(sp.dma_start(wr[:, :, :], by_rows(A["L0_ffn_router_w"])))
                loads(sp.dma_start(br[:, :], A["L0_ffn_router_b"].partition_broadcast(P)))
                with sp.Fori(0, E // 2) as i:
                    for b in (1, 0):
                        e = i * 2 + (1 - b)
                        after(sp, S.counted(f"h{b}"), i + (1 - b))
                        sp.dma_start(w1[b][:, :, :], A["L0_ffn_exp_w1"][bass.ds(e, 1)].rearrange(
                            "e (c p) n -> p (e c) n", p=P)).then_inc(S.counted(f"w1_{b}"), 16)
                        after(sp, S.counted(f"y{b}"), i + (1 - b))
                        sp.dma_start(w2[b][:, :, :], A["L0_ffn_exp_w2"][bass.ds(e, 1)].rearrange(
                            "e (c p) n -> p (e c) n", p=P)).then_inc(S.counted(f"w2_{b}"), 16)

            @block.vector
            def _(dve):
                link = Link(dve, S.sem("dve_link"))
                norm_vector(dve, link, S, "n", R.x[:, :], xn[:, :], nw)
                turn_vector(dve, S, "n", xT, pt)
                dve.wait_ge(S.sem("b1_turned"), 1)
                dve.tensor_copy(b1[:, :, :], pm[:, 0:(E + 1) * FC].rearrange("p (e f) -> p e f", f=FC)).then_inc(
                    S.sem("b1_ready"), 1)
                dve.wait_ge(S.sem("small"), loads.total)
                dve.wait_ge(S.sem("router"), 1)
                link(dve.tensor_tensor(lg[:, :], pt[:, 0:E], br[:, :], ALU.add))
                softmax8_vector(dve, link, S, "r", lg[:, :], pr[:, :], sw)
                first_of_max(dve, link, oh, pr[:, :], sw[:, 3:4], tmp[:, :], R.idx_down[:, :])
                link(dve.scalar_tensor_tensor(lg[:, :], oh[:, 0:E], -2.0, pr[:, :], ALU.mult, ALU.add))
                first_of_max(dve, link, oh2, lg[:, :], sw[:, 4:5], tmp[:, :], R.idx_down[:, :])
                link(dve.tensor_tensor(oh[:, 0:E], oh[:, 0:E], oh2[:, 0:E], ALU.add))
                link(dve.tensor_tensor(sw[:, 5:6], sw[:, 3:4], sw[:, 4:5], ALU.add))
                link(dve.tensor_scalar(sw[:, 5:6], sw[:, 5:6], 1e-9, None, ALU.add))
                link(dve.reciprocal(sw[:, 5:6], sw[:, 5:6]))
                link(dve.tensor_tensor(wt[:, :], pr[:, :], oh[:, 0:E], ALU.mult))
                link(dve.tensor_scalar(wt[:, :], wt[:, :], sw[:, 5:6], None, ALU.mult))
                dve.sem_inc(S.sem("weights_of_experts"), 1)
                dve.wait_ge(S.sem("we_turned"), 1)
                dve.tensor_copy(weT[:, :], pm[0:E, P:2 * P]).then_inc(S.sem("weT_ready"), 1)
                dve.wait_ge(S.sem("b2_mixed"), 1)
                link(dve.tensor_tensor(acc[:, :], pm[:, DIM:2 * DIM], R.x[:, :], ALU.add))
                link(dve.tensor_tensor(acc[:, :], acc[:, :], b2s[:, :], ALU.add))
                after(dve, S.counted("y0"), 1)
                dve.tensor_tensor(acc[:, :], acc[:, :], py[0][:, 0:DIM], ALU.add).then_inc(S.counted("added0"), 1)
                with dve.Fori(0, E // 2) as i:
                    for b in (1, 0):
                        e = i * 2 + (1 - b)
                        after(dve, S.counted(f"y{b}"), i + (2 - b))
                        after(dve, S.counted(f"added{1 - b}"), i + 1)
                        dve.scalar_tensor_tensor(acc[:, :], py[b][:, 0:DIM], wt[:, bass.ds(e, 1)], acc[:, :],
                                                 ALU.mult, ALU.add).then_inc(S.counted(f"added{b}"), 1)
                after(dve, S.counted("added0"), E // 2 + 1)
                dve.tensor_copy(R.x[:, :], acc[:, :])

            @block.scalar
            def _(act):
                norm_scalar(act, S, "n", nw)
                softmax8_scalar(act, S, "r", pr[:, :], sw)
                act.wait_ge(S.sem("b1_ready"), 1)
                after(act, S.counted("h0"), 1)
                gelu(act, 0, lambda f: b1[:, E, f:f + 1])
                with act.Fori(0, E // 2) as i:
                    for b in (1, 0):
                        e = i * 2 + (1 - b)
                        act.wait_ge(S.sem("b1_ready"), 1)
                        after(act, S.counted(f"h{b}"), i + (2 - b))
                        after(act, S.counted(f"y{b}"), i + (1 - b))
                        gelu(act, b, lambda f: b1[:, bass.ds(e, 1), f])

            @block.tensor
            def _(pe):
                turn_tensor(pe, S, "n", xn, pt, R.ident)
                pe.wait_ge(S.sem("small"), loads.total)
                pe.transpose(pm[:, 0:(E + 1) * FC], b1r[:, :], R.ident[0:(E + 1) * FC, 0:(E + 1) * FC]).then_inc(
                    S.sem("b1_turned"), 1)
                pe.wait_ge(S.sem("n_xT"), 1)
                for c in range(DC):
                    last = pe.matmul(pt[:, 0:E], xT[:, c, :], wr[:, c, :], start=(c == 0), stop=(c == DC - 1))
                last.then_inc(S.sem("router"), 1)
                after(pe, S.counted("w1_0"), 16)
                hidden(pe, 0)
                pe.wait_ge(S.sem("weights_of_experts"), 1)
                pe.wait_ge(S.sem("b1_ready"), 1)
                pe.transpose(pm[0:E, P:2 * P], wt[:, :], R.ident[:, :]).then_inc(S.sem("we_turned"), 1)
                pe.wait_ge(S.sem("weT_ready"), 1)
                pe.matmul(pm[:, DIM:2 * DIM], weT[:, :], b2[:, :], start=True, stop=True).then_inc(
                    S.sem("b2_mixed"), 1)
                def finish(i, b):
                    after(pe, S.counted(f"w2_{b}"), (i + 1) * 16)
                    after(pe, S.counted(f"hT{b}"), i + 1)
                    after(pe, S.counted(f"added{b}"), i)
                    output(pe, b)

                with pe.Fori(0, E // 2) as i:
                    for b in (1, 0):
                        after(pe, S.counted(f"w1_{b}"), (i + (2 - b)) * 16)
                        after(pe, S.counted(f"hT{b}"), i + (1 - b))
                        hidden(pe, b)
                        finish(i, 1 - b)
                finish(E // 2, 0)

            @block.gpsimd
            def _(pool):
                start_counts(pool, S)


def l1_ffn(nc, A, R):
    E, FF = 8, 1024
    FC = FF // P
    with Stage(nc, "l1f") as S:
        w1 = [S.sb(f"w1_{b}", [P, DC, FF]) for b in range(2)]
        w2 = [S.sb(f"w2_{b}", [P, FC, DIM]) for b in range(2)]
        b1, b1r, b2 = S.sb("b1", [P, E, FC]), S.sb("b1r", [E * FC, P]), S.sb("b2", [E, DIM])
        wr, br = S.sb("wr", [P, DC, E]), S.sb("br", [P, E])
        xn, xT, nw = S.sb("xn", [P, DIM]), S.sb("xT", [P, DC, P]), S.sb("nw", [P, 16])
        lg, pr, tmp, oh = S.sb("lg", [P, E]), S.sb("pr", [P, E]), S.sb("tmp", [P, E]), S.sb("oh", [P, E + 1])
        sw, ohw, ones = S.sb("sw", [P, 4]), S.sb("ohw", [P, E, P]), S.sb("ones", [E, P])
        xe = S.sb("xe", [P, E, DC, P])
        hT = [S.sb(f"hT{b}", [P, FC, P]) for b in range(2)]
        xv = [S.sb(f"xv{b}", [P, DC, P]) for b in range(2)]
        pt, pb = S.psum("pt"), S.psum("pb", 2)
        ph = [S.psum(f"ph{b}", 2) for b in range(2)]
        py = S.psum("py")
        loads = Loads(S.sem("small"))
        with S.nc.Block() as block:
            @block.sync
            def _(sp):
                loads(sp.dma_start(b1r[:, :], A["L1_ffn_b1"].rearrange("e (f p) -> (e f) p", p=P)))
                loads(sp.dma_start(b2[:, :], A["L1_ffn_b2"]))
                loads(sp.dma_start(wr[:, :, :], by_rows(A["L1_ffn_Wr"])))
                loads(sp.dma_start(br[:, :], A["L1_ffn_br"].partition_broadcast(P)))
                with sp.Fori(0, E // 2) as i:
                    for b in range(2):
                        e = i * 2 + b
                        after(sp, S.counted(f"h{b}"), i)
                        sp.dma_start(w1[b][:, :, :], A["L1_ffn_W1"][bass.ds(e, 1)].rearrange(
                            "e (c p) n -> p (e c) n", p=P)).then_inc(S.counted(f"w1_{b}"), 16)
                        after(sp, S.counted(f"used{b}"), i)
                        sp.dma_start(w2[b][:, :, :], A["L1_ffn_W2"][bass.ds(e, 1)].rearrange(
                            "e (c p) n -> p (e c) n", p=P)).then_inc(S.counted(f"w2_{b}"), 16)

            @block.vector
            def _(dve):
                link = Link(dve, S.sem("dve_link"))
                link(dve.memset(ones[:, :], 1.0))
                norm_vector(dve, link, S, "n", R.x[:, :], xn[:, :], nw)
                turn_vector(dve, S, "n", xT, pt)
                dve.wait_ge(S.sem("b1_turned"), 1)
                dve.tensor_copy(b1[:, :, :], pb[:, 0, 0:E * FC].rearrange("p (e f) -> p e f", f=FC)).then_inc(
                    S.sem("b1_ready"), 1)
                dve.wait_ge(S.sem("small"), loads.total)
                dve.wait_ge(S.sem("router"), 1)
                link(dve.tensor_tensor(lg[:, :], pt[:, 0:E], br[:, :], ALU.add))
                softmax8_vector(dve, link, S, "r", lg[:, :], pr[:, :], sw)
                first_of_max(dve, link, oh, pr[:, :], sw[:, 3:4], tmp[:, :], R.idx_down[:, :])
                dve.tensor_copy(ohw[:, :, :], oh[:, 0:E].unsqueeze(2).broadcast_to([P, E, P])).then_inc(
                    S.sem("chosen"), 1)
                dve.wait_ge(S.sem("chosen_rows"), 1)
                for c in range(DC):
                    last = dve.tensor_tensor(xe[:, :, c, :], xT[:, c, :].unsqueeze(1).broadcast_to([P, E, P]),
                                             pb[:, :, :].rearrange("p a (b t) -> p (a b) t", t=P), ALU.mult)
                    link(last)
                dve.sem_inc(S.sem("xe"), 1)
                with dve.Fori(0, E // 2) as i:
                    for b in range(2):
                        after(dve, S.counted(f"h{b}"), i)
                        dve.tensor_copy(xv[b][:, :, :], xe[:, bass.ds(i * 2 + b, 1)].squeeze(1)).then_inc(
                            S.counted(f"xv{b}"), 1)
                dve.wait_ge(S.sem("y"), 1)
                dve.tensor_tensor(R.x[:, :], R.x[:, :], py[:, 0:DIM], ALU.add)

            @block.scalar
            def _(act):
                norm_scalar(act, S, "n", nw)
                softmax8_scalar(act, S, "r", pr[:, :], sw)
                act.wait_ge(S.sem("b1_ready"), 1)
                with act.Fori(0, E // 2) as i:
                    for b in range(2):
                        act.wait_ge(S.sem("b1_ready"), 1)
                        after(act, S.counted(f"h{b}"), i + 1)
                        after(act, S.counted(f"used{b}"), i)
                        for f in range(FC):
                            last = act.activation(hT[b][:, f, :], ph[b][:, f // 4, (f % 4) * P:(f % 4 + 1) * P],
                                                  ACT.Relu, bias=b1[:, bass.ds(i * 2 + b, 1), f])
                        last.then_inc(S.counted(f"hT{b}"), 1)

            @block.tensor
            def _(pe):
                turn_tensor(pe, S, "n", xn, pt, R.ident)
                pe.wait_ge(S.sem("small"), loads.total)
                pe.transpose(pb[:, 0, 0:E * FC], b1r[:, :], R.ident[0:E * FC, 0:E * FC]).then_inc(
                    S.sem("b1_turned"), 1)
                pe.wait_ge(S.sem("n_xT"), 1)
                for c in range(DC):
                    last = pe.matmul(pt[:, 0:E], xT[:, c, :], wr[:, c, :], start=(c == 0), stop=(c == DC - 1))
                last.then_inc(S.sem("router"), 1)
                pe.wait_ge(S.sem("chosen"), 1)
                pe.wait_ge(S.sem("b1_ready"), 1)
                for e in range(E):
                    last = pe.matmul(pb[:, e // 4, (e % 4) * P:(e % 4 + 1) * P], ohw[:, e, :], R.ident[:, :],
                                     start=True, stop=True)
                last.then_inc(S.sem("chosen_rows"), 1)
                pe.matmul(py[:, 0:DIM], ones[:, :], b2[:, :], start=True, stop=False, skip_group_check=True)
                def hidden(b, i):
                    after(pe, S.counted(f"w1_{b}"), (i + 1) * 16)
                    after(pe, S.counted(f"xv{b}"), i + 1)
                    after(pe, S.counted(f"hT{b}"), i)
                    for f in range(FC):
                        for c in range(DC):
                            last = pe.matmul(ph[b][:, f // 4, (f % 4) * P:(f % 4 + 1) * P],
                                             w1[b][:, c, f * P:(f + 1) * P], xv[b][:, c, :],
                                             start=(c == 0), stop=(c == DC - 1))
                    last.then_inc(S.counted(f"h{b}"), 1)

                def output(b, i):
                    after(pe, S.counted(f"w2_{b}"), (i + 1) * 16)
                    after(pe, S.counted(f"hT{b}"), i + 1)
                    for f in range(FC):
                        last = pe.matmul(py[:, 0:DIM], hT[b][:, f, :], w2[b][:, f, :], start=False, stop=False,
                                         skip_group_check=True)
                    last.then_inc(S.counted(f"used{b}"), 1)

                run_ahead(pe, E // 2, hidden, lambda ahead, now: (hidden(*ahead), output(*now)), output)
                for b in range(2):
                    after(pe, S.counted(f"used{b}"), E // 2)
                pe.sem_inc(S.sem("y"), 1)

            @block.gpsimd
            def _(pool):
                start_counts(pool, S)


def l2_ffn(nc, A, R):
    E, HID = 8, 128
    with Stage(nc, "l2f") as S:
        w1, b1, w2, b2 = S.sb("w1", [P, DC, HID]), S.sb("b1", [P, 1]), S.sb("w2", [P, E]), S.sb("b2", [P, E])
        we, be = S.sb("we", [P, E, DC, DIM]), S.sb("be", [E, DIM])
        xn, xT, nw = S.sb("xn", [P, DIM]), S.sb("xT", [P, DC, P]), S.sb("nw", [P, 16])
        hT = S.sb("hT", [P, P])
        lg, pr, tmp, oh = S.sb("lg", [P, E]), S.sb("pr", [P, E]), S.sb("tmp", [P, E]), S.sb("oh", [P, E + 1])
        sw, ohw, ohT = S.sb("sw", [P, 4]), S.sb("ohw", [P, E, P]), S.sb("ohT", [E, P])
        xe = S.sb("xe", [P, E, DC, P])
        pt, ph, pl, po, py = [S.psum(n) for n in ("pt", "ph", "pl", "po", "py")]
        pb = S.psum("pb", 2)
        loads = Loads(S.sem("loads"))
        experts = Loads(S.sem("experts"))
        with S.nc.Block() as block:
            @block.sync
            def _(sp):
                loads(sp.dma_start(w1[:, :, :], by_rows(A["L2_ffn_w1"])))
                loads(sp.dma_start(b1[:, :], column(A["L2_ffn_b1"]), allow_slow_non_contiguous=True))
                loads(sp.dma_start(w2[:, :], A["L2_ffn_w2"]))
                loads(sp.dma_start(b2[:, :], A["L2_ffn_b2"].partition_broadcast(P)))
                loads(sp.dma_start(be[:, :], A["L2_ffn_expert_b"]))
                experts(sp.dma_start(we[:, :, :, :].rearrange("p e c n -> p (e c) n"),
                                     A["L2_ffn_expert_W"].rearrange("e (c p) n -> p (e c) n", p=P)))

            @block.vector
            def _(dve):
                link = Link(dve, S.sem("dve_link"))
                norm_vector(dve, link, S, "n", R.x[:, :], xn[:, :], nw)
                turn_vector(dve, S, "n", xT, pt)
                dve.wait_ge(S.sem("loads"), loads.total)
                dve.wait_ge(S.sem("h"), 1)
                dve.tensor_scalar(hT[:, :], ph[:, 0:P], b1[:, 0:1], 0.0, ALU.add, ALU.max).then_inc(S.sem("hT"), 1)
                dve.wait_ge(S.sem("router"), 1)
                link(dve.tensor_tensor(lg[:, :], pl[:, 0:E], b2[:, :], ALU.add))
                softmax8_vector(dve, link, S, "r", lg[:, :], pr[:, :], sw)
                first_of_max(dve, link, oh, pr[:, :], sw[:, 3:4], tmp[:, :], R.idx_down[:, :])
                dve.tensor_copy(ohw[:, :, :], oh[:, 0:E].unsqueeze(2).broadcast_to([P, E, P])).then_inc(
                    S.sem("chosen"), 1)
                dve.wait_ge(S.sem("chosen_rows"), 1)
                dve.tensor_copy(ohT[:, :], po[0:E, 0:P]).then_inc(S.sem("ohT"), 1)
                for c in range(DC):
                    link(dve.tensor_tensor(xe[:, :, c, :], xT[:, c, :].unsqueeze(1).broadcast_to([P, E, P]),
                                           pb[:, :, :].rearrange("p a (b t) -> p (a b) t", t=P), ALU.mult))
                dve.sem_inc(S.sem("xe"), 1)
                dve.wait_ge(S.sem("y"), 1)
                dve.tensor_tensor(R.x[:, :], R.x[:, :], py[:, 0:DIM], ALU.add)

            @block.scalar
            def _(act):
                norm_scalar(act, S, "n", nw)
                softmax8_scalar(act, S, "r", pr[:, :], sw)

            @block.tensor
            def _(pe):
                turn_tensor(pe, S, "n", xn, pt, R.ident)
                pe.wait_ge(S.sem("loads"), loads.total)
                pe.wait_ge(S.sem("n_xT"), 1)
                for c in range(DC):
                    last = pe.matmul(ph[:, 0:P], w1[:, c, :], xT[:, c, :], start=(c == 0), stop=(c == DC - 1))
                last.then_inc(S.sem("h"), 1)
                pe.wait_ge(S.sem("hT"), 1)
                pe.matmul(pl[:, 0:E], hT[:, :], w2[:, :], start=True, stop=True).then_inc(S.sem("router"), 1)
                pe.wait_ge(S.sem("chosen"), 1)
                for e in range(E):
                    pe.matmul(pb[:, e // 4, (e % 4) * P:(e % 4 + 1) * P], ohw[:, e, :], R.ident[:, :],
                              start=True, stop=True)
                pe.transpose(po[0:E, 0:P], oh[:, 0:E], R.ident[:, :]).then_inc(S.sem("chosen_rows"), 1)
                pe.wait_ge(S.sem("ohT"), 1)
                pe.matmul(py[:, 0:DIM], ohT[:, :], be[:, :], start=True, stop=False)
                pe.wait_ge(S.sem("experts"), experts.total)
                pe.wait_ge(S.sem("xe"), 1)
                for e in range(E):
                    for c in range(DC):
                        last = pe.matmul(py[:, 0:DIM], xe[:, e, c, :], we[:, e, c, :], start=False,
                                         stop=(e == E - 1 and c == DC - 1))
                last.then_inc(S.sem("y"), 1)



class Residents:
    pass


def constants(keys):
    f = np.float32
    idx = np.arange(P)
    inv_freq = (1.0 / np.power(f(10000.0), np.arange(0, 64, 2, dtype=f) / f(64))).astype(f)
    theta = (np.arange(keys, dtype=f)[:, None] * inv_freq[None, :]).astype(f)
    cos, sin = np.cos(theta).astype(f).T, np.sin(theta).astype(f).T
    diff = idx[None, :] - idx[:, None]
    head16 = (idx[:, None] // 16 == np.arange(8)[None, :]).astype(f)
    head64 = ((idx[:, None] // 32) % 2 == np.arange(2)[None, :]).astype(f)
    count = np.broadcast_to(np.arange(32, dtype=f), (P, 32))
    return {
        "c_ident": np.eye(P, dtype=f),
        "c_head16": head16, "c_head64": head64,
        "c_count": np.ascontiguousarray(count),
        "c_lag": np.maximum(diff - 1, 0).astype(f), "c_later": (diff > 0).astype(f),
        "c_cos": np.ascontiguousarray(np.tile(cos, (4, 1))), "c_sin": np.ascontiguousarray(np.tile(sin, (4, 1))),
    }


def halves_together(w):
    return w.reshape(w.shape[0], 4, 2, 2, 32).transpose(0, 1, 3, 2, 4).reshape(w.shape[0], 512)


def layout(inputs):
    a = {k: np.asarray(v) for k, v in inputs.items()}
    out = constants(a["ctx_1024"].shape[1])
    flip = ["L0_attn_W_in", "L0_attn_W_out", "L1_xattn_wq", "L1_xattn_wk", "L1_xattn_wv", "L1_attn_W_r",
            "L1_attn_W_k", "L1_attn_W_v", "L1_attn_W_g", "L1_attn_W_o", "L2_xattn_w_in", "L2_xattn_wp_w1",
            "L2_xattn_wp_w2", "L2_xattn_w_out", "L3_attn_Wq", "L3_attn_Wk", "L3_attn_Wv"]
    for k, v in a.items():
        out[k] = v.T if k in flip else v
    out["ctx"] = a["ctx_1024"][0]
    out["ctxT"] = a["ctx_1024"][0].T
    out["L0_xattn_Wq"] = halves_together(a["L0_xattn_Wq"])
    out["L0_xattn_Wk"] = halves_together(a["L0_xattn_Wkv"][:, :512])
    out["L0_xattn_Wv"] = a["L0_xattn_Wkv"][:, 512:]
    out["mask_row"] = a["mask_BxS2_ff1"].reshape(-1, P)
    out["mask_qk"] = a["mask_BxSxS2_bk0"][0]
    for k in ("L0_attn_conv_w", "L2_attn_W_conv"):
        out[k] = a[k][:, 0, :]
    for k in ("k", "v", "r", "g"):
        out[f"L1_attn_time_mix_{k}"] = a[f"L1_attn_time_mix_{k}"].reshape(-1)
    for k in ("x", "ctx_1024", "mask_BxS2_ff1", "mask_BxSxS2_bk0", "L0_xattn_Wkv"):
        out.pop(k, None)
    out["x_in"] = a["x"][0]
    return {k: np.ascontiguousarray(v) for k, v in out.items()}


def program(nc, A, x_name, y_name, layers):
    R = Residents()
    keys = A["ctx"].shape[0]
    R.keys = keys
    with ExitStack() as memory:
        def sb(name, shape, dt=F32):
            return memory.enter_context(nc.sbuf_tensor(name, shape, dt))
        R.x = sb("tokens", [P, DIM])
        R.ident = sb("ident", [P, P])
        R.count = sb("count", [P, 32])
        R.count8 = sb("count8", [P, 8])
        R.idx_down = sb("idx_down", [P, 8])
        R.nT = nc.dram_tensor("scratch_nT", (DC, P, keys), F32, kind="Internal").ap()
        R.KT = nc.dram_tensor("scratch_KT", (4, P, keys), F32, kind="Internal").ap()
        R.KS = nc.dram_tensor("scratch_KS", (3 * DC, P, keys), BF16, kind="Internal").ap()
        R.ones_row = nc.dram_tensor("scratch_ones", (1, CHUNK), BF16, kind="Internal").ap()
        ones = sb("ones_row", [1, CHUNK], BF16)
        loaded = memory.enter_context(nc.semaphore("loaded"))
        counted = memory.enter_context(nc.semaphore("counted"))
        stored = memory.enter_context(nc.semaphore("stored"))
        with nc.Block() as block:
            @block.sync
            def _(sp):
                sp.dma_start(R.x[:, :], A[x_name]).then_inc(loaded, 16)
                sp.dma_start(R.ident[:, :], A["c_ident"]).then_inc(loaded, 16)
                sp.dma_start(R.count[:, :], A["c_count"]).then_inc(loaded, 16)
                sp.wait_ge(counted, 1)
                sp.dma_start(R.ones_row, ones[:, :]).then_inc(stored, 16)
                sp.wait_ge(stored, 16)

            @block.vector
            def _(dve):
                dve.memset(ones[:, :], 1.0).then_inc(counted, 1)
                dve.wait_ge(loaded, 48)
                dve.tensor_scalar(R.count8[:, :], R.count[:, 0:8], 8.0, None, ALU.mult)
                dve.tensor_scalar(R.idx_down[:, :], R.count[:, 0:8], -1.0, 8.0, ALU.mult, ALU.add)
        ctx_norm(nc, A, R)
        for layer in layers:
            LAYERS[layer](nc, A, R)
        with nc.Block() as block:
            @block.sync
            def _(sp):
                sp.dma_start(A[y_name], R.x[:, :]).then_inc(stored, 16)
                sp.wait_ge(stored, 32)


LAYERS = {
    "l0_xattn": l0_xattn, "l0_attn": l0_attn, "l0_ffn": l0_ffn,
    "l1_xattn": l1_xattn, "l1_attn": l1_attn, "l1_ffn": l1_ffn,
    "l2_xattn": l2_xattn, "l2_attn": l2_attn, "l2_ffn": l2_ffn,
    "l3_xattn": l3_xattn, "l3_attn": l3_attn, "l3_ffn": l3_ffn,
}



def kernel(**inputs):
    import concourse.bacc as bacc
    from concourse.bass_utils import run_bass_kernel_spmd

    nc = bacc.Bacc("TRN2", target_bir_lowering=False, num_devices=1)
    arrays = layout(inputs)
    A = {name: nc.dram_tensor(name, a.shape, mybir.dt.from_np(a.dtype), kind="ExternalInput").ap()
         for name, a in arrays.items()}
    A["x_out"] = nc.dram_tensor("x_out", (P, DIM), F32, kind="ExternalOutput").ap()
    program(nc, A, "x_in", "x_out", list(LAYERS))
    result = run_bass_kernel_spmd(nc, [arrays], core_ids=[0])
    return result.results[0]["x_out"].reshape(1, P, DIM)
```
